# Optimizing a Trainium2 kernel written in Bass

```python
import numpy as np
import jax
import jax.numpy as jnp

def _softmax(x, axis=-1):
    return jax.nn.softmax(x, axis=axis)

def _gelu(x):
    return jax.nn.gelu(x, approximate=True)

def _silu(x):
    return jax.nn.silu(x)

def _sigmoid(x):
    return jax.nn.sigmoid(x)

def _layernorm(x, axis=-1, eps=1e-05):
    m = jnp.mean(x, axis=axis, keepdims=True)
    v = jnp.var(x, axis=axis, keepdims=True)
    return (x - m) / jnp.sqrt(v + eps)

def _scatter_add(tgt, idx, src, axis=0):
    return tgt.at[idx].add(src)

def _segment_sum(src, seg, n):
    return jax.ops.segment_sum(src, seg, n)
kernel_name = 'mk_gps_d2_gnn_r32_18985d'

def setup_inputs(seed: int=0):
    np.random.seed(seed)
    _w = jnp.asarray

    def _rec_inputs():
        import jax
        import jax.numpy as jnp
        _gk = jax.random.key(seed)
        x = -0.0003713 + 1 * jax.random.normal(jax.random.fold_in(_gk, 1), (3125, 256), jnp.float32)
        _s = jax.random.randint(jax.random.fold_in(_gk, 2), (25000,), 0, 3125, jnp.int32)
        _d = jax.random.randint(jax.random.fold_in(_gk, 3), (25000,), 0, 3125, jnp.int32)
        _loop = jnp.arange(3125, dtype=jnp.int32)
        src = jnp.concatenate([_s, _d, _loop])
        dst = jnp.concatenate([_d, _s, _loop])
        _o = jnp.argsort(dst, stable=True)
        src = src[_o]
        dst = dst[_o]
        edge_attr_10 = jax.random.uniform(jax.random.fold_in(_gk, 12), (53125, 10), jnp.float32, 0.0, 1)
        edge_attr_4 = 0.00109026 + 0.999989 * jax.random.normal(jax.random.fold_in(_gk, 13), (53125, 4), jnp.float32)
        return (x, src, dst, edge_attr_10, edge_attr_4)
    x, src, dst, edge_attr_10, edge_attr_4 = _rec_inputs()

    def _L0_gnn_setup():
        import jax, jax.numpy as jnp
        import numpy as np
        N, IN, H, C = (50000, 256, 8, 32)
        E = 25000
        key = jax.random.key(seed)
        ks = jax.random.split(key, 10)
        s = 1.0 / np.sqrt(IN)
        inp = {'x': jax.random.normal(ks[0], (N, IN), dtype=jnp.float32), 'edge_index': jax.random.randint(ks[1], (2, E), 0, N, dtype=jnp.int32), 'Wq': jax.random.uniform(ks[2], (IN, H * C), jnp.float32, -s, s), 'bq': jnp.zeros((H * C,), jnp.float32), 'Wk': jax.random.uniform(ks[3], (IN, H * C), jnp.float32, -s, s), 'bk': jnp.zeros((H * C,), jnp.float32), 'Wv': jax.random.uniform(ks[4], (IN, H * C), jnp.float32, -s, s), 'bv': jnp.zeros((H * C,), jnp.float32), 'Ws': jax.random.uniform(ks[5], (IN, H * C), jnp.float32, -s, s), 'bs': jnp.zeros((H * C,), jnp.float32)}
        return inp
    _L0_gnn_all = _L0_gnn_setup()
    _L0_gnn_in = {k: v for k, v in _L0_gnn_all.items() if k in ('Wq', 'bq', 'Wk', 'bk', 'Wv', 'bv', 'Ws', 'bs')}
    del _L0_gnn_all

    def _L0_mix_setup():
        import jax, jax.numpy as jnp
        import numpy as np
        HEADS = 8
        DIM_HEAD = 64
        EPS = 1e-05

        def _inst_norm_lastdim(t):
            mu = jnp.mean(t, axis=-1, keepdims=True)
            var = jnp.mean(jnp.square(t - mu), axis=-1, keepdims=True)
            return (t - mu) * jax.lax.rsqrt(var + EPS)
        key = jax.random.key(seed)
        k1, k2, k3, k4 = jax.random.split(key, 4)
        b, n, dim = (4, 256, 256)
        inner = HEADS * DIM_HEAD
        x = jax.random.normal(k1, (b, n, dim), dtype=jnp.float32)
        Wqkv = jax.random.normal(k2, (3 * inner, dim), dtype=jnp.float32) * (1.0 / np.sqrt(dim))
        Wout = jax.random.normal(k3, (dim, inner), dtype=jnp.float32) * (1.0 / np.sqrt(inner))
        bout = jax.random.normal(k4, (dim,), dtype=jnp.float32) * 0.01
        return {'x': x, 'Wqkv': Wqkv, 'Wout': Wout, 'bout': bout}
    _L0_mix_all = _L0_mix_setup()
    _L0_mix_in = {k: v for k, v in _L0_mix_all.items() if k in ('Wqkv', 'Wout', 'bout')}
    del _L0_mix_all

    def _L0_ffn_setup():
        import math
        import jax, jax.numpy as jnp
        import numpy as np
        CAPACITY_FACTOR = 1.25
        key = jax.random.key(seed)
        ks = jax.random.split(key, 5)
        B, L, D, F, E = (8, 256, 256, 1024, 8)
        h = jax.random.normal(ks[0], (B, L, D), dtype=jnp.float32)
        gate_w = jax.random.normal(ks[1], (D, E), dtype=jnp.float32) * 0.02
        gate_b = jnp.zeros((E,), dtype=jnp.float32)
        w1 = jax.random.normal(ks[2], (E, D, F), dtype=jnp.float32) * (1.0 / math.sqrt(D))
        b1 = jnp.zeros((E, F), dtype=jnp.float32)
        w2 = jax.random.normal(ks[3], (E, F, D), dtype=jnp.float32) * (1.0 / math.sqrt(F))
        b2 = jnp.zeros((E, D), dtype=jnp.float32)
        return {'h': h, 'gate_w': gate_w, 'gate_b': gate_b, 'w1': w1, 'b1': b1, 'w2': w2, 'b2': b2}
    _L0_ffn_all = _L0_ffn_setup()
    _L0_ffn_in = {k: v for k, v in _L0_ffn_all.items() if k in ('gate_w', 'gate_b', 'w1', 'b1', 'w2', 'b2')}
    del _L0_ffn_all

    def _L1_gnn_setup():
        import jax, jax.numpy as jnp
        import numpy as np
        MUL = 64
        N_NODES = 50000
        N_EDGES = 25000
        NUM_NEIGHBORS = 16.0
        SILU_NORM = 1.679177
        key = jax.random.key(seed)
        ks = jax.random.split(key, 9)
        node_in = jax.random.normal(ks[0], (N_NODES, 4 * MUL), dtype=jnp.float32)
        edge_src = jax.random.randint(ks[1], (N_EDGES,), 0, N_NODES)
        edge_dst = jax.random.randint(ks[2], (N_EDGES,), 0, N_NODES)
        edge_attr = jax.random.normal(ks[3], (N_EDGES, 4), dtype=jnp.float32)
        edge_len_emb = jax.random.uniform(ks[4], (N_EDGES, 10), dtype=jnp.float32)
        w_00_0 = jax.random.normal(ks[5], (MUL, MUL), dtype=jnp.float32)
        w_11_0 = jax.random.normal(ks[6], (MUL, MUL), dtype=jnp.float32)
        w_01_1 = jax.random.normal(ks[7], (MUL, MUL), dtype=jnp.float32)
        w_10_1 = jax.random.normal(ks[8], (MUL, MUL), dtype=jnp.float32)
        kf = jax.random.split(jax.random.fold_in(key, 1), 2)
        fc_w1 = jax.random.normal(kf[0], (10, 64), dtype=jnp.float32)
        fc_w2 = jax.random.normal(kf[1], (64, 1), dtype=jnp.float32)
        return {'node_in': node_in, 'edge_attr': edge_attr, 'edge_len_emb': edge_len_emb, 'w_00_0': w_00_0, 'w_11_0': w_11_0, 'w_01_1': w_01_1, 'w_10_1': w_10_1, 'fc_w1': fc_w1, 'fc_w2': fc_w2, 'edge_src': edge_src, 'edge_dst': edge_dst}
    _L1_gnn_all = _L1_gnn_setup()
    _L1_gnn_in = {k: v for k, v in _L1_gnn_all.items() if k in ('w_00_0', 'w_11_0', 'w_01_1', 'w_10_1', 'fc_w1', 'fc_w2')}
    del _L1_gnn_all

    def _L1_mix_setup():
        import jax, jax.numpy as jnp
        import numpy as np
        B, L, D, H = (4, 512, 256, 8)
        DK = D // H

        def _heads(t):
            b, l, d = t.shape
            return t.reshape(b, l, H, DK).transpose(0, 2, 1, 3)
        key = jax.random.key(seed)
        ks = jax.random.split(key, 9)
        s = 0.02
        return {'x': jax.random.normal(ks[0], (B, L, D), dtype=jnp.float32), 'Wq': jax.random.normal(ks[1], (D, D), dtype=jnp.float32) * s, 'bq': jnp.zeros((D,), dtype=jnp.float32), 'Wk': jax.random.normal(ks[2], (D, D), dtype=jnp.float32) * s, 'bk': jnp.zeros((D,), dtype=jnp.float32), 'Wv': jax.random.normal(ks[3], (D, D), dtype=jnp.float32) * s, 'bv': jnp.zeros((D,), dtype=jnp.float32), 'Wfc': jax.random.normal(ks[4], (D, D), dtype=jnp.float32) * s, 'bfc': jnp.zeros((D,), dtype=jnp.float32)}
    _L1_mix_all = _L1_mix_setup()
    _L1_mix_in = {k: v for k, v in _L1_mix_all.items() if k in ('Wq', 'bq', 'Wk', 'bk', 'Wv', 'bv', 'Wfc', 'bfc')}
    del _L1_mix_all

    def _L1_ffn_setup():
        import jax, jax.numpy as jnp
        import numpy as np
        B, N, D = (16, 128, 256)
        NUM_EXPERTS, TOP_K, HEADS = (4, 2, 4)
        N_EDGES = 32768
        LN_EPS = 1e-05

        def _layernorm(x, g, b):
            mu = x.mean(-1, keepdims=True)
            var = ((x - mu) ** 2).mean(-1, keepdims=True)
            return (x - mu) * jax.lax.rsqrt(var + LN_EPS) * g + b

        def _forward(x, edge_index, W_gat, att_src, att_dst, b_gat, ln_gamma, ln_beta, W1, b1, W2, b2):
            Bc, Nc, Dc = x.shape
            M = Bc * Nc
            x_flat = x.reshape(M, Dc)
            h = (x_flat @ W_gat).reshape(M, HEADS, NUM_EXPERTS)
            loops = jnp.arange(M, dtype=edge_index.dtype)
            src = jnp.concatenate([edge_index[0], loops])
            dst = jnp.concatenate([edge_index[1], loops])
            a_src = (h * att_src).sum(-1)
            a_dst = (h * att_dst).sum(-1)
            e = jax.nn.leaky_relu(a_src[src] + a_dst[dst], negative_slope=0.2)
            e_max = jax.ops.segment_max(e, dst, num_segments=M)
            ee = jnp.exp(e - e_max[dst])
            denom = jax.ops.segment_sum(ee, dst, num_segments=M)
            alpha = ee / (denom[dst] + 1e-16)
            msg = h[src] * alpha[:, :, None]
            agg = jax.ops.segment_sum(msg, dst, num_segments=M).reshape(M, HEADS * NUM_EXPERTS) + b_gat
            scores = _layernorm(agg, ln_gamma, ln_beta).reshape(M, HEADS, NUM_EXPERTS).mean(1)
            scores = scores.reshape(Bc, Nc, NUM_EXPERTS)
            topk_s, topk_i = jax.lax.top_k(scores, TOP_K)
            w = jax.nn.softmax(topk_s, axis=-1)
            out = jnp.zeros_like(x)
            for ei in range(NUM_EXPERTS):
                g = jnp.where(topk_i == ei, w, 0.0).sum(-1)
                hh = jax.nn.gelu(x @ W1[ei] + b1[ei], approximate=False)
                out = out + g[..., None] * (hh @ W2[ei] + b2[ei])
            return out
        key = jax.random.key(seed)
        ks = jax.random.split(key, 8)
        s = 0.05
        return {'x': jax.random.normal(ks[0], (B, N, D), jnp.float32), 'W_gat': jax.random.normal(ks[1], (D, HEADS * NUM_EXPERTS), jnp.float32) * s, 'att_src': jax.random.normal(ks[2], (HEADS, NUM_EXPERTS), jnp.float32) * s, 'att_dst': jax.random.normal(ks[3], (HEADS, NUM_EXPERTS), jnp.float32) * s, 'b_gat': jnp.zeros((HEADS * NUM_EXPERTS,), jnp.float32), 'ln_gamma': jnp.ones((HEADS * NUM_EXPERTS,), jnp.float32), 'ln_beta': jnp.zeros((HEADS * NUM_EXPERTS,), jnp.float32), 'W1': jax.random.normal(ks[4], (NUM_EXPERTS, D, 2 * D), jnp.float32) * s, 'b1': jnp.zeros((NUM_EXPERTS, 2 * D), jnp.float32), 'W2': jax.random.normal(ks[5], (NUM_EXPERTS, 2 * D, D), jnp.float32) * s, 'b2': jnp.zeros((NUM_EXPERTS, D), jnp.float32), 'edge_index': jax.random.randint(ks[6], (2, N_EDGES), 0, B * N, jnp.int32)}
    _L1_ffn_all = _L1_ffn_setup()
    _L1_ffn_in = {k: v for k, v in _L1_ffn_all.items() if k in ('W_gat', 'att_src', 'att_dst', 'b_gat', 'ln_gamma', 'ln_beta', 'W1', 'b1', 'W2', 'b2', 'edge_index')}
    del _L1_ffn_all
    return {'x': x, 'src': src, 'dst': dst, 'edge_attr_10': edge_attr_10, 'edge_attr_4': edge_attr_4, 'L0_gnn_Wq': _L0_gnn_in['Wq'], 'L0_gnn_bq': _L0_gnn_in['bq'], 'L0_gnn_Wk': _L0_gnn_in['Wk'], 'L0_gnn_bk': _L0_gnn_in['bk'], 'L0_gnn_Wv': _L0_gnn_in['Wv'], 'L0_gnn_bv': _L0_gnn_in['bv'], 'L0_gnn_Ws': _L0_gnn_in['Ws'], 'L0_gnn_bs': _L0_gnn_in['bs'], 'L0_mix_Wqkv': _L0_mix_in['Wqkv'], 'L0_mix_Wout': _L0_mix_in['Wout'], 'L0_mix_bout': _L0_mix_in['bout'], 'L0_ffn_gate_w': _L0_ffn_in['gate_w'], 'L0_ffn_gate_b': _L0_ffn_in['gate_b'], 'L0_ffn_w1': _L0_ffn_in['w1'], 'L0_ffn_b1': _L0_ffn_in['b1'], 'L0_ffn_w2': _L0_ffn_in['w2'], 'L0_ffn_b2': _L0_ffn_in['b2'], 'L1_gnn_w_00_0': _L1_gnn_in['w_00_0'], 'L1_gnn_w_11_0': _L1_gnn_in['w_11_0'], 'L1_gnn_w_01_1': _L1_gnn_in['w_01_1'], 'L1_gnn_w_10_1': _L1_gnn_in['w_10_1'], 'L1_gnn_fc_w1': _L1_gnn_in['fc_w1'], 'L1_gnn_fc_w2': _L1_gnn_in['fc_w2'], 'L1_mix_Wq': _L1_mix_in['Wq'], 'L1_mix_bq': _L1_mix_in['bq'], 'L1_mix_Wk': _L1_mix_in['Wk'], 'L1_mix_bk': _L1_mix_in['bk'], 'L1_mix_Wv': _L1_mix_in['Wv'], 'L1_mix_bv': _L1_mix_in['bv'], 'L1_mix_Wfc': _L1_mix_in['Wfc'], 'L1_mix_bfc': _L1_mix_in['bfc'], 'L1_ffn_W_gat': _L1_ffn_in['W_gat'], 'L1_ffn_att_src': _L1_ffn_in['att_src'], 'L1_ffn_att_dst': _L1_ffn_in['att_dst'], 'L1_ffn_b_gat': _L1_ffn_in['b_gat'], 'L1_ffn_ln_gamma': _L1_ffn_in['ln_gamma'], 'L1_ffn_ln_beta': _L1_ffn_in['ln_beta'], 'L1_ffn_W1': _L1_ffn_in['W1'], 'L1_ffn_b1': _L1_ffn_in['b1'], 'L1_ffn_W2': _L1_ffn_in['W2'], 'L1_ffn_b2': _L1_ffn_in['b2'], 'L1_ffn_edge_index': _L1_ffn_in['edge_index']}

def reference(x, src, dst, edge_attr_10, edge_attr_4, L0_gnn_Wq, L0_gnn_bq, L0_gnn_Wk, L0_gnn_bk, L0_gnn_Wv, L0_gnn_bv, L0_gnn_Ws, L0_gnn_bs, L0_mix_Wqkv, L0_mix_Wout, L0_mix_bout, L0_ffn_gate_w, L0_ffn_gate_b, L0_ffn_w1, L0_ffn_b1, L0_ffn_w2, L0_ffn_b2, L1_gnn_w_00_0, L1_gnn_w_11_0, L1_gnn_w_01_1, L1_gnn_w_10_1, L1_gnn_fc_w1, L1_gnn_fc_w2, L1_mix_Wq, L1_mix_bq, L1_mix_Wk, L1_mix_bk, L1_mix_Wv, L1_mix_bv, L1_mix_Wfc, L1_mix_bfc, L1_ffn_W_gat, L1_ffn_att_src, L1_ffn_att_dst, L1_ffn_b_gat, L1_ffn_ln_gamma, L1_ffn_ln_beta, L1_ffn_W1, L1_ffn_b1, L1_ffn_W2, L1_ffn_b2, L1_ffn_edge_index):
    import jax
    import jax.numpy as jnp

    def _L0_gnn_ref(x, edge_index, Wq, bq, Wk, bk, Wv, bv, Ws, bs):
        import jax, jax.numpy as jnp
        import numpy as np
        N, IN, H, C = (50000, 256, 8, 32)
        E = 25000
        n = x.shape[0]
        q = (x @ Wq + bq).reshape(n, H, C)
        k = (x @ Wk + bk).reshape(n, H, C)
        v = (x @ Wv + bv).reshape(n, H, C)
        src, dst = (edge_index[0], edge_index[1])
        alpha = jnp.einsum('ehc,ehc->eh', q[dst], k[src]) / jnp.sqrt(jnp.float32(C))
        amax = jax.ops.segment_max(alpha, dst, num_segments=n)
        ex = jnp.exp(alpha - amax[dst])
        denom = jax.ops.segment_sum(ex, dst, num_segments=n)
        attn = ex / denom[dst]
        msg = (v[src] * attn[:, :, None]).reshape(-1, H * C)
        out = jax.ops.segment_sum(msg, dst, num_segments=n)
        return out + x @ Ws + bs

    def _L0_mix_ref(x, Wqkv, Wout, bout):
        import jax, jax.numpy as jnp
        import numpy as np
        HEADS = 8
        DIM_HEAD = 64
        EPS = 1e-05

        def _inst_norm_lastdim(t):
            mu = jnp.mean(t, axis=-1, keepdims=True)
            var = jnp.mean(jnp.square(t - mu), axis=-1, keepdims=True)
            return (t - mu) * jax.lax.rsqrt(var + EPS)
        b, n, dim = x.shape
        qkv = jnp.einsum('bnc,fc->bnf', x, Wqkv)
        q, k, v = jnp.split(qkv, 3, axis=-1)

        def to_heads(t):
            return t.reshape(b, n, HEADS, DIM_HEAD).transpose(0, 2, 1, 3)
        q, k, v = (to_heads(q), to_heads(k), to_heads(v))
        k = _inst_norm_lastdim(k)
        v = _inst_norm_lastdim(v)
        dots = jnp.einsum('bhnd,bhne->bhde', k, v)
        out = jnp.einsum('bhnd,bhde->bhne', q, dots) / n
        out = out.transpose(0, 2, 1, 3).reshape(b, n, HEADS * DIM_HEAD)
        return jnp.einsum('bnf,cf->bnc', out, Wout) + bout

    def _L0_ffn_ref(h, gate_w, gate_b, w1, b1, w2, b2):
        import math
        import jax, jax.numpy as jnp
        import numpy as np
        CAPACITY_FACTOR = 1.25
        B, L, D = h.shape
        E = gate_w.shape[1]
        T = B * L
        C = max(1, math.ceil(CAPACITY_FACTOR * T / E))
        x = h.reshape(T, D)
        logits = x @ gate_w + gate_b
        probs = jax.nn.softmax(logits, axis=-1)
        idx = jnp.argmax(probs, axis=-1)
        prb = jnp.take_along_axis(probs, idx[:, None], axis=1)[:, 0]
        one_hot = jax.nn.one_hot(idx, E, dtype=jnp.float32)
        pos = (jnp.cumsum(one_hot, axis=0) * one_hot).sum(-1).astype(jnp.int32) - 1
        kept = pos < C
        pos_safe = jnp.where(kept, pos, C)
        buf = jnp.zeros((E, C, D), dtype=h.dtype).at[idx, pos_safe].set(x, mode='drop')
        hmid = jax.nn.relu(jnp.einsum('ecd,edf->ecf', buf, w1) + b1[:, None, :])
        ybuf = jnp.einsum('ecf,efd->ecd', hmid, w2) + b2[:, None, :]
        pos_g = jnp.minimum(pos, C - 1)
        y_tok = ybuf[idx, pos_g] * (prb * kept)[:, None]
        y = y_tok.reshape(B, L, D)
        y = jnp.nan_to_num(y, nan=0.0, posinf=10000.0, neginf=-10000.0)
        return y

    def _L1_gnn_ref(node_in, edge_attr, edge_len_emb, w_00_0, w_11_0, w_01_1, w_10_1, fc_w1, fc_w2, edge_src, edge_dst):
        import jax, jax.numpy as jnp
        import numpy as np
        MUL = 64
        N_NODES = 50000
        N_EDGES = 25000
        NUM_NEIGHBORS = 16.0
        SILU_NORM = 1.679177
        src = node_in[edge_src]
        s0 = src[:, :MUL]
        s1 = src[:, MUL:].reshape(-1, MUL, 3)
        a0 = edge_attr[:, 0:1]
        a1 = edge_attr[:, 1:4]
        alpha = np.float32(1.0 / np.sqrt(2.0 * MUL))
        inv_sqrt3 = np.float32(1.0 / np.sqrt(3.0))
        out0 = alpha * (jnp.einsum('ei,io->eo', s0 * a0, w_00_0) + inv_sqrt3 * jnp.einsum('eim,em,io->eo', s1, a1, w_11_0))
        out1 = alpha * (jnp.einsum('ei,io,em->eom', s0, w_01_1, a1) + jnp.einsum('eim,io->eom', s1 * a0[:, :, None], w_10_1))
        msg_ang = jnp.concatenate([out0, out1.reshape(-1, 3 * MUL)], axis=1)
        h = jax.nn.silu(edge_len_emb @ fc_w1 / np.float32(np.sqrt(10.0))) * np.float32(SILU_NORM)
        msg_rad = h @ fc_w2 / np.float32(np.sqrt(64.0))
        messages = msg_ang * msg_rad
        agg = jax.ops.segment_sum(messages, edge_dst, num_segments=node_in.shape[0])
        return agg / np.float32(np.sqrt(NUM_NEIGHBORS))

    def _L1_mix_ref(x, Wq, bq, Wk, bk, Wv, bv, Wfc, bfc):
        import jax, jax.numpy as jnp
        import numpy as np
        B, L, D, H = (4, 512, 256, 8)
        DK = D // H

        def _heads(t):
            b, l, d = t.shape
            return t.reshape(b, l, H, DK).transpose(0, 2, 1, 3)
        q = _heads(x @ Wq.T + bq)
        k = _heads(x @ Wk.T + bk)
        v = _heads(x @ Wv.T + bv)
        seq_len = q.shape[-2]
        p_attn = jnp.einsum('bhnd,bhne->bhde', k, v) / seq_len
        out = jnp.einsum('bhnd,bhde->bhne', q, p_attn)
        out = out.transpose(0, 2, 1, 3).reshape(x.shape[0], seq_len, H * DK)
        return out @ Wfc.T + bfc

    def _L1_ffn_ref(x, W_gat, att_src, att_dst, b_gat, ln_gamma, ln_beta, W1, b1, W2, b2, edge_index):
        import jax, jax.numpy as jnp
        import numpy as np
        B, N, D = (16, 128, 256)
        NUM_EXPERTS, TOP_K, HEADS = (4, 2, 4)
        N_EDGES = 32768
        LN_EPS = 1e-05

        def _layernorm(x, g, b):
            mu = x.mean(-1, keepdims=True)
            var = ((x - mu) ** 2).mean(-1, keepdims=True)
            return (x - mu) * jax.lax.rsqrt(var + LN_EPS) * g + b

        def _forward(x, edge_index, W_gat, att_src, att_dst, b_gat, ln_gamma, ln_beta, W1, b1, W2, b2):
            Bc, Nc, Dc = x.shape
            M = Bc * Nc
            x_flat = x.reshape(M, Dc)
            h = (x_flat @ W_gat).reshape(M, HEADS, NUM_EXPERTS)
            loops = jnp.arange(M, dtype=edge_index.dtype)
            src = jnp.concatenate([edge_index[0], loops])
            dst = jnp.concatenate([edge_index[1], loops])
            a_src = (h * att_src).sum(-1)
            a_dst = (h * att_dst).sum(-1)
            e = jax.nn.leaky_relu(a_src[src] + a_dst[dst], negative_slope=0.2)
            e_max = jax.ops.segment_max(e, dst, num_segments=M)
            ee = jnp.exp(e - e_max[dst])
            denom = jax.ops.segment_sum(ee, dst, num_segments=M)
            alpha = ee / (denom[dst] + 1e-16)
            msg = h[src] * alpha[:, :, None]
            agg = jax.ops.segment_sum(msg, dst, num_segments=M).reshape(M, HEADS * NUM_EXPERTS) + b_gat
            scores = _layernorm(agg, ln_gamma, ln_beta).reshape(M, HEADS, NUM_EXPERTS).mean(1)
            scores = scores.reshape(Bc, Nc, NUM_EXPERTS)
            topk_s, topk_i = jax.lax.top_k(scores, TOP_K)
            w = jax.nn.softmax(topk_s, axis=-1)
            out = jnp.zeros_like(x)
            for ei in range(NUM_EXPERTS):
                g = jnp.where(topk_i == ei, w, 0.0).sum(-1)
                hh = jax.nn.gelu(x @ W1[ei] + b1[ei], approximate=False)
                out = out + g[..., None] * (hh @ W2[ei] + b2[ei])
            return out
        return _forward(x, edge_index, W_gat, att_src, att_dst, b_gat, ln_gamma, ln_beta, W1, b1, W2, b2)
    edge_index = jnp.stack([src, dst])
    xn = _layernorm(x, axis=-1)
    x = x + _L0_gnn_ref(xn, edge_index, L0_gnn_Wq, L0_gnn_bq, L0_gnn_Wk, L0_gnn_bk, L0_gnn_Wv, L0_gnn_bv, L0_gnn_Ws, L0_gnn_bs) + _L0_mix_ref(xn[None], L0_mix_Wqkv, L0_mix_Wout, L0_mix_bout)[0]
    x = x + _L0_ffn_ref(_layernorm(x, axis=-1)[None], L0_ffn_gate_w, L0_ffn_gate_b, L0_ffn_w1, L0_ffn_b1, L0_ffn_w2, L0_ffn_b2)[0]
    xn = _layernorm(x, axis=-1)
    x = x + _L1_gnn_ref(xn, edge_attr_4, edge_attr_10, L1_gnn_w_00_0, L1_gnn_w_11_0, L1_gnn_w_01_1, L1_gnn_w_10_1, L1_gnn_fc_w1, L1_gnn_fc_w2, src, dst) + _L1_mix_ref(xn[None], L1_mix_Wq, L1_mix_bq, L1_mix_Wk, L1_mix_bk, L1_mix_Wv, L1_mix_bv, L1_mix_Wfc, L1_mix_bfc)[0]
    x = x + _L1_ffn_ref(_layernorm(x, axis=-1)[None], L1_ffn_W_gat, L1_ffn_att_src, L1_ffn_att_dst, L1_ffn_b_gat, L1_ffn_ln_gamma, L1_ffn_ln_beta, L1_ffn_W1, L1_ffn_b1, L1_ffn_W2, L1_ffn_b2, L1_ffn_edge_index)[0]
    return x

_drawn_inputs = setup_inputs


def setup_inputs(seed=0):
    import zlib

    import numpy as np

    out = dict(_drawn_inputs(seed))
    spreads = {'L0_gnn_bq': (0.0, 0.36),
     'L0_gnn_bk': (0.0, 2.0),
     'L0_gnn_bv': (0.0, 0.1),
     'L0_gnn_bs': (0.0, 0.1),
     'L0_ffn_gate_b': (0.0, 0.1),
     'L0_ffn_b1': (0.0, 0.457),
     'L0_ffn_b2': (0.0, 0.361),
     'L1_mix_bq': (0.0, 0.678),
     'L1_mix_bk': (0.0, 0.56),
     'L1_mix_bv': (0.0, 0.532),
     'L1_mix_bfc': (0.0, 0.525),
     'L1_ffn_b_gat': (0.0, 0.403),
     'L1_ffn_ln_gamma': (1.0, 0.6),
     'L1_ffn_ln_beta': (0.0, 0.8),
     'L1_ffn_b1': (0.0, 0.8),
     'L1_ffn_b2': (0.0, 0.775)}
    factors = {'L1_mix_Wq': 4.483,
     'L1_mix_Wk': 8.0,
     'L1_mix_Wv': 6.916,
     'L1_mix_Wfc': 3.901,
     'L1_ffn_att_dst': 83.021,
     'L1_ffn_att_src': 24.217}
    for name, (base, spread) in spreads.items():
        noise = np.random.default_rng([zlib.crc32(name.encode()), seed]).standard_normal(out[name].shape)
        drawn = base * np.exp(spread * noise) if base else spread * noise
        out[name] = jnp.asarray(drawn.astype(out[name].dtype))
    for name, factor in factors.items():
        out[name] = (out[name] * factor).astype(out[name].dtype)
    return out
```

```python
from contextlib import ExitStack

import concourse.bass as bass
from concourse import mybir
from concourse.bass import ds

F32 = mybir.dt.float32
I32 = mybir.dt.int32
ALU = mybir.AluOpType
ACT = mybir.ActivationFunctionType
AX = mybir.AxisListType

P = 128
N = 3125
D = 256
NB = (N + P - 1) // P
NPAD = NB * P
LAST = N - (NB - 1) * P
KC = D // P
EPS = 1e-5
LOW = -1.0e30
RESET = -1.0e32
NONODE = NPAD

E1 = 53125
C1 = (E1 + P - 1) // P
U = 8
T1 = C1 + NB - 1
G1 = (T1 + P - 1) // P
H1 = 8
EG = 32768
CG = EG // P
C2 = (CG + NB + U - 1) // U * U
T2 = C2 + NB - 1
G2 = (T2 + P - 1) // P
NH = NB + 1
H2 = 4
assert T1 % U == 0 and T2 % U == 0

NE = 8
FE = 1024
CAP = -(-5 * N // (4 * NE))
SLOTS = NE * CAP
NX = 4
FX = 512
MH = 16
DH = 64


class Chain:

    def __init__(self, eng, sem, base=0):
        self.eng, self.sem, self.base, self.n = eng, sem, base, 0

    def link(self, ins):
        self.n += 1
        ins.then_inc(self.sem, 1)
        self.eng.wait_ge(self.sem, self.base + self.n)


class Scope:

    def __init__(self, nc):
        self.nc, self.stack = nc, ExitStack()

    def __enter__(self):
        self.stack.__enter__()
        return self

    def __exit__(self, *a):
        return self.stack.__exit__(*a)

    def sb(self, name, shape, dt=F32):
        return self.stack.enter_context(self.nc.sbuf_tensor(name, shape, dt))

    def ps(self, name, shape, dt=F32):
        return self.stack.enter_context(self.nc.psum_tensor(name, shape, dt))

    def sem(self, name):
        sem = self.nc.alloc_semaphore(name)
        Scope.used.append(sem)
        return sem

    used = []


def recycle_semaphores(nc):
    nc.clear_and_free_semaphores(list(Scope.used))
    Scope.used.clear()
    nc.all_engine_barrier()


def wide(ap, shape):
    return ap.to_broadcast(shape)


def make_constants(nc, k):
    with Scope(nc) as s:
        made = s.sem("constants_made")
        with nc.Block() as block:
            @block.gpsimd
            def _(pool):
                nc.gpsimd.memset(k.ident[:, :], 0.0).then_inc(made, 1)
                nc.gpsimd.memset(k.ones[:, :], 1.0).then_inc(made, 1)
                nc.gpsimd.memset(k.upper[:, :], 1.0).then_inc(made, 1)
                nc.gpsimd.iota(k.count_row[:, :], [[1, 512]], base=0, channel_multiplier=0,
                               allow_small_or_imprecise_dtypes=True).then_inc(made, 1)
                nc.gpsimd.iota(k.count_col[:, :], [[P, 4]], base=0, channel_multiplier=1,
                               allow_small_or_imprecise_dtypes=True).then_inc(made, 1)
                nc.gpsimd.memset(k.armed_dummy[:, :], 0.0).then_inc(k.armed, 1)
                pool.wait_ge(made, 5)
                nc.gpsimd.affine_select(out=k.ident[:, :], in_=k.ident[:, :], compare_op=ALU.not_equal, fill=1.0,
                                        base=0, pattern=[[-1, P]], channel_multiplier=1).then_inc(made, 1)
                nc.gpsimd.affine_select(out=k.upper[:, :], in_=k.upper[:, :], compare_op=ALU.is_gt, fill=0.0,
                                        base=0, pattern=[[1, P]], channel_multiplier=-1).then_inc(made, 1)
                nc.gpsimd.iota(k.node_id[:, :], [[P, NB]], base=0, channel_multiplier=1,
                               allow_small_or_imprecise_dtypes=True).then_inc(made, 1)
                pool.wait_ge(made, 8)

            @block.vector
            def _(dve):
                dve.wait_ge(made, 8)
                nc.vector.tensor_scalar(k.node_mask[:, :], k.node_id[:, :], float(N), None, ALU.is_lt).then_inc(made, 1)
                dve.wait_ge(made, 9)


def build_steps(nc, k, name, pairs, chunks, groups, steps, valid, starts, ends, rel, src, dst, block_row, chunk_i):
    flat = pairs.rearrange("a b -> (a b)")
    windows = flat.rearrange("(c w) -> c w", w=2 * P)
    with Scope(nc) as s:
        last_i = s.sb(name + "last_i", [1, chunks], I32)
        last_b = s.sb(name + "last_b", [1, chunks], I32)
        end_step = s.sb(name + "end_step", [1, chunks])
        below = s.sb(name + "below", [P, groups, chunks])
        cut = s.sb(name + "cut", [P, 8, groups])
        block_i = s.sb(name + "block_i", [P, groups], I32)
        edges = [s.sb(name + f"edges{j}", [P, groups, P, 2], I32) for j in range(3)]
        here = s.sb(name + "here", [P, 2, groups, P])
        near = s.sb(name + "near", [P, 2, groups, P])
        rel_t = s.sb(name + "rel_t", [P, groups, P])
        tmp = s.sb(name + "tmp", [P, groups, P])
        wide_end = s.ps(name + "wide_end", [P, 512])
        turned = [s.ps(name + f"turned{j}", [P, 512]) for j in range(3)]
        block_dram = nc.dram_tensor(name + "block_of_step", [groups * P], I32, kind="Internal").ap()
        loaded, cmp_done, spread, ready, got, chain, flipped, bdone = (
            s.sem(name + x) for x in ("loaded", "cmp_done", "spread", "ready", "got", "chain", "flipped", "bdone"))
        with nc.Block() as block:
            @block.sync
            def _(sp):
                sp.dma_start(last_i[:, :], pairs[P:chunks * P + 1:P, 0:1].rearrange("c b -> b c"),
                             allow_slow_non_contiguous=True).then_inc(loaded, 16)
                sp.wait_ge(ready, 2)
                sp.dma_start(block_dram.rearrange("(g p) -> p g", p=P), block_i[:, :],
                             allow_slow_non_contiguous=True).then_inc(bdone, 16)
                sp.wait_ge(bdone, 16)
                sp.dma_start(block_row[:, 0:groups * P], block_dram.rearrange("(a n) -> a n", a=1)).then_inc(bdone, 16)
                sp.wait_ge(bdone, 32)

            @block.tensor
            def _(pe):
                pe.wait_ge(cmp_done, 1)
                nc.tensor.matmul(wide_end[:, 0:chunks], k.ones[0:1, :], end_step[:, :], start=True, stop=True).then_inc(spread, 1)
                pe.wait_ge(cmp_done, 2)
                for j, x in enumerate((rel_t, here[:, 0], here[:, 1])):
                    for g in range(groups):
                        ins = nc.tensor.transpose(turned[j][:, g * P:(g + 1) * P], x[:, g, :], k.ident[:, :])
                    ins.then_inc(flipped, 1)

            @block.gpsimd
            def _(pool):
                pool.wait_ge(ready, 1)
                for g in range(groups):
                    for j in range(3):
                        nc.gpsimd.indirect_dma_start(
                            out=edges[j][:, g].rearrange("p e b -> p (e b)"), out_offset=None, in_=windows,
                            in_offset=bass.IndirectOffsetOnAxis(ap=chunk_i[:, g:g + 1], axis=0),
                            element_offset=2 * j).then_inc(got, 16)

            @block.vector
            def _(dve):
                c = Chain(dve, chain)
                v = nc.vector
                dve.wait_ge(loaded, 16)
                c.link(v.tensor_scalar(last_b[:, :], last_i[:, :], 7, None, ALU.arith_shift_right))
                c.link(v.tensor_copy(end_step[:, :], last_b[:, :]))
                c.link(v.tensor_scalar(end_step[:, :], end_step[:, :], float(NB - 1), None, ALU.min))
                v.tensor_tensor(end_step[:, :], end_step[:, :], k.count_row[0:1, 0:chunks], ALU.add).then_inc(cmp_done, 1)
                dve.wait_ge(spread, 1)
                c.link(v.tensor_tensor(below[:, :, :], wide(wide_end[:, 0:chunks].unsqueeze(1), [P, groups, chunks]),
                                       wide(k.count_col[:, 0:groups].unsqueeze(2), [P, groups, chunks]), ALU.is_lt))
                c.link(v.tensor_reduce(cut[:, 0], below[:, :, :], AX.X, ALU.add))
                c.link(v.tensor_scalar(cut[:, 1], cut[:, 0], float(chunks - 1), None, ALU.min))
                v.tensor_copy(chunk_i[:, :], cut[:, 1]).then_inc(ready, 1)
                c.link(v.tensor_tensor(cut[:, 2], k.count_col[:, 0:groups], cut[:, 0], ALU.subtract))
                c.link(v.tensor_scalar(cut[:, 3], cut[:, 2], float(NB - 1), None, ALU.min))
                v.tensor_copy(block_i[:, :], cut[:, 3]).then_inc(ready, 1)
                c.link(v.tensor_scalar(cut[:, 4], cut[:, 0], float(chunks), 1.0e6, ALU.is_ge, ALU.mult))
                c.link(v.scalar_tensor_tensor(out=cut[:, 5], in0=cut[:, 2], scalar=float(P), in1=cut[:, 4],
                                              op0=ALU.mult, op1=ALU.add))
                dve.wait_ge(got, 48 * groups)
                v.tensor_copy(near[:, 0], edges[0][:, :, :, 0])
                v.tensor_copy(near[:, 1], edges[2][:, :, :, 0])
                v.tensor_copy(here[:, 1], edges[1][:, :, :, 1])
                c.link(v.tensor_copy(here[:, 0], edges[1][:, :, :, 0]))
                c.link(v.tensor_tensor(rel_t[:, :, :], here[:, 0], wide(cut[:, 5].unsqueeze(2), [P, groups, P]), ALU.subtract))
                c.link(v.tensor_scalar(valid[:, :, :], rel_t[:, :, :], 0.0, None, ALU.is_ge))
                c.link(v.tensor_scalar(tmp[:, :, :], rel_t[:, :, :], float(P), None, ALU.is_lt))
                c.link(v.tensor_tensor(valid[:, :, :], valid[:, :, :], tmp[:, :, :], ALU.mult))
                for flags, j in ((starts, 0), (ends, 1)):
                    c.link(v.tensor_tensor(tmp[:, :, :], here[:, 0], near[:, j], ALU.not_equal))
                    c.link(v.scalar_tensor_tensor(out=flags[:, :, :], in0=tmp[:, :, :], scalar=RESET, in1=valid[:, :, :],
                                                  op0=ALU.mult, op1=ALU.mult))
                v.tensor_scalar(here[:, 0], here[:, 0], float(NPAD - 1), None, ALU.min).then_inc(cmp_done, 1)
                dve.wait_ge(flipped, 3)
                for j, x in enumerate((rel, dst, src)):
                    c.link(v.tensor_copy(x[:, 0:groups * P], turned[j][:, 0:groups * P]))


def segment_softmax(nc, k, name, groups, heads, score, valid, starts, ends, scale):
    J = groups * heads // 4
    with Scope(nc) as s:
        x = s.sb(name + "x", [P, groups, heads, P])
        f = s.sb(name + "f", [P, groups, heads, P])
        b = s.sb(name + "b", [P, groups, heads, P])
        hole = s.sb(name + "hole", [P, groups, P])
        edge_val = s.sb(name + "edge_val", [P, groups, heads])
        edge_rst = s.sb(name + "edge_rst", [P, groups, heads])
        rst1 = s.sb(name + "rst1", [P, groups])
        carry = s.sb(name + "carry", [P, groups, heads])
        val_t = s.sb(name + "val_t", [heads, groups * P])
        rst_t = s.sb(name + "rst_t", [heads, groups * P])
        scan_t = s.sb(name + "scan_t", [heads, groups * P + 1])
        bank = [s.ps(name + f"bank{j}", [P, 4, P]) for j in range(min(J, 8))]
        assert J <= 8
        chain, turned, masked, summed, across, carried, back, final, expd, gone = (
            s.sem(name + q) for q in ("chain", "turned", "masked", "summed", "across", "carried", "back", "final", "expd", "gone"))
        with nc.Block() as block:
            @block.tensor
            def _(pe):
                for g in range(groups):
                    for h in range(heads):
                        q = g * heads + h
                        nc.tensor.transpose(bank[q // 4][:, q % 4, :], score[:, g * P:(g + 1) * P, h],
                                            k.ident[:, :]).then_inc(turned, 1)
                for way in range(2):
                    pe.wait_ge(summed, way + 1)
                    for g in range(groups):
                        nc.tensor.transpose(bank[0][0:heads, g, :], edge_val[:, g, :], k.ident[:, :])
                    for g in range(groups):
                        ins = nc.tensor.transpose(bank[1][0:heads, g, :], edge_rst[:, g, :], k.ident[:, :])
                    ins.then_inc(across, 1)
                    pe.wait_ge(carried, way + 1)
                    off = 0 if way == 0 else 1
                    for g in range(groups):
                        ins = nc.tensor.transpose(bank[2][:, 0, g * heads:(g + 1) * heads],
                                                  scan_t[:, off + g * P:off + (g + 1) * P],
                                                  k.ident[0:heads, 0:heads])
                    ins.then_inc(back, 1)
                pe.wait_ge(final, 1)
                for g in range(groups):
                    for h in range(heads):
                        q = g * heads + h
                        nc.tensor.transpose(bank[q // 4][:, q % 4, :], x[:, g, h, :], k.ident[:, :]).then_inc(turned, 1)

            @block.scalar
            def _(act):
                act.wait_ge(expd, 1)
                nc.scalar.activation(x[:, :, :, :], x[:, :, :, :], ACT.Exp, scale=scale).then_inc(gone, 1)

            @block.vector
            def _(dve):
                v = nc.vector
                c = Chain(dve, chain)
                c.link(v.tensor_scalar(hole[:, :, :], valid[:, :, :], 1.0, -LOW, ALU.subtract, ALU.mult))
                for q in range(J):
                    g, h0 = q * 4 // heads, q * 4 % heads
                    dve.wait_ge(turned, 4 * q + 4)
                    v.tensor_tensor(x[:, g, h0:h0 + 4, :], bank[q][:, :, :],
                                    wide(valid[:, g, :].unsqueeze(1), [P, 4, P]), ALU.mult).then_inc(masked, 1)
                for g in range(groups):
                    dve.wait_ge(masked, (g + 1) * heads // 4)
                    c.link(v.tensor_tensor(x[:, g], x[:, g], wide(hole[:, g, :].unsqueeze(1), [P, heads, P]), ALU.add))

                def scans(out, flags, data, way, initial):
                    for g in range(groups):
                        for h in range(heads):
                            o, r, a = out[:, g, h, :], flags[:, g, :], data[:, g, h, :]
                            if way:
                                o, r, a = o[:, ::-1], r[:, ::-1], a[:, ::-1]
                            ins = v.tensor_tensor_scan(o, r, a, LOW if initial is None else initial[:, g, h:h + 1],
                                                       ALU.add, ALU.max)
                    c.link(ins)

                for way, (out, flags, data) in enumerate(((f, starts, x), (b, ends, f))):
                    scans(out, flags, data, way, None)
                    at = P - 1 if way == 0 else 0
                    v.tensor_copy(edge_val[:, :, :], out[:, :, :, at])
                    c.link(v.tensor_reduce(rst1[:, :], flags[:, :, :], AX.X, ALU.min))
                    v.tensor_copy(edge_rst[:, :, :], wide(rst1[:, :].unsqueeze(2), [P, groups, heads])).then_inc(summed, 1)
                    dve.wait_ge(across, way + 1)
                    v.tensor_copy(val_t[:, :], bank[0][0:heads, 0:groups, :].rearrange("p a b -> p (a b)"))
                    c.link(v.tensor_copy(rst_t[:, :], bank[1][0:heads, 0:groups, :].rearrange("p a b -> p (a b)")))
                    n = groups * P
                    if way == 0:
                        v.memset(scan_t[:, 0:1], LOW)
                        v.tensor_tensor_scan(scan_t[:, 1:n + 1], rst_t[:, :], val_t[:, :], LOW, ALU.add, ALU.max).then_inc(carried, 1)
                    else:
                        v.memset(scan_t[:, n:n + 1], LOW)
                        v.tensor_tensor_scan(scan_t[:, 0:n][:, ::-1], rst_t[:, ::-1], val_t[:, ::-1], LOW,
                                             ALU.add, ALU.max).then_inc(carried, 1)
                    dve.wait_ge(back, way + 1)
                    c.link(v.tensor_copy(carry[:, :, :], bank[2][:, 0, 0:groups * heads].rearrange("p (g h) -> p g h", g=groups)))
                    scans(out, flags, data, way, carry)
                v.tensor_tensor(x[:, :, :, :], x[:, :, :, :], b[:, :, :, :], ALU.subtract).then_inc(expd, 1)
                dve.wait_ge(gone, 1)
                for g in range(groups):
                    ins = v.tensor_tensor(x[:, g], x[:, g], wide(valid[:, g, :].unsqueeze(1), [P, heads, P]), ALU.mult)
                ins.then_inc(final, 1)
                for q in range(J):
                    g, h0 = q * 4 // heads, q * 4 % heads
                    dve.wait_ge(turned, groups * heads + 4 * q + 4)
                    ins = v.tensor_copy(score[:, g * P:(g + 1) * P, h0:h0 + 4].rearrange("p t h -> p h t"), bank[q][:, :, :])
                c.link(ins)


def layer_stats(nc, k, name):
    with Scope(nc) as s:
        parts = s.sb(name + "parts", [P, NB, 6])
        t = s.sb(name + "t", [P, 4, NB])
        chain, inverse, rooted = s.sem(name + "chain"), s.sem(name + "inverse"), s.sem(name + "rooted")
        with nc.Block() as block:
            @block.scalar
            def _(act):
                act.wait_ge(inverse, 1)
                nc.scalar.activation(k.rstd[:, :], t[:, 1], ACT.Sqrt).then_inc(rooted, 1)

            @block.vector
            def _(dve):
                v = nc.vector
                with dve.Fori(0, NB) as b:
                    v.bn_stats(parts[:, ds(b, 1), :], k.X[:, ds(b, 1), :]).then_inc(chain, 1)
                dve.wait_ge(chain, NB)
                c = Chain(dve, chain, NB)
                c.link(v.tensor_tensor(t[:, 0], parts[:, :, 1], parts[:, :, 4], ALU.subtract))
                c.link(v.tensor_tensor(t[:, 0], t[:, 0], t[:, 0], ALU.mult))
                v.tensor_tensor(t[:, 3], parts[:, :, 1], parts[:, :, 4], ALU.add)
                c.link(v.tensor_tensor(t[:, 1], parts[:, :, 2], parts[:, :, 5], ALU.add))
                c.link(v.scalar_tensor_tensor(out=t[:, 2], in0=t[:, 0], scalar=D / 4.0, in1=t[:, 1], op0=ALU.mult, op1=ALU.add))
                c.link(v.tensor_scalar(t[:, 2], t[:, 2], 1.0 / D, EPS, ALU.mult, ALU.add))
                v.reciprocal(t[:, 1], t[:, 2]).then_inc(inverse, 1)
                dve.wait_ge(rooted, 1)
                c.link(v.tensor_tensor(k.rstd[:, :], k.rstd[:, :], k.node_mask[:, :], ALU.mult))
                c.link(v.scalar_tensor_tensor(out=k.shift[:, :], in0=t[:, 3], scalar=-0.5, in1=k.rstd[:, :],
                                              op0=ALU.mult, op1=ALU.mult))


def load_all(nc, k, a):
    with Scope(nc) as s:
        mix_kv = s.sb("mix_kv", [P, 8, D])
        mix_out = s.sb("mix_out", [P, KC, 512])
        fc = [s.sb(f"fc{j}", [P, KC, D]) for j in range(3)]
        bank = [s.ps(f"turn_bank{j}", [P, 512]) for j in range(8)]
        got_x, got_w, cleared, turned, kept = (s.sem(q) for q in ("got_x", "got_w", "cleared", "turned", "kept"))
        jobs = [(mix_kv[:, j, c * P:(c + 1) * P], k.mix_kvT[:, c, j * P:(j + 1) * P]) for c in range(KC) for j in range(8)]
        jobs += [(mix_out[:, j, c * P:(c + 1) * P], k.mix_outT[:, c, j * P:(j + 1) * P]) for c in range(4) for j in range(KC)]
        for t in range(3):
            jobs += [(fc[t][:, j, c * P:(c + 1) * P], k.fcT[t][:, c, j * P:(j + 1) * P]) for c in range(KC) for j in range(KC)]
        loads = [(k.W0[:, :, j * D:(j + 1) * D], a["L0_gnn_" + w].rearrange("(c p) f -> p c f", p=P))
                 for j, w in enumerate(("Wq", "Wk", "Wv", "Ws"))]
        loads += [(k.bias0[:, j * D:(j + 1) * D], a["L0_gnn_" + w].rearrange("(a f) -> a f", a=1))
                  for j, w in enumerate(("bq", "bk", "bv", "bs"))]
        loads += [(k.bias0[:, 4 * D:5 * D], a["L0_mix_bout"].rearrange("(a f) -> a f", a=1)),
                  (k.mix_q[:, :, :], a["L0_mix_Wqkv"][0:512, :].rearrange("(j p) c -> p j c", p=P)),
                  (mix_kv[:, :, :], a["L0_mix_Wqkv"][512:1536, :].rearrange("(j p) c -> p j c", p=P)),
                  (mix_out[:, :, :], a["L0_mix_Wout"].rearrange("(j p) f -> p j f", p=P)),
                  (k.gate[:, :, :], a["L0_ffn_gate_w"].rearrange("(c p) e -> p c e", p=P)),
                  (k.gate_b[:, :], a["L0_ffn_gate_b"].rearrange("(a f) -> a f", a=1)),
                  (k.fc_q[:, :, :], a["L1_mix_Wq"].rearrange("(j p) c -> p j c", p=P))]
        loads += [(fc[t][:, :, :], a["L1_mix_" + w].rearrange("(j p) c -> p j c", p=P)) for t, w in enumerate(("Wk", "Wv", "Wfc"))]
        loads += [(k.bias1[:, j * D:(j + 1) * D], a["L1_mix_" + w].rearrange("(a f) -> a f", a=1))
                  for j, w in enumerate(("bk", "bv", "bfc"))]
        loads += [(k.bq_col[:, :], a["L1_mix_bq"].rearrange("(c p) -> p c", p=P))]
        loads += [(k.gat_w[:, :, :], a["L1_ffn_W_gat"].rearrange("(c p) e -> p c e", p=P))]
        with nc.Block() as block:
            @block.sync
            def _(sp):
                sp.wait_ge(cleared, 1)
                sp.dma_start(k.X[:, 0:NB - 1, :], a["x"][0:(NB - 1) * P, :].rearrange("(b p) d -> p b d", p=P)).then_inc(got_x, 16)
                sp.dma_start(k.X[0:LAST, NB - 1, :], a["x"][(NB - 1) * P:N, :]).then_inc(got_x, 16)
                for to, of in loads:
                    sp.dma_start(to, of, allow_slow_non_contiguous=True).then_inc(got_w, 16)
                for j, w in enumerate(("att_src", "att_dst")):
                    sp.dma_start(k.gat_rows[:, j * 16:(j + 1) * 16],
                                 a["L1_ffn_" + w].rearrange("h e -> (h e)").rearrange("(a f) -> a f", a=1)).then_inc(got_w, 16)
                for j, w in enumerate(("b_gat", "ln_gamma", "ln_beta")):
                    sp.dma_start(k.gat_rows[:, (j + 2) * 16:(j + 3) * 16],
                                 a["L1_ffn_" + w].rearrange("(a f) -> a f", a=1)).then_inc(got_w, 16)
                sp.wait_ge(got_x, 32)
                sp.wait_ge(got_w, 16 * (len(loads) + 5))

            @block.tensor
            def _(pe):
                pe.wait_ge(got_w, 16 * (len(loads) + 5))
                for j, (x, _y) in enumerate(jobs):
                    if j >= 8:
                        pe.wait_ge(kept, j - 7)
                    nc.tensor.transpose(bank[j % 8][:, 0:P], x, k.ident[:, :]).then_inc(turned, 1)

            @block.vector
            def _(dve):
                nc.vector.memset(k.X[:, NB - 1, :], 0.0).then_inc(cleared, 1)
                for j, (_x, y) in enumerate(jobs):
                    dve.wait_ge(turned, j + 1)
                    nc.vector.tensor_copy(y, bank[j % 8][:, 0:P]).then_inc(kept, 1)


def normed_block(nc, k, act, b, slot, sem):
    nc.scalar.activation(slot, k.X[:, ds(b, 1), :].rearrange("p b d -> p (b d)"), ACT.Identity,
                         bias=k.shift[:, ds(b, 1)], scale=k.rstd[:, ds(b, 1)]).then_inc(sem, 1)


B5 = 5
assert NB % B5 == 0


def project0(nc, k, q_tab, k_tab, v_tab):
    PER = 7
    with Scope(nc) as s:
        xn = s.sb("p0_xn", [P, B5, D])
        xT = s.sb("p0_xT", [P, B5, KC, P])
        qkv = s.sb("p0_qkv", [P, B5, 3 * D])
        kv = s.sb("p0_kv", [P, B5, MH, DH])
        cen = s.sb("p0_cen", [P, MH, DH])
        sq = s.sb("p0_sq", [P, MH, DH])
        st = s.sb("p0_st", [P, 4, MH])
        zero = s.sb("p0_zero", [P, 512])
        ps_t = s.ps("p0_t", [P, KC, P])
        ps_a = s.ps("p0_a", [P, 512])
        ps_b = s.ps("p0_b", [P, 512])
        ps_m = s.ps("p0_m", [P, MH, DH])
        dots = s.ps("p0_dots", [P, 4, P])
        normed, turned, kept, ab_done, ab_used, m_done, m_used, heads, chain, zeroed, dotted = (
            s.sem("p0_" + q) for q in ("normed", "turned", "kept", "ab_done", "ab_used", "m_done", "m_used", "heads", "chain",
                                       "zeroed", "dotted"))
        inverse, rooted = s.sem("p0_inverse"), s.sem("p0_rooted")
        out = [s.sem(f"p0_out{j}") for j in range(B5)]
        with nc.Block() as block:
            @block.scalar
            def _(act):
                act.sem_inc(ab_used, 1)

                def turn(i, first=False):
                    for j in range(B5):
                        b = i * B5 + j
                        act.wait_ge(turned, b + 1)
                        act.wait_ge(k.armed, 1)
                        normed_block(nc, k, act, b, xn[:, j, :], normed)
                        if not first:
                            act.wait_ge(out[j], i * 48)
                        act.wait_ge(ab_done, b + 1)
                        nc.scalar.activation(qkv[:, j, 0:512], ps_a[:, :], ACT.Copy)
                        nc.scalar.activation(qkv[:, j, 512:768], ps_b[:, 0:D], ACT.Copy).then_inc(ab_used, 1)
                        act.wait_ge(inverse, b + 1)
                        nc.scalar.activation(st[:, 3], st[:, 0], ACT.Sqrt).then_inc(rooted, 1)
                turn(0, True)
                with act.Fori(1, NB // B5) as i:
                    turn(i)

            @block.sync
            def _(sp):
                with sp.Fori(0, NB // B5) as i:
                    for j in range(B5):
                        b = i * B5 + j
                        sp.wait_ge(ab_used, b + 2)
                        for n, tab in enumerate((q_tab, k_tab, v_tab)):
                            sp.dma_start(tab[ds(b * P, P), :], qkv[:, j, n * D:(n + 1) * D]).then_inc(out[j], 16)
                for j in range(B5):
                    sp.wait_ge(out[j], 48 * (NB // B5))

            @block.tensor
            def _(pe):
                def product():
                    for q in range(4):
                        ins = nc.tensor.matmul(dots[:, q, :], kv[:, jj, 8 + 2 * q:10 + 2 * q, :].rearrange("p h d -> p (h d)"),
                                               kv[:, jj, 2 * q:2 * q + 2, :].rearrange("p h d -> p (h d)"),
                                               start=False, stop=False, skip_group_check=True)
                    return ins

                pe.sem_inc(turned, B5)
                pe.wait_ge(zeroed, 2)
                nc.tensor.matmul(dots[:, :, :].rearrange("p a b -> p (a b)"), zero[:, 0:P], zero[:, :], start=True, stop=False,
                                 skip_group_check=True)
                with pe.Fori(0, NB // B5) as i:
                    for j in range(B5):
                        b = i * B5 + j
                        pe.wait_ge(normed, b + 1)
                        pe.wait_ge(kept, b + 1)
                        for c in range(KC):
                            ins = nc.tensor.transpose(ps_t[:, c, :], xn[:, j, c * P:(c + 1) * P], k.ident[:, :])
                        ins.then_inc(turned, 1)
                        pe.wait_ge(kept, b + 2)
                        pe.wait_ge(ab_used, b + 1)
                        for ps, lo, n in ((ps_a, 0, 512), (ps_b, 512, 256)):
                            nc.tensor.matmul(ps[:, 0:n], k.ones[0:1, :], k.bias0[:, lo:lo + n], start=True, stop=False)
                            for c in range(KC):
                                ins = nc.tensor.matmul(ps[:, 0:n], xT[:, j, c, :], k.W0[:, c, lo:lo + n],
                                                       start=False, stop=(c == KC - 1))
                        ins.then_inc(ab_done, 1)
                        pe.wait_ge(m_used, b + 1)
                        for n in range(2):
                            for c in range(KC):
                                ins = nc.tensor.matmul(ps_m[:, 8 * n:8 * n + 8, :].rearrange("p h d -> p (h d)"), xT[:, j, c, :],
                                                       k.mix_kvT[:, c, n * 512:(n + 1) * 512], start=(c == 0), stop=(c == KC - 1))
                        ins.then_inc(m_done, 1)
                        jj = (j - 1) % B5
                        pe.wait_ge(heads, b + 1)
                        product()
                pe.wait_ge(heads, NB + 1)
                jj = B5 - 1
                product().then_inc(dotted, 1)

            @block.vector
            def _(dve):
                v = nc.vector
                v.memset(zero[:, :], 0.0).then_inc(zeroed, 1)
                v.memset(kv[:, B5 - 1], 0.0).then_inc(zeroed, 1)
                dve.sem_inc(kept, 1)
                dve.sem_inc(m_used, 1)
                dve.sem_inc(heads, 1)
                dve.wait_ge(zeroed, 2)
                with dve.Fori(0, NB // B5) as i:
                    c = Chain(dve, chain, i * (PER * B5))
                    for j in range(B5):
                        b = i * B5 + j
                        dve.wait_ge(turned, b + B5 + 1)
                        v.tensor_copy(xT[:, j], ps_t[:, :, :]).then_inc(kept, 1)
                        dve.wait_ge(m_done, b + 1)
                        c.link(v.tensor_reduce(st[:, 0], ps_m[:, :, :], AX.X, ALU.add))
                        c.link(v.tensor_scalar(st[:, 1], st[:, 0], 1.0 / DH, None, ALU.mult))
                        c.link(v.tensor_tensor(cen[:, :, :], ps_m[:, :, :], wide(st[:, 1].unsqueeze(2), [P, MH, DH]), ALU.subtract))
                        dve.sem_inc(m_used, 1)
                        c.link(v.tensor_tensor(sq[:, :, :], cen[:, :, :], cen[:, :, :], ALU.mult))
                        c.link(v.tensor_reduce(st[:, 2], sq[:, :, :], AX.X, ALU.add))
                        c.link(v.tensor_scalar(st[:, 2], st[:, 2], 1.0 / DH, EPS, ALU.mult, ALU.add))
                        v.reciprocal(st[:, 0], st[:, 2]).then_inc(inverse, 1)
                        dve.wait_ge(rooted, b + 1)
                        c.link(v.tensor_tensor(kv[:, j], cen[:, :, :], wide(st[:, 3].unsqueeze(2), [P, MH, DH]), ALU.mult))
                        dve.sem_inc(heads, 1)
                    assert c.n == PER * B5
                dve.wait_ge(dotted, 1)
                v.memset(k.dotsT[:, :, :], 0.0).then_inc(zeroed, 1)
                dve.wait_ge(zeroed, 3)
                for h in range(2):
                    ins = v.tensor_scalar(k.dotsT[h * DH:(h + 1) * DH, :, h * DH:(h + 1) * DH],
                                          dots[h * DH:(h + 1) * DH, :, h * DH:(h + 1) * DH], 1.0 / N, None, ALU.mult)
                ins.then_inc(zeroed, 1)
                dve.wait_ge(zeroed, 4)


def mixer_matrix0(nc, k):
    with Scope(nc) as s:
        ps = [s.ps(f"g0_{q}", [P, 512]) for q in range(6)]
        t = s.sb("g0_t", [P, 4, D])
        ready, done = s.sem("g0_ready"), s.sem("g0_done")
        with nc.Block() as block:
            @block.tensor
            def _(pe):
                for q in range(4):
                    nc.tensor.matmul(ps[q][:, 0:D], k.dotsT[:, q, :], k.mix_outT[:, q, :], start=True, stop=True).then_inc(ready, 1)
                pe.wait_ge(done, 4)
                for c in range(KC):
                    for q in range(4):
                        ins = nc.tensor.matmul(ps[4 + c][:, 0:D], k.mix_q[:, q, c * P:(c + 1) * P], t[:, q, :],
                                               start=(q == 0), stop=(q == 3))
                    ins.then_inc(ready, 1)

            @block.vector
            def _(dve):
                v = nc.vector
                for q in range(4):
                    dve.wait_ge(ready, q + 1)
                    v.tensor_copy(t[:, q, :], ps[q][:, 0:D]).then_inc(done, 1)
                for c in range(KC):
                    dve.wait_ge(ready, 5 + c)
                    v.tensor_tensor(k.W0[:, c, 3 * D:4 * D], k.W0[:, c, 3 * D:4 * D], ps[4 + c][:, 0:D], ALU.add).then_inc(done, 1)
                v.tensor_tensor(k.bias0[:, 3 * D:4 * D], k.bias0[:, 3 * D:4 * D], k.bias0[:, 4 * D:5 * D], ALU.add).then_inc(done, 1)
                dve.wait_ge(done, 7)


def edge_scores(nc, k, e, q_tab, k_tab, score):
    HD = D // H1
    PER = 1
    with Scope(nc) as s:
        ix = s.sb("es_ix", [P, 2, 2, U], I32)
        qg = s.sb("es_q", [P, 2, U, D])
        kg = s.sb("es_k", [P, 2, U, D])
        listed, freed, chain, took = s.sem("es_listed"), s.sem("es_freed"), s.sem("es_chain"), s.sem("es_took")
        got = [[s.sem(f"es_got{h}{u}") for u in range(2)] for h in range(2)]
        turns = T1 // U
        assert turns % 2 == 1
        with nc.Block() as block:
            def pool_turn(h, i):
                nc.gpsimd.tensor_copy(ix[:, h, 0, :], e.dst[:, ds(i * U, U)])
                nc.gpsimd.tensor_copy(ix[:, h, 1, :], e.src[:, ds(i * U, U)]).then_inc(listed, 1)

            @block.gpsimd
            def _(pool):
                def turn(i, h):
                    pool.wait_ge(freed, i + 1)
                    pool.wait_ge(k.armed, 1)
                    pool_turn(h, i)
                    pool.wait_ge(k.armed, 1)
                    pool.wait_ge(listed, i + 1)
                    for u in range(U):
                        for n, (to, tab) in enumerate(((qg, q_tab), (kg, k_tab))):
                            nc.gpsimd.indirect_dma_start(
                                out=to[:, h, u, :], out_offset=None, in_=tab,
                                in_offset=bass.IndirectOffsetOnAxis(ap=ix[:, h, n, u:u + 1], axis=0)).then_inc(got[h][n], 16)
                with pool.Fori(0, turns // 2) as w:
                    turn(w * 2, 0)
                    turn(w * 2 + 1, 1)
                turn(turns - 1, 0)

            @block.vector
            def _(dve):
                v = nc.vector
                dve.sem_inc(freed, 2)

                def turn(i, w, h):
                    for n in range(2):
                        dve.wait_ge(got[h][n], w * (16 * U) + 16 * U)
                    v.tensor_tensor(qg[:, h], qg[:, h], kg[:, h], ALU.mult).then_inc(chain, 1)
                    dve.wait_ge(chain, i + 1)
                    v.tensor_reduce(score[:, ds(i * U, U), :].rearrange("p t h -> p (t h)"),
                                    qg[:, h].rearrange("p u (h d) -> p (u h) d", d=HD), AX.X, ALU.add).then_inc(freed, 1)
                with dve.Fori(0, turns // 2) as w:
                    turn(w * 2, w, 0)
                    turn(w * 2 + 1, w, 1)
                turn(turns - 1, turns // 2, 0)
                v.memset(score[:, T1:G1 * P, :], 0.0).then_inc(took, 1)
                dve.wait_ge(took, 1)
                dve.wait_ge(freed, turns + 2)




def block_of(dve, e, t):
    return dve.value_load(e.block_row[0:1, ds(t, 1)], min_val=0, max_val=NB - 1)


def attend(nc, k, e, v_tab, weight, acc):
    HD = D // H1
    W = D + H1
    turns = T1 // U
    with Scope(nc) as s:
        ix = s.sb("at_ix", [P, 2, U], I32)
        vg = s.sb("at_v", [P, 2, U, D])
        msg = s.sb("at_msg", [P, 2, U, W])
        hot = s.sb("at_hot", [P, 2, U, P])
        ps = [s.ps(f"at_ps{u}", [P, 512]) for u in range(U)]
        listed, freed, built, chain, summed, added = (s.sem("at_" + q) for q in ("listed", "freed", "built", "chain", "summed", "added"))
        got = [s.sem(f"at_got{h}") for h in range(2)]
        with nc.Block() as block:
            @block.gpsimd
            def _(pool):
                def turn(i, h):
                    pool.wait_ge(freed, i + 1)
                    pool.wait_ge(k.armed, 1)
                    nc.gpsimd.tensor_copy(ix[:, h, :], e.src[:, ds(i * U, U)]).then_inc(listed, 1)
                    pool.wait_ge(k.armed, 1)
                    pool.wait_ge(listed, i + 1)
                    for u in range(U):
                        nc.gpsimd.indirect_dma_start(
                            out=vg[:, h, u, :], out_offset=None, in_=v_tab,
                            in_offset=bass.IndirectOffsetOnAxis(ap=ix[:, h, u:u + 1], axis=0)).then_inc(got[h], 16)
                with pool.Fori(0, turns // 2) as w:
                    turn(w * 2, 0)
                    turn(w * 2 + 1, 1)
                turn(turns - 1, 0)

            @block.tensor
            def _(pe):
                def turn(i, h):
                    pe.wait_ge(built, i + 1)
                    for u in range(U):
                        pe.wait_ge(added, i * U + (u + 1))
                        nc.tensor.matmul(ps[u][:, 0:W], hot[:, h, u, :], msg[:, h, u, :], start=True, stop=True).then_inc(summed, 1)
                with pe.Fori(0, turns // 2) as w:
                    turn(w * 2, 0)
                    turn(w * 2 + 1, 1)
                turn(turns - 1, 0)

            @block.vector
            def _(dve):
                v = nc.vector
                dve.sem_inc(freed, 2)
                dve.sem_inc(added, U)

                def build(i, w, h):
                    v.tensor_tensor(hot[:, h], wide(k.count_row[:, 0:P].unsqueeze(1), [P, U, P]),
                                    wide(e.rel[:, ds(i * U, U)].unsqueeze(2), [P, U, P]), ALU.is_equal)
                    v.tensor_copy(msg[:, h, :, D:W], weight[:, ds(i * U, U), :])
                    dve.wait_ge(got[h], w * (16 * U) + 16 * U)
                    v.tensor_tensor(msg[:, h, :, 0:D].rearrange("p u (g d) -> p u g d", d=HD),
                                    vg[:, h].rearrange("p u (g d) -> p u g d", d=HD),
                                    wide(weight[:, ds(i * U, U), :].unsqueeze(3), [P, U, H1, HD]), ALU.mult).then_inc(built, 1)
                    dve.wait_ge(built, i + 1)
                    dve.sem_inc(freed, 1)

                def add(i):
                    for u in range(U):
                        b = block_of(dve, e, i * U + u)
                        dve.wait_ge(summed, i * U + (u + 1))
                        dve.wait_ge(added, i * U + (u + U))
                        dve.wait_ge(k.armed, 1)
                        v.tensor_tensor(acc[:, ds(b, 1), :].rearrange("p a w -> p (a w)"),
                                        acc[:, ds(b, 1), :].rearrange("p a w -> p (a w)"),
                                        ps[u][:, 0:W], ALU.add).then_inc(added, 1)
                build(0, 0, 0)
                with dve.Fori(0, turns // 2) as w:
                    build(w * 2 + 1, w, 1)
                    add(w * 2)
                    build(w * 2 + 2, w + 1, 0)
                    add(w * 2 + 1)
                add(turns - 1)
                dve.wait_ge(added, T1 + U)


def combine0(nc, k, acc):
    with Scope(nc) as s:
        xn = s.sb("c0_xn", [P, B5, D])
        xT = s.sb("c0_xT", [P, B5, KC, P])
        rd = s.sb("c0_rd", [P, NB, H1])
        ps_t = s.ps("c0_t", [P, KC, P])
        ps_o = [s.ps(f"c0_o{j}", [P, D]) for j in range(B5)]
        normed, turned, kept, done, chain = (s.sem("c0_" + q) for q in ("normed", "turned", "kept", "done", "chain"))
        HD = D // H1
        with nc.Block() as block:
            @block.scalar
            def _(act):
                with act.Fori(0, NB // B5) as i:
                    for j in range(B5):
                        act.wait_ge(turned, i * B5 + j + 1)
                        act.wait_ge(k.armed, 1)
                        normed_block(nc, k, act, i * B5 + j, xn[:, j, :], normed)

            @block.tensor
            def _(pe):
                pe.sem_inc(turned, B5)
                with pe.Fori(0, NB // B5) as i:
                    for j in range(B5):
                        b = i * B5 + j
                        pe.wait_ge(normed, b + 1)
                        pe.wait_ge(kept, b + 1)
                        for c in range(KC):
                            ins = nc.tensor.transpose(ps_t[:, c, :], xn[:, j, c * P:(c + 1) * P], k.ident[:, :])
                        ins.then_inc(turned, 1)
                        pe.wait_ge(kept, b + 2)
                        nc.tensor.matmul(ps_o[j][:, :], k.ones[0:1, :], k.bias0[:, 3 * D:4 * D], start=True, stop=False)
                        for c in range(KC):
                            ins = nc.tensor.matmul(ps_o[j][:, :], xT[:, j, c, :], k.W0[:, c, 3 * D:4 * D], start=False, stop=(c == KC - 1))
                        ins.then_inc(done, 1)

            @block.vector
            def _(dve):
                v = nc.vector
                dve.sem_inc(kept, 1)
                c = Chain(dve, chain)
                c.link(v.tensor_scalar(rd[:, :, :], acc[:, :, D:D + H1], 1e-30, None, ALU.max))
                c.link(v.reciprocal(rd[:, :, :], rd[:, :, :]))
                with dve.Fori(0, NB // B5) as i:
                    c = Chain(dve, chain, i * (3 * B5) + 2)
                    for j in range(B5):
                        b = i * B5 + j
                        xb = k.X[:, ds(b, 1), :].rearrange("p a d -> p (a d)")
                        ab = acc[:, ds(b, 1), 0:D].rearrange("p a (g d) -> p (a g) d", d=HD)
                        dve.wait_ge(turned, b + B5 + 1)
                        v.tensor_copy(xT[:, j], ps_t[:, :, :]).then_inc(kept, 1)
                        c.link(v.tensor_tensor(ab, ab, wide(rd[:, ds(b, 1), :].rearrange("p a g -> p (a g)").unsqueeze(2), [P, H1, HD]), ALU.mult))
                        c.link(v.tensor_tensor(xb, xb, acc[:, ds(b, 1), 0:D].rearrange("p a d -> p (a d)"), ALU.add))
                        dve.wait_ge(done, b + 1)
                        c.link(v.tensor_tensor(xb, xb, ps_o[j][:, :], ALU.add))
                    assert c.n == 3 * B5


def gate0(nc, k, XN, logits):
    with Scope(nc) as s:
        xn = s.sb("r0_xn", [P, B5, D])
        xT = s.sb("r0_xT", [P, B5, KC, P])
        ps_t = s.ps("r0_t", [P, KC, P])
        ps_l = [s.ps(f"r0_l{j}", [P, NE]) for j in range(B5)]
        normed, turned, kept, done, moved = (s.sem("r0_" + q) for q in ("normed", "turned", "kept", "done", "moved"))
        with nc.Block() as block:
            @block.scalar
            def _(act):
                with act.Fori(0, NB // B5) as i:
                    for j in range(B5):
                        b = i * B5 + j
                        act.wait_ge(turned, b + 1)
                        act.wait_ge(k.armed, 1)
                        normed_block(nc, k, act, b, xn[:, j, :], normed)
                        normed_block(nc, k, act, b, XN[:, ds(b, 1), :].rearrange("p a d -> p (a d)"), moved)
                act.wait_ge(moved, NB)

            @block.tensor
            def _(pe):
                pe.sem_inc(turned, B5)
                with pe.Fori(0, NB // B5) as i:
                    for j in range(B5):
                        b = i * B5 + j
                        pe.wait_ge(normed, b + 1)
                        pe.wait_ge(kept, 2 * b + 1)
                        for c in range(KC):
                            ins = nc.tensor.transpose(ps_t[:, c, :], xn[:, j, c * P:(c + 1) * P], k.ident[:, :])
                        ins.then_inc(turned, 1)
                        pe.wait_ge(kept, 2 * b + 2)
                        nc.tensor.matmul(ps_l[j][:, :], k.ones[0:1, :], k.gate_b[:, :], start=True, stop=False)
                        for c in range(KC):
                            ins = nc.tensor.matmul(ps_l[j][:, :], xT[:, j, c, :], k.gate[:, c, :], start=False, stop=(c == KC - 1))
                        ins.then_inc(done, 1)

            @block.vector
            def _(dve):
                v = nc.vector
                dve.sem_inc(kept, 1)
                with dve.Fori(0, NB // B5) as i:
                    for j in range(B5):
                        b = i * B5 + j
                        dve.wait_ge(turned, b + B5 + 1)
                        v.tensor_copy(xT[:, j], ps_t[:, :, :]).then_inc(kept, 1)
                        dve.wait_ge(done, b + 1)
                        dve.wait_ge(k.armed, 1)
                        v.tensor_copy(logits[:, ds(b, 1), :].rearrange("p a e -> p (a e)"), ps_l[j][:, :]).then_inc(kept, 1)
                dve.wait_ge(kept, 2 * NB + 1)


def route0(nc, k, XN, logits, buf, slot_i, factor):
    with Scope(nc) as s:
        S = [P, NB, NE]
        t = s.sb("ro_t", [P, 8, NB, NE])
        r = s.sb("ro_r", [P, 10, NB])
        send_i = s.sb("ro_send", [P, NB], I32)
        ps_in = s.ps("ro_in", [P, NB * NE])
        ps_all = s.ps("ro_all", [P, NB * NE])
        zero = s.sb("ro_zero", [P, 512])
        chain, asked, exped, hot, counted, sent, clear, cleared = (
            s.sem("ro_" + q) for q in ("chain", "asked", "exped", "hot", "counted", "sent", "clear", "cleared"))
        per_part = SLOTS * D // P
        run = next(x for x in range(512, 0, -1) if per_part % x == 0)
        with nc.Block() as block:
            @block.sync
            def _(sp):
                sp.wait_ge(clear, 1)
                sp.dma_start(buf[0:SLOTS, :].rearrange("s d -> (s d)").rearrange("(p m r) -> p m r", p=P, r=run),
                             wide(zero[:, 0:run].unsqueeze(1), [P, per_part // run, run])).then_inc(cleared, 16)
                sp.wait_ge(cleared, 16)

            @block.scalar
            def _(act):
                act.wait_ge(asked, 1)
                nc.scalar.activation(t[:, 1], t[:, 0], ACT.Exp).then_inc(exped, 1)

            @block.tensor
            def _(pe):
                pe.wait_ge(hot, 1)
                rhs = t[:, 3].rearrange("p b e -> p (b e)")
                nc.tensor.matmul(ps_in[:, :], k.upper[:, :], rhs, start=True, stop=True)
                nc.tensor.matmul(ps_all[:, :], k.ones[:, :], rhs, start=True, stop=True).then_inc(counted, 1)

            @block.gpsimd
            def _(pool):
                pool.wait_ge(asked, 2)
                pool.wait_ge(cleared, 16)
                for b in range(NB):
                    n = P if b < NB - 1 else LAST
                    nc.gpsimd.indirect_dma_start(
                        out=buf, out_offset=bass.IndirectOffsetOnAxis(ap=send_i[0:n, b:b + 1], axis=0),
                        in_=XN[0:n, b, :], in_offset=None).then_inc(sent, 16)
                pool.wait_ge(sent, 16 * NB)

            @block.vector
            def _(dve):
                v = nc.vector
                c = Chain(dve, chain)
                v.memset(zero[:, :], 0.0).then_inc(clear, 1)
                c.link(v.tensor_reduce(r[:, 0], logits[:, :, :], AX.X, ALU.max))
                v.tensor_tensor(t[:, 0], logits[:, :, :], wide(r[:, 0].unsqueeze(2), S), ALU.subtract).then_inc(asked, 1)
                dve.wait_ge(exped, 1)
                v.tensor_reduce(r[:, 1], t[:, 1], AX.X, ALU.add)
                c.link(v.tensor_reduce(r[:, 2], t[:, 1], AX.X, ALU.max))
                v.reciprocal(r[:, 3], r[:, 1])
                c.link(v.tensor_tensor(t[:, 2], t[:, 1], wide(r[:, 2].unsqueeze(2), S), ALU.is_lt))
                c.link(v.scalar_tensor_tensor(out=t[:, 2], in0=t[:, 2], scalar=100.0, in1=wide(k.count_row[:, 0:NE].unsqueeze(1), S),
                                              op0=ALU.mult, op1=ALU.add))
                c.link(v.tensor_reduce(r[:, 4], t[:, 2], AX.X, ALU.min))
                v.tensor_tensor(t[:, 3], t[:, 2], wide(r[:, 4].unsqueeze(2), S), ALU.is_equal).then_inc(hot, 1)
                dve.wait_ge(counted, 1)
                tot = ps_all[:, :].rearrange("p (b e) -> p b e", e=NE)
                for e in range(NE):
                    ins = v.tensor_tensor_scan(t[:, 4, :, e], wide(k.ones[:, 0:1], [P, NB]), tot[:, :, e], 0.0, ALU.mult, ALU.add)
                c.link(ins)
                c.link(v.tensor_tensor(t[:, 5], t[:, 4], tot, ALU.subtract))
                c.link(v.tensor_tensor(t[:, 5], t[:, 5], ps_in[:, :].rearrange("p (b e) -> p b e", e=NE), ALU.add))
                c.link(v.tensor_tensor(t[:, 5], t[:, 5], t[:, 3], ALU.mult))
                c.link(v.tensor_reduce(r[:, 5], t[:, 5], AX.X, ALU.add))
                v.tensor_scalar(r[:, 6], r[:, 5], float(CAP), None, ALU.is_lt)
                c.link(v.tensor_scalar(r[:, 7], r[:, 5], float(CAP - 1), None, ALU.min))
                v.tensor_tensor(r[:, 3], r[:, 3], r[:, 2], ALU.mult)
                c.link(v.scalar_tensor_tensor(out=r[:, 8], in0=r[:, 4], scalar=float(CAP), in1=r[:, 7], op0=ALU.mult, op1=ALU.add))
                v.tensor_tensor(factor[:, :], r[:, 3], r[:, 6], ALU.mult)
                v.tensor_copy(slot_i[:, :], r[:, 8])
                c.link(v.tensor_scalar(r[:, 7], k.node_id[:, :], float(SLOTS), None, ALU.add))
                c.link(v.tensor_tensor(r[:, 9], r[:, 8], r[:, 7], ALU.subtract))
                c.link(v.tensor_tensor(r[:, 9], r[:, 9], r[:, 6], ALU.mult))
                c.link(v.tensor_tensor(r[:, 9], r[:, 9], r[:, 7], ALU.add))
                c.link(v.tensor_copy(send_i[:, :], r[:, 9]))
                dve.sem_inc(asked, 1)


def experts0(nc, k, a, buf, out_buf):
    FC = FE // P
    TC = [(q * P, min(P, CAP - q * P)) for q in range((CAP + P - 1) // P)]
    w1_v = a["L0_ffn_w1"].rearrange("e (c p) f -> e p c f", p=P)
    w2_v = a["L0_ffn_w2"].rearrange("e (c p) f -> e p c f", p=P)
    b1_v = a["L0_ffn_b1"].rearrange("e (c p) -> e p c", p=P)
    with Scope(nc) as s:
        w1 = s.sb("x0_w1", [P, 2, KC, FE])
        w2 = s.sb("x0_w2", [P, 2, FC, D])
        b1 = s.sb("x0_b1", [P, 2, FC])
        b2 = s.sb("x0_b2", [1, 2, D])
        rows = s.sb("x0_rows", [P, 2, len(TC), D])
        xT = s.sb("x0_xT", [P, KC, CAP])
        hid = s.sb("x0_hid", [P, FC, CAP])
        y = s.sb("x0_y", [P, 2, len(TC), D])
        ps_t = [s.ps(f"x0_t{c}", [P, 512]) for c in range(KC)]
        ps_h = [s.ps(f"x0_h{j}", [P, 512]) for j in range(2)]
        ps_y = [s.ps(f"x0_y{j}", [P, 512]) for j in range(2)]
        turned, kept, h_done, h_kept, y_done, y_kept, used = (
            s.sem("x0_" + q) for q in ("turned", "kept", "h_done", "h_kept", "y_done", "y_kept", "used"))
        got = [s.sem(f"x0_got{j}") for j in range(2)]
        out = [s.sem(f"x0_out{j}") for j in range(2)]
        NL = 4 + len(TC)

        with nc.Block() as block:
            @block.sync
            def _(sp):
                with sp.Fori(0, NE // 2) as i:
                    for j in range(2):
                        e = i * 2 + j
                        sp.wait_ge(used, e + 1)
                        for c, (o, n) in enumerate(TC):
                            sp.dma_start(rows[0:n, j, c, :], buf[ds(e * CAP + o, n), :]).then_inc(got[j], 16)
                        sp.dma_start(w1[:, j], w1_v[ds(e, 1)].rearrange("a p c f -> p (a c) f")).then_inc(got[j], 16)
                        sp.dma_start(b1[:, j], b1_v[ds(e, 1)].rearrange("a p c -> p (a c)"),
                                     allow_slow_non_contiguous=True).then_inc(got[j], 16)
                        sp.dma_start(w2[:, j], w2_v[ds(e, 1)].rearrange("a p c f -> p (a c) f")).then_inc(got[j], 16)
                        sp.dma_start(b2[:, j, :], a["L0_ffn_b2"][ds(e, 1), :]).then_inc(got[j], 16)

            @block.tensor
            def _(pe):
                pe.sem_inc(used, 2)
                with pe.Fori(0, NE // 2) as i:
                    for j in range(2):
                        e = i * 2 + j
                        pe.wait_ge(got[j], i * (16 * NL) + 16 * NL)
                        pe.wait_ge(kept, e + 1)
                        for c in range(KC):
                            for q, (o, n) in enumerate(TC):
                                ins = nc.tensor.transpose(ps_t[c][:, o:o + n], rows[0:n, j, q, c * P:(c + 1) * P], k.ident[0:n, 0:n])
                        ins.then_inc(turned, 1)
                        pe.wait_ge(kept, e + 2)
                        for f in range(FC):
                            pe.wait_ge(h_kept, e * FC + (f + 1))
                            for c in range(KC):
                                ins = nc.tensor.matmul(ps_h[f % 2][:, 0:CAP], w1[:, j, c, f * P:(f + 1) * P], xT[:, c, :],
                                                       start=(c == 0), stop=(c == KC - 1))
                            ins.then_inc(h_done, 1)
                        pe.wait_ge(h_kept, e * FC + (FC + 2))
                        for q, (o, n) in enumerate(TC):
                            pe.wait_ge(y_kept, e * len(TC) + (q + 1))
                            nc.tensor.matmul(ps_y[q % 2][0:n, 0:D], k.ones[0:1, 0:n], b2[:, j, :], start=True, stop=False)
                            for f in range(FC):
                                ins = nc.tensor.matmul(ps_y[q % 2][0:n, 0:D], hid[:, f, o:o + n], w2[:, j, f, :],
                                                       start=False, stop=(f == FC - 1))
                            ins.then_inc(y_done, 1)
                        pe.wait_ge(y_done, e * len(TC) + len(TC))
                        pe.sem_inc(used, 1)

            @block.scalar
            def _(act):
                act.sem_inc(h_kept, 2)
                with act.Fori(0, NE // 2) as i:
                    for j in range(2):
                        e = i * 2 + j
                        for f in range(FC):
                            act.wait_ge(h_done, e * FC + (f + 1))
                            nc.scalar.activation(hid[:, f, :], ps_h[f % 2][:, 0:CAP], ACT.Relu, bias=b1[:, j, f:f + 1]).then_inc(h_kept, 1)
                        act.wait_ge(y_kept, e * len(TC) + (2 + len(TC)))
                        for q, (o, n) in enumerate(TC):
                            act.dma_start(out_buf[ds(e * CAP + o, n), :], y[0:n, j, q, :]).then_inc(out[j], 16)
                for j in range(2):
                    act.wait_ge(out[j], 16 * len(TC) * (NE // 2))

            @block.vector
            def _(dve):
                v = nc.vector
                dve.sem_inc(kept, 1)
                dve.sem_inc(y_kept, 2)

                def turn(i, first=False):
                    for j in range(2):
                        e = i * 2 + j
                        dve.wait_ge(turned, e + 1)
                        v.tensor_copy(xT[:, 0, :], ps_t[0][:, 0:CAP])
                        v.tensor_copy(xT[:, 1, :], ps_t[1][:, 0:CAP]).then_inc(kept, 1)
                        if not first:
                            dve.wait_ge(out[j], i * (16 * len(TC)))
                        for q, (o, n) in enumerate(TC):
                            dve.wait_ge(y_done, e * len(TC) + (q + 1))
                            v.tensor_copy(y[0:n, j, q, :], ps_y[q % 2][0:n, 0:D]).then_inc(y_kept, 1)
                turn(0, True)
                with dve.Fori(1, NE // 2) as i:
                    turn(i)


def return0(nc, k, out_buf, slot_i, factor):
    with Scope(nc) as s:
        y = s.sb("re_y", [P, NB, D])
        z = s.sb("re_z", [P, NB, D])
        m = s.sb("re_m", [P, NB, D], I32)
        got, chain = s.sem("re_got"), s.sem("re_chain")
        with nc.Block() as block:
            @block.gpsimd
            def _(pool):
                pool.wait_ge(chain, 2)
                for b in range(NB):
                    nc.gpsimd.indirect_dma_start(
                        out=y[:, b, :], out_offset=None, in_=out_buf,
                        in_offset=bass.IndirectOffsetOnAxis(ap=slot_i[:, b:b + 1], axis=0)).then_inc(got, 16)

            @block.vector
            def _(dve):
                v = nc.vector
                c = Chain(dve, chain)
                c.link(v.tensor_scalar(slot_i[:, :], slot_i[:, :], 0, None, ALU.max))
                c.link(v.tensor_scalar(slot_i[:, :], slot_i[:, :], SLOTS - 1, None, ALU.min))
                dve.wait_ge(got, 16 * NB)
                c.link(v.tensor_tensor(y[:, :, :], y[:, :, :], wide(factor[:, :].unsqueeze(2), [P, NB, D]), ALU.mult))
                v.memset(z[:, :, :], 0.0)
                c.link(v.tensor_tensor(m[:, :, :], y[:, :, :], y[:, :, :], ALU.is_equal))
                c.link(v.copy_predicated(z[:, :, :], m[:, :, :], y[:, :, :]))
                for sign, test in ((1.0, ALU.is_gt), (-1.0, ALU.is_lt)):
                    c.link(v.tensor_scalar(m[:, :, :], z[:, :, :], sign * 3.4028234663852886e38, None, test))
                    c.link(v.memset(y[:, :, :], sign * 1.0e4))
                    c.link(v.copy_predicated(z[:, :, :], m[:, :, :], y[:, :, :]))
                c.link(v.tensor_tensor(k.X[:, :, :], k.X[:, :, :], z[:, :, :], ALU.add))


def sort_edges(nc, k, edge_index, pairs):
    turns = C2 // U
    BF = mybir.dt.bfloat16
    src_v = edge_index[0:1, :].rearrange("a (p c) -> (a p) c", p=P)
    dst_v = edge_index[1:2, :].rearrange("a (p c) -> (a p) c", p=P)
    with Scope(nc) as s:
        pair = s.sb("so_pair", [P, C2, 2], I32)
        given = s.sb("so_given", [P, 2, CG], I32)
        loop = s.sb("so_loop", [P, 2, NB])
        key = s.sb("so_key", [P, C2])
        digit_i = s.sb("so_digit_i", [P, 2, C2], I32)
        digit = s.sb("so_digit", [P, 2, C2])
        count = s.sb("so_count", [P, C2, NH])
        before = s.sb("so_before", [P, C2, NH])
        lo = s.sb("so_lo", [P, U, P], BF)
        hi = s.sb("so_hi", [P, U, NH], BF)
        low = s.sb("so_low", [P, P])
        tot = s.sb("so_tot", [P, 4, NH])
        keys = s.sb("so_keys", [P, 2, U])
        same = s.sb("so_same", [P, U, P])
        lo_t = s.sb("so_lo_t", [P, U, P])
        pick = s.sb("so_pick", [P, U, NH])
        place = s.sb("so_place", [P, 4, U])
        place_i = s.sb("so_place_i", [P, C2], I32)
        ix = s.sb("so_ix", [P, 2, U], I32)
        pr = s.sb("so_pr", [P, 2, U, 2], I32)
        edge = s.sb("so_edge", [1, 2, P, 2], I32)
        ps_c = s.ps("so_c", [P, U, NH])
        ps_r = s.ps("so_r", [P, U, P])
        ps_l = s.ps("so_l", [P, U, P])
        ps_g = s.ps("so_g", [P, U, NH])
        ps_s = s.ps("so_s", [P, 2, NH])
        got, iotas, chain, hot, counted, tabled, summed, rowed, keyed, picked, looked, listed, ended = (
            s.sem("so_" + q) for q in ("got", "iotas", "chain", "hot", "counted", "tabled", "summed", "rowed", "keyed", "picked",
                                       "looked", "listed", "ended"))
        sent = [s.sem(f"so_sent{h}") for h in range(2)]
        placed = s.sem("so_placed")
        B_LINKS, C_LINKS = 8, 6
        with nc.Block() as block:
            @block.sync
            def _(sp):
                sp.dma_start(given[:, 0, :], dst_v).then_inc(got, 16)
                sp.dma_start(given[:, 1, :], src_v).then_inc(got, 16)
                sp.wait_ge(iotas, 3)
                sp.dma_start(pairs[0:1, :], edge[0:1, 0, 0, :]).then_inc(ended, 16)
                sp.dma_start(pairs[C2 * P + 1:(C2 + 1) * P, :].rearrange("(a r) b -> a r b", a=1), edge[:, 1, 0:P - 1, :]).then_inc(ended, 16)
                sp.wait_ge(ended, 32)

            @block.gpsimd
            def _(pool):
                nc.gpsimd.memset(edge[:, 0], -1).then_inc(iotas, 1)
                nc.gpsimd.memset(edge[:, 1], NONODE).then_inc(iotas, 1)
                pool.wait_ge(iotas, 2)
                nc.gpsimd.memset(ix[:, :, :], 0).then_inc(iotas, 1)
                pool.wait_ge(iotas, 3)

                def turn(i, w, h):
                    pool.wait_ge(placed, i + 1)
                    if w is not None:
                        pool.wait_ge(sent[h], w * (16 * U))
                    pool.wait_ge(k.armed, 1)
                    nc.gpsimd.tensor_copy(ix[:, h, :], place_i[:, ds(i * U, U)])
                    nc.gpsimd.tensor_copy(pr[:, h], pair[:, ds(i * U, U), :]).then_inc(listed, 1)
                    pool.wait_ge(k.armed, 1)
                    pool.wait_ge(listed, i + 1)
                    for u in range(U):
                        nc.gpsimd.indirect_dma_start(
                            out=pairs, out_offset=bass.IndirectOffsetOnAxis(ap=ix[:, h, u:u + 1], axis=0),
                            in_=pr[:, h, u, :], in_offset=None).then_inc(sent[h], 16)
                turn(0, None, 0)
                turn(1, None, 1)
                with pool.Fori(1, turns // 2) as w:
                    turn(w * 2, w, 0)
                    turn(w * 2 + 1, w, 1)
                for h in range(2):
                    pool.wait_ge(sent[h], 16 * U * (turns // 2))

            @block.tensor
            def _(pe):
                with pe.Fori(0, turns) as i:
                    pe.wait_ge(hot, i + 1)
                    for u in range(U):
                        ins = nc.tensor.matmul(ps_c[:, u, :], lo[:, u, :], hi[:, u, :], start=True, stop=True)
                    ins.then_inc(counted, 1)
                pe.wait_ge(tabled, 1)
                nc.tensor.matmul(ps_s[:, 0, :], k.upper[:, :], tot[:, 0], start=True, stop=True)
                nc.tensor.matmul(ps_s[:, 1, :], k.ones[:, :], tot[:, 0], start=True, stop=True).then_inc(summed, 1)
                with pe.Fori(0, turns) as i:
                    pe.wait_ge(keyed, i + 1)
                    for u in range(U):
                        nc.tensor.transpose(ps_r[:, u, :], wide(keys[:, 0, u:u + 1], [P, P]), k.ident[:, :])
                        ins = nc.tensor.transpose(ps_l[:, u, :], wide(keys[:, 1, u:u + 1], [P, P]), k.ident[:, :])
                    ins.then_inc(rowed, 1)
                    pe.wait_ge(picked, i + 1)
                    for u in range(U):
                        ins = nc.tensor.matmul(ps_g[:, u, :], lo_t[:, u, :],
                                               before[:, ds(i * U + u, 1), :].rearrange("p a h -> p (a h)"), start=True, stop=True)
                    ins.then_inc(looked, 1)

            @block.vector
            def _(dve):
                v = nc.vector
                c = Chain(dve, chain)
                dve.wait_ge(got, 32)
                v.tensor_copy(pair[:, 0:CG, 0], given[:, 0, :])
                v.tensor_copy(pair[:, 0:CG, 1], given[:, 1, :])
                v.memset(pair[:, CG:C2, 0], NONODE)
                c.link(v.memset(pair[:, CG:C2, 1], 0))
                v.tensor_copy(loop[:, 0, :], k.node_id[:, :])
                c.link(v.tensor_scalar(loop[:, 1, :], k.node_id[:, :], float(NONODE), None, ALU.subtract))
                c.link(v.tensor_tensor(loop[:, 1, :], loop[:, 1, :], k.node_mask[:, :], ALU.mult))
                c.link(v.tensor_scalar(loop[:, 1, :], loop[:, 1, :], float(NONODE), None, ALU.add))
                c.link(v.tensor_tensor(loop[:, 0, :], loop[:, 0, :], k.node_mask[:, :], ALU.mult))
                v.tensor_copy(pair[:, CG:CG + NB, 0], loop[:, 1, :])
                c.link(v.tensor_copy(pair[:, CG:CG + NB, 1], loop[:, 0, :]))
                c.link(v.tensor_scalar(digit_i[:, 0, :], pair[:, :, 0], P - 1, None, ALU.bitwise_and))
                c.link(v.tensor_scalar(digit_i[:, 1, :], pair[:, :, 0], 7, None, ALU.arith_shift_right))
                v.tensor_copy(key[:, :], pair[:, :, 0])
                c.link(v.tensor_copy(digit[:, :, :], digit_i[:, :, :]))
                c.link(v.tensor_tensor(low[:, :], wide(k.count_col[:, 0:1], [P, P]), k.count_row[:, 0:P], ALU.is_gt))
                base = c.n
                with dve.Fori(0, turns) as i:
                    v.tensor_tensor(lo[:, :, :], wide(k.count_row[:, 0:P].unsqueeze(1), [P, U, P]),
                                    wide(digit[:, 0, ds(i * U, U)].unsqueeze(2), [P, U, P]), ALU.is_equal)
                    v.tensor_tensor(hi[:, :, :], wide(k.count_row[:, 0:NH].unsqueeze(1), [P, U, NH]),
                                    wide(digit[:, 1, ds(i * U, U)].unsqueeze(2), [P, U, NH]), ALU.is_equal).then_inc(hot, 1)
                    dve.wait_ge(counted, i + 1)
                    dve.wait_ge(k.armed, 1)
                    v.tensor_copy(count[:, ds(i * U, U), :], ps_c[:, :, :]).then_inc(chain, 1)
                dve.wait_ge(chain, base + turns)
                c = Chain(dve, chain, base + turns)
                v.tensor_reduce(tot[:, 0], count[:, :, :].rearrange("p c h -> p h c"), AX.X, ALU.add).then_inc(tabled, 1)
                dve.wait_ge(summed, 1)
                c.link(v.tensor_tensor_scan(tot[:, 1], wide(k.ones[:, 0:1], [P, NH]), ps_s[:, 1, :], 0.0, ALU.mult, ALU.add))
                c.link(v.tensor_tensor(tot[:, 1], tot[:, 1], ps_s[:, 1, :], ALU.subtract))
                c.link(v.tensor_tensor(tot[:, 1], tot[:, 1], ps_s[:, 0, :], ALU.add))
                for x in range(NH):
                    ins = v.tensor_tensor_scan(before[:, :, x], wide(k.ones[:, 0:1], [P, C2]), count[:, :, x],
                                               tot[:, 1, x:x + 1], ALU.mult, ALU.add)
                c.link(ins)
                c.link(v.tensor_tensor(before[:, :, :], before[:, :, :], count[:, :, :], ALU.subtract))
                base += turns + c.n
                with dve.Fori(0, turns) as i:
                    c = Chain(dve, chain, i * C_LINKS + base)
                    v.tensor_copy(keys[:, 1], digit[:, 0, ds(i * U, U)])
                    v.tensor_copy(keys[:, 0], key[:, ds(i * U, U)]).then_inc(keyed, 1)
                    v.tensor_tensor(pick[:, :, :], wide(k.count_row[:, 0:NH].unsqueeze(1), [P, U, NH]),
                                    wide(digit[:, 1, ds(i * U, U)].unsqueeze(2), [P, U, NH]), ALU.is_equal)
                    dve.wait_ge(keyed, i + 1)
                    dve.wait_ge(rowed, i + 1)
                    v.tensor_scalar(lo_t[:, :, :], ps_l[:, :, :], k.count_col[:, 0:1], None, ALU.is_equal).then_inc(picked, 1)
                    c.link(v.tensor_tensor(same[:, :, :], ps_r[:, :, :], wide(keys[:, 0].unsqueeze(2), [P, U, P]), ALU.is_equal))
                    c.link(v.tensor_tensor(same[:, :, :], same[:, :, :], wide(low[:, :].unsqueeze(1), [P, U, P]), ALU.mult))
                    c.link(v.tensor_reduce(place[:, 0], same[:, :, :], AX.X, ALU.add))
                    dve.wait_ge(looked, i + 1)
                    c.link(v.tensor_tensor(pick[:, :, :], pick[:, :, :], ps_g[:, :, :], ALU.mult))
                    c.link(v.tensor_reduce(place[:, 1], pick[:, :, :], AX.X, ALU.add))
                    c.link(v.scalar_tensor_tensor(out=place[:, 2], in0=place[:, 0], scalar=1.0, in1=place[:, 1], op0=ALU.add, op1=ALU.add))
                    v.tensor_copy(place_i[:, ds(i * U, U)], place[:, 2]).then_inc(placed, 1)
                    assert c.n == C_LINKS


def edge_factors(nc, k, a, attr, emb_t, e, factor, scale):
    LD = 2048
    Q = 512
    loads = C1 * P // LD
    assert loads % 2 == 0 and C1 * P % LD == 0
    SILU_NORM = 1.679177
    with Scope(nc) as s:
        emb = s.sb("ef_emb", [10, 2, LD])
        w1 = s.sb("ef_w1", [10, 64])
        w2 = s.sb("ef_w2", [64, 1])
        h = s.sb("ef_h", [64, 2, Q])
        at = s.sb("ef_at", [P, C1, 4])
        rad = s.sb("ef_rad", [P, C1])
        rows = s.sb("ef_rows", [P, G1, 4, P])
        ps_h = [s.ps(f"ef_h{j}", [64, Q]) for j in range(2)]
        ps_r = s.ps("ef_r", [P, C1])
        bank = [s.ps(f"ef_bank{j}", [P, 4, P]) for j in range(G1)]
        tab = nc.dram_tensor("edge_factor_rows", [C1, 4 * P], F32, kind="Internal").ap()
        got_w, hid, acted, radial, made, turned, moved, spread, back, chain = (
            s.sem("ef_" + q) for q in ("got_w", "hid", "acted", "radial", "made", "turned", "moved", "spread", "back", "chain"))
        got = [s.sem(f"ef_got{j}") for j in range(2)]
        R = LD // Q
        with nc.Block() as block:
            @block.sync
            def _(sp):
                sp.dma_start(w1[:, :], a["L1_gnn_fc_w1"]).then_inc(got_w, 16)
                sp.dma_start(w2[:, :], a["L1_gnn_fc_w2"]).then_inc(got_w, 16)
                sp.dma_start(at[:, :, :], attr).then_inc(got_w, 16)
                with sp.Fori(0, loads // 2) as i:
                    for j in range(2):
                        sp.wait_ge(hid, i * (2 * R) + (j + 1) * R)
                        sp.dma_start(emb[:, j, :], emb_t[:, ds(i * (2 * LD) + j * LD, LD)]).then_inc(got[j], 16)
                sp.wait_ge(moved, G1)
                for g in range(G1):
                    n = min(P, C1 - g * P)
                    sp.dma_start(tab[g * P:g * P + n, :], rows[0:n, g].rearrange("p m e -> p (m e)")).then_inc(spread, 16)
                sp.wait_ge(spread, 16 * G1)

            @block.tensor
            def _(pe):
                pe.sem_inc(hid, 2 * R)
                pe.wait_ge(got_w, 48)
                with pe.Fori(0, loads // 2) as i:
                    for j in range(2):
                        pe.wait_ge(got[j], i * 16 + 16)
                        for r in range(R):
                            n = i * (2 * R) + (j * R + r)
                            pe.wait_ge(radial, n + 1)
                            nc.tensor.matmul(ps_h[r % 2][:, :], w1[:, :], emb[:, j, r * Q:(r + 1) * Q], start=True, stop=True).then_inc(hid, 1)
                            pe.wait_ge(acted, n + 1)
                            pe.wait_ge(k.armed, 1)
                            for q in range(Q // P):
                                ins = nc.tensor.matmul(ps_r[:, ds(n * (Q // P) + q, 1)], h[:, r % 2, q * P:(q + 1) * P], w2[:, :],
                                                       start=True, stop=True)
                            ins.then_inc(radial, 1)
                pe.wait_ge(made, 1)
                for g in range(G1):
                    n = min(P, C1 - g * P)
                    for m in range(4):
                        ins = nc.tensor.transpose(bank[g][0:n, m, :], at[:, g * P:g * P + n, m], k.ident[:, :])
                    ins.then_inc(turned, 1)
                pe.wait_ge(moved, G1)
                pe.wait_ge(back, 16 * G1)
                for g in range(G1):
                    for m in range(4):
                        ins = nc.tensor.transpose(bank[g][:, m, :], rows[:, g, m, :], k.ident[:, :])
                    ins.then_inc(turned, 1)

            @block.scalar
            def _(act):
                act.sem_inc(radial, 2)
                with act.Fori(0, loads * R // 2) as i:
                    for j in range(2):
                        act.wait_ge(hid, i * 2 + (j + 1 + 2 * R))
                        nc.scalar.activation(h[:, j, :], ps_h[j][:, :], ACT.Silu, scale=float(10.0 ** -0.5)).then_inc(acted, 1)

            @block.gpsimd
            def _(pool):
                pool.wait_ge(spread, 16 * G1)
                for g in range(G1):
                    nc.gpsimd.indirect_dma_start(
                        out=rows[:, g].rearrange("p m e -> p (m e)"), out_offset=None, in_=tab,
                        in_offset=bass.IndirectOffsetOnAxis(ap=e.chunk[:, g:g + 1], axis=0)).then_inc(back, 16)

            @block.vector
            def _(dve):
                v = nc.vector
                c = Chain(dve, chain)
                dve.wait_ge(got_w, 48)
                dve.wait_ge(radial, loads * R + 2)
                c.link(v.tensor_scalar(rad[:, :], ps_r[:, :], float(SILU_NORM / 8.0 * scale), None, ALU.mult))
                v.tensor_tensor(at[:, :, :], at[:, :, :], wide(rad[:, :].unsqueeze(2), [P, C1, 4]), ALU.mult).then_inc(made, 1)
                for g in range(G1):
                    n = min(P, C1 - g * P)
                    dve.wait_ge(turned, g + 1)
                    v.tensor_copy(rows[0:n, g], bank[g][0:n]).then_inc(moved, 1)
                for g in range(G1):
                    dve.wait_ge(turned, G1 + g + 1)
                    ins = v.tensor_copy(factor[:, g * P:(g + 1) * P, :].rearrange("p t m -> p m t"), bank[g][:, :, :])
                c.link(ins)


def gram1(nc, k, x_tab, sums):
    with Scope(nc) as s:
        xn = s.sb("g1_xn", [P, B5, D])
        zero = s.sb("g1_zero", [P, 512])
        ps = [s.ps(f"g1_{c}", [P, 512]) for c in range(KC)]
        ps_row = s.ps("g1_row", [P, 512])
        normed, used, zeroed, done, moved = (s.sem("g1_" + q) for q in ("normed", "used", "zeroed", "done", "moved"))
        out = [s.sem(f"g1_out{j}") for j in range(B5)]
        with nc.Block() as block:
            @block.scalar
            def _(act):
                def turn(i, first=False):
                    for j in range(B5):
                        act.wait_ge(used, i * B5 + j + 1)
                        if not first:
                            act.wait_ge(out[j], i * 16)
                        act.wait_ge(k.armed, 1)
                        normed_block(nc, k, act, i * B5 + j, xn[:, j, :], normed)
                turn(0, True)
                with act.Fori(1, NB // B5) as i:
                    turn(i)

            @block.sync
            def _(sp):
                with sp.Fori(0, NB // B5) as i:
                    for j in range(B5):
                        sp.wait_ge(normed, i * B5 + j + 1)
                        sp.dma_start(x_tab[ds((i * B5 + j) * P, P), :], xn[:, j, :]).then_inc(out[j], 16)
                for j in range(B5):
                    sp.wait_ge(out[j], 16 * (NB // B5))

            @block.tensor
            def _(pe):
                pe.sem_inc(used, B5)
                pe.wait_ge(zeroed, 1)
                for x in (*ps, ps_row):
                    nc.tensor.matmul(x[:, :], zero[:, 0:P], zero[:, :], start=True, stop=False, skip_group_check=True)
                with pe.Fori(0, NB // B5) as i:
                    for j in range(B5):
                        pe.wait_ge(normed, i * B5 + j + 1)
                        for c in range(KC):
                            nc.tensor.matmul(ps[c][:, 0:D], xn[:, j, c * P:(c + 1) * P], xn[:, j, :], start=False, stop=False, skip_group_check=True)
                            nc.tensor.matmul(ps[c][:, D:D + 1], xn[:, j, c * P:(c + 1) * P], k.ones[:, 0:1], start=False, stop=False, skip_group_check=True)
                        nc.tensor.matmul(ps_row[0:1, 0:D], k.ones[:, 0:1], xn[:, j, :], start=False, stop=False, skip_group_check=True).then_inc(used, 1)
                pe.wait_ge(used, NB + B5)
                pe.sem_inc(done, 1)

            @block.vector
            def _(dve):
                v = nc.vector
                v.memset(zero[:, :], 0.0).then_inc(zeroed, 1)
                dve.wait_ge(done, 1)
                for c in range(KC):
                    v.tensor_copy(sums[:, c, 0:D + 1], ps[c][:, 0:D + 1])
                v.tensor_copy(sums[0:1, 2, 0:D], ps_row[0:1, 0:D]).then_inc(moved, 1)
                dve.wait_ge(moved, 1)


def mixer_matrix1(nc, k, sums, G, g_bias):
    HD = 32
    with Scope(nc) as s:
        u = s.sb("m1x_u", [P, KC, D])
        vs = s.sb("m1x_vs", [1, D])
        pT = s.sb("m1x_pT", [P, KC, P])
        mask = s.sb("m1x_mask", [P, P])
        t = s.sb("m1x_t", [P, KC, D])
        n_row = s.sb("m1x_n", [1, 1])
        ps = [s.ps(f"m1x_{j}", [P, 512]) for j in range(6)]
        step, ready = s.sem("m1x_step"), s.sem("m1x_ready")
        wkT, wvT, wfcT = k.fcT
        bk, bv, bfc = (k.bias1[:, j * D:(j + 1) * D] for j in range(3))
        with nc.Block() as block:
            @block.tensor
            def _(pe):
                pe.wait_ge(step, 1)
                for c in range(KC):
                    for q in range(KC):
                        nc.tensor.matmul(ps[c][:, 0:D], sums[:, q, c * P:(c + 1) * P], wvT[:, q, :], start=(q == 0), stop=False)
                    nc.tensor.matmul(ps[c][:, 0:D], sums[0:1, 2, c * P:(c + 1) * P], bv, start=False, stop=True)
                for q in range(KC):
                    nc.tensor.matmul(ps[2][0:1, 0:D], sums[:, q, D:D + 1], wvT[:, q, :], start=(q == 0), stop=False)
                nc.tensor.matmul(ps[2][0:1, 0:D], n_row[:, :], bv, start=False, stop=True).then_inc(ready, 1)
                pe.wait_ge(step, 2)
                for c in range(KC):
                    for q in range(KC):
                        nc.tensor.matmul(ps[3][:, c * P:(c + 1) * P], u[:, q, c * P:(c + 1) * P], wkT[:, q, c * P:(c + 1) * P],
                                         start=(q == 0), stop=False, skip_group_check=True)
                    ins = nc.tensor.matmul(ps[3][:, c * P:(c + 1) * P], vs[:, c * P:(c + 1) * P], bk[:, c * P:(c + 1) * P],
                                           start=False, stop=True, skip_group_check=True)
                ins.then_inc(ready, 1)
                pe.wait_ge(step, 3)
                for c in range(KC):
                    ins = nc.tensor.matmul(ps[c][:, 0:D], pT[:, c, :], wfcT[:, c, :], start=True, stop=True)
                ins.then_inc(ready, 1)
                pe.wait_ge(step, 4)
                for c in range(KC):
                    for q in range(KC):
                        nc.tensor.matmul(ps[4 + c][:, 0:D], k.fc_q[:, q, c * P:(c + 1) * P], t[:, q, :], start=(q == 0), stop=(q == KC - 1))
                for q in range(KC):
                    nc.tensor.matmul(ps[2][0:1, 0:D], k.bq_col[:, q:q + 1], t[:, q, :], start=(q == 0), stop=False)
                nc.tensor.matmul(ps[2][0:1, 0:D], k.ones[0:1, 0:1], bfc, start=False, stop=True).then_inc(ready, 1)

            @block.vector
            def _(dve):
                v = nc.vector
                v.memset(n_row[:, :], float(N))
                v.memset(mask[:, :], 0.0).then_inc(step, 1)
                dve.wait_ge(step, 1)
                for h in range(P // HD):
                    v.memset(mask[h * HD:(h + 1) * HD, h * HD:(h + 1) * HD], 1.0 / N)
                dve.wait_ge(ready, 1)
                for c in range(KC):
                    v.tensor_copy(u[:, c, :], ps[c][:, 0:D])
                v.tensor_copy(vs[:, :], ps[2][0:1, 0:D]).then_inc(step, 1)
                dve.wait_ge(ready, 2)
                dve.wait_ge(step, 2)
                v.tensor_tensor(pT[:, :, :], ps[3][:, 0:2 * P].rearrange("p (c d) -> p c d", d=P),
                                wide(mask[:, :].unsqueeze(1), [P, KC, P]), ALU.mult).then_inc(step, 1)
                dve.wait_ge(ready, 3)
                v.tensor_copy(t[:, 0, :], ps[0][:, 0:D])
                v.tensor_copy(t[:, 1, :], ps[1][:, 0:D]).then_inc(step, 1)
                dve.wait_ge(ready, 4)
                for c in range(KC):
                    v.tensor_copy(G[:, c, :], ps[4 + c][:, 0:D])
                v.tensor_copy(g_bias[:, :], ps[2][0:1, 0:D]).then_inc(step, 1)
                dve.wait_ge(step, 5)


def convolve(nc, k, e, x_tab, factor, acc):
    turns = T1 // U
    M = 64
    with Scope(nc) as s:
        ix = s.sb("cv_ix", [P, 2, U], I32)
        xg = s.sb("cv_x", [P, 2, U, D])
        hot = s.sb("cv_hot", [P, 2, U, P])
        wt = s.sb("cv_wt", [P, 2, U, 4, P])
        ps = [s.ps(f"cv_ps{u}", [P, 512]) for u in range(U)]
        listed, freed, built, chain, summed, added = (s.sem("cv_" + q) for q in ("listed", "freed", "built", "chain", "summed", "added"))
        got = [s.sem(f"cv_got{h}") for h in range(2)]
        with nc.Block() as block:
            @block.gpsimd
            def _(pool):
                def turn(i, h):
                    pool.wait_ge(freed, i + 1)
                    pool.wait_ge(k.armed, 1)
                    nc.gpsimd.tensor_copy(ix[:, h, :], e.src[:, ds(i * U, U)]).then_inc(listed, 1)
                    pool.wait_ge(k.armed, 1)
                    pool.wait_ge(listed, i + 1)
                    for u in range(U):
                        nc.gpsimd.indirect_dma_start(
                            out=xg[:, h, u, :], out_offset=None, in_=x_tab,
                            in_offset=bass.IndirectOffsetOnAxis(ap=ix[:, h, u:u + 1], axis=0)).then_inc(got[h], 16)
                with pool.Fori(0, turns // 2) as w:
                    turn(w * 2, 0)
                    turn(w * 2 + 1, 1)
                turn(turns - 1, 0)

            @block.tensor
            def _(pe):
                pe.sem_inc(freed, 2)

                def turn(i, w, h):
                    pe.wait_ge(built, i + 1)
                    pe.wait_ge(got[h], w * (16 * U) + 16 * U)
                    for u in range(U):
                        pe.wait_ge(added, i * U + (u + 1))
                        row = xg[:, h, u, :]
                        s0, s1 = row[:, 0:M], row[:, M:D].rearrange("p (i m) -> p m i", m=3)
                        nc.tensor.matmul(ps[u][:, 0:M], wt[:, h, u, 0, :], s0, start=True, stop=False, skip_group_check=True)
                        nc.tensor.matmul(ps[u][:, M:D].rearrange("p (m i) -> p m i", m=3), wt[:, h, u, 0, :], s1,
                                         start=False, stop=False, skip_group_check=True)
                        for m in range(3):
                            nc.tensor.matmul(ps[u][:, D + m * M:D + (m + 1) * M], wt[:, h, u, 1 + m, :], s0,
                                             start=False, stop=False, skip_group_check=True)
                            ins = nc.tensor.matmul(ps[u][:, D + 3 * M:512], wt[:, h, u, 1 + m, :], s1[:, m, :],
                                                   start=False, stop=(m == 2), skip_group_check=True)
                        ins.then_inc(summed, 1)
                    pe.wait_ge(summed, i * U + U)
                    pe.sem_inc(freed, 1)
                with pe.Fori(0, turns // 2) as w:
                    turn(w * 2, w, 0)
                    turn(w * 2 + 1, w, 1)
                turn(turns - 1, turns // 2, 0)

            @block.vector
            def _(dve):
                v = nc.vector
                dve.sem_inc(added, U)

                def build(i, h):
                    v.tensor_tensor(hot[:, h], wide(k.count_row[:, 0:P].unsqueeze(1), [P, U, P]),
                                    wide(e.rel[:, ds(i * U, U)].unsqueeze(2), [P, U, P]), ALU.is_equal).then_inc(chain, 1)
                    dve.wait_ge(chain, i + 1)
                    for m in range(4):
                        ins = v.tensor_tensor(wt[:, h, :, m, :], hot[:, h],
                                              wide(factor[:, ds(i * U, U), m:m + 1], [P, U, P]), ALU.mult)
                    ins.then_inc(built, 1)

                def add(i):
                    for u in range(U):
                        b = block_of(dve, e, i * U + u)
                        dve.wait_ge(summed, i * U + (u + 1))
                        dve.wait_ge(added, i * U + (u + U))
                        dve.wait_ge(k.armed, 1)
                        v.tensor_tensor(acc[:, ds(b, 1), :].rearrange("p a w -> p (a w)"),
                                        acc[:, ds(b, 1), :].rearrange("p a w -> p (a w)"),
                                        ps[u][:, :], ALU.add).then_inc(added, 1)
                build(0, 0)
                with dve.Fori(0, turns // 2) as w:
                    build(w * 2 + 1, 1)
                    add(w * 2)
                    build(w * 2 + 2, 0)
                    add(w * 2 + 1)
                add(turns - 1)
                dve.wait_ge(added, T1 + U)


def combine1(nc, k, a, acc, G, g_bias):
    M = 64
    with Scope(nc) as s:
        xn = s.sb("c1_xn", [P, B5, D])
        ac = s.sb("c1_ac", [P, B5, 512])
        xT = s.sb("c1_xT", [P, B5, KC, P])
        aT = s.sb("c1_aT", [P, B5, 4, P])
        w = s.sb("c1_w", [P, 4, D])
        raw = s.sb("c1_raw", [P, 4, M])
        ps_t = s.ps("c1_t", [P, 512])
        ps_a = s.ps("c1_a", [P, 512])
        ps_o = [s.ps(f"c1_o{j}", [P, 512]) for j in range(B5)]
        got, cleared, wready, normed, turned, kept, done, chain = (
            s.sem("c1_" + q) for q in ("got", "cleared", "wready", "normed", "turned", "kept", "done", "chain"))
        names = ("L1_gnn_w_00_0", "L1_gnn_w_10_1", "L1_gnn_w_01_1", "L1_gnn_w_11_0")
        with nc.Block() as block:
            @block.sync
            def _(sp):
                for j, n in enumerate(names):
                    for half in range(2):
                        sp.dma_start(raw[half * M:(half + 1) * M, j, :], a[n]).then_inc(got, 16)
                sp.wait_ge(got, 128)

            @block.scalar
            def _(act):
                with act.Fori(0, NB // B5) as i:
                    for j in range(B5):
                        b = i * B5 + j
                        act.wait_ge(turned, b + 1)
                        act.wait_ge(k.armed, 1)
                        nc.scalar.activation(ac[:, j, :], acc[:, ds(b, 1), :].rearrange("p a w -> p (a w)"), ACT.Copy)
                        normed_block(nc, k, act, b, xn[:, j, :], normed)

            @block.tensor
            def _(pe):
                pe.sem_inc(turned, B5)
                pe.wait_ge(wready, 1)
                with pe.Fori(0, NB // B5) as i:
                    for j in range(B5):
                        b = i * B5 + j
                        pe.wait_ge(normed, b + 1)
                        pe.wait_ge(kept, b + 1)
                        for c in range(KC):
                            nc.tensor.transpose(ps_t[:, c * P:(c + 1) * P], xn[:, j, c * P:(c + 1) * P], k.ident[:, :])
                        for c in range(4):
                            ins = nc.tensor.transpose(ps_a[:, c * P:(c + 1) * P], ac[:, j, c * P:(c + 1) * P], k.ident[:, :])
                        ins.then_inc(turned, 1)
                        pe.wait_ge(kept, b + 2)
                        nc.tensor.matmul(ps_o[j][:, 0:D], k.ones[0:1, :], g_bias[:, :], start=True, stop=False)
                        for c in range(KC):
                            nc.tensor.matmul(ps_o[j][:, 0:D], xT[:, j, c, :], G[:, c, :], start=False, stop=False)
                        for c in range(4):
                            ins = nc.tensor.matmul(ps_o[j][:, 0:D], aT[:, j, c, :], w[:, c, :], start=False, stop=(c == 3))
                        ins.then_inc(done, 1)

            @block.vector
            def _(dve):
                v = nc.vector
                v.memset(w[:, :, :], 0.0).then_inc(cleared, 1)
                dve.wait_ge(cleared, 1)
                dve.wait_ge(got, 128)
                for r in range(8):
                    lo, c = (r % 2) * M, r // 2
                    if r == 0:
                        ins = v.tensor_copy(w[lo:lo + M, c, 0:M], raw[lo:lo + M, 0, :])
                    elif r == 7:
                        ins = v.tensor_scalar(w[lo:lo + M, c, 0:M], raw[lo:lo + M, 3, :], float(3.0 ** -0.5), None, ALU.mult)
                    else:
                        m, j = (r - 1, 1) if r < 4 else (r - 4, 2)
                        ins = v.tensor_copy(w[lo:lo + M, c, M + m:D:3], raw[lo:lo + M, j, :])
                ins.then_inc(wready, 1)
                dve.sem_inc(kept, 1)
                with dve.Fori(0, NB // B5) as i:
                    for j in range(B5):
                        b = i * B5 + j
                        xb = k.X[:, ds(b, 1), :].rearrange("p a d -> p (a d)")
                        dve.wait_ge(turned, b + B5 + 1)
                        v.tensor_copy(xT[:, j], ps_t[:, 0:D].rearrange("p (c t) -> p c t", t=P))
                        v.tensor_copy(aT[:, j], ps_a[:, :].rearrange("p (c t) -> p c t", t=P)).then_inc(kept, 1)
                        dve.wait_ge(done, b + 1)
                        dve.wait_ge(k.armed, 1)
                        v.tensor_tensor(xb, xb, ps_o[j][:, 0:D], ALU.add).then_inc(chain, 1)
                dve.wait_ge(chain, NB)


GW = 24


def gate_rows(nc, k, h_tab, xnT, row_cols):
    with Scope(nc) as s:
        xn = s.sb("gr_xn", [P, B5, D])
        xT = s.sb("gr_xT", [P, B5, KC, P])
        h = s.sb("gr_h", [P, B5, GW])
        pr = s.sb("gr_pr", [P, 2, 16])
        ps_t = s.ps("gr_t", [P, KC, P])
        ps_h = [s.ps(f"gr_h{j}", [P, 16]) for j in range(B5)]
        ps_c = s.ps("gr_c", [P, 80])
        normed, turned, kept, done, ready, chain, spread = (
            s.sem("gr_" + q) for q in ("normed", "turned", "kept", "done", "ready", "chain", "spread"))
        out = [s.sem(f"gr_out{j}") for j in range(B5)]
        PER = 3
        with nc.Block() as block:
            @block.scalar
            def _(act):
                with act.Fori(0, NB // B5) as i:
                    for j in range(B5):
                        act.wait_ge(turned, i * B5 + j + 1)
                        act.wait_ge(k.armed, 1)
                        normed_block(nc, k, act, i * B5 + j, xn[:, j, :], normed)

            @block.sync
            def _(sp):
                with sp.Fori(0, NB // B5) as i:
                    for j in range(B5):
                        sp.wait_ge(ready, i * B5 + j + 1)
                        sp.dma_start(h_tab[ds((i * B5 + j) * P, P), :], h[:, j, :]).then_inc(out[j], 16)
                for j in range(B5):
                    sp.wait_ge(out[j], 16 * (NB // B5))

            @block.tensor
            def _(pe):
                nc.tensor.matmul(ps_c[:, :], k.ones[0:1, :], k.gat_rows[:, :], start=True, stop=True).then_inc(spread, 1)
                pe.sem_inc(turned, B5)
                with pe.Fori(0, NB // B5) as i:
                    for j in range(B5):
                        b = i * B5 + j
                        pe.wait_ge(normed, b + 1)
                        pe.wait_ge(kept, 2 * b + 1)
                        for c in range(KC):
                            ins = nc.tensor.transpose(ps_t[:, c, :], xn[:, j, c * P:(c + 1) * P], k.ident[:, :])
                        ins.then_inc(turned, 1)
                        pe.wait_ge(kept, 2 * b + 3)
                        for c in range(KC):
                            ins = nc.tensor.matmul(ps_h[j][:, :], xT[:, j, c, :], k.gat_w[:, c, :], start=(c == 0), stop=(c == KC - 1))
                        ins.then_inc(done, 1)

            @block.vector
            def _(dve):
                v = nc.vector
                dve.sem_inc(kept, 1)
                dve.wait_ge(spread, 1)
                v.tensor_copy(row_cols[:, :], ps_c[:, :]).then_inc(chain, 1)
                dve.wait_ge(chain, 1)

                def turn(i, first=False):
                    c = Chain(dve, chain, i * (PER * B5) + 1)
                    for j in range(B5):
                        b = i * B5 + j
                        dve.wait_ge(turned, b + B5 + 1)
                        v.tensor_copy(xT[:, j], ps_t[:, :, :]).then_inc(kept, 1)
                        v.tensor_copy(xnT[:, :, ds(b * P, P)], ps_t[:, :, :]).then_inc(kept, 1)
                        if not first:
                            dve.wait_ge(out[j], i * 16)
                        dve.wait_ge(done, b + 1)
                        c.link(v.tensor_copy(h[:, j, 0:16], ps_h[j][:, :]))
                        v.tensor_tensor(pr[:, 0], h[:, j, 0:16], row_cols[:, 0:16], ALU.mult)
                        c.link(v.tensor_tensor(pr[:, 1], h[:, j, 0:16], row_cols[:, 16:32], ALU.mult))
                        c.link(v.tensor_reduce(h[:, j, 16:24], pr[:, :, :].rearrange("p a (h e) -> p (a h) e", e=NX), AX.X, ALU.add))
                        dve.sem_inc(ready, 1)
                    assert c.n == PER * B5
                turn(0, True)
                with dve.Fori(1, NB // B5) as i:
                    turn(i)


def gate_scores(nc, k, e, h_tab, rows, score):
    turns = T2 // U
    with Scope(nc) as s:
        ix = s.sb("gs_ix", [P, 2, 2, U], I32)
        hg = s.sb("gs_h", [P, 2, U, GW])
        dg = s.sb("gs_d", [P, 2, U, GW])
        t = s.sb("gs_t", [P, U, H2])
        listed, freed, chain, took = s.sem("gs_listed"), s.sem("gs_freed"), s.sem("gs_chain"), s.sem("gs_took")
        got = [s.sem(f"gs_got{h}") for h in range(2)]
        assert turns % 2 == 1
        with nc.Block() as block:
            @block.gpsimd
            def _(pool):
                def turn(i, h):
                    pool.wait_ge(freed, i + 1)
                    pool.wait_ge(k.armed, 1)
                    nc.gpsimd.tensor_copy(ix[:, h, 0, :], e.src[:, ds(i * U, U)])
                    nc.gpsimd.tensor_copy(ix[:, h, 1, :], e.dst[:, ds(i * U, U)]).then_inc(listed, 1)
                    pool.wait_ge(k.armed, 1)
                    pool.wait_ge(listed, i + 1)
                    for u in range(U):
                        for n, to in enumerate((hg, dg)):
                            nc.gpsimd.indirect_dma_start(
                                out=to[:, h, u, :], out_offset=None, in_=h_tab,
                                in_offset=bass.IndirectOffsetOnAxis(ap=ix[:, h, n, u:u + 1], axis=0)).then_inc(got[h], 16)
                with pool.Fori(0, turns // 2) as w:
                    turn(w * 2, 0)
                    turn(w * 2 + 1, 1)
                turn(turns - 1, 0)

            @block.vector
            def _(dve):
                v = nc.vector
                dve.sem_inc(freed, 2)

                def turn(i, w, h):
                    c = Chain(dve, chain, i * 3)
                    dve.wait_ge(got[h], w * (32 * U) + 32 * U)
                    c.link(v.tensor_tensor(t[:, :, :], hg[:, h, :, 16:20], dg[:, h, :, 20:24], ALU.add))
                    v.tensor_copy(rows[:, ds(i * U, U), :], hg[:, h, :, 0:16])
                    c.link(v.scalar_tensor_tensor(out=score[:, ds(i * U, U), :], in0=t[:, :, :], scalar=0.2, in1=t[:, :, :],
                                                  op0=ALU.mult, op1=ALU.max))
                    dve.sem_inc(freed, 1)
                    c.n += 1
                    dve.sem_inc(chain, 1)
                with dve.Fori(0, turns // 2) as w:
                    turn(w * 2, w, 0)
                    turn(w * 2 + 1, w, 1)
                turn(turns - 1, turns // 2, 0)
                v.memset(score[:, T2:G2 * P, :], 0.0).then_inc(took, 1)
                dve.wait_ge(took, 1)


def gate_sums(nc, k, e, rows, weight, acc):
    W = 16 + H2
    turns = T2 // U
    with Scope(nc) as s:
        msg = s.sb("gu_msg", [P, 2, U, W])
        hot = s.sb("gu_hot", [P, 2, U, P])
        ps = [s.ps(f"gu_ps{u}", [P, 512]) for u in range(U)]
        built, summed, added = (s.sem("gu_" + q) for q in ("built", "summed", "added"))
        with nc.Block() as block:
            @block.tensor
            def _(pe):
                def turn(i, h):
                    pe.wait_ge(built, i + 1)
                    for u in range(U):
                        pe.wait_ge(added, i * U + (u + 1))
                        nc.tensor.matmul(ps[u][:, 0:W], hot[:, h, u, :], msg[:, h, u, :], start=True, stop=True).then_inc(summed, 1)
                with pe.Fori(0, turns // 2) as w:
                    turn(w * 2, 0)
                    turn(w * 2 + 1, 1)
                turn(turns - 1, 0)

            @block.vector
            def _(dve):
                v = nc.vector
                dve.sem_inc(added, U)

                def build(i, h):
                    v.tensor_tensor(hot[:, h], wide(k.count_row[:, 0:P].unsqueeze(1), [P, U, P]),
                                    wide(e.rel[:, ds(i * U, U)].unsqueeze(2), [P, U, P]), ALU.is_equal)
                    v.tensor_copy(msg[:, h, :, 16:W], weight[:, ds(i * U, U), :])
                    v.tensor_tensor(msg[:, h, :, 0:16].rearrange("p u (g d) -> p u g d", d=NX),
                                    rows[:, ds(i * U, U), :].rearrange("p u (g d) -> p u g d", d=NX),
                                    wide(weight[:, ds(i * U, U), :].unsqueeze(3), [P, U, H2, NX]), ALU.mult).then_inc(built, 1)

                def add(i):
                    for u in range(U):
                        b = block_of(dve, e, i * U + u)
                        dve.wait_ge(summed, i * U + (u + 1))
                        dve.wait_ge(added, i * U + (u + U))
                        dve.wait_ge(k.armed, 1)
                        v.tensor_tensor(acc[:, ds(b, 1), :].rearrange("p a w -> p (a w)"),
                                        acc[:, ds(b, 1), :].rearrange("p a w -> p (a w)"),
                                        ps[u][:, 0:W], ALU.add).then_inc(added, 1)
                build(0, 0)
                with dve.Fori(0, turns // 2) as w:
                    build(w * 2 + 1, 1)
                    add(w * 2)
                    build(w * 2 + 2, 0)
                    add(w * 2 + 1)
                add(turns - 1)
                dve.wait_ge(added, T2 + U)


def top_two(nc, k, acc, row_cols, gates):
    with Scope(nc) as s:
        S16, S4 = [P, NB, 16], [P, NB, NX]
        t = s.sb("tt_t", [P, 3, NB, 16])
        q = s.sb("tt_q", [P, 8, NB, NX])
        r = s.sb("tt_r", [P, 10, NB])
        chain, ask, ans = s.sem("tt_chain"), s.sem("tt_ask"), s.sem("tt_ans")
        with nc.Block() as block:
            @block.scalar
            def _(act):
                act.wait_ge(ask, 1)
                nc.scalar.activation(r[:, 3], r[:, 2], ACT.Sqrt).then_inc(ans, 1)
                act.wait_ge(ask, 2)
                nc.scalar.activation(r[:, 7], r[:, 6], ACT.Exp).then_inc(ans, 1)

            @block.vector
            def _(dve):
                v = nc.vector
                c = Chain(dve, chain)
                row = lambda j: wide(row_cols[:, 16 * j:16 * j + 16].unsqueeze(1), S16)
                c.link(v.tensor_scalar(q[:, 0], acc[:, :, 16:20], 1e-16, None, ALU.add))
                c.link(v.reciprocal(q[:, 1], q[:, 0]))
                c.link(v.tensor_tensor(t[:, 0].rearrange("p b (h e) -> p b h e", e=NX),
                                       acc[:, :, 0:16].rearrange("p b (h e) -> p b h e", e=NX),
                                       wide(q[:, 1].unsqueeze(3), [P, NB, H2, NX]), ALU.mult))
                c.link(v.tensor_tensor(t[:, 0], t[:, 0], row(2), ALU.add))
                c.link(v.tensor_reduce(r[:, 0], t[:, 0], AX.X, ALU.add))
                c.link(v.tensor_scalar(r[:, 0], r[:, 0], 1.0 / 16, None, ALU.mult))
                c.link(v.tensor_tensor(t[:, 0], t[:, 0], wide(r[:, 0].unsqueeze(2), S16), ALU.subtract))
                c.link(v.tensor_tensor(t[:, 1], t[:, 0], t[:, 0], ALU.mult))
                c.link(v.tensor_reduce(r[:, 1], t[:, 1], AX.X, ALU.add))
                c.link(v.tensor_scalar(r[:, 1], r[:, 1], 1.0 / 16, EPS, ALU.mult, ALU.add))
                v.reciprocal(r[:, 2], r[:, 1]).then_inc(ask, 1)
                dve.wait_ge(ans, 1)
                c.link(v.tensor_tensor(t[:, 0], t[:, 0], wide(r[:, 3].unsqueeze(2), S16), ALU.mult))
                c.link(v.tensor_tensor(t[:, 0], t[:, 0], row(3), ALU.mult))
                c.link(v.tensor_tensor(t[:, 0], t[:, 0], row(4), ALU.add))
                c.link(v.tensor_reduce(q[:, 2], t[:, 0].rearrange("p b (h e) -> p b e h", e=NX), AX.X, ALU.add))
                c.link(v.tensor_scalar(q[:, 2], q[:, 2], 1.0 / H2, None, ALU.mult))
                count = wide(k.count_row[:, 0:NX].unsqueeze(1), S4)

                def first_best(score, best, hot, tmp):
                    c.link(v.tensor_reduce(best, score, AX.X, ALU.max))
                    c.link(v.tensor_tensor(tmp, score, wide(best.unsqueeze(2), S4), ALU.is_lt))
                    c.link(v.scalar_tensor_tensor(out=tmp, in0=tmp, scalar=100.0, in1=count, op0=ALU.mult, op1=ALU.add))
                    c.link(v.tensor_reduce(r[:, 8], tmp, AX.X, ALU.min))
                    c.link(v.tensor_tensor(hot, tmp, wide(r[:, 8].unsqueeze(2), S4), ALU.is_equal))
                first_best(q[:, 2], r[:, 4], q[:, 3], q[:, 5])
                c.link(v.scalar_tensor_tensor(out=q[:, 6], in0=q[:, 3], scalar=LOW, in1=q[:, 2], op0=ALU.mult, op1=ALU.add))
                first_best(q[:, 6], r[:, 5], q[:, 4], q[:, 5])
                v.tensor_tensor(r[:, 6], r[:, 5], r[:, 4], ALU.subtract).then_inc(ask, 1)
                dve.wait_ge(ans, 2)
                c.link(v.tensor_scalar(r[:, 8], r[:, 7], 1.0, None, ALU.add))
                c.link(v.reciprocal(r[:, 9], r[:, 8]))
                c.link(v.tensor_tensor(r[:, 7], r[:, 7], r[:, 9], ALU.mult))
                v.tensor_tensor(q[:, 3], q[:, 3], wide(r[:, 9].unsqueeze(2), S4), ALU.mult)
                c.link(v.tensor_tensor(q[:, 4], q[:, 4], wide(r[:, 7].unsqueeze(2), S4), ALU.mult))
                c.link(v.tensor_tensor(gates[:, :, :], q[:, 3], q[:, 4], ALU.add))


def experts1(nc, k, a, xnT, gates):
    FC = FX // P
    HALF = B5 * P // 2
    with Scope(nc) as s:
        w1 = s.sb("x1_w1", [P, NX, KC, FX])
        w2 = s.sb("x1_w2", [P, NX, FC, D])
        b1 = s.sb("x1_b1", [P, NX, FC])
        b2 = s.sb("x1_b2", [1, NX, D])
        hid = s.sb("x1_hid", [P, 2, FC, B5 * P])
        ps_h = [s.ps(f"x1_h{j}", [P, 512]) for j in range(4)]
        ps_y = [s.ps(f"x1_y{j}", [P, 512]) for j in range(4)]
        got, h_done, h_kept, y_done, added = (s.sem("x1_" + q) for q in ("got", "h_done", "h_kept", "y_done", "added"))
        NH_ = 2 * FC * NX
        NY_ = B5 * NX
        with nc.Block() as block:
            @block.sync
            def _(sp):
                for e in range(NX):
                    sp.dma_start(w1[:, e], a["L1_ffn_W1"][e].rearrange("(c p) f -> p c f", p=P)).then_inc(got, 16)
                    sp.dma_start(w2[:, e], a["L1_ffn_W2"][e].rearrange("(c p) f -> p c f", p=P)).then_inc(got, 16)
                sp.dma_start(b1[:, :, :], a["L1_ffn_b1"].rearrange("e (c p) -> p e c", p=P), allow_slow_non_contiguous=True).then_inc(got, 16)
                sp.dma_start(b2[:, :, :], a["L1_ffn_b2"].rearrange("(a e) d -> a e d", a=1)).then_inc(got, 16)
                sp.wait_ge(got, 160)

            @block.tensor
            def _(pe):
                pe.wait_ge(got, 160)
                with pe.Fori(0, NB // B5) as i:
                    for e in range(NX):
                        for f in range(FC):
                            for half in range(2):
                                n = (e * FC + f) * 2 + half
                                pe.wait_ge(h_kept, i * NH_ + (n + 1))
                                for c in range(KC):
                                    ins = nc.tensor.matmul(ps_h[n % 4][:, 0:HALF], w1[:, e, c, f * P:(f + 1) * P],
                                                           xnT[:, c:c + 1, ds(i * (B5 * P) + half * HALF, HALF)].rearrange("p a t -> p (a t)"),
                                                           start=(c == 0), stop=(c == KC - 1))
                                ins.then_inc(h_done, 1)
                        pe.wait_ge(h_kept, i * NH_ + ((e + 1) * 2 * FC + 4))
                        for j in range(B5):
                            n = e * B5 + j
                            pe.wait_ge(added, i * NY_ + (n + 1))
                            nc.tensor.matmul(ps_y[n % 4][:, 0:D], k.ones[0:1, :], b2[:, e, :], start=True, stop=False)
                            for f in range(FC):
                                ins = nc.tensor.matmul(ps_y[n % 4][:, 0:D], hid[:, e % 2, f, j * P:(j + 1) * P], w2[:, e, f, :],
                                                       start=False, stop=(f == FC - 1))
                            ins.then_inc(y_done, 1)

            @block.scalar
            def _(act):
                act.sem_inc(h_kept, 4)
                with act.Fori(0, NB // B5) as i:
                    for e in range(NX):
                        for f in range(FC):
                            for half in range(2):
                                n = (e * FC + f) * 2 + half
                                act.wait_ge(h_done, i * NH_ + (n + 1))
                                nc.scalar.activation(hid[:, e % 2, f, half * HALF:(half + 1) * HALF], ps_h[n % 4][:, 0:HALF], ACT.Gelu,
                                                     bias=b1[:, e, f:f + 1]).then_inc(h_kept, 1)

            @block.vector
            def _(dve):
                v = nc.vector
                dve.sem_inc(added, 4)
                with dve.Fori(0, NB // B5) as i:
                    for e in range(NX):
                        for j in range(B5):
                            n = e * B5 + j
                            b = i * B5 + j
                            xb = k.X[:, ds(b, 1), :].rearrange("p a d -> p (a d)")
                            dve.wait_ge(y_done, i * NY_ + (n + 1))
                            dve.wait_ge(added, i * NY_ + (n + 1))
                            dve.wait_ge(k.armed, 1)
                            v.scalar_tensor_tensor(out=xb, in0=ps_y[n % 4][:, 0:D],
                                                   scalar=gates[:, ds(b, 1), e:e + 1].rearrange("p a b -> p (a b)"),
                                                   in1=xb, op0=ALU.mult, op1=ALU.add).then_inc(added, 1)
                dve.wait_ge(added, (NB // B5) * NY_ + 4)


def store(nc, k, out):
    with Scope(nc) as s:
        stored = s.sem("stored")
        with nc.Block() as block:
            @block.sync
            def _(sp):
                sp.dma_start(out[0:(NB - 1) * P, :].rearrange("(b p) d -> p b d", p=P), k.X[:, 0:NB - 1, :]).then_inc(stored, 16)
                sp.dma_start(out[(NB - 1) * P:N, :], k.X[0:LAST, NB - 1, :]).then_inc(stored, 16)
                sp.wait_ge(stored, 32)


class Kept:

    def __init__(self, s):
        self.ident = s.sb("ident", [P, P])
        self.ones = s.sb("ones", [P, P])
        self.upper = s.sb("upper", [P, P])
        self.count_row = s.sb("count_row", [P, 512])
        self.count_col = s.sb("count_col", [P, 4])
        self.armed_dummy = s.sb("armed_dummy", [P, 1])
        self.node_id = s.sb("node_id", [P, NB])
        self.node_mask = s.sb("node_mask", [P, NB])
        self.X = s.sb("X", [P, NB, D])
        self.rstd = s.sb("rstd", [P, NB])
        self.shift = s.sb("shift", [P, NB])
        self.W0 = s.sb("W0", [P, KC, 4 * D])
        self.bias0 = s.sb("bias0", [1, 5 * D])
        self.mix_q = s.sb("mix_q", [P, 4, D])
        self.mix_kvT = s.sb("mix_kvT", [P, KC, 1024])
        self.mix_outT = s.sb("mix_outT", [P, 4, D])
        self.dotsT = s.sb("dotsT", [P, 4, P])
        self.gate = s.sb("gate", [P, KC, NE])
        self.gate_b = s.sb("gate_b", [1, NE])
        self.fc_q = s.sb("fc_q", [P, KC, D])
        self.bias1 = s.sb("bias1", [1, 3 * D])
        self.bq_col = s.sb("bq_col", [P, KC])
        self.gat_w = s.sb("gat_w", [P, KC, 16])
        self.gat_rows = s.sb("gat_rows", [1, 80])
        self.fcT = [s.sb(f"fcT{j}", [P, KC, D]) for j in range(3)]


class Graph:

    def __init__(self, s, name, groups):
        self.valid, self.starts, self.ends = (s.sb(name + x, [P, groups, P]) for x in ("valid", "starts", "ends"))
        self.rel = s.sb(name + "rel", [P, groups * P])
        self.src, self.dst = (s.sb(name + x, [P, groups * P], I32) for x in ("src", "dst"))
        self.block_row = s.sb(name + "block_row", [1, groups * P], I32)
        self.chunk = s.sb(name + "chunk", [P, groups], I32)


def program(nc, a, out):
    with Scope(nc) as s:
        k = Kept(s)
        k.armed = nc.alloc_semaphore("armed")
        Scope.used.clear()

        def dram(name, shape, dt=F32):
            return nc.dram_tensor(name, shape, dt, kind="Internal").ap()

        def steps(e, name, pairs, chunks, groups, n):
            build_steps(nc, k, name, pairs, chunks, groups, n, e.valid, e.starts, e.ends, e.rel, e.src, e.dst,
                        e.block_row, e.chunk)

        def cleared(scope, name, shape):
            acc, done = scope.sb(name, shape), scope.sem(name + "_cleared")
            with nc.Block() as block:
                @block.vector
                def _(dve):
                    nc.vector.memset(acc[:, :, :], 0.0).then_inc(done, 1)
                    dve.wait_ge(done, 1)
            return acc

        q_tab, k_tab, v_tab, x_tab = (dram(n + "_tab", [NPAD, D]) for n in "qkvx")
        h_tab = dram("h_tab", [NPAD, GW])
        slots, slots_out = dram("expert_rows", [SLOTS + NPAD, D]), dram("expert_out", [SLOTS, D])
        make_constants(nc, k)
        load_all(nc, k, a)
        e1 = Graph(s, "e1_", G1)
        steps(e1, "s1_", a["pairs"], C1, G1, T1)

        layer_stats(nc, k, "n0_")
        project0(nc, k, q_tab, k_tab, v_tab)
        mixer_matrix0(nc, k)
        with Scope(nc) as t:
            acc = cleared(t, "acc0", [P, NB, D + H1])
            with Scope(nc) as t2:
                score = t2.sb("score1", [P, G1 * P, H1])
                edge_scores(nc, k, e1, q_tab, k_tab, score)
                segment_softmax(nc, k, "m1_", G1, H1, score, e1.valid, e1.starts, e1.ends, float((D // H1) ** -0.5))
                attend(nc, k, e1, v_tab, score, acc)
            combine0(nc, k, acc)
        layer_stats(nc, k, "n1_")
        with Scope(nc) as t:
            XN = t.sb("XN", [P, NB, D])
            logits = t.sb("logits", [P, NB, NE])
            slot_i = t.sb("slot_i", [P, NB], I32)
            factor = t.sb("factor", [P, NB])
            gate0(nc, k, XN, logits)
            route0(nc, k, XN, logits, slots, slot_i, factor)
            experts0(nc, k, a, slots, slots_out)
            return0(nc, k, slots_out, slot_i, factor)

        recycle_semaphores(nc)

        layer_stats(nc, k, "n2_")
        with Scope(nc) as t:
            G = t.sb("G", [P, KC, D])
            g_bias = t.sb("g_bias", [1, D])
            with Scope(nc) as t2:
                sums = t2.sb("sums", [P, 3, D + 1])
                gram1(nc, k, x_tab, sums)
                mixer_matrix1(nc, k, sums, G, g_bias)
            acc = cleared(t, "acc1", [P, NB, 512])
            with Scope(nc) as t2:
                factors = t2.sb("factors", [P, G1 * P, 4])
                edge_factors(nc, k, a, a["attr"], a["emb_t"], e1, factors, 128.0 ** -0.5 * 16.0 ** -0.5)
                convolve(nc, k, e1, x_tab, factors, acc)
            combine1(nc, k, a, acc, G, g_bias)

        pairs2 = dram("pairs2", [(C2 + 1) * P, 2], I32)
        sort_edges(nc, k, a["L1_ffn_edge_index"], pairs2)
        e2 = Graph(s, "e2_", G2)
        steps(e2, "s2_", pairs2, C2, G2, T2)
        layer_stats(nc, k, "n3_")
        xnT = s.sb("xnT", [P, KC, NPAD])
        row_cols = s.sb("row_cols", [P, 80])
        gates = s.sb("gates", [P, NB, NX])
        gate_rows(nc, k, h_tab, xnT, row_cols)
        with Scope(nc) as t:
            acc = cleared(t, "acc2", [P, NB, 16 + H2])
            rows = t.sb("gate_edge_rows", [P, G2 * P, 16])
            score = t.sb("score2", [P, G2 * P, H2])
            gate_scores(nc, k, e2, h_tab, rows, score)
            segment_softmax(nc, k, "m2_", G2, H2, score, e2.valid, e2.starts, e2.ends, 1.0)
            gate_sums(nc, k, e2, rows, score, acc)
            top_two(nc, k, acc, row_cols, gates)
        experts1(nc, k, a, xnT, gates)
        store(nc, k, out)


_PLAIN = ["x", "L0_gnn_Wq", "L0_gnn_bq", "L0_gnn_Wk", "L0_gnn_bk", "L0_gnn_Wv", "L0_gnn_bv", "L0_gnn_Ws", "L0_gnn_bs",
          "L0_mix_Wqkv", "L0_mix_Wout", "L0_mix_bout", "L0_ffn_gate_w", "L0_ffn_gate_b", "L0_ffn_w1", "L0_ffn_b1", "L0_ffn_w2",
          "L0_ffn_b2", "L1_gnn_w_00_0", "L1_gnn_w_11_0", "L1_gnn_w_01_1", "L1_gnn_w_10_1", "L1_gnn_fc_w1", "L1_gnn_fc_w2",
          "L1_mix_Wq", "L1_mix_bq", "L1_mix_Wk", "L1_mix_bk", "L1_mix_Wv", "L1_mix_bv", "L1_mix_Wfc", "L1_mix_bfc",
          "L1_ffn_W_gat", "L1_ffn_att_src", "L1_ffn_att_dst", "L1_ffn_b_gat", "L1_ffn_ln_gamma", "L1_ffn_ln_beta",
          "L1_ffn_W1", "L1_ffn_b1", "L1_ffn_W2", "L1_ffn_b2", "L1_ffn_edge_index"]


def kernel(**inputs):
    import numpy as np
    import concourse.bacc as bacc
    from concourse.bass_utils import run_bass_kernel_spmd

    arrays = {n: np.ascontiguousarray(inputs[n]) for n in _PLAIN}
    dst, src = np.asarray(inputs["dst"]), np.asarray(inputs["src"])
    pairs = np.full(((C1 + 1) * P, 2), NONODE, dst.dtype)
    pairs[:, 1] = 0
    pairs[0, 0] = -1
    pairs[1:E1 + 1, 0] = dst
    pairs[1:E1 + 1, 1] = src
    arrays["pairs"] = pairs
    attr = np.zeros((C1 * P, 4), np.float32)
    attr[:E1] = np.asarray(inputs["edge_attr_4"])
    arrays["attr"] = np.ascontiguousarray(attr.reshape(C1, P, 4).transpose(1, 0, 2))
    emb = np.zeros((10, C1 * P), np.float32)
    emb[:, :E1] = np.asarray(inputs["edge_attr_10"]).T
    arrays["emb_t"] = emb

    nc = bacc.Bacc("TRN2", target_bir_lowering=False, num_devices=1)
    a = {n: nc.dram_tensor(f"in_{n}", list(v.shape), mybir.dt.from_np(v.dtype), kind="ExternalInput").ap()
         for n, v in arrays.items()}
    out = nc.dram_tensor("out", [N, D], F32, kind="ExternalOutput").ap()
    program(nc, a, out)
    r = run_bass_kernel_spmd(nc, [{f"in_{n}": v for n, v in arrays.items()}], core_ids=[0])
    return r.results[0]["out"]
```

```python
from contextlib import ExitStack

import concourse.bass as bass
from concourse import mybir
from concourse.bass import ds

F32 = mybir.dt.float32
I32 = mybir.dt.int32
BF = mybir.dt.bfloat16
ALU = mybir.AluOpType
ACT = mybir.ActivationFunctionType
AX = mybir.AxisListType

P = 128
N = 3125
D = 256
NB = (N + P - 1) // P
NPAD = NB * P
LAST = N - (NB - 1) * P
KC = D // P
EPS = 1e-5
LOW = -1.0e30
RESET = -1.0e32
NONODE = NPAD

E1 = 53125
C1 = (E1 + P - 1) // P
U = 8
T1 = C1 + NB - 1
G1 = (T1 + P - 1) // P
H1 = 8
EG = 32768
CG = EG // P
C2 = (CG + NB + U - 1) // U * U
T2 = C2 + NB - 1
G2 = (T2 + P - 1) // P
NH = NB + 1
H2 = 4
assert T1 % U == 0 and T2 % U == 0

NE = 8
FE = 1024
CAP = -(-5 * N // (4 * NE))
SLOTS = NE * CAP
NX = 4
FX = 512
MH = 16
DH = 64


class Chain:

    def __init__(self, eng, sem, base=0):
        self.eng, self.sem, self.base, self.n = eng, sem, base, 0

    def link(self, ins):
        self.n += 1
        ins.then_inc(self.sem, 1)
        self.eng.wait_ge(self.sem, self.base + self.n)


class Scope:

    def __init__(self, nc):
        self.nc, self.stack = nc, ExitStack()

    def __enter__(self):
        self.stack.__enter__()
        return self

    def __exit__(self, *a):
        return self.stack.__exit__(*a)

    def sb(self, name, shape, dt=F32):
        return self.stack.enter_context(self.nc.sbuf_tensor(name, shape, dt))

    def ps(self, name, shape, dt=F32):
        return self.stack.enter_context(self.nc.psum_tensor(name, shape, dt))

    def sem(self, name):
        sem = self.nc.alloc_semaphore(name)
        Scope.used.append(sem)
        return sem

    used = []


def recycle_semaphores(nc):
    nc.clear_and_free_semaphores(list(Scope.used))
    Scope.used.clear()
    nc.all_engine_barrier()


def wide(ap, shape):
    return ap.to_broadcast(shape)


def make_constants(nc, k):
    with Scope(nc) as s:
        made = s.sem("constants_made")
        with nc.Block() as block:
            @block.gpsimd
            def _(pool):
                nc.gpsimd.memset(k.ident[:, :], 0.0).then_inc(made, 1)
                nc.gpsimd.memset(k.ones[:, :], 1.0).then_inc(made, 1)
                nc.gpsimd.memset(k.ones_h[:, :], 1.0).then_inc(made, 1)
                nc.gpsimd.memset(k.upper[:, :], 1.0).then_inc(made, 1)
                nc.gpsimd.iota(k.count_row[:, :], [[1, 512]], base=0, channel_multiplier=0,
                               allow_small_or_imprecise_dtypes=True).then_inc(made, 1)
                nc.gpsimd.iota(k.count_col[:, :], [[P, 4]], base=0, channel_multiplier=1,
                               allow_small_or_imprecise_dtypes=True).then_inc(made, 1)
                nc.gpsimd.memset(k.armed_dummy[:, :], 0.0).then_inc(k.armed, 1)
                pool.wait_ge(made, 6)
                nc.gpsimd.affine_select(out=k.ident[:, :], in_=k.ident[:, :], compare_op=ALU.not_equal, fill=1.0,
                                        base=0, pattern=[[-1, P]], channel_multiplier=1).then_inc(made, 1)
                nc.gpsimd.affine_select(out=k.upper[:, :], in_=k.upper[:, :], compare_op=ALU.is_gt, fill=0.0,
                                        base=0, pattern=[[1, P]], channel_multiplier=-1).then_inc(made, 1)
                nc.gpsimd.iota(k.node_id[:, :], [[P, NB]], base=0, channel_multiplier=1,
                               allow_small_or_imprecise_dtypes=True).then_inc(made, 1)
                pool.wait_ge(made, 9)

            @block.vector
            def _(dve):
                v = nc.vector
                dve.wait_ge(made, 9)
                nc.vector.tensor_scalar(k.node_mask[:, :], k.node_id[:, :], float(N), None, ALU.is_lt).then_inc(made, 1)
                v.tensor_copy(k.ident_h[:, :], k.ident[:, :]).then_inc(made, 1)
                dve.wait_ge(made, 11)


def build_steps(nc, k, name, pairs, chunks, groups, steps, valid, starts, ends, rel, src, rel_rows, block_row, chunk_i):
    flat = pairs.rearrange("a b -> (a b)")
    windows = flat.rearrange("(c w) -> c w", w=2 * P)
    with Scope(nc) as s:
        last_i = s.sb(name + "last_i", [1, chunks], I32)
        last_b = s.sb(name + "last_b", [1, chunks], I32)
        end_step = s.sb(name + "end_step", [1, chunks])
        below = s.sb(name + "below", [P, groups, chunks])
        cut = s.sb(name + "cut", [P, 8, groups])
        block_i = s.sb(name + "block_i", [P, groups], I32)
        edges = [s.sb(name + f"edges{j}", [P, groups, P, 2], I32) for j in range(3)]
        here = s.sb(name + "here", [P, 2, groups, P])
        near = s.sb(name + "near", [P, 2, groups, P])
        rel_t = s.sb(name + "rel_t", [P, groups, P])
        rel_h = s.sb(name + "rel_h", [P, groups, P], BF)
        tmp = s.sb(name + "tmp", [P, groups, P])
        wide_end = s.ps(name + "wide_end", [P, 512])
        turned = [s.ps(name + f"turned{j}", [P, 512]) for j in range(2)]
        block_dram = nc.dram_tensor(name + "block_of_step", [groups * P], I32, kind="Internal").ap()
        loaded, cmp_done, spread, ready, got, chain, flipped, bdone = (
            s.sem(name + x) for x in ("loaded", "cmp_done", "spread", "ready", "got", "chain", "flipped", "bdone"))
        with nc.Block() as block:
            @block.sync
            def _(sp):
                sp.dma_start(last_i[:, :], pairs[P:chunks * P + 1:P, 0:1].rearrange("c b -> b c"),
                             allow_slow_non_contiguous=True).then_inc(loaded, 16)
                sp.wait_ge(ready, 2)
                sp.dma_start(block_dram.rearrange("(g p) -> p g", p=P), block_i[:, :],
                             allow_slow_non_contiguous=True).then_inc(bdone, 16)
                sp.wait_ge(bdone, 16)
                sp.dma_start(block_row[:, 0:groups * P], block_dram.rearrange("(a n) -> a n", a=1)).then_inc(bdone, 16)
                sp.wait_ge(ready, 3)
                sp.dma_start(rel_rows.rearrange("(g p) e -> p g e", p=P), rel_h[:, :, :]).then_inc(bdone, 16)
                sp.wait_ge(bdone, 48)

            @block.tensor
            def _(pe):
                pe.wait_ge(cmp_done, 1)
                nc.tensor.matmul(wide_end[:, 0:chunks], k.ones[0:1, :], end_step[:, :], start=True, stop=True).then_inc(spread, 1)
                pe.wait_ge(cmp_done, 2)
                for j, x in enumerate((rel_t, here[:, 1])):
                    for g in range(groups):
                        ins = nc.tensor.transpose(turned[j][:, g * P:(g + 1) * P], x[:, g, :], k.ident[:, :])
                    ins.then_inc(flipped, 1)

            @block.gpsimd
            def _(pool):
                pool.wait_ge(ready, 1)
                for g in range(groups):
                    for j in range(3):
                        nc.gpsimd.indirect_dma_start(
                            out=edges[j][:, g].rearrange("p e b -> p (e b)"), out_offset=None, in_=windows,
                            in_offset=bass.IndirectOffsetOnAxis(ap=chunk_i[:, g:g + 1], axis=0),
                            element_offset=2 * j).then_inc(got, 16)

            @block.vector
            def _(dve):
                c = Chain(dve, chain)
                v = nc.vector
                dve.wait_ge(loaded, 16)
                c.link(v.tensor_scalar(last_b[:, :], last_i[:, :], 7, None, ALU.arith_shift_right))
                c.link(v.tensor_copy(end_step[:, :], last_b[:, :]))
                c.link(v.tensor_scalar(end_step[:, :], end_step[:, :], float(NB - 1), None, ALU.min))
                v.tensor_tensor(end_step[:, :], end_step[:, :], k.count_row[0:1, 0:chunks], ALU.add).then_inc(cmp_done, 1)
                dve.wait_ge(spread, 1)
                c.link(v.tensor_tensor(below[:, :, :], wide(wide_end[:, 0:chunks].unsqueeze(1), [P, groups, chunks]),
                                       wide(k.count_col[:, 0:groups].unsqueeze(2), [P, groups, chunks]), ALU.is_lt))
                c.link(v.tensor_reduce(cut[:, 0], below[:, :, :], AX.X, ALU.add))
                c.link(v.tensor_scalar(cut[:, 1], cut[:, 0], float(chunks - 1), None, ALU.min))
                v.tensor_copy(chunk_i[:, :], cut[:, 1]).then_inc(ready, 1)
                c.link(v.tensor_tensor(cut[:, 2], k.count_col[:, 0:groups], cut[:, 0], ALU.subtract))
                c.link(v.tensor_scalar(cut[:, 3], cut[:, 2], float(NB - 1), None, ALU.min))
                v.tensor_copy(block_i[:, :], cut[:, 3]).then_inc(ready, 1)
                c.link(v.tensor_scalar(cut[:, 4], cut[:, 0], float(chunks), 1.0e6, ALU.is_ge, ALU.mult))
                c.link(v.scalar_tensor_tensor(out=cut[:, 5], in0=cut[:, 2], scalar=float(P), in1=cut[:, 4],
                                              op0=ALU.mult, op1=ALU.add))
                dve.wait_ge(got, 48 * groups)
                v.tensor_copy(near[:, 0], edges[0][:, :, :, 0])
                v.tensor_copy(near[:, 1], edges[2][:, :, :, 0])
                v.tensor_copy(here[:, 1], edges[1][:, :, :, 1])
                c.link(v.tensor_copy(here[:, 0], edges[1][:, :, :, 0]))
                c.link(v.tensor_tensor(rel_t[:, :, :], here[:, 0], wide(cut[:, 5].unsqueeze(2), [P, groups, P]), ALU.subtract))
                v.tensor_copy(rel_h[:, :, :], rel_t[:, :, :]).then_inc(ready, 1)
                c.link(v.tensor_scalar(valid[:, :, :], rel_t[:, :, :], 0.0, None, ALU.is_ge))
                c.link(v.tensor_scalar(tmp[:, :, :], rel_t[:, :, :], float(P), None, ALU.is_lt))
                c.link(v.tensor_tensor(valid[:, :, :], valid[:, :, :], tmp[:, :, :], ALU.mult))
                for flags, j in ((starts, 0), (ends, 1)):
                    c.link(v.tensor_tensor(tmp[:, :, :], here[:, 0], near[:, j], ALU.not_equal))
                    c.link(v.scalar_tensor_tensor(out=flags[:, :, :], in0=tmp[:, :, :], scalar=RESET, in1=valid[:, :, :],
                                                  op0=ALU.mult, op1=ALU.mult))
                dve.sem_inc(cmp_done, 1)
                dve.wait_ge(flipped, 2)
                for j, x in enumerate((rel, src)):
                    c.link(v.tensor_copy(x[:, 0:groups * P], turned[j][:, 0:groups * P]))


def segment_softmax(nc, k, name, groups, heads, score, valid, starts, ends, scale):
    J = groups * heads // 4
    with Scope(nc) as s:
        x = s.sb(name + "x", [P, groups, heads, P])
        f = s.sb(name + "f", [P, groups, heads, P])
        b = s.sb(name + "b", [P, groups, heads, P])
        hole = s.sb(name + "hole", [P, groups, P])
        edge_val = s.sb(name + "edge_val", [P, groups, heads])
        edge_rst = s.sb(name + "edge_rst", [P, groups, heads])
        rst1 = s.sb(name + "rst1", [P, groups])
        carry = s.sb(name + "carry", [P, groups, heads])
        val_t = s.sb(name + "val_t", [heads, groups * P])
        rst_t = s.sb(name + "rst_t", [heads, groups * P])
        scan_t = s.sb(name + "scan_t", [heads, groups * P + 1])
        bank = [s.ps(name + f"bank{j}", [P, 4, P]) for j in range(min(J, 8))]
        assert J <= 8
        chain, turned, masked, summed, across, carried, back, final, expd, gone = (
            s.sem(name + q) for q in ("chain", "turned", "masked", "summed", "across", "carried", "back", "final", "expd", "gone"))
        with nc.Block() as block:
            @block.tensor
            def _(pe):
                for g in range(groups):
                    for h in range(heads):
                        q = g * heads + h
                        nc.tensor.transpose(bank[q // 4][:, q % 4, :], score[:, g * P:(g + 1) * P, h],
                                            k.ident[:, :]).then_inc(turned, 1)
                for way in range(2):
                    pe.wait_ge(summed, way + 1)
                    for g in range(groups):
                        nc.tensor.transpose(bank[0][0:heads, g, :], edge_val[:, g, :], k.ident[:, :])
                    for g in range(groups):
                        ins = nc.tensor.transpose(bank[1][0:heads, g, :], edge_rst[:, g, :], k.ident[:, :])
                    ins.then_inc(across, 1)
                    pe.wait_ge(carried, way + 1)
                    off = 0 if way == 0 else 1
                    for g in range(groups):
                        ins = nc.tensor.transpose(bank[2][:, 0, g * heads:(g + 1) * heads],
                                                  scan_t[:, off + g * P:off + (g + 1) * P],
                                                  k.ident[0:heads, 0:heads])
                    ins.then_inc(back, 1)
                pe.wait_ge(final, 1)
                for g in range(groups):
                    for h in range(heads):
                        q = g * heads + h
                        nc.tensor.transpose(bank[q // 4][:, q % 4, :], x[:, g, h, :], k.ident[:, :]).then_inc(turned, 1)

            @block.scalar
            def _(act):
                act.wait_ge(expd, 1)
                nc.scalar.activation(x[:, :, :, :], x[:, :, :, :], ACT.Exp, scale=scale).then_inc(gone, 1)

            @block.vector
            def _(dve):
                v = nc.vector
                c = Chain(dve, chain)
                c.link(v.tensor_scalar(hole[:, :, :], valid[:, :, :], 1.0, -LOW, ALU.subtract, ALU.mult))
                for q in range(J):
                    g, h0 = q * 4 // heads, q * 4 % heads
                    dve.wait_ge(turned, 4 * q + 4)
                    v.tensor_tensor(x[:, g, h0:h0 + 4, :], bank[q][:, :, :],
                                    wide(valid[:, g, :].unsqueeze(1), [P, 4, P]), ALU.mult).then_inc(masked, 1)
                for g in range(groups):
                    dve.wait_ge(masked, (g + 1) * heads // 4)
                    c.link(v.tensor_tensor(x[:, g], x[:, g], wide(hole[:, g, :].unsqueeze(1), [P, heads, P]), ALU.add))

                def scans(out, flags, data, way, initial):
                    for g in range(groups):
                        for h in range(heads):
                            o, r, a = out[:, g, h, :], flags[:, g, :], data[:, g, h, :]
                            if way:
                                o, r, a = o[:, ::-1], r[:, ::-1], a[:, ::-1]
                            ins = v.tensor_tensor_scan(o, r, a, LOW if initial is None else initial[:, g, h:h + 1],
                                                       ALU.add, ALU.max)
                    c.link(ins)

                for way, (out, flags, data) in enumerate(((f, starts, x), (b, ends, f))):
                    scans(out, flags, data, way, None)
                    at = P - 1 if way == 0 else 0
                    v.tensor_copy(edge_val[:, :, :], out[:, :, :, at])
                    c.link(v.tensor_reduce(rst1[:, :], flags[:, :, :], AX.X, ALU.min))
                    v.tensor_copy(edge_rst[:, :, :], wide(rst1[:, :].unsqueeze(2), [P, groups, heads])).then_inc(summed, 1)
                    dve.wait_ge(across, way + 1)
                    v.tensor_copy(val_t[:, :], bank[0][0:heads, 0:groups, :].rearrange("p a b -> p (a b)"))
                    c.link(v.tensor_copy(rst_t[:, :], bank[1][0:heads, 0:groups, :].rearrange("p a b -> p (a b)")))
                    n = groups * P
                    if way == 0:
                        v.memset(scan_t[:, 0:1], LOW)
                        v.tensor_tensor_scan(scan_t[:, 1:n + 1], rst_t[:, :], val_t[:, :], LOW, ALU.add, ALU.max).then_inc(carried, 1)
                    else:
                        v.memset(scan_t[:, n:n + 1], LOW)
                        v.tensor_tensor_scan(scan_t[:, 0:n][:, ::-1], rst_t[:, ::-1], val_t[:, ::-1], LOW,
                                             ALU.add, ALU.max).then_inc(carried, 1)
                    dve.wait_ge(back, way + 1)
                    c.link(v.tensor_copy(carry[:, :, :], bank[2][:, 0, 0:groups * heads].rearrange("p (g h) -> p g h", g=groups)))
                    scans(out, flags, data, way, carry)
                v.tensor_tensor(x[:, :, :, :], x[:, :, :, :], b[:, :, :, :], ALU.subtract).then_inc(expd, 1)
                dve.wait_ge(gone, 1)
                for g in range(groups):
                    ins = v.tensor_tensor(x[:, g], x[:, g], wide(valid[:, g, :].unsqueeze(1), [P, heads, P]), ALU.mult)
                ins.then_inc(final, 1)
                for q in range(J):
                    g, h0 = q * 4 // heads, q * 4 % heads
                    dve.wait_ge(turned, groups * heads + 4 * q + 4)
                    ins = v.tensor_copy(score[:, g * P:(g + 1) * P, h0:h0 + 4].rearrange("p t h -> p h t"), bank[q][:, :, :])
                c.link(ins)


def layer_stats(nc, k, name):
    with Scope(nc) as s:
        parts = s.sb(name + "parts", [P, NB, 6])
        t = s.sb(name + "t", [P, 4, NB])
        chain, inverse, rooted = s.sem(name + "chain"), s.sem(name + "inverse"), s.sem(name + "rooted")
        with nc.Block() as block:
            @block.scalar
            def _(act):
                act.wait_ge(inverse, 1)
                nc.scalar.activation(k.rstd[:, :], t[:, 1], ACT.Sqrt).then_inc(rooted, 1)

            @block.vector
            def _(dve):
                v = nc.vector
                with dve.Fori(0, NB) as b:
                    v.bn_stats(parts[:, ds(b, 1), :], k.X[:, ds(b, 1), :]).then_inc(chain, 1)
                dve.wait_ge(chain, NB)
                c = Chain(dve, chain, NB)
                c.link(v.tensor_tensor(t[:, 0], parts[:, :, 1], parts[:, :, 4], ALU.subtract))
                c.link(v.tensor_tensor(t[:, 0], t[:, 0], t[:, 0], ALU.mult))
                v.tensor_tensor(t[:, 3], parts[:, :, 1], parts[:, :, 4], ALU.add)
                c.link(v.tensor_tensor(t[:, 1], parts[:, :, 2], parts[:, :, 5], ALU.add))
                c.link(v.scalar_tensor_tensor(out=t[:, 2], in0=t[:, 0], scalar=D / 4.0, in1=t[:, 1], op0=ALU.mult, op1=ALU.add))
                c.link(v.tensor_scalar(t[:, 2], t[:, 2], 1.0 / D, EPS, ALU.mult, ALU.add))
                v.reciprocal(t[:, 1], t[:, 2]).then_inc(inverse, 1)
                dve.wait_ge(rooted, 1)
                c.link(v.tensor_tensor(k.rstd[:, :], k.rstd[:, :], k.node_mask[:, :], ALU.mult))
                c.link(v.scalar_tensor_tensor(out=k.shift[:, :], in0=t[:, 3], scalar=-0.5, in1=k.rstd[:, :],
                                              op0=ALU.mult, op1=ALU.mult))


def load_all(nc, k, a):
    with Scope(nc) as s:
        mix_kv = s.sb("mix_kv", [P, 8, D])
        mix_out = s.sb("mix_out", [P, KC, 512])
        fc = [s.sb(f"fc{j}", [P, KC, D]) for j in range(3)]
        bank = [s.ps(f"turn_bank{j}", [P, 512]) for j in range(8)]
        got_x, got_w, cleared, turned, kept = (s.sem(q) for q in ("got_x", "got_w", "cleared", "turned", "kept"))
        jobs = [(mix_kv[:, j, c * P:(c + 1) * P], k.mix_kvT[:, c, j * P:(j + 1) * P]) for c in range(KC) for j in range(8)]
        jobs += [(mix_out[:, j, c * P:(c + 1) * P], k.mix_outT[:, c, j * P:(j + 1) * P]) for c in range(4) for j in range(KC)]
        for t in range(3):
            jobs += [(fc[t][:, j, c * P:(c + 1) * P], k.fcT[t][:, c, j * P:(j + 1) * P]) for c in range(KC) for j in range(KC)]
        loads = [(k.W0[:, :, j * D:(j + 1) * D], a["L0_gnn_" + w].rearrange("(c p) f -> p c f", p=P))
                 for j, w in enumerate(("Wq", "Wk", "Wv", "Ws"))]
        loads += [(k.bias0[:, j * D:(j + 1) * D], a["L0_gnn_" + w].rearrange("(a f) -> a f", a=1))
                  for j, w in enumerate(("bq", "bk", "bv", "bs"))]
        loads += [(k.bias0[:, 4 * D:5 * D], a["L0_mix_bout"].rearrange("(a f) -> a f", a=1)),
                  (k.mix_q[:, :, :], a["L0_mix_Wqkv"][0:512, :].rearrange("(j p) c -> p j c", p=P)),
                  (mix_kv[:, :, :], a["L0_mix_Wqkv"][512:1536, :].rearrange("(j p) c -> p j c", p=P)),
                  (mix_out[:, :, :], a["L0_mix_Wout"].rearrange("(j p) f -> p j f", p=P)),
                  (k.gate[:, :, :], a["L0_ffn_gate_w"].rearrange("(c p) e -> p c e", p=P)),
                  (k.gate_b[:, :], a["L0_ffn_gate_b"].rearrange("(a f) -> a f", a=1)),
                  (k.fc_q[:, :, :], a["L1_mix_Wq"].rearrange("(j p) c -> p j c", p=P))]
        loads += [(fc[t][:, :, :], a["L1_mix_" + w].rearrange("(j p) c -> p j c", p=P)) for t, w in enumerate(("Wk", "Wv", "Wfc"))]
        loads += [(k.bias1[:, j * D:(j + 1) * D], a["L1_mix_" + w].rearrange("(a f) -> a f", a=1))
                  for j, w in enumerate(("bk", "bv", "bfc"))]
        loads += [(k.bq_col[:, :], a["L1_mix_bq"].rearrange("(c p) -> p c", p=P))]
        loads += [(k.gat_w[:, :, :], a["L1_ffn_W_gat"].rearrange("(c p) e -> p c e", p=P))]
        with nc.Block() as block:
            @block.sync
            def _(sp):
                sp.wait_ge(cleared, 1)
                sp.dma_start(k.X[:, 0:NB - 1, :], a["x"][0:(NB - 1) * P, :].rearrange("(b p) d -> p b d", p=P)).then_inc(got_x, 16)
                sp.dma_start(k.X[0:LAST, NB - 1, :], a["x"][(NB - 1) * P:N, :]).then_inc(got_x, 16)
                for to, of in loads:
                    sp.dma_start(to, of, allow_slow_non_contiguous=True).then_inc(got_w, 16)
                for j, w in enumerate(("att_src", "att_dst")):
                    sp.dma_start(k.gat_rows[:, j * 16:(j + 1) * 16],
                                 a["L1_ffn_" + w].rearrange("h e -> (h e)").rearrange("(a f) -> a f", a=1)).then_inc(got_w, 16)
                for j, w in enumerate(("b_gat", "ln_gamma", "ln_beta")):
                    sp.dma_start(k.gat_rows[:, (j + 2) * 16:(j + 3) * 16],
                                 a["L1_ffn_" + w].rearrange("(a f) -> a f", a=1)).then_inc(got_w, 16)
                sp.wait_ge(got_x, 32)
                sp.wait_ge(got_w, 16 * (len(loads) + 5))

            @block.tensor
            def _(pe):
                pe.wait_ge(got_w, 16 * (len(loads) + 5))
                for j, (x, _y) in enumerate(jobs):
                    if j >= 8:
                        pe.wait_ge(kept, j - 7)
                    nc.tensor.transpose(bank[j % 8][:, 0:P], x, k.ident[:, :]).then_inc(turned, 1)

            @block.vector
            def _(dve):
                nc.vector.memset(k.X[:, NB - 1, :], 0.0).then_inc(cleared, 1)
                for j, (_x, y) in enumerate(jobs):
                    dve.wait_ge(turned, j + 1)
                    nc.vector.tensor_copy(y, bank[j % 8][:, 0:P]).then_inc(kept, 1)


def normed_block(nc, k, act, b, slot, sem):
    nc.scalar.activation(slot, k.X[:, ds(b, 1), :].rearrange("p b d -> p (b d)"), ACT.Identity,
                         bias=k.shift[:, ds(b, 1)], scale=k.rstd[:, ds(b, 1)]).then_inc(sem, 1)


B5 = 5
assert NB % B5 == 0


def project0(nc, k, q_parts, k_tab, v_tab):
    PER = 5
    LASTT = NB // B5 - 1
    with Scope(nc) as s:
        xn = s.sb("p0_xn", [P, B5, D])
        xT = s.sb("p0_xT", [P, B5, KC, P])
        qkv = s.sb("p0_qkv", [P, B5, 3 * D])
        kv = s.sb("p0_kv", [P, B5, MH, DH])
        sq = s.sb("p0_sq", [P, MH, DH])
        st = s.sb("p0_st", [P, 3, MH])
        mean = s.sb("p0_mean", [P, KC, MH])
        zero = s.sb("p0_zero", [P, 512])
        rest = s.sb("p0_rest", [P, D])
        part = s.sb("p0_part", [P, 3, D], BF)
        ps_t = s.ps("p0_t", [P, KC, P])
        ps_a = s.ps("p0_a", [P, 512])
        ps_b = s.ps("p0_b", [P, 512])
        ps_m = s.ps("p0_m", [P, MH, DH])
        dots = s.ps("p0_dots", [P, 4, P])
        normed, turned, kept, ab_done, ab_used, m_done, squared, k_kept, heads, chain, zeroed, centred, dotted = (
            s.sem("p0_" + q) for q in ("normed", "turned", "kept", "ab_done", "ab_used", "m_done", "squared", "k_kept", "heads",
                                       "chain", "zeroed", "centred", "dotted"))
        inverse, rooted = s.sem("p0_inverse"), s.sem("p0_rooted")
        split, parted = s.sem("p0_split"), s.sem("p0_parted")
        out = [s.sem(f"p0_out{j}") for j in range(B5)]
        K8 = MH // 2
        with nc.Block() as block:
            @block.scalar
            def _(act):
                act.sem_inc(ab_used, 1)
                act.sem_inc(k_kept, 1)

                def norm(b, j):
                    act.wait_ge(turned, b + 1)
                    act.wait_ge(k.armed, 1)
                    normed_block(nc, k, act, b, xn[:, j, :], normed)

                def turn(i, first=False, last=False):
                    for j in range(B5):
                        b = i * B5 + j
                        if not (last and j == B5 - 1):
                            norm(b + 1, (j + 1) % B5)
                        if not first:
                            act.wait_ge(out[j], i * 32)
                        act.wait_ge(parted, b + 1)
                        act.wait_ge(ab_done, b + 1)
                        nc.scalar.activation(qkv[:, j, 0:512], ps_a[:, :], ACT.Copy)
                        nc.scalar.activation(qkv[:, j, 512:768], ps_b[:, 0:D], ACT.Copy).then_inc(ab_used, 1)
                        act.wait_ge(m_done, b + 1)
                        nc.scalar.activation(sq[:, :, :], ps_m[:, :, :], ACT.Square).then_inc(squared, 1)
                        nc.scalar.activation(kv[:, j, 0:K8, :], ps_m[:, 0:K8, :], ACT.Copy).then_inc(k_kept, 1)
                        act.wait_ge(inverse, b + 1)
                        nc.scalar.activation(st[:, 2, 0:K8], st[:, 1, 0:K8], ACT.Sqrt).then_inc(rooted, 1)
                norm(0, 0)
                turn(0, first=True)
                with act.Fori(1, LASTT) as i:
                    turn(i)
                turn(LASTT, last=True)

            @block.sync
            def _(sp):
                with sp.Fori(0, NB // B5) as i:
                    for j in range(B5):
                        b = i * B5 + j
                        sp.wait_ge(ab_used, b + 2)
                        for n, tab in enumerate((k_tab, v_tab)):
                            sp.dma_start(tab[ds(b * P, P), :], qkv[:, j, (n + 1) * D:(n + 2) * D]).then_inc(out[j], 16)
                for j in range(B5):
                    sp.wait_ge(out[j], 32 * (NB // B5))

            @block.gpsimd
            def _(pool):
                pool.sem_inc(parted, B5)
                pool.wait_ge(zeroed, 2)
                with pool.Fori(0, NB // B5) as i:
                    def link(n, ins):
                        ins.then_inc(split, 1)
                        pool.wait_ge(k.armed, 1)
                        pool.wait_ge(split, i * (5 * B5) + (n + 1))

                    for j in range(B5):
                        b = i * B5 + j
                        pool.wait_ge(k.armed, 1)
                        pool.wait_ge(ab_used, b + 2)
                        link(5 * j + 0, nc.gpsimd.tensor_tensor(part[:, 0, :], qkv[:, j, 0:D], zero[:, 0:D], ALU.subtract))
                        link(5 * j + 1, nc.gpsimd.tensor_tensor(rest[:, :], qkv[:, j, 0:D], part[:, 0, :], ALU.subtract))
                        link(5 * j + 2, nc.gpsimd.tensor_tensor(part[:, 1, :], rest[:, :], zero[:, 0:D], ALU.subtract))
                        link(5 * j + 3, nc.gpsimd.tensor_tensor(part[:, 2, :], rest[:, :], part[:, 1, :], ALU.subtract))
                        link(5 * j + 4, nc.gpsimd.tensor_copy(q_parts[:, ds(b, 1)].rearrange("p a n d -> p (a n) d"), part[:, :, :]))
                        pool.sem_inc(parted, 1)

            @block.tensor
            def _(pe):
                def turned_block(b, j):
                    pe.wait_ge(normed, b + 1)
                    pe.wait_ge(kept, b + 1)
                    for c in range(KC):
                        ins = nc.tensor.transpose(ps_t[:, c, :], xn[:, j, c * P:(c + 1) * P], k.ident[:, :])
                    ins.then_inc(turned, 1)

                def product(j):
                    for q in range(4):
                        ins = nc.tensor.matmul(dots[:, q, :], kv[:, j, 8 + 2 * q:10 + 2 * q, :].rearrange("p h d -> p (h d)"),
                                               kv[:, j, 2 * q:2 * q + 2, :].rearrange("p h d -> p (h d)"),
                                               start=False, stop=False, skip_group_check=True)
                    return ins

                def turn(i, last=False):
                    for j in range(B5):
                        b = i * B5 + j
                        pe.wait_ge(kept, b + 2)
                        pe.wait_ge(ab_used, b + 1)
                        for ps, lo, n in ((ps_a, 0, 512), (ps_b, 512, 256)):
                            nc.tensor.matmul(ps[:, 0:n], k.ones[0:1, :], k.bias0[:, lo:lo + n], start=True, stop=False)
                            for c in range(KC):
                                ins = nc.tensor.matmul(ps[:, 0:n], xT[:, j, c, :], k.W0[:, c, lo:lo + n],
                                                       start=False, stop=(c == KC - 1))
                        ins.then_inc(ab_done, 1)
                        if not (last and j == B5 - 1):
                            turned_block(b + 1, (j + 1) % B5)
                        pe.wait_ge(k_kept, b + 1)
                        pe.wait_ge(heads, b + 1)
                        for n in range(2):
                            for c in range(KC):
                                ins = nc.tensor.matmul(ps_m[:, 8 * n:8 * n + 8, :].rearrange("p h d -> p (h d)"), xT[:, j, c, :],
                                                       k.mix_kvT[:, c, n * 512:(n + 1) * 512], start=(c == 0), stop=(c == KC - 1))
                        ins.then_inc(m_done, 1)
                        product((j - 1) % B5)
                pe.sem_inc(turned, B5)
                pe.wait_ge(zeroed, 2)
                pe.wait_ge(centred, 3)
                nc.tensor.matmul(dots[:, :, :].rearrange("p a b -> p (a b)"), zero[:, 0:P], zero[:, :], start=True, stop=False,
                                 skip_group_check=True)
                turned_block(0, 0)
                with pe.Fori(0, LASTT) as i:
                    turn(i)
                turn(LASTT, last=True)
                pe.wait_ge(heads, NB + 1)
                pe.wait_ge(k_kept, NB + 1)
                product(B5 - 1).then_inc(dotted, 1)

            @block.vector
            def _(dve):
                v = nc.vector
                v.memset(zero[:, :], 0.0).then_inc(zeroed, 1)
                v.memset(kv[:, B5 - 1], 0.0).then_inc(zeroed, 1)
                dve.sem_inc(kept, 1)
                dve.sem_inc(heads, 1)
                heads_of = k.mix_kvT[:, :, :].rearrange("p c (h d) -> p c h d", d=DH)
                c = Chain(dve, centred)
                c.link(v.tensor_reduce(mean[:, :, :], heads_of, AX.X, ALU.add))
                c.link(v.tensor_scalar(mean[:, :, :], mean[:, :, :], 1.0 / DH, None, ALU.mult))
                c.link(v.tensor_tensor(heads_of, heads_of, wide(mean[:, :, :].unsqueeze(3), [P, KC, MH, DH]), ALU.subtract))
                dve.wait_ge(zeroed, 2)

                def keep(b, j):
                    dve.wait_ge(turned, b + B5 + 1)
                    v.tensor_copy(xT[:, j], ps_t[:, :, :]).then_inc(kept, 1)

                def turn(i, last=False):
                    c = Chain(dve, chain, i * (PER * B5))
                    for j in range(B5):
                        b = i * B5 + j
                        if not (last and j == B5 - 1):
                            keep(b + 1, (j + 1) % B5)
                        dve.wait_ge(squared, b + 1)
                        c.link(v.tensor_reduce(st[:, 0], sq[:, :, :], AX.X, ALU.add))
                        c.link(v.tensor_scalar(st[:, 0], st[:, 0], 1.0 / DH, EPS, ALU.mult, ALU.add))
                        c.link(v.reciprocal(st[:, 1], st[:, 0]))
                        c.link(v.tensor_tensor(st[:, 1, 0:K8], st[:, 1, 0:K8], st[:, 1, K8:MH], ALU.mult))
                        dve.sem_inc(inverse, 1)
                        dve.wait_ge(rooted, b + 1)
                        c.link(v.tensor_tensor(kv[:, j, K8:MH, :], ps_m[:, K8:MH, :], wide(st[:, 2, 0:K8].unsqueeze(2), [P, K8, DH]), ALU.mult))
                        dve.sem_inc(heads, 1)
                    assert c.n == PER * B5
                keep(0, 0)
                with dve.Fori(0, LASTT) as i:
                    turn(i)
                turn(LASTT, last=True)
                dve.wait_ge(dotted, 1)
                v.memset(k.dotsT[:, :, :], 0.0).then_inc(zeroed, 1)
                dve.wait_ge(zeroed, 3)
                for h in range(2):
                    ins = v.tensor_scalar(k.dotsT[h * DH:(h + 1) * DH, :, h * DH:(h + 1) * DH],
                                          dots[h * DH:(h + 1) * DH, :, h * DH:(h + 1) * DH], 1.0 / N, None, ALU.mult)
                ins.then_inc(zeroed, 1)
                dve.wait_ge(zeroed, 4)


def mixer_matrix0(nc, k):
    with Scope(nc) as s:
        ps = [s.ps(f"g0_{q}", [P, 512]) for q in range(6)]
        t = s.sb("g0_t", [P, 4, D])
        ready, done = s.sem("g0_ready"), s.sem("g0_done")
        with nc.Block() as block:
            @block.tensor
            def _(pe):
                for q in range(4):
                    nc.tensor.matmul(ps[q][:, 0:D], k.dotsT[:, q, :], k.mix_outT[:, q, :], start=True, stop=True).then_inc(ready, 1)
                pe.wait_ge(done, 4)
                for c in range(KC):
                    for q in range(4):
                        ins = nc.tensor.matmul(ps[4 + c][:, 0:D], k.mix_q[:, q, c * P:(c + 1) * P], t[:, q, :],
                                               start=(q == 0), stop=(q == 3))
                    ins.then_inc(ready, 1)

            @block.vector
            def _(dve):
                v = nc.vector
                for q in range(4):
                    dve.wait_ge(ready, q + 1)
                    v.tensor_copy(t[:, q, :], ps[q][:, 0:D]).then_inc(done, 1)
                for c in range(KC):
                    dve.wait_ge(ready, 5 + c)
                    v.tensor_tensor(k.W0[:, c, 3 * D:4 * D], k.W0[:, c, 3 * D:4 * D], ps[4 + c][:, 0:D], ALU.add).then_inc(done, 1)
                v.tensor_tensor(k.bias0[:, 3 * D:4 * D], k.bias0[:, 3 * D:4 * D], k.bias0[:, 4 * D:5 * D], ALU.add).then_inc(done, 1)
                dve.wait_ge(done, 7)


def edge_scores(nc, k, e, q_parts, k_tab, score):
    HD = D // H1
    HU = U // 2
    with Scope(nc) as s:
        ix = s.sb("es_ix", [P, 2, U], I32)
        kg = s.sb("es_k", [P, 2, U, D])
        rel_row = s.sb("es_rel_row", [1, 2, U * P], BF)
        hot = s.sb("es_hot", [P, 2, U * P], BF)
        ps_b = s.ps("es_b", [P, U * P])
        ps_q = s.ps("es_q", [P, U, D])
        listed, freed, spread, hotted, asked, multiplied, took = (
            s.sem("es_" + q) for q in ("listed", "freed", "spread", "hotted", "asked", "multiplied", "took"))
        got = [s.sem(f"es_got{h}") for h in range(2)]
        row = [s.sem(f"es_row{h}") for h in range(2)]
        turns = T1 // U
        assert turns % 2 == 1
        with nc.Block() as block:
            @block.gpsimd
            def _(pool):
                def turn(i, h):
                    pool.wait_ge(freed, i + 1)
                    pool.wait_ge(k.armed, 1)
                    nc.gpsimd.tensor_copy(ix[:, h, :], e.src[:, ds(i * U, U)]).then_inc(listed, 1)
                    pool.wait_ge(k.armed, 1)
                    pool.wait_ge(listed, i + 1)
                    for u in range(U):
                        nc.gpsimd.indirect_dma_start(
                            out=kg[:, h, u, :], out_offset=None, in_=k_tab,
                            in_offset=bass.IndirectOffsetOnAxis(ap=ix[:, h, u:u + 1], axis=0)).then_inc(got[h], 16)
                with pool.Fori(0, turns // 2) as w:
                    turn(w * 2, 0)
                    turn(w * 2 + 1, 1)
                turn(turns - 1, 0)

            @block.sync
            def _(sp):
                def turn(i, h):
                    sp.wait_ge(spread, i + 1)
                    sp.dma_start(rel_row[:, h, :], e.rel_rows[ds(i * U, U), :].rearrange("t e -> (t e)").rearrange("(a n) -> a n", a=1)).then_inc(row[h], 16)
                with sp.Fori(0, turns // 2) as w:
                    turn(w * 2, 0)
                    turn(w * 2 + 1, 1)
                turn(turns - 1, 0)

            @block.tensor
            def _(pe):
                pe.sem_inc(spread, 2)

                def spread_row(i, w, h):
                    pe.wait_ge(row[h], w * 16 + 16)
                    pe.wait_ge(hotted, i + 1)
                    for n in range(0, U * P, 512):
                        ins = nc.tensor.matmul(ps_b[:, n:n + 512], k.ones_h[:, :], rel_row[:, h, n:n + 512], start=True, stop=True)
                    ins.then_inc(spread, 1)

                def fetch(i, h):
                    pe.wait_ge(hotted, i + 2)
                    for u, b in enumerate(blocks_of(nc, mybir.EngineType.PE, e, i)):
                        if u % HU == 0:
                            pe.wait_ge(multiplied, i * 2 + (u // HU + 1))
                            pe.wait_ge(k.armed, 1)
                        for n in range(3):
                            ins = nc.tensor.matmul(ps_q[:, u, :], hot[:, h, u * P:(u + 1) * P],
                                                   q_parts[:, ds(b, 1), n, :].rearrange("p a d -> p (a d)"), start=(n == 0), stop=(n == 2))
                        if u % HU == HU - 1:
                            ins.then_inc(asked, 1)
                spread_row(0, 0, 0)
                with pe.Fori(0, turns // 2) as w:
                    spread_row(w * 2 + 1, w, 1)
                    fetch(w * 2, 0)
                    spread_row(w * 2 + 2, w + 1, 0)
                    fetch(w * 2 + 1, 1)
                fetch(turns - 1, 0)

            @block.vector
            def _(dve):
                v = nc.vector
                dve.sem_inc(freed, 2)
                dve.sem_inc(hotted, 1)
                dve.sem_inc(multiplied, 2)

                def mark(i, h):
                    dve.wait_ge(spread, i + 3)
                    v.tensor_scalar(hot[:, h, :], ps_b[:, :], k.count_col[:, 0:1], None, ALU.is_equal).then_inc(hotted, 1)

                def reduce(i, w, h):
                    dve.wait_ge(got[h], w * (16 * U) + 16 * U)
                    for n in range(2):
                        dve.wait_ge(asked, i * 2 + (n + 1))
                        rows = kg[:, h, n * HU:(n + 1) * HU, :]
                        v.tensor_tensor(rows, rows, ps_q[:, n * HU:(n + 1) * HU, :], ALU.mult).then_inc(multiplied, 1)
                    dve.wait_ge(multiplied, i * 2 + 4)
                    v.tensor_reduce(score[:, ds(i * U, U), :].rearrange("p t h -> p (t h)"),
                                    kg[:, h].rearrange("p u (h d) -> p (u h) d", d=HD), AX.X, ALU.add).then_inc(freed, 1)
                mark(0, 0)
                with dve.Fori(0, turns // 2) as w:
                    mark(w * 2 + 1, 1)
                    reduce(w * 2, w, 0)
                    mark(w * 2 + 2, 0)
                    reduce(w * 2 + 1, w, 1)
                reduce(turns - 1, turns // 2, 0)
                v.memset(score[:, T1:G1 * P, :], 0.0).then_inc(took, 1)
                dve.wait_ge(took, 1)
                dve.wait_ge(freed, turns + 2)


def blocks_of(nc, engine, e, i):
    return nc.values_load_multi_w_load_instructions(e.block_row[0:1, ds(i * U, U)], engines=(engine,), min_val=0, max_val=NB - 1)[1]


def attend(nc, k, e, v_tab, weight, acc):
    HD = D // H1
    W = D + H1
    turns = T1 // U
    with Scope(nc) as s:
        ix = s.sb("at_ix", [P, 2, U], I32)
        vg = s.sb("at_v", [P, 2, U, D])
        msg = s.sb("at_msg", [P, 2, U, W])
        hot = s.sb("at_hot", [P, 2, U, P])
        ps = [s.ps(f"at_ps{u}", [P, 512]) for u in range(U)]
        listed, built, summed, added = (s.sem("at_" + q) for q in ("listed", "built", "summed", "added"))
        got = [s.sem(f"at_got{h}") for h in range(2)]
        with nc.Block() as block:
            @block.gpsimd
            def _(pool):
                def turn(i, h):
                    pool.wait_ge(built, i + 1)
                    pool.wait_ge(k.armed, 1)
                    nc.gpsimd.tensor_copy(ix[:, h, :], e.src[:, ds(i * U, U)]).then_inc(listed, 1)
                    pool.wait_ge(k.armed, 1)
                    pool.wait_ge(listed, i + 1)
                    for u in range(U):
                        nc.gpsimd.indirect_dma_start(
                            out=vg[:, h, u, :], out_offset=None, in_=v_tab,
                            in_offset=bass.IndirectOffsetOnAxis(ap=ix[:, h, u:u + 1], axis=0)).then_inc(got[h], 16)
                with pool.Fori(0, turns // 2) as w:
                    turn(w * 2, 0)
                    turn(w * 2 + 1, 1)
                turn(turns - 1, 0)

            @block.tensor
            def _(pe):
                def turn(i, h):
                    pe.wait_ge(built, i + 3)
                    for u in range(U):
                        pe.wait_ge(added, i * U + (u + 1))
                        nc.tensor.matmul(ps[u][:, 0:W], hot[:, h, u, :], msg[:, h, u, :], start=True, stop=True).then_inc(summed, 1)
                with pe.Fori(0, turns // 2) as w:
                    turn(w * 2, 0)
                    turn(w * 2 + 1, 1)
                turn(turns - 1, 0)

            @block.vector
            def _(dve):
                v = nc.vector
                dve.sem_inc(built, 2)
                dve.sem_inc(added, U)

                def build(i, w, h):
                    v.tensor_tensor(hot[:, h], wide(k.count_row[:, 0:P].unsqueeze(1), [P, U, P]),
                                    wide(e.rel[:, ds(i * U, U)].unsqueeze(2), [P, U, P]), ALU.is_equal)
                    v.tensor_copy(msg[:, h, :, D:W], weight[:, ds(i * U, U), :])
                    dve.wait_ge(got[h], w * (16 * U) + 16 * U)
                    v.tensor_tensor(msg[:, h, :, 0:D].rearrange("p u (g d) -> p u g d", d=HD),
                                    vg[:, h].rearrange("p u (g d) -> p u g d", d=HD),
                                    wide(weight[:, ds(i * U, U), :].unsqueeze(3), [P, U, H1, HD]), ALU.mult).then_inc(built, 1)

                def add(i):
                    for u, b in enumerate(blocks_of(nc, mybir.EngineType.DVE, e, i)):
                        dve.wait_ge(summed, i * U + (u + 1))
                        dve.wait_ge(added, i * U + (u + U))
                        dve.wait_ge(k.armed, 1)
                        row = acc[:, ds(b, 1), :].rearrange("p a w -> p (a w)")
                        v.tensor_tensor(row, row, ps[u][:, 0:W], ALU.add).then_inc(added, 1)
                build(0, 0, 0)
                with dve.Fori(0, turns // 2) as w:
                    build(w * 2 + 1, w, 1)
                    add(w * 2)
                    build(w * 2 + 2, w + 1, 0)
                    add(w * 2 + 1)
                add(turns - 1)
                dve.wait_ge(added, T1 + U)


def combine0(nc, k, acc):
    with Scope(nc) as s:
        xn = s.sb("c0_xn", [P, B5, D])
        xT = s.sb("c0_xT", [P, B5, KC, P])
        rd = s.sb("c0_rd", [P, NB, H1])
        ps_t = s.ps("c0_t", [P, KC, P])
        ps_o = [s.ps(f"c0_o{j}", [P, D]) for j in range(B5)]
        normed, turned, kept, done, chain = (s.sem("c0_" + q) for q in ("normed", "turned", "kept", "done", "chain"))
        HD = D // H1
        with nc.Block() as block:
            @block.scalar
            def _(act):
                with act.Fori(0, NB // B5) as i:
                    for j in range(B5):
                        act.wait_ge(turned, i * B5 + j + 1)
                        act.wait_ge(k.armed, 1)
                        normed_block(nc, k, act, i * B5 + j, xn[:, j, :], normed)

            @block.tensor
            def _(pe):
                pe.sem_inc(turned, B5)
                with pe.Fori(0, NB // B5) as i:
                    for j in range(B5):
                        b = i * B5 + j
                        pe.wait_ge(normed, b + 1)
                        pe.wait_ge(kept, b + 1)
                        for c in range(KC):
                            ins = nc.tensor.transpose(ps_t[:, c, :], xn[:, j, c * P:(c + 1) * P], k.ident[:, :])
                        ins.then_inc(turned, 1)
                        pe.wait_ge(kept, b + 2)
                        nc.tensor.matmul(ps_o[j][:, :], k.ones[0:1, :], k.bias0[:, 3 * D:4 * D], start=True, stop=False)
                        for c in range(KC):
                            ins = nc.tensor.matmul(ps_o[j][:, :], xT[:, j, c, :], k.W0[:, c, 3 * D:4 * D], start=False, stop=(c == KC - 1))
                        ins.then_inc(done, 1)

            @block.vector
            def _(dve):
                v = nc.vector
                dve.sem_inc(kept, 1)
                c = Chain(dve, chain)
                c.link(v.tensor_scalar(rd[:, :, :], acc[:, :, D:D + H1], 1e-30, None, ALU.max))
                c.link(v.reciprocal(rd[:, :, :], rd[:, :, :]))
                with dve.Fori(0, NB // B5) as i:
                    c = Chain(dve, chain, i * (3 * B5) + 2)
                    for j in range(B5):
                        b = i * B5 + j
                        xb = k.X[:, ds(b, 1), :].rearrange("p a d -> p (a d)")
                        ab = acc[:, ds(b, 1), 0:D].rearrange("p a (g d) -> p (a g) d", d=HD)
                        dve.wait_ge(turned, b + B5 + 1)
                        v.tensor_copy(xT[:, j], ps_t[:, :, :]).then_inc(kept, 1)
                        c.link(v.tensor_tensor(ab, ab, wide(rd[:, ds(b, 1), :].rearrange("p a g -> p (a g)").unsqueeze(2), [P, H1, HD]), ALU.mult))
                        c.link(v.tensor_tensor(xb, xb, acc[:, ds(b, 1), 0:D].rearrange("p a d -> p (a d)"), ALU.add))
                        dve.wait_ge(done, b + 1)
                        c.link(v.tensor_tensor(xb, xb, ps_o[j][:, :], ALU.add))
                    assert c.n == 3 * B5


def gate0(nc, k, XN, logits):
    with Scope(nc) as s:
        xn = s.sb("r0_xn", [P, B5, D])
        xT = s.sb("r0_xT", [P, B5, KC, P])
        ps_t = s.ps("r0_t", [P, KC, P])
        ps_l = [s.ps(f"r0_l{j}", [P, NE]) for j in range(B5)]
        normed, turned, kept, done, moved = (s.sem("r0_" + q) for q in ("normed", "turned", "kept", "done", "moved"))
        with nc.Block() as block:
            @block.scalar
            def _(act):
                with act.Fori(0, NB // B5) as i:
                    for j in range(B5):
                        b = i * B5 + j
                        act.wait_ge(turned, b + 1)
                        act.wait_ge(k.armed, 1)
                        normed_block(nc, k, act, b, xn[:, j, :], normed)
                        normed_block(nc, k, act, b, XN[:, ds(b, 1), :].rearrange("p a d -> p (a d)"), moved)
                act.wait_ge(moved, NB)

            @block.tensor
            def _(pe):
                pe.sem_inc(turned, B5)
                with pe.Fori(0, NB // B5) as i:
                    for j in range(B5):
                        b = i * B5 + j
                        pe.wait_ge(normed, b + 1)
                        pe.wait_ge(kept, 2 * b + 1)
                        for c in range(KC):
                            ins = nc.tensor.transpose(ps_t[:, c, :], xn[:, j, c * P:(c + 1) * P], k.ident[:, :])
                        ins.then_inc(turned, 1)
                        pe.wait_ge(kept, 2 * b + 2)
                        nc.tensor.matmul(ps_l[j][:, :], k.ones[0:1, :], k.gate_b[:, :], start=True, stop=False)
                        for c in range(KC):
                            ins = nc.tensor.matmul(ps_l[j][:, :], xT[:, j, c, :], k.gate[:, c, :], start=False, stop=(c == KC - 1))
                        ins.then_inc(done, 1)

            @block.vector
            def _(dve):
                v = nc.vector
                dve.sem_inc(kept, 1)
                with dve.Fori(0, NB // B5) as i:
                    for j in range(B5):
                        b = i * B5 + j
                        dve.wait_ge(turned, b + B5 + 1)
                        v.tensor_copy(xT[:, j], ps_t[:, :, :]).then_inc(kept, 1)
                        dve.wait_ge(done, b + 1)
                        dve.wait_ge(k.armed, 1)
                        v.tensor_copy(logits[:, ds(b, 1), :].rearrange("p a e -> p (a e)"), ps_l[j][:, :]).then_inc(kept, 1)
                dve.wait_ge(kept, 2 * NB + 1)


def route0(nc, k, XN, logits, buf, slot_i, factor):
    with Scope(nc) as s:
        S = [P, NB, NE]
        t = s.sb("ro_t", [P, 8, NB, NE])
        r = s.sb("ro_r", [P, 10, NB])
        send_i = s.sb("ro_send", [P, NB], I32)
        ps_in = s.ps("ro_in", [P, NB * NE])
        ps_all = s.ps("ro_all", [P, NB * NE])
        zero = s.sb("ro_zero", [P, 512])
        chain, asked, exped, hot, counted, sent, clear, cleared = (
            s.sem("ro_" + q) for q in ("chain", "asked", "exped", "hot", "counted", "sent", "clear", "cleared"))
        per_part = SLOTS * D // P
        run = next(x for x in range(512, 0, -1) if per_part % x == 0)
        with nc.Block() as block:
            @block.sync
            def _(sp):
                sp.wait_ge(clear, 1)
                sp.dma_start(buf[0:SLOTS, :].rearrange("s d -> (s d)").rearrange("(p m r) -> p m r", p=P, r=run),
                             wide(zero[:, 0:run].unsqueeze(1), [P, per_part // run, run])).then_inc(cleared, 16)
                sp.wait_ge(cleared, 16)

            @block.scalar
            def _(act):
                act.wait_ge(asked, 1)
                nc.scalar.activation(t[:, 1], t[:, 0], ACT.Exp).then_inc(exped, 1)

            @block.tensor
            def _(pe):
                pe.wait_ge(hot, 1)
                rhs = t[:, 3].rearrange("p b e -> p (b e)")
                nc.tensor.matmul(ps_in[:, :], k.upper[:, :], rhs, start=True, stop=True)
                nc.tensor.matmul(ps_all[:, :], k.ones[:, :], rhs, start=True, stop=True).then_inc(counted, 1)

            @block.gpsimd
            def _(pool):
                pool.wait_ge(asked, 2)
                pool.wait_ge(cleared, 16)
                for b in range(NB):
                    n = P if b < NB - 1 else LAST
                    nc.gpsimd.indirect_dma_start(
                        out=buf, out_offset=bass.IndirectOffsetOnAxis(ap=send_i[0:n, b:b + 1], axis=0),
                        in_=XN[0:n, b, :], in_offset=None).then_inc(sent, 16)
                pool.wait_ge(sent, 16 * NB)

            @block.vector
            def _(dve):
                v = nc.vector
                c = Chain(dve, chain)
                v.memset(zero[:, :], 0.0).then_inc(clear, 1)
                c.link(v.tensor_reduce(r[:, 0], logits[:, :, :], AX.X, ALU.max))
                v.tensor_tensor(t[:, 0], logits[:, :, :], wide(r[:, 0].unsqueeze(2), S), ALU.subtract).then_inc(asked, 1)
                dve.wait_ge(exped, 1)
                v.tensor_reduce(r[:, 1], t[:, 1], AX.X, ALU.add)
                c.link(v.tensor_reduce(r[:, 2], t[:, 1], AX.X, ALU.max))
                v.reciprocal(r[:, 3], r[:, 1])
                c.link(v.tensor_tensor(t[:, 2], t[:, 1], wide(r[:, 2].unsqueeze(2), S), ALU.is_lt))
                c.link(v.scalar_tensor_tensor(out=t[:, 2], in0=t[:, 2], scalar=100.0, in1=wide(k.count_row[:, 0:NE].unsqueeze(1), S),
                                              op0=ALU.mult, op1=ALU.add))
                c.link(v.tensor_reduce(r[:, 4], t[:, 2], AX.X, ALU.min))
                v.tensor_tensor(t[:, 3], t[:, 2], wide(r[:, 4].unsqueeze(2), S), ALU.is_equal).then_inc(hot, 1)
                dve.wait_ge(counted, 1)
                tot = ps_all[:, :].rearrange("p (b e) -> p b e", e=NE)
                for e in range(NE):
                    ins = v.tensor_tensor_scan(t[:, 4, :, e], wide(k.ones[:, 0:1], [P, NB]), tot[:, :, e], 0.0, ALU.mult, ALU.add)
                c.link(ins)
                c.link(v.tensor_tensor(t[:, 5], t[:, 4], tot, ALU.subtract))
                c.link(v.tensor_tensor(t[:, 5], t[:, 5], ps_in[:, :].rearrange("p (b e) -> p b e", e=NE), ALU.add))
                c.link(v.tensor_tensor(t[:, 5], t[:, 5], t[:, 3], ALU.mult))
                c.link(v.tensor_reduce(r[:, 5], t[:, 5], AX.X, ALU.add))
                v.tensor_scalar(r[:, 6], r[:, 5], float(CAP), None, ALU.is_lt)
                c.link(v.tensor_scalar(r[:, 7], r[:, 5], float(CAP - 1), None, ALU.min))
                v.tensor_tensor(r[:, 3], r[:, 3], r[:, 2], ALU.mult)
                c.link(v.scalar_tensor_tensor(out=r[:, 8], in0=r[:, 4], scalar=float(CAP), in1=r[:, 7], op0=ALU.mult, op1=ALU.add))
                v.tensor_tensor(factor[:, :], r[:, 3], r[:, 6], ALU.mult)
                v.tensor_copy(slot_i[:, :], r[:, 8])
                c.link(v.tensor_scalar(r[:, 7], k.node_id[:, :], float(SLOTS), None, ALU.add))
                c.link(v.tensor_tensor(r[:, 9], r[:, 8], r[:, 7], ALU.subtract))
                c.link(v.tensor_tensor(r[:, 9], r[:, 9], r[:, 6], ALU.mult))
                c.link(v.tensor_tensor(r[:, 9], r[:, 9], r[:, 7], ALU.add))
                c.link(v.tensor_copy(send_i[:, :], r[:, 9]))
                dve.sem_inc(asked, 1)


def experts0(nc, k, a, buf, out_buf):
    FC = FE // P
    TC = [(q * P, min(P, CAP - q * P)) for q in range((CAP + P - 1) // P)]
    w1_v = a["L0_ffn_w1"].rearrange("e (c p) f -> e p c f", p=P)
    w2_v = a["L0_ffn_w2"].rearrange("e (c p) f -> e p c f", p=P)
    b1_v = a["L0_ffn_b1"].rearrange("e (c p) -> e p c", p=P)
    with Scope(nc) as s:
        w1 = s.sb("x0_w1", [P, 2, KC, FE])
        w2 = s.sb("x0_w2", [P, 2, FC, D])
        b1 = s.sb("x0_b1", [P, 2, FC])
        b2 = s.sb("x0_b2", [1, 2, D])
        rows = s.sb("x0_rows", [P, 2, len(TC), D])
        xT = s.sb("x0_xT", [P, KC, CAP])
        hid = s.sb("x0_hid", [P, FC, CAP])
        y = s.sb("x0_y", [P, 2, len(TC), D])
        ps_t = [s.ps(f"x0_t{c}", [P, 512]) for c in range(KC)]
        ps_h = [s.ps(f"x0_h{j}", [P, 512]) for j in range(2)]
        ps_y = [s.ps(f"x0_y{j}", [P, 512]) for j in range(2)]
        turned, kept, h_done, h_kept, y_done, y_kept, used = (
            s.sem("x0_" + q) for q in ("turned", "kept", "h_done", "h_kept", "y_done", "y_kept", "used"))
        got = [s.sem(f"x0_got{j}") for j in range(2)]
        out = [s.sem(f"x0_out{j}") for j in range(2)]
        NL = 4 + len(TC)

        with nc.Block() as block:
            @block.sync
            def _(sp):
                with sp.Fori(0, NE // 2) as i:
                    for j in range(2):
                        e = i * 2 + j
                        sp.wait_ge(used, e + 1)
                        for c, (o, n) in enumerate(TC):
                            sp.dma_start(rows[0:n, j, c, :], buf[ds(e * CAP + o, n), :]).then_inc(got[j], 16)
                        sp.dma_start(w1[:, j], w1_v[ds(e, 1)].rearrange("a p c f -> p (a c) f")).then_inc(got[j], 16)
                        sp.dma_start(b1[:, j], b1_v[ds(e, 1)].rearrange("a p c -> p (a c)"),
                                     allow_slow_non_contiguous=True).then_inc(got[j], 16)
                        sp.dma_start(w2[:, j], w2_v[ds(e, 1)].rearrange("a p c f -> p (a c) f")).then_inc(got[j], 16)
                        sp.dma_start(b2[:, j, :], a["L0_ffn_b2"][ds(e, 1), :]).then_inc(got[j], 16)

            @block.tensor
            def _(pe):
                pe.sem_inc(used, 2)
                with pe.Fori(0, NE // 2) as i:
                    for j in range(2):
                        e = i * 2 + j
                        pe.wait_ge(got[j], i * (16 * NL) + 16 * NL)
                        pe.wait_ge(kept, e + 1)
                        for c in range(KC):
                            for q, (o, n) in enumerate(TC):
                                ins = nc.tensor.transpose(ps_t[c][:, o:o + n], rows[0:n, j, q, c * P:(c + 1) * P], k.ident[0:n, 0:n])
                        ins.then_inc(turned, 1)
                        pe.wait_ge(kept, e + 2)
                        for f in range(FC):
                            pe.wait_ge(h_kept, e * FC + (f + 1))
                            for c in range(KC):
                                ins = nc.tensor.matmul(ps_h[f % 2][:, 0:CAP], w1[:, j, c, f * P:(f + 1) * P], xT[:, c, :],
                                                       start=(c == 0), stop=(c == KC - 1))
                            ins.then_inc(h_done, 1)
                        pe.wait_ge(h_kept, e * FC + (FC + 2))
                        for q, (o, n) in enumerate(TC):
                            pe.wait_ge(y_kept, e * len(TC) + (q + 1))
                            nc.tensor.matmul(ps_y[q % 2][0:n, 0:D], k.ones[0:1, 0:n], b2[:, j, :], start=True, stop=False)
                            for f in range(FC):
                                ins = nc.tensor.matmul(ps_y[q % 2][0:n, 0:D], hid[:, f, o:o + n], w2[:, j, f, :],
                                                       start=False, stop=(f == FC - 1))
                            ins.then_inc(y_done, 1)
                        pe.wait_ge(y_done, e * len(TC) + len(TC))
                        pe.sem_inc(used, 1)

            @block.scalar
            def _(act):
                act.sem_inc(h_kept, 2)
                with act.Fori(0, NE // 2) as i:
                    for j in range(2):
                        e = i * 2 + j
                        for f in range(FC):
                            act.wait_ge(h_done, e * FC + (f + 1))
                            nc.scalar.activation(hid[:, f, :], ps_h[f % 2][:, 0:CAP], ACT.Relu, bias=b1[:, j, f:f + 1]).then_inc(h_kept, 1)
                        act.wait_ge(y_kept, e * len(TC) + (2 + len(TC)))
                        for q, (o, n) in enumerate(TC):
                            act.dma_start(out_buf[ds(e * CAP + o, n), :], y[0:n, j, q, :]).then_inc(out[j], 16)
                for j in range(2):
                    act.wait_ge(out[j], 16 * len(TC) * (NE // 2))

            @block.vector
            def _(dve):
                v = nc.vector
                dve.sem_inc(kept, 1)
                dve.sem_inc(y_kept, 2)

                def turn(i, first=False):
                    for j in range(2):
                        e = i * 2 + j
                        dve.wait_ge(turned, e + 1)
                        v.tensor_copy(xT[:, 0, :], ps_t[0][:, 0:CAP])
                        v.tensor_copy(xT[:, 1, :], ps_t[1][:, 0:CAP]).then_inc(kept, 1)
                        if not first:
                            dve.wait_ge(out[j], i * (16 * len(TC)))
                        for q, (o, n) in enumerate(TC):
                            dve.wait_ge(y_done, e * len(TC) + (q + 1))
                            v.tensor_copy(y[0:n, j, q, :], ps_y[q % 2][0:n, 0:D]).then_inc(y_kept, 1)
                turn(0, True)
                with dve.Fori(1, NE // 2) as i:
                    turn(i)


def return0(nc, k, out_buf, slot_i, factor):
    with Scope(nc) as s:
        y = s.sb("re_y", [P, NB, D])
        z = s.sb("re_z", [P, NB, D])
        m = s.sb("re_m", [P, NB, D], I32)
        got, chain = s.sem("re_got"), s.sem("re_chain")
        with nc.Block() as block:
            @block.gpsimd
            def _(pool):
                pool.wait_ge(chain, 2)
                for b in range(NB):
                    nc.gpsimd.indirect_dma_start(
                        out=y[:, b, :], out_offset=None, in_=out_buf,
                        in_offset=bass.IndirectOffsetOnAxis(ap=slot_i[:, b:b + 1], axis=0)).then_inc(got, 16)

            @block.vector
            def _(dve):
                v = nc.vector
                c = Chain(dve, chain)
                c.link(v.tensor_scalar(slot_i[:, :], slot_i[:, :], 0, None, ALU.max))
                c.link(v.tensor_scalar(slot_i[:, :], slot_i[:, :], SLOTS - 1, None, ALU.min))
                dve.wait_ge(got, 16 * NB)
                c.link(v.tensor_tensor(y[:, :, :], y[:, :, :], wide(factor[:, :].unsqueeze(2), [P, NB, D]), ALU.mult))
                v.memset(z[:, :, :], 0.0)
                c.link(v.tensor_tensor(m[:, :, :], y[:, :, :], y[:, :, :], ALU.is_equal))
                c.link(v.copy_predicated(z[:, :, :], m[:, :, :], y[:, :, :]))
                for sign, test in ((1.0, ALU.is_gt), (-1.0, ALU.is_lt)):
                    c.link(v.tensor_scalar(m[:, :, :], z[:, :, :], sign * 3.4028234663852886e38, None, test))
                    c.link(v.memset(y[:, :, :], sign * 1.0e4))
                    c.link(v.copy_predicated(z[:, :, :], m[:, :, :], y[:, :, :]))
                c.link(v.tensor_tensor(k.X[:, :, :], k.X[:, :, :], z[:, :, :], ALU.add))


def sort_edges(nc, k, edge_index, pairs):
    turns = C2 // U
    src_v = edge_index[0:1, :].rearrange("a (p c) -> (a p) c", p=P)
    dst_v = edge_index[1:2, :].rearrange("a (p c) -> (a p) c", p=P)
    with Scope(nc) as s:
        pair = s.sb("so_pair", [P, C2, 2], I32)
        given = s.sb("so_given", [P, 2, CG], I32)
        loop = s.sb("so_loop", [P, 2, NB])
        key = s.sb("so_key", [P, C2])
        digit_i = s.sb("so_digit_i", [P, 2, C2], I32)
        digit = s.sb("so_digit", [P, 2, C2])
        count = s.sb("so_count", [P, C2, NH])
        before = s.sb("so_before", [P, C2, NH])
        lo_h = s.sb("so_lo_h", [P, C2], BF)
        top_h = s.sb("so_top_h", [P, C2], BF)
        lo = s.sb("so_lo", [P, 2, U, P], BF)
        hi = s.sb("so_hi", [P, 2, U, NH], BF)
        low = s.sb("so_low", [P, P])
        tot = s.sb("so_tot", [P, 4, NH])
        same = s.sb("so_same", [P, U, P])
        lo_t = s.sb("so_lo_t", [P, U, P])
        pick = s.sb("so_pick", [P, U, NH])
        place = s.sb("so_place", [P, 4, U])
        place_i = s.sb("so_place_i", [P, C2], I32)
        ix = s.sb("so_ix", [P, 2, U], I32)
        pr = s.sb("so_pr", [P, 2, U, 2], I32)
        edge = s.sb("so_edge", [1, 2, P, 2], I32)
        ps_c = [s.ps(f"so_c{h}", [P, U, NH]) for h in range(2)]
        ps_r = s.ps("so_r", [P, U, P])
        ps_l = s.ps("so_l", [P, U, P])
        ps_g = s.ps("so_g", [P, U, NH])
        ps_s = s.ps("so_s", [P, 2, NH])
        got, iotas, chain, hot, counted, tabled, summed, rowed, ranked, picked, looked, listed, ended = (
            s.sem("so_" + q) for q in ("got", "iotas", "chain", "hot", "counted", "tabled", "summed", "rowed", "ranked", "picked",
                                       "looked", "listed", "ended"))
        sent = [s.sem(f"so_sent{h}") for h in range(2)]
        placed = s.sem("so_placed")
        C_LINKS = 3
        with nc.Block() as block:
            @block.sync
            def _(sp):
                sp.dma_start(given[:, 0, :], dst_v).then_inc(got, 16)
                sp.dma_start(given[:, 1, :], src_v).then_inc(got, 16)
                sp.wait_ge(iotas, 3)
                sp.dma_start(pairs[0:1, :], edge[0:1, 0, 0, :]).then_inc(ended, 16)
                sp.dma_start(pairs[C2 * P + 1:(C2 + 1) * P, :].rearrange("(a r) b -> a r b", a=1), edge[:, 1, 0:P - 1, :]).then_inc(ended, 16)
                sp.wait_ge(ended, 32)

            @block.gpsimd
            def _(pool):
                nc.gpsimd.memset(edge[:, 0], -1).then_inc(iotas, 1)
                nc.gpsimd.memset(edge[:, 1], NONODE).then_inc(iotas, 1)
                pool.wait_ge(iotas, 2)
                nc.gpsimd.memset(ix[:, :, :], 0).then_inc(iotas, 1)
                pool.wait_ge(iotas, 3)

                def turn(i, w, h):
                    pool.wait_ge(placed, i + 1)
                    if w is not None:
                        pool.wait_ge(sent[h], w * (16 * U))
                    pool.wait_ge(k.armed, 1)
                    nc.gpsimd.tensor_copy(ix[:, h, :], place_i[:, ds(i * U, U)])
                    nc.gpsimd.tensor_copy(pr[:, h], pair[:, ds(i * U, U), :]).then_inc(listed, 1)
                    pool.wait_ge(k.armed, 1)
                    pool.wait_ge(listed, i + 1)
                    for u in range(U):
                        nc.gpsimd.indirect_dma_start(
                            out=pairs, out_offset=bass.IndirectOffsetOnAxis(ap=ix[:, h, u:u + 1], axis=0),
                            in_=pr[:, h, u, :], in_offset=None).then_inc(sent[h], 16)
                turn(0, None, 0)
                turn(1, None, 1)
                with pool.Fori(1, turns // 2) as w:
                    turn(w * 2, w, 0)
                    turn(w * 2 + 1, w, 1)
                for h in range(2):
                    pool.wait_ge(sent[h], 16 * U * (turns // 2))

            @block.tensor
            def _(pe):
                def tally(i, h):
                    pe.wait_ge(hot, i + 1)
                    for u in range(U):
                        ins = nc.tensor.matmul(ps_c[h][:, u, :], lo[:, h, u, :], hi[:, h, u, :], start=True, stop=True)
                    ins.then_inc(counted, 1)
                with pe.Fori(0, turns // 2) as w:
                    tally(w * 2, 0)
                    tally(w * 2 + 1, 1)
                pe.wait_ge(tabled, 1)
                nc.tensor.matmul(ps_s[:, 0, :], k.upper[:, :], tot[:, 0], start=True, stop=True)
                nc.tensor.matmul(ps_s[:, 1, :], k.ones[:, :], tot[:, 0], start=True, stop=True).then_inc(summed, 1)
                with pe.Fori(0, turns) as i:
                    pe.wait_ge(ranked, i + 1)
                    for u in range(U):
                        low_col, top_col = (wide(x[:, ds(i * U + u, 1)], [P, P]) for x in (lo_h, top_h))
                        nc.tensor.matmul(ps_l[:, u, :], low_col, k.ident_h[:, :], start=True, stop=True)
                        nc.tensor.matmul(ps_r[:, u, :], low_col, k.ident_h[:, :], start=True, stop=False)
                        ins = nc.tensor.matmul(ps_r[:, u, :], top_col, k.ident_h[:, :], start=False, stop=True)
                    ins.then_inc(rowed, 1)
                    pe.wait_ge(picked, i + 1)
                    for u in range(U):
                        ins = nc.tensor.matmul(ps_g[:, u, :], lo_t[:, u, :],
                                               before[:, ds(i * U + u, 1), :].rearrange("p a h -> p (a h)"), start=True, stop=True)
                    ins.then_inc(looked, 1)

            @block.vector
            def _(dve):
                v = nc.vector
                c = Chain(dve, chain)
                dve.wait_ge(got, 32)
                v.tensor_copy(pair[:, 0:CG, 0], given[:, 0, :])
                v.tensor_copy(pair[:, 0:CG, 1], given[:, 1, :])
                v.memset(pair[:, CG:C2, 0], NONODE)
                c.link(v.memset(pair[:, CG:C2, 1], 0))
                v.tensor_copy(loop[:, 0, :], k.node_id[:, :])
                c.link(v.tensor_scalar(loop[:, 1, :], k.node_id[:, :], float(NONODE), None, ALU.subtract))
                c.link(v.tensor_tensor(loop[:, 1, :], loop[:, 1, :], k.node_mask[:, :], ALU.mult))
                c.link(v.tensor_scalar(loop[:, 1, :], loop[:, 1, :], float(NONODE), None, ALU.add))
                c.link(v.tensor_tensor(loop[:, 0, :], loop[:, 0, :], k.node_mask[:, :], ALU.mult))
                v.tensor_copy(pair[:, CG:CG + NB, 0], loop[:, 1, :])
                c.link(v.tensor_copy(pair[:, CG:CG + NB, 1], loop[:, 0, :]))
                c.link(v.tensor_scalar(digit_i[:, 0, :], pair[:, :, 0], P - 1, None, ALU.bitwise_and))
                c.link(v.tensor_scalar(digit_i[:, 1, :], pair[:, :, 0], 7, None, ALU.arith_shift_right))
                v.tensor_copy(key[:, :], pair[:, :, 0])
                c.link(v.tensor_copy(digit[:, :, :], digit_i[:, :, :]))
                c.link(v.tensor_tensor(low[:, :], wide(k.count_col[:, 0:1], [P, P]), k.count_row[:, 0:P], ALU.is_gt))
                v.tensor_copy(lo_h[:, :], digit[:, 0, :])
                c.link(v.tensor_scalar(top_h[:, :], digit[:, 1, :], float(P), None, ALU.mult))
                base = c.n

                def mark(i, h):
                    v.tensor_tensor(lo[:, h], wide(k.count_row[:, 0:P].unsqueeze(1), [P, U, P]),
                                    wide(digit[:, 0, ds(i * U, U)].unsqueeze(2), [P, U, P]), ALU.is_equal)
                    v.tensor_tensor(hi[:, h], wide(k.count_row[:, 0:NH].unsqueeze(1), [P, U, NH]),
                                    wide(digit[:, 1, ds(i * U, U)].unsqueeze(2), [P, U, NH]), ALU.is_equal).then_inc(hot, 1)

                def keep(i, h):
                    dve.wait_ge(counted, i + 1)
                    dve.wait_ge(k.armed, 1)
                    v.tensor_copy(count[:, ds(i * U, U), :], ps_c[h][:, :, :]).then_inc(chain, 1)
                assert turns % 2 == 0
                mark(0, 0)
                with dve.Fori(0, turns // 2 - 1) as w:
                    mark(w * 2 + 1, 1)
                    keep(w * 2, 0)
                    mark(w * 2 + 2, 0)
                    keep(w * 2 + 1, 1)
                mark(turns - 1, 1)
                keep(turns - 2, 0)
                keep(turns - 1, 1)
                dve.wait_ge(chain, base + turns)
                c = Chain(dve, chain, base + turns)
                v.tensor_reduce(tot[:, 0], count[:, :, :].rearrange("p c h -> p h c"), AX.X, ALU.add).then_inc(tabled, 1)
                dve.wait_ge(summed, 1)
                c.link(v.tensor_tensor_scan(tot[:, 1], wide(k.ones[:, 0:1], [P, NH]), ps_s[:, 1, :], 0.0, ALU.mult, ALU.add))
                c.link(v.tensor_tensor(tot[:, 1], tot[:, 1], ps_s[:, 1, :], ALU.subtract))
                c.link(v.tensor_tensor(tot[:, 1], tot[:, 1], ps_s[:, 0, :], ALU.add))
                for x in range(NH):
                    ins = v.tensor_tensor_scan(before[:, :, x], wide(k.ones[:, 0:1], [P, C2]), count[:, :, x],
                                               tot[:, 1, x:x + 1], ALU.mult, ALU.add)
                c.link(ins)
                c.link(v.tensor_tensor(before[:, :, :], before[:, :, :], count[:, :, :], ALU.subtract))
                base += turns + c.n
                dve.sem_inc(ranked, 1)
                with dve.Fori(0, turns) as i:
                    c = Chain(dve, chain, i * C_LINKS + base)
                    v.tensor_tensor(pick[:, :, :], wide(k.count_row[:, 0:NH].unsqueeze(1), [P, U, NH]),
                                    wide(digit[:, 1, ds(i * U, U)].unsqueeze(2), [P, U, NH]), ALU.is_equal)
                    dve.wait_ge(rowed, i + 1)
                    v.tensor_scalar(lo_t[:, :, :], ps_l[:, :, :], k.count_col[:, 0:1], None, ALU.is_equal).then_inc(picked, 1)
                    dve.wait_ge(k.armed, 1)
                    for u in range(U):
                        ins = v.scalar_tensor_tensor(out=same[:, u, :], in0=ps_r[:, u, :], scalar=key[:, ds(i * U + u, 1)], in1=low[:, :],
                                                     op0=ALU.is_equal, op1=ALU.mult, accum_out=place[:, 0, u:u + 1])
                    ins.then_inc(ranked, 1)
                    dve.wait_ge(looked, i + 1)
                    c.link(v.tensor_tensor(pick[:, :, :], pick[:, :, :], ps_g[:, :, :], ALU.mult))
                    c.link(v.tensor_reduce(place[:, 1], pick[:, :, :], AX.X, ALU.add))
                    dve.wait_ge(ranked, i + 2)
                    c.link(v.scalar_tensor_tensor(out=place[:, 2], in0=place[:, 0], scalar=1.0, in1=place[:, 1], op0=ALU.add, op1=ALU.add))
                    v.tensor_copy(place_i[:, ds(i * U, U)], place[:, 2]).then_inc(placed, 1)
                    dve.wait_ge(placed, i + 1)
                    assert c.n == C_LINKS


def edge_factors(nc, k, a, attr, emb_t, e, factor, scale):
    LD = 2048
    Q = 512
    W2 = 2
    R = LD // W2 // Q
    loads = C1 * P // LD
    assert loads % 2 == 0 and C1 * P % LD == 0
    SILU_NORM = 1.679177
    with Scope(nc) as s:
        emb = s.sb("ef_emb", [10 * W2, 2, LD // W2])
        w1 = s.sb("ef_w1", [10 * W2, 64 * W2])
        w2 = s.sb("ef_w2", [64 * W2, W2])
        h = s.sb("ef_h", [64 * W2, 2 * R, Q])
        rad = s.sb("ef_rad", [W2, 2, LD // W2])
        angular = s.sb("ef_angular", [P, G1, P, 4])
        radial_by_step = s.sb("ef_radial_by_step", [P, G1, P])
        rows = s.sb("ef_rows", [P, G1, 4, P])
        bank = [s.ps(f"ef_bank{j}", [P, 4, P]) for j in range(max(G1, 2 * R))]
        ps_h = [x.rearrange("p a b -> p (a b)") for x in bank]
        ps_r = [s.ps(f"ef_r{j}", [W2, Q]) for j in range(2 * R)]
        rad_tab = nc.dram_tensor("edge_radial", [C1, P], F32, kind="Internal").ap()
        rad_loads = rad_tab.rearrange("c e -> (c e)").rearrange("(l a n) -> l a n", a=W2, n=LD // W2)
        emb_loads = emb_t.rearrange("f (l a n) -> l a f n", a=W2, n=LD // W2)
        attr_tab = attr.rearrange("(c e) m -> c (e m)", e=P)
        zeroed, got_w, hid, acted, radial, taken, made, turned, by_step, chain = (
            s.sem("ef_" + q) for q in ("zeroed", "got_w", "hid", "acted", "radial", "taken", "made", "turned", "by_step", "chain"))
        got = [s.sem(f"ef_got{j}") for j in range(2)]
        stored = [s.sem(f"ef_stored{j}") for j in range(2)]
        with nc.Block() as block:
            @block.sync
            def _(sp):
                sp.wait_ge(zeroed, 3)
                for n in range(W2):
                    sp.dma_start(w1[n * 10:(n + 1) * 10, n * 64:(n + 1) * 64], a["L1_gnn_fc_w1"]).then_inc(got_w, 16)
                    sp.dma_start(w2[n * 64:(n + 1) * 64, n:n + 1], a["L1_gnn_fc_w2"]).then_inc(got_w, 16)
                with sp.Fori(0, loads // 2) as i:
                    for j in range(2):
                        sp.wait_ge(hid, i * (2 * R) + (j + 1) * R)
                        for n in range(W2):
                            sp.dma_start(emb[n * 10:(n + 1) * 10, j, :],
                                         emb_loads[ds(i * 2 + j, 1), n].rearrange("l f n -> (l f) n")).then_inc(got[j], 16)

            @block.tensor
            def _(pe):
                pe.sem_inc(hid, 2 * R)
                pe.wait_ge(got_w, 32 * W2)
                with pe.Fori(0, loads // 2) as i:
                    for j in range(2):
                        pe.wait_ge(got[j], i * (16 * W2) + 16 * W2)
                        n = i * (2 * R) + j * R
                        for r in range(R):
                            pe.wait_ge(acted, n + (r + 1))
                            nc.tensor.matmul(ps_h[j * R + r], w1[:, :], emb[:, j, r * Q:(r + 1) * Q], start=True, stop=True).then_inc(hid, 1)
                        for r in range(R):
                            pe.wait_ge(k.armed, 1)
                            pe.wait_ge(acted, n + (r + 1 + R))
                            pe.wait_ge(taken, n + (r + 1))
                            nc.tensor.matmul(ps_r[(1 - j) * R + r][:, :], w2[:, :], h[:, (1 - j) * R + r, :], start=True, stop=True).then_inc(radial, 1)
                for r in range(R):
                    pe.wait_ge(acted, loads * R + (r + 1 + R))
                    pe.wait_ge(taken, loads * R + (r + 1))
                    nc.tensor.matmul(ps_r[R + r][:, :], w2[:, :], h[:, R + r, :], start=True, stop=True).then_inc(radial, 1)
                for g in range(G1):
                    pe.wait_ge(made, g + 1)
                    for m in range(4):
                        ins = nc.tensor.transpose(bank[g][:, m, :], rows[:, g, m, :], k.ident[:, :])
                    ins.then_inc(turned, 1)

            @block.scalar
            def _(act):
                act.sem_inc(acted, 2 * R)
                act.sem_inc(radial, R)
                with act.Fori(0, loads // 2) as i:
                    for r in range(2 * R):
                        act.wait_ge(hid, i * (2 * R) + (r + 1 + 2 * R))
                        act.wait_ge(radial, i * (2 * R) + (r + 1))
                        nc.scalar.activation(h[:, r, :], ps_h[r], ACT.Silu, scale=float(10.0 ** -0.5)).then_inc(acted, 1)

            @block.gpsimd
            def _(pool):
                for g in range(G1):
                    nc.gpsimd.indirect_dma_start(
                        out=angular[:, g].rearrange("p e m -> p (e m)"), out_offset=None, in_=attr_tab,
                        in_offset=bass.IndirectOffsetOnAxis(ap=e.chunk[:, g:g + 1], axis=0)).then_inc(by_step, 16)
                with pool.Fori(0, loads // 2) as i:
                    for j in range(2):
                        pool.wait_ge(k.armed, 1)
                        pool.wait_ge(taken, i * (2 * R) + (j * R + 4 * R))
                        pool.dma_start(rad_loads[ds(i * 2 + j, 1)].rearrange("l a n -> (l a) n"), rad[:, j, :]).then_inc(stored[j], 16)
                for j in range(2):
                    pool.wait_ge(stored[j], 16 * (loads // 2))
                for g in range(G1):
                    nc.gpsimd.indirect_dma_start(
                        out=radial_by_step[:, g], out_offset=None, in_=rad_tab,
                        in_offset=bass.IndirectOffsetOnAxis(ap=e.chunk[:, g:g + 1], axis=0)).then_inc(by_step, 16)

            @block.vector
            def _(dve):
                v = nc.vector
                v.memset(w1[:, :], 0.0).then_inc(zeroed, 1)
                v.memset(w2[:, :], 0.0).then_inc(zeroed, 1)
                v.memset(h[:, R:2 * R, :], 0.0).then_inc(zeroed, 1)
                dve.sem_inc(taken, 2 * R)
                dve.wait_ge(radial, 2 * R)
                dve.sem_inc(taken, R)

                def turn(i, first=False):
                    for j in range(2):
                        if not first:
                            dve.wait_ge(stored[j], i * 16)
                        for r in range(R):
                            dve.wait_ge(radial, i * (2 * R) + (j * R + r + 1 + 2 * R))
                            v.tensor_scalar(rad[:, j, r * Q:(r + 1) * Q], ps_r[j * R + r][:, :], float(SILU_NORM / 8.0 * scale), None,
                                            ALU.mult).then_inc(taken, 1)
                turn(0, True)
                with dve.Fori(1, loads // 2) as i:
                    turn(i)
                dve.wait_ge(by_step, 32 * G1)
                for g in range(G1):
                    v.tensor_tensor(rows[:, g], angular[:, g].rearrange("p e m -> p m e"),
                                    wide(radial_by_step[:, g].unsqueeze(1), [P, 4, P]), ALU.mult).then_inc(made, 1)
                for g in range(G1):
                    dve.wait_ge(turned, g + 1)
                    ins = v.tensor_copy(factor[:, g * P:(g + 1) * P, :].rearrange("p t m -> p m t"), bank[g][:, :, :])
                ins.then_inc(chain, 1)
                dve.wait_ge(chain, 1)


def gram1(nc, k, x_tab, sums):
    with Scope(nc) as s:
        xn = s.sb("g1_xn", [P, B5, D])
        xp = s.sb("g1_xp", [P, B5, D])
        zero = s.sb("g1_zero", [P, 512])
        ps = [s.ps(f"g1_{c}", [P, 512]) for c in range(KC)]
        ps_row = s.ps("g1_row", [P, 512])
        normed, used, zeroed, done, moved = (s.sem("g1_" + q) for q in ("normed", "used", "zeroed", "done", "moved"))
        out = [s.sem(f"g1_out{j}") for j in range(B5)]
        with nc.Block() as block:
            @block.scalar
            def _(act):
                def turn(i, first=False):
                    for j in range(B5):
                        act.wait_ge(used, i * B5 + j + 1)
                        if not first:
                            act.wait_ge(out[j], i * 16)
                        act.wait_ge(k.armed, 1)
                        b = i * B5 + j
                        for lo, n, m in ((0, 64, 1), (64, 192, 3)):
                            nc.scalar.activation(xp[:, j, lo:lo + n].rearrange("p (m i) -> p m i", m=m),
                                                 k.X[:, ds(b, 1), lo:lo + n].rearrange("p b d -> p (b d)").rearrange("p (i m) -> p m i", m=m),
                                                 ACT.Identity, bias=k.shift[:, ds(b, 1)], scale=k.rstd[:, ds(b, 1)])
                        normed_block(nc, k, act, b, xn[:, j, :], normed)
                turn(0, True)
                with act.Fori(1, NB // B5) as i:
                    turn(i)

            @block.sync
            def _(sp):
                with sp.Fori(0, NB // B5) as i:
                    for j in range(B5):
                        sp.wait_ge(normed, i * B5 + j + 1)
                        sp.dma_start(x_tab[ds((i * B5 + j) * P, P), :], xp[:, j, :]).then_inc(out[j], 16)
                for j in range(B5):
                    sp.wait_ge(out[j], 16 * (NB // B5))

            @block.tensor
            def _(pe):
                pe.sem_inc(used, B5)
                pe.wait_ge(zeroed, 1)
                for x in (*ps, ps_row):
                    nc.tensor.matmul(x[:, :], zero[:, 0:P], zero[:, :], start=True, stop=False, skip_group_check=True)
                with pe.Fori(0, NB // B5) as i:
                    for j in range(B5):
                        pe.wait_ge(normed, i * B5 + j + 1)
                        for c in range(KC):
                            nc.tensor.matmul(ps[c][:, 0:D], xn[:, j, c * P:(c + 1) * P], xn[:, j, :], start=False, stop=False, skip_group_check=True)
                            nc.tensor.matmul(ps[c][:, D:D + 1], xn[:, j, c * P:(c + 1) * P], k.ones[:, 0:1], start=False, stop=False, skip_group_check=True)
                        nc.tensor.matmul(ps_row[0:1, 0:D], k.ones[:, 0:1], xn[:, j, :], start=False, stop=False, skip_group_check=True).then_inc(used, 1)
                pe.wait_ge(used, NB + B5)
                pe.sem_inc(done, 1)

            @block.vector
            def _(dve):
                v = nc.vector
                v.memset(zero[:, :], 0.0).then_inc(zeroed, 1)
                dve.wait_ge(done, 1)
                for c in range(KC):
                    v.tensor_copy(sums[:, c, 0:D + 1], ps[c][:, 0:D + 1])
                v.tensor_copy(sums[0:1, 2, 0:D], ps_row[0:1, 0:D]).then_inc(moved, 1)
                dve.wait_ge(moved, 1)


def mixer_matrix1(nc, k, sums, G, g_bias):
    HD = 32
    with Scope(nc) as s:
        u = s.sb("m1x_u", [P, KC, D])
        vs = s.sb("m1x_vs", [1, D])
        pT = s.sb("m1x_pT", [P, KC, P])
        mask = s.sb("m1x_mask", [P, P])
        t = s.sb("m1x_t", [P, KC, D])
        n_row = s.sb("m1x_n", [1, 1])
        ps = [s.ps(f"m1x_{j}", [P, 512]) for j in range(6)]
        step, ready = s.sem("m1x_step"), s.sem("m1x_ready")
        wkT, wvT, wfcT = k.fcT
        bk, bv, bfc = (k.bias1[:, j * D:(j + 1) * D] for j in range(3))
        with nc.Block() as block:
            @block.tensor
            def _(pe):
                pe.wait_ge(step, 1)
                for c in range(KC):
                    for q in range(KC):
                        nc.tensor.matmul(ps[c][:, 0:D], sums[:, q, c * P:(c + 1) * P], wvT[:, q, :], start=(q == 0), stop=False)
                    nc.tensor.matmul(ps[c][:, 0:D], sums[0:1, 2, c * P:(c + 1) * P], bv, start=False, stop=True)
                for q in range(KC):
                    nc.tensor.matmul(ps[2][0:1, 0:D], sums[:, q, D:D + 1], wvT[:, q, :], start=(q == 0), stop=False)
                nc.tensor.matmul(ps[2][0:1, 0:D], n_row[:, :], bv, start=False, stop=True).then_inc(ready, 1)
                pe.wait_ge(step, 2)
                for c in range(KC):
                    for q in range(KC):
                        nc.tensor.matmul(ps[3][:, c * P:(c + 1) * P], u[:, q, c * P:(c + 1) * P], wkT[:, q, c * P:(c + 1) * P],
                                         start=(q == 0), stop=False, skip_group_check=True)
                    ins = nc.tensor.matmul(ps[3][:, c * P:(c + 1) * P], vs[:, c * P:(c + 1) * P], bk[:, c * P:(c + 1) * P],
                                           start=False, stop=True, skip_group_check=True)
                ins.then_inc(ready, 1)
                pe.wait_ge(step, 3)
                for c in range(KC):
                    ins = nc.tensor.matmul(ps[c][:, 0:D], pT[:, c, :], wfcT[:, c, :], start=True, stop=True)
                ins.then_inc(ready, 1)
                pe.wait_ge(step, 4)
                for c in range(KC):
                    for q in range(KC):
                        nc.tensor.matmul(ps[4 + c][:, 0:D], k.fc_q[:, q, c * P:(c + 1) * P], t[:, q, :], start=(q == 0), stop=(q == KC - 1))
                for q in range(KC):
                    nc.tensor.matmul(ps[2][0:1, 0:D], k.bq_col[:, q:q + 1], t[:, q, :], start=(q == 0), stop=False)
                nc.tensor.matmul(ps[2][0:1, 0:D], k.ones[0:1, 0:1], bfc, start=False, stop=True).then_inc(ready, 1)

            @block.vector
            def _(dve):
                v = nc.vector
                v.memset(n_row[:, :], float(N))
                v.memset(mask[:, :], 0.0).then_inc(step, 1)
                dve.wait_ge(step, 1)
                for h in range(P // HD):
                    v.memset(mask[h * HD:(h + 1) * HD, h * HD:(h + 1) * HD], 1.0 / N)
                dve.wait_ge(ready, 1)
                for c in range(KC):
                    v.tensor_copy(u[:, c, :], ps[c][:, 0:D])
                v.tensor_copy(vs[:, :], ps[2][0:1, 0:D]).then_inc(step, 1)
                dve.wait_ge(ready, 2)
                dve.wait_ge(step, 2)
                v.tensor_tensor(pT[:, :, :], ps[3][:, 0:2 * P].rearrange("p (c d) -> p c d", d=P),
                                wide(mask[:, :].unsqueeze(1), [P, KC, P]), ALU.mult).then_inc(step, 1)
                dve.wait_ge(ready, 3)
                v.tensor_copy(t[:, 0, :], ps[0][:, 0:D])
                v.tensor_copy(t[:, 1, :], ps[1][:, 0:D]).then_inc(step, 1)
                dve.wait_ge(ready, 4)
                for c in range(KC):
                    v.tensor_copy(G[:, c, :], ps[4 + c][:, 0:D])
                v.tensor_copy(g_bias[:, :], ps[2][0:1, 0:D]).then_inc(step, 1)
                dve.wait_ge(step, 5)


def convolve(nc, k, e, x_tab, factor, acc):
    turns = T1 // U
    M = 64
    with Scope(nc) as s:
        ix = s.sb("cv_ix", [P, 2, U], I32)
        xg = s.sb("cv_x", [P, 2, U, D])
        hot = s.sb("cv_hot", [P, 2, U, P])
        msg = s.sb("cv_msg", [P, 2, U, 512])
        s1w = s.sb("cv_s1w", [P, U, 3, M])
        ps = [s.ps(f"cv_ps{u}", [P, 512]) for u in range(U)]
        listed, freed, built, chain, summed, added = (s.sem("cv_" + q) for q in ("listed", "freed", "built", "chain", "summed", "added"))
        scaled = s.sem("cv_scaled")
        got = [s.sem(f"cv_got{h}") for h in range(2)]
        with nc.Block() as block:
            @block.gpsimd
            def _(pool):
                def turn(i, h):
                    pool.wait_ge(freed, i + 1)
                    pool.wait_ge(scaled, i + 1)
                    pool.wait_ge(k.armed, 1)
                    nc.gpsimd.tensor_copy(ix[:, h, :], e.src[:, ds(i * U, U)]).then_inc(listed, 1)
                    pool.wait_ge(k.armed, 1)
                    pool.wait_ge(listed, i + 1)
                    for u in range(U):
                        nc.gpsimd.indirect_dma_start(
                            out=xg[:, h, u, :], out_offset=None, in_=x_tab,
                            in_offset=bass.IndirectOffsetOnAxis(ap=ix[:, h, u:u + 1], axis=0)).then_inc(got[h], 16)
                with pool.Fori(0, turns // 2) as w:
                    turn(w * 2, 0)
                    turn(w * 2 + 1, 1)
                turn(turns - 1, 0)

            @block.tensor
            def _(pe):
                def turn(i, h):
                    pe.wait_ge(built, i + 1)
                    pe.wait_ge(scaled, i + 3)
                    for u in range(U):
                        pe.wait_ge(added, i * (2 * U) + (2 * u + 2))
                        nc.tensor.matmul(ps[u][:, :], hot[:, h, u, :], msg[:, h, u, :], start=True, stop=True).then_inc(summed, 1)
                with pe.Fori(0, turns // 2) as w:
                    turn(w * 2, 0)
                    turn(w * 2 + 1, 1)
                turn(turns - 1, 0)

            @block.scalar
            def _(act):
                act.sem_inc(scaled, 2)
                act.sem_inc(summed, 2 * U)

                def turn(i, w, h):
                    act.wait_ge(got[h], w * (16 * U) + 16 * U)
                    act.wait_ge(summed, i * U + U)
                    act.wait_ge(k.armed, 1)
                    for u in range(U):
                        nc.scalar.activation(msg[:, h, u, 0:D], xg[:, h, u, :], ACT.Copy, scale=factor[:, ds(i * U + u, 1), 0])
                        for m in range(3):
                            ins = nc.scalar.activation(msg[:, h, u, D + m * M:D + (m + 1) * M], xg[:, h, u, 0:M], ACT.Copy,
                                                       scale=factor[:, ds(i * U + u, 1), 1 + m])
                    ins.then_inc(scaled, 1)
                with act.Fori(0, turns // 2) as w:
                    turn(w * 2, w, 0)
                    turn(w * 2 + 1, w, 1)
                turn(turns - 1, turns // 2, 0)

            @block.vector
            def _(dve):
                v = nc.vector
                dve.sem_inc(added, 2 * U)
                dve.sem_inc(freed, 2)
                S = [P, U, 3, M]

                def build(i, w, h):
                    v.tensor_tensor(hot[:, h], wide(k.count_row[:, 0:P].unsqueeze(1), [P, U, P]),
                                    wide(e.rel[:, ds(i * U, U)].unsqueeze(2), [P, U, P]), ALU.is_equal)
                    dve.wait_ge(got[h], (0 if w is None else w) * (16 * U) + 16 * U)
                    if w is not None:
                        dve.wait_ge(built, i)
                    dve.wait_ge(k.armed, 1)
                    weights = wide(factor[:, ds(i * U, U), 1:4].unsqueeze(3), S)
                    v.tensor_tensor(s1w[:, :, :, :], xg[:, h, :, M:D].rearrange("p u (m i) -> p u m i", m=3), weights, ALU.mult).then_inc(freed, 1)
                    last = msg[:, h, :, D + 3 * M:512]
                    dve.wait_ge(freed, i + 3)
                    v.tensor_tensor(last, s1w[:, :, 0, :], s1w[:, :, 1, :], ALU.add).then_inc(chain, 1)
                    dve.wait_ge(chain, i + 1)
                    v.tensor_tensor(last, last, s1w[:, :, 2, :], ALU.add).then_inc(built, 1)

                def add(i):
                    for u, b in enumerate(blocks_of(nc, mybir.EngineType.DVE, e, i)):
                        dve.wait_ge(summed, i * U + (u + 1 + 2 * U))
                        for n in range(2):
                            dve.wait_ge(added, i * (2 * U) + (2 * (u + U) + n - 1))
                            dve.wait_ge(k.armed, 1)
                            row = acc[:, ds(b, 1), n * D:(n + 1) * D].rearrange("p a w -> p (a w)")
                            v.tensor_tensor(row, row, ps[u][:, n * D:(n + 1) * D], ALU.add).then_inc(added, 1)
                build(0, None, 0)
                with dve.Fori(0, turns // 2) as w:
                    build(w * 2 + 1, w, 1)
                    add(w * 2)
                    build(w * 2 + 2, w + 1, 0)
                    add(w * 2 + 1)
                add(turns - 1)
                dve.wait_ge(added, 2 * (T1 + U))


def combine1(nc, k, a, acc, G, g_bias):
    M = 64
    with Scope(nc) as s:
        xn = s.sb("c1_xn", [P, B5, D])
        ac = s.sb("c1_ac", [P, B5, 512])
        xT = s.sb("c1_xT", [P, B5, KC, P])
        aT = s.sb("c1_aT", [P, B5, 4, P])
        w = s.sb("c1_w", [P, 4, D])
        raw = s.sb("c1_raw", [P, 4, M])
        ps_t = s.ps("c1_t", [P, 512])
        ps_a = s.ps("c1_a", [P, 512])
        ps_o = [s.ps(f"c1_o{j}", [P, 512]) for j in range(B5)]
        got, cleared, wready, normed, turned, kept, done, chain = (
            s.sem("c1_" + q) for q in ("got", "cleared", "wready", "normed", "turned", "kept", "done", "chain"))
        names = ("L1_gnn_w_00_0", "L1_gnn_w_10_1", "L1_gnn_w_01_1", "L1_gnn_w_11_0")
        with nc.Block() as block:
            @block.sync
            def _(sp):
                for j, n in enumerate(names):
                    for half in range(2):
                        sp.dma_start(raw[half * M:(half + 1) * M, j, :], a[n]).then_inc(got, 16)
                sp.wait_ge(got, 128)

            @block.scalar
            def _(act):
                with act.Fori(0, NB // B5) as i:
                    for j in range(B5):
                        b = i * B5 + j
                        act.wait_ge(turned, b + 1)
                        act.wait_ge(k.armed, 1)
                        nc.scalar.activation(ac[:, j, :], acc[:, ds(b, 1), :].rearrange("p a w -> p (a w)"), ACT.Copy)
                        normed_block(nc, k, act, b, xn[:, j, :], normed)

            @block.tensor
            def _(pe):
                pe.sem_inc(turned, B5)
                pe.wait_ge(wready, 1)
                with pe.Fori(0, NB // B5) as i:
                    for j in range(B5):
                        b = i * B5 + j
                        pe.wait_ge(normed, b + 1)
                        pe.wait_ge(kept, b + 1)
                        for c in range(KC):
                            nc.tensor.transpose(ps_t[:, c * P:(c + 1) * P], xn[:, j, c * P:(c + 1) * P], k.ident[:, :])
                        for c in range(4):
                            ins = nc.tensor.transpose(ps_a[:, c * P:(c + 1) * P], ac[:, j, c * P:(c + 1) * P], k.ident[:, :])
                        ins.then_inc(turned, 1)
                        pe.wait_ge(kept, b + 2)
                        nc.tensor.matmul(ps_o[j][:, 0:D], k.ones[0:1, :], g_bias[:, :], start=True, stop=False)
                        for c in range(KC):
                            nc.tensor.matmul(ps_o[j][:, 0:D], xT[:, j, c, :], G[:, c, :], start=False, stop=False)
                        for c in range(4):
                            ins = nc.tensor.matmul(ps_o[j][:, 0:D], aT[:, j, c, :], w[:, c, :], start=False, stop=(c == 3))
                        ins.then_inc(done, 1)

            @block.vector
            def _(dve):
                v = nc.vector
                v.memset(w[:, :, :], 0.0).then_inc(cleared, 1)
                dve.wait_ge(cleared, 1)
                dve.wait_ge(got, 128)
                for r in range(8):
                    lo, c = (r % 2) * M, r // 2
                    if r == 0:
                        ins = v.tensor_copy(w[lo:lo + M, c, 0:M], raw[lo:lo + M, 0, :])
                    elif r == 7:
                        ins = v.tensor_scalar(w[lo:lo + M, c, 0:M], raw[lo:lo + M, 3, :], float(3.0 ** -0.5), None, ALU.mult)
                    else:
                        m, j = (r - 1, 1) if r < 4 else (r - 4, 2)
                        ins = v.tensor_copy(w[lo:lo + M, c, M + m:D:3], raw[lo:lo + M, j, :])
                ins.then_inc(wready, 1)
                dve.sem_inc(kept, 1)
                with dve.Fori(0, NB // B5) as i:
                    for j in range(B5):
                        b = i * B5 + j
                        xb = k.X[:, ds(b, 1), :].rearrange("p a d -> p (a d)")
                        dve.wait_ge(turned, b + B5 + 1)
                        v.tensor_copy(xT[:, j], ps_t[:, 0:D].rearrange("p (c t) -> p c t", t=P))
                        v.tensor_copy(aT[:, j], ps_a[:, :].rearrange("p (c t) -> p c t", t=P)).then_inc(kept, 1)
                        dve.wait_ge(done, b + 1)
                        dve.wait_ge(k.armed, 1)
                        v.tensor_tensor(xb, xb, ps_o[j][:, 0:D], ALU.add).then_inc(chain, 1)
                dve.wait_ge(chain, NB)


GW = 16 + H2


def gate_rows(nc, k, h_tab, d_parts, xnT, row_cols):
    with Scope(nc) as s:
        xn = s.sb("gr_xn", [P, B5, D])
        xT = s.sb("gr_xT", [P, B5, KC, P])
        h = s.sb("gr_h", [P, B5, GW + H2])
        as_dst = s.sb("gr_as_dst", [P, NB, H2])
        pr = s.sb("gr_pr", [P, 2, 16])
        ps_t = s.ps("gr_t", [P, KC, P])
        ps_h = [s.ps(f"gr_h{j}", [P, 16]) for j in range(B5)]
        ps_c = s.ps("gr_c", [P, 80])
        normed, turned, kept, done, ready, chain, spread = (
            s.sem("gr_" + q) for q in ("normed", "turned", "kept", "done", "ready", "chain", "spread"))
        out = [s.sem(f"gr_out{j}") for j in range(B5)]
        PER = 4
        with nc.Block() as block:
            @block.scalar
            def _(act):
                with act.Fori(0, NB // B5) as i:
                    for j in range(B5):
                        act.wait_ge(turned, i * B5 + j + 1)
                        act.wait_ge(k.armed, 1)
                        normed_block(nc, k, act, i * B5 + j, xn[:, j, :], normed)

            @block.sync
            def _(sp):
                with sp.Fori(0, NB // B5) as i:
                    for j in range(B5):
                        sp.wait_ge(ready, i * B5 + j + 1)
                        sp.dma_start(h_tab[ds((i * B5 + j) * P, P), :], h[:, j, 0:GW]).then_inc(out[j], 16)
                for j in range(B5):
                    sp.wait_ge(out[j], 16 * (NB // B5))

            @block.tensor
            def _(pe):
                nc.tensor.matmul(ps_c[:, :], k.ones[0:1, :], k.gat_rows[:, :], start=True, stop=True).then_inc(spread, 1)
                pe.sem_inc(turned, B5)
                with pe.Fori(0, NB // B5) as i:
                    for j in range(B5):
                        b = i * B5 + j
                        pe.wait_ge(normed, b + 1)
                        pe.wait_ge(kept, 2 * b + 1)
                        for c in range(KC):
                            ins = nc.tensor.transpose(ps_t[:, c, :], xn[:, j, c * P:(c + 1) * P], k.ident[:, :])
                        ins.then_inc(turned, 1)
                        pe.wait_ge(kept, 2 * b + 3)
                        for c in range(KC):
                            ins = nc.tensor.matmul(ps_h[j][:, :], xT[:, j, c, :], k.gat_w[:, c, :], start=(c == 0), stop=(c == KC - 1))
                        ins.then_inc(done, 1)

            @block.vector
            def _(dve):
                v = nc.vector
                dve.sem_inc(kept, 1)
                dve.wait_ge(spread, 1)
                v.tensor_copy(row_cols[:, :], ps_c[:, :]).then_inc(chain, 1)
                dve.wait_ge(chain, 1)

                def turn(i, first=False):
                    c = Chain(dve, chain, i * (PER * B5) + 1)
                    for j in range(B5):
                        b = i * B5 + j
                        dve.wait_ge(turned, b + B5 + 1)
                        v.tensor_copy(xT[:, j], ps_t[:, :, :]).then_inc(kept, 1)
                        v.tensor_copy(xnT[:, :, ds(b * P, P)], ps_t[:, :, :]).then_inc(kept, 1)
                        if not first:
                            dve.wait_ge(out[j], i * 16)
                        dve.wait_ge(done, b + 1)
                        c.link(v.tensor_copy(h[:, j, 0:16], ps_h[j][:, :]))
                        v.tensor_tensor(pr[:, 0], h[:, j, 0:16], row_cols[:, 0:16], ALU.mult)
                        c.link(v.tensor_tensor(pr[:, 1], h[:, j, 0:16], row_cols[:, 16:32], ALU.mult))
                        c.link(v.tensor_reduce(h[:, j, 16:24], pr[:, :, :].rearrange("p a (h e) -> p (a h) e", e=NX), AX.X, ALU.add))
                        dve.sem_inc(ready, 1)
                        c.link(v.tensor_copy(as_dst[:, ds(b, 1), :].rearrange("p a h -> p (a h)"), h[:, j, GW:GW + H2]))
                    assert c.n == PER * B5
                turn(0, True)
                with dve.Fori(1, NB // B5) as i:
                    turn(i)
                c = Chain(dve, chain, NB * PER + 1)
                c.link(v.tensor_copy(d_parts[:, :, 0, :], as_dst[:, :, :]))
                for n in range(2):
                    c.link(v.tensor_tensor(as_dst[:, :, :], as_dst[:, :, :], d_parts[:, :, n, :], ALU.subtract))
                    c.link(v.tensor_copy(d_parts[:, :, n + 1, :], as_dst[:, :, :]))


def gate_scores(nc, k, e, h_tab, d_parts, rows, score):
    turns = T2 // U
    with Scope(nc) as s:
        ix = s.sb("gs_ix", [P, 2, U], I32)
        hg = s.sb("gs_h", [P, 2, U, GW])
        rel_row = s.sb("gs_rel_row", [1, 2, U * P], BF)
        hot = s.sb("gs_hot", [P, 2, U * P], BF)
        t = s.sb("gs_t", [P, U, H2])
        ps_b = s.ps("gs_b", [P, U * P])
        ps_d = [s.ps(f"gs_d{h}", [P, 512]) for h in range(2)]
        listed, freed, spread, hotted, asked, chain, took = (
            s.sem("gs_" + q) for q in ("listed", "freed", "spread", "hotted", "asked", "chain", "took"))
        got = [s.sem(f"gs_got{h}") for h in range(2)]
        row = [s.sem(f"gs_row{h}") for h in range(2)]
        assert turns % 2 == 1
        with nc.Block() as block:
            @block.gpsimd
            def _(pool):
                def turn(i, h):
                    pool.wait_ge(freed, i + 1)
                    pool.wait_ge(k.armed, 1)
                    nc.gpsimd.tensor_copy(ix[:, h, :], e.src[:, ds(i * U, U)]).then_inc(listed, 1)
                    pool.wait_ge(k.armed, 1)
                    pool.wait_ge(listed, i + 1)
                    for u in range(U):
                        nc.gpsimd.indirect_dma_start(
                            out=hg[:, h, u, :], out_offset=None, in_=h_tab,
                            in_offset=bass.IndirectOffsetOnAxis(ap=ix[:, h, u:u + 1], axis=0)).then_inc(got[h], 16)
                with pool.Fori(0, turns // 2) as w:
                    turn(w * 2, 0)
                    turn(w * 2 + 1, 1)
                turn(turns - 1, 0)

            @block.sync
            def _(sp):
                def turn(i, h):
                    sp.wait_ge(spread, i + 1)
                    sp.dma_start(rel_row[:, h, :], e.rel_rows[ds(i * U, U), :].rearrange("t e -> (t e)").rearrange("(a n) -> a n", a=1)).then_inc(row[h], 16)
                with sp.Fori(0, turns // 2) as w:
                    turn(w * 2, 0)
                    turn(w * 2 + 1, 1)
                turn(turns - 1, 0)

            @block.tensor
            def _(pe):
                pe.sem_inc(spread, 2)

                def spread_row(i, w, h):
                    pe.wait_ge(row[h], w * 16 + 16)
                    pe.wait_ge(hotted, i + 1)
                    for n in range(0, U * P, 512):
                        ins = nc.tensor.matmul(ps_b[:, n:n + 512], k.ones_h[:, :], rel_row[:, h, n:n + 512], start=True, stop=True)
                    ins.then_inc(spread, 1)

                def fetch(i, h):
                    pe.wait_ge(hotted, i + 2)
                    pe.wait_ge(freed, i + 1)
                    pe.wait_ge(k.armed, 1)
                    for u, b in enumerate(blocks_of(nc, mybir.EngineType.PE, e, i)):
                        for n in range(3):
                            ins = nc.tensor.matmul(ps_d[h][:, u * H2:(u + 1) * H2], hot[:, h, u * P:(u + 1) * P],
                                                   d_parts[:, ds(b, 1), n, :].rearrange("p a h -> p (a h)"), start=(n == 0), stop=(n == 2))
                    ins.then_inc(asked, 1)
                spread_row(0, 0, 0)
                with pe.Fori(0, turns // 2) as w:
                    spread_row(w * 2 + 1, w, 1)
                    fetch(w * 2, 0)
                    spread_row(w * 2 + 2, w + 1, 0)
                    fetch(w * 2 + 1, 1)
                fetch(turns - 1, 0)

            @block.vector
            def _(dve):
                v = nc.vector
                dve.sem_inc(freed, 2)
                dve.sem_inc(hotted, 1)

                def mark(i, h):
                    dve.wait_ge(spread, i + 3)
                    v.tensor_scalar(hot[:, h, :], ps_b[:, :], k.count_col[:, 0:1], None, ALU.is_equal).then_inc(hotted, 1)

                def add(i, w, h):
                    dve.wait_ge(got[h], w * (16 * U) + 16 * U)
                    dve.wait_ge(asked, i + 1)
                    v.tensor_tensor(t[:, :, :], hg[:, h, :, 16:GW], ps_d[h][:, 0:U * H2].rearrange("p (u h) -> p u h", h=H2), ALU.add).then_inc(chain, 1)
                    dve.wait_ge(k.armed, 1)
                    v.tensor_copy(rows[:, ds(i * U, U), :], hg[:, h, :, 0:16]).then_inc(freed, 1)
                    dve.wait_ge(chain, i * 2 + 1)
                    v.scalar_tensor_tensor(out=score[:, ds(i * U, U), :], in0=t[:, :, :], scalar=0.2, in1=t[:, :, :],
                                           op0=ALU.mult, op1=ALU.max).then_inc(chain, 1)
                    dve.wait_ge(chain, i * 2 + 2)
                mark(0, 0)
                with dve.Fori(0, turns // 2) as w:
                    mark(w * 2 + 1, 1)
                    add(w * 2, w, 0)
                    mark(w * 2 + 2, 0)
                    add(w * 2 + 1, w, 1)
                add(turns - 1, turns // 2, 0)
                v.memset(score[:, T2:G2 * P, :], 0.0).then_inc(took, 1)
                dve.wait_ge(took, 1)
                dve.wait_ge(freed, turns + 2)


def gate_sums(nc, k, e, rows, weight, acc):
    W = 16 + H2
    turns = T2 // U
    with Scope(nc) as s:
        msg = s.sb("gu_msg", [P, 2, U, W])
        hot = s.sb("gu_hot", [P, 2, U, P])
        ps = [s.ps(f"gu_ps{u}", [P, 512]) for u in range(U)]
        built, summed, added = (s.sem("gu_" + q) for q in ("built", "summed", "added"))
        with nc.Block() as block:
            @block.tensor
            def _(pe):
                def turn(i, h):
                    pe.wait_ge(built, i + 1)
                    for u in range(U):
                        pe.wait_ge(added, i * U + (u + 1))
                        nc.tensor.matmul(ps[u][:, 0:W], hot[:, h, u, :], msg[:, h, u, :], start=True, stop=True).then_inc(summed, 1)
                with pe.Fori(0, turns // 2) as w:
                    turn(w * 2, 0)
                    turn(w * 2 + 1, 1)
                turn(turns - 1, 0)

            @block.vector
            def _(dve):
                v = nc.vector
                dve.sem_inc(added, U)

                def build(i, h):
                    v.tensor_tensor(hot[:, h], wide(k.count_row[:, 0:P].unsqueeze(1), [P, U, P]),
                                    wide(e.rel[:, ds(i * U, U)].unsqueeze(2), [P, U, P]), ALU.is_equal)
                    v.tensor_copy(msg[:, h, :, 16:W], weight[:, ds(i * U, U), :])
                    v.tensor_tensor(msg[:, h, :, 0:16].rearrange("p u (g d) -> p u g d", d=NX),
                                    rows[:, ds(i * U, U), :].rearrange("p u (g d) -> p u g d", d=NX),
                                    wide(weight[:, ds(i * U, U), :].unsqueeze(3), [P, U, H2, NX]), ALU.mult).then_inc(built, 1)

                def add(i):
                    for u, b in enumerate(blocks_of(nc, mybir.EngineType.DVE, e, i)):
                        dve.wait_ge(summed, i * U + (u + 1))
                        dve.wait_ge(added, i * U + (u + U))
                        dve.wait_ge(k.armed, 1)
                        v.tensor_tensor(acc[:, ds(b, 1), :].rearrange("p a w -> p (a w)"),
                                        acc[:, ds(b, 1), :].rearrange("p a w -> p (a w)"),
                                        ps[u][:, 0:W], ALU.add).then_inc(added, 1)
                build(0, 0)
                with dve.Fori(0, turns // 2) as w:
                    build(w * 2 + 1, 1)
                    add(w * 2)
                    build(w * 2 + 2, 0)
                    add(w * 2 + 1)
                add(turns - 1)
                dve.wait_ge(added, T2 + U)


def top_two(nc, k, acc, row_cols, gates):
    with Scope(nc) as s:
        S16, S4 = [P, NB, 16], [P, NB, NX]
        t = s.sb("tt_t", [P, 3, NB, 16])
        q = s.sb("tt_q", [P, 8, NB, NX])
        r = s.sb("tt_r", [P, 10, NB])
        chain, ask, ans = s.sem("tt_chain"), s.sem("tt_ask"), s.sem("tt_ans")
        with nc.Block() as block:
            @block.scalar
            def _(act):
                act.wait_ge(ask, 1)
                nc.scalar.activation(r[:, 3], r[:, 2], ACT.Sqrt).then_inc(ans, 1)
                act.wait_ge(ask, 2)
                nc.scalar.activation(r[:, 7], r[:, 6], ACT.Exp).then_inc(ans, 1)

            @block.vector
            def _(dve):
                v = nc.vector
                c = Chain(dve, chain)
                row = lambda j: wide(row_cols[:, 16 * j:16 * j + 16].unsqueeze(1), S16)
                c.link(v.tensor_scalar(q[:, 0], acc[:, :, 16:20], 1e-16, None, ALU.add))
                c.link(v.reciprocal(q[:, 1], q[:, 0]))
                c.link(v.tensor_tensor(t[:, 0].rearrange("p b (h e) -> p b h e", e=NX),
                                       acc[:, :, 0:16].rearrange("p b (h e) -> p b h e", e=NX),
                                       wide(q[:, 1].unsqueeze(3), [P, NB, H2, NX]), ALU.mult))
                c.link(v.tensor_tensor(t[:, 0], t[:, 0], row(2), ALU.add))
                c.link(v.tensor_reduce(r[:, 0], t[:, 0], AX.X, ALU.add))
                c.link(v.tensor_scalar(r[:, 0], r[:, 0], 1.0 / 16, None, ALU.mult))
                c.link(v.tensor_tensor(t[:, 0], t[:, 0], wide(r[:, 0].unsqueeze(2), S16), ALU.subtract))
                c.link(v.tensor_tensor(t[:, 1], t[:, 0], t[:, 0], ALU.mult))
                c.link(v.tensor_reduce(r[:, 1], t[:, 1], AX.X, ALU.add))
                c.link(v.tensor_scalar(r[:, 1], r[:, 1], 1.0 / 16, EPS, ALU.mult, ALU.add))
                v.reciprocal(r[:, 2], r[:, 1]).then_inc(ask, 1)
                dve.wait_ge(ans, 1)
                c.link(v.tensor_tensor(t[:, 0], t[:, 0], wide(r[:, 3].unsqueeze(2), S16), ALU.mult))
                c.link(v.tensor_tensor(t[:, 0], t[:, 0], row(3), ALU.mult))
                c.link(v.tensor_tensor(t[:, 0], t[:, 0], row(4), ALU.add))
                c.link(v.tensor_reduce(q[:, 2], t[:, 0].rearrange("p b (h e) -> p b e h", e=NX), AX.X, ALU.add))
                c.link(v.tensor_scalar(q[:, 2], q[:, 2], 1.0 / H2, None, ALU.mult))
                count = wide(k.count_row[:, 0:NX].unsqueeze(1), S4)

                def first_best(score, best, hot, tmp):
                    c.link(v.tensor_reduce(best, score, AX.X, ALU.max))
                    c.link(v.tensor_tensor(tmp, score, wide(best.unsqueeze(2), S4), ALU.is_lt))
                    c.link(v.scalar_tensor_tensor(out=tmp, in0=tmp, scalar=100.0, in1=count, op0=ALU.mult, op1=ALU.add))
                    c.link(v.tensor_reduce(r[:, 8], tmp, AX.X, ALU.min))
                    c.link(v.tensor_tensor(hot, tmp, wide(r[:, 8].unsqueeze(2), S4), ALU.is_equal))
                first_best(q[:, 2], r[:, 4], q[:, 3], q[:, 5])
                c.link(v.scalar_tensor_tensor(out=q[:, 6], in0=q[:, 3], scalar=LOW, in1=q[:, 2], op0=ALU.mult, op1=ALU.add))
                first_best(q[:, 6], r[:, 5], q[:, 4], q[:, 5])
                v.tensor_tensor(r[:, 6], r[:, 5], r[:, 4], ALU.subtract).then_inc(ask, 1)
                dve.wait_ge(ans, 2)
                c.link(v.tensor_scalar(r[:, 8], r[:, 7], 1.0, None, ALU.add))
                c.link(v.reciprocal(r[:, 9], r[:, 8]))
                c.link(v.tensor_tensor(r[:, 7], r[:, 7], r[:, 9], ALU.mult))
                v.tensor_tensor(q[:, 3], q[:, 3], wide(r[:, 9].unsqueeze(2), S4), ALU.mult)
                c.link(v.tensor_tensor(q[:, 4], q[:, 4], wide(r[:, 7].unsqueeze(2), S4), ALU.mult))
                c.link(v.tensor_tensor(gates[:, :, :], q[:, 3], q[:, 4], ALU.add))


def experts1(nc, k, a, xnT, gates):
    FC = FX // P
    HALF = B5 * P // 2
    with Scope(nc) as s:
        w1 = s.sb("x1_w1", [P, NX, KC, FX])
        w2 = s.sb("x1_w2", [P, NX, FC, D])
        b1 = s.sb("x1_b1", [P, NX, FC])
        b2 = s.sb("x1_b2", [1, NX, D])
        hid = s.sb("x1_hid", [P, 2, FC, B5 * P])
        ps_h = [s.ps(f"x1_h{j}", [P, 512]) for j in range(4)]
        ps_y = [s.ps(f"x1_y{j}", [P, 512]) for j in range(4)]
        got, h_done, h_kept, y_done, added = (s.sem("x1_" + q) for q in ("got", "h_done", "h_kept", "y_done", "added"))
        NH_ = 2 * FC * NX
        NY_ = B5 * NX
        with nc.Block() as block:
            @block.sync
            def _(sp):
                for e in range(NX):
                    sp.dma_start(w1[:, e], a["L1_ffn_W1"][e].rearrange("(c p) f -> p c f", p=P)).then_inc(got, 16)
                    sp.dma_start(w2[:, e], a["L1_ffn_W2"][e].rearrange("(c p) f -> p c f", p=P)).then_inc(got, 16)
                sp.dma_start(b1[:, :, :], a["L1_ffn_b1"].rearrange("e (c p) -> p e c", p=P), allow_slow_non_contiguous=True).then_inc(got, 16)
                sp.dma_start(b2[:, :, :], a["L1_ffn_b2"].rearrange("(a e) d -> a e d", a=1)).then_inc(got, 16)
                sp.wait_ge(got, 160)

            @block.tensor
            def _(pe):
                pe.wait_ge(got, 160)
                with pe.Fori(0, NB // B5) as i:
                    for e in range(NX):
                        for f in range(FC):
                            for half in range(2):
                                n = (e * FC + f) * 2 + half
                                pe.wait_ge(h_kept, i * NH_ + (n + 1))
                                for c in range(KC):
                                    ins = nc.tensor.matmul(ps_h[n % 4][:, 0:HALF], w1[:, e, c, f * P:(f + 1) * P],
                                                           xnT[:, c:c + 1, ds(i * (B5 * P) + half * HALF, HALF)].rearrange("p a t -> p (a t)"),
                                                           start=(c == 0), stop=(c == KC - 1))
                                ins.then_inc(h_done, 1)
                        pe.wait_ge(h_kept, i * NH_ + ((e + 1) * 2 * FC + 4))
                        for j in range(B5):
                            n = e * B5 + j
                            pe.wait_ge(added, i * NY_ + (n + 1))
                            nc.tensor.matmul(ps_y[n % 4][:, 0:D], k.ones[0:1, :], b2[:, e, :], start=True, stop=False)
                            for f in range(FC):
                                ins = nc.tensor.matmul(ps_y[n % 4][:, 0:D], hid[:, e % 2, f, j * P:(j + 1) * P], w2[:, e, f, :],
                                                       start=False, stop=(f == FC - 1))
                            ins.then_inc(y_done, 1)

            @block.scalar
            def _(act):
                act.sem_inc(h_kept, 4)
                with act.Fori(0, NB // B5) as i:
                    for e in range(NX):
                        for f in range(FC):
                            for half in range(2):
                                n = (e * FC + f) * 2 + half
                                act.wait_ge(h_done, i * NH_ + (n + 1))
                                nc.scalar.activation(hid[:, e % 2, f, half * HALF:(half + 1) * HALF], ps_h[n % 4][:, 0:HALF], ACT.Gelu,
                                                     bias=b1[:, e, f:f + 1]).then_inc(h_kept, 1)

            @block.vector
            def _(dve):
                v = nc.vector
                dve.sem_inc(added, 4)
                with dve.Fori(0, NB // B5) as i:
                    for e in range(NX):
                        for j in range(B5):
                            n = e * B5 + j
                            b = i * B5 + j
                            xb = k.X[:, ds(b, 1), :].rearrange("p a d -> p (a d)")
                            dve.wait_ge(y_done, i * NY_ + (n + 1))
                            dve.wait_ge(added, i * NY_ + (n + 1))
                            dve.wait_ge(k.armed, 1)
                            v.scalar_tensor_tensor(out=xb, in0=ps_y[n % 4][:, 0:D],
                                                   scalar=gates[:, ds(b, 1), e:e + 1].rearrange("p a b -> p (a b)"),
                                                   in1=xb, op0=ALU.mult, op1=ALU.add).then_inc(added, 1)
                dve.wait_ge(added, (NB // B5) * NY_ + 4)


def store(nc, k, out):
    with Scope(nc) as s:
        stored = s.sem("stored")
        with nc.Block() as block:
            @block.sync
            def _(sp):
                sp.dma_start(out[0:(NB - 1) * P, :].rearrange("(b p) d -> p b d", p=P), k.X[:, 0:NB - 1, :]).then_inc(stored, 16)
                sp.dma_start(out[(NB - 1) * P:N, :], k.X[0:LAST, NB - 1, :]).then_inc(stored, 16)
                sp.wait_ge(stored, 32)


class Kept:

    def __init__(self, s):
        self.ident = s.sb("ident", [P, P])
        self.ident_h = s.sb("ident_h", [P, P], BF)
        self.ones = s.sb("ones", [P, P])
        self.ones_h = s.sb("ones_h", [1, P], BF)
        self.upper = s.sb("upper", [P, P])
        self.count_row = s.sb("count_row", [P, 512])
        self.count_col = s.sb("count_col", [P, 4])
        self.armed_dummy = s.sb("armed_dummy", [P, 1])
        self.node_id = s.sb("node_id", [P, NB])
        self.node_mask = s.sb("node_mask", [P, NB])
        self.X = s.sb("X", [P, NB, D])
        self.rstd = s.sb("rstd", [P, NB])
        self.shift = s.sb("shift", [P, NB])
        self.W0 = s.sb("W0", [P, KC, 4 * D])
        self.bias0 = s.sb("bias0", [1, 5 * D])
        self.mix_q = s.sb("mix_q", [P, 4, D])
        self.mix_kvT = s.sb("mix_kvT", [P, KC, 1024])
        self.mix_outT = s.sb("mix_outT", [P, 4, D])
        self.dotsT = s.sb("dotsT", [P, 4, P])
        self.gate = s.sb("gate", [P, KC, NE])
        self.gate_b = s.sb("gate_b", [1, NE])
        self.fc_q = s.sb("fc_q", [P, KC, D])
        self.bias1 = s.sb("bias1", [1, 3 * D])
        self.bq_col = s.sb("bq_col", [P, KC])
        self.gat_w = s.sb("gat_w", [P, KC, 16])
        self.gat_rows = s.sb("gat_rows", [1, 80])
        self.fcT = [s.sb(f"fcT{j}", [P, KC, D]) for j in range(3)]


class Graph:

    def __init__(self, s, name, groups):
        self.valid, self.starts, self.ends = (s.sb(name + x, [P, groups, P]) for x in ("valid", "starts", "ends"))
        self.rel = s.sb(name + "rel", [P, groups * P])
        self.src = s.sb(name + "src", [P, groups * P], I32)
        self.rel_rows = s.nc.dram_tensor(name + "rel_rows", [groups * P, P], BF, kind="Internal").ap()
        self.block_row = s.sb(name + "block_row", [1, groups * P], I32)
        self.chunk = s.sb(name + "chunk", [P, groups], I32)


def program(nc, a, out):
    with Scope(nc) as s:
        k = Kept(s)
        k.armed = nc.alloc_semaphore("armed")
        Scope.used.clear()

        def dram(name, shape, dt=F32):
            return nc.dram_tensor(name, shape, dt, kind="Internal").ap()

        def steps(e, name, pairs, chunks, groups, n):
            build_steps(nc, k, name, pairs, chunks, groups, n, e.valid, e.starts, e.ends, e.rel, e.src, e.rel_rows,
                        e.block_row, e.chunk)

        def cleared(scope, name, shape):
            acc, done = scope.sb(name, shape), scope.sem(name + "_cleared")
            with nc.Block() as block:
                @block.vector
                def _(dve):
                    nc.vector.memset(acc[:, :, :], 0.0).then_inc(done, 1)
                    dve.wait_ge(done, 1)
            return acc

        k_tab, v_tab, x_tab = (dram(n + "_tab", [NPAD, D]) for n in "kvx")
        h_tab = dram("h_tab", [NPAD, GW])
        slots, slots_out = dram("expert_rows", [SLOTS + NPAD, D]), dram("expert_out", [SLOTS, D])
        make_constants(nc, k)
        load_all(nc, k, a)
        e1 = Graph(s, "e1_", G1)
        steps(e1, "s1_", a["pairs"], C1, G1, T1)

        layer_stats(nc, k, "n0_")
        with Scope(nc) as t:
            score = t.sb("score1", [P, G1 * P, H1])
            with Scope(nc) as t2:
                q_parts = t2.sb("q_parts", [P, NB, 3, D], BF)
                project0(nc, k, q_parts, k_tab, v_tab)
                mixer_matrix0(nc, k)
                edge_scores(nc, k, e1, q_parts, k_tab, score)
            segment_softmax(nc, k, "m1_", G1, H1, score, e1.valid, e1.starts, e1.ends, float((D // H1) ** -0.5))
            acc = cleared(t, "acc0", [P, NB, D + H1])
            attend(nc, k, e1, v_tab, score, acc)
            combine0(nc, k, acc)
        layer_stats(nc, k, "n1_")
        with Scope(nc) as t:
            XN = t.sb("XN", [P, NB, D])
            logits = t.sb("logits", [P, NB, NE])
            slot_i = t.sb("slot_i", [P, NB], I32)
            factor = t.sb("factor", [P, NB])
            gate0(nc, k, XN, logits)
            route0(nc, k, XN, logits, slots, slot_i, factor)
            experts0(nc, k, a, slots, slots_out)
            return0(nc, k, slots_out, slot_i, factor)

        recycle_semaphores(nc)

        layer_stats(nc, k, "n2_")
        with Scope(nc) as t:
            G = t.sb("G", [P, KC, D])
            g_bias = t.sb("g_bias", [1, D])
            with Scope(nc) as t2:
                sums = t2.sb("sums", [P, 3, D + 1])
                gram1(nc, k, x_tab, sums)
                mixer_matrix1(nc, k, sums, G, g_bias)
            acc = cleared(t, "acc1", [P, NB, 512])
            with Scope(nc) as t2:
                factors = t2.sb("factors", [P, G1 * P, 4])
                edge_factors(nc, k, a, a["attr"], a["emb_t"], e1, factors, 128.0 ** -0.5 * 16.0 ** -0.5)
                convolve(nc, k, e1, x_tab, factors, acc)
            combine1(nc, k, a, acc, G, g_bias)

        pairs2 = dram("pairs2", [(C2 + 1) * P, 2], I32)
        sort_edges(nc, k, a["L1_ffn_edge_index"], pairs2)
        e2 = Graph(s, "e2_", G2)
        steps(e2, "s2_", pairs2, C2, G2, T2)
        layer_stats(nc, k, "n3_")
        xnT = s.sb("xnT", [P, KC, NPAD])
        row_cols = s.sb("row_cols", [P, 80])
        gates = s.sb("gates", [P, NB, NX])
        d_parts = s.sb("d_parts", [P, NB, 3, H2], BF)
        gate_rows(nc, k, h_tab, d_parts, xnT, row_cols)
        with Scope(nc) as t:
            acc = cleared(t, "acc2", [P, NB, 16 + H2])
            rows = t.sb("gate_edge_rows", [P, G2 * P, 16])
            score = t.sb("score2", [P, G2 * P, H2])
            gate_scores(nc, k, e2, h_tab, d_parts, rows, score)
            segment_softmax(nc, k, "m2_", G2, H2, score, e2.valid, e2.starts, e2.ends, 1.0)
            gate_sums(nc, k, e2, rows, score, acc)
            top_two(nc, k, acc, row_cols, gates)
        experts1(nc, k, a, xnT, gates)
        store(nc, k, out)


_PLAIN = ["x", "L0_gnn_Wq", "L0_gnn_bq", "L0_gnn_Wk", "L0_gnn_bk", "L0_gnn_Wv", "L0_gnn_bv", "L0_gnn_Ws", "L0_gnn_bs",
          "L0_mix_Wqkv", "L0_mix_Wout", "L0_mix_bout", "L0_ffn_gate_w", "L0_ffn_gate_b", "L0_ffn_w1", "L0_ffn_b1", "L0_ffn_w2",
          "L0_ffn_b2", "L1_gnn_w_00_0", "L1_gnn_w_11_0", "L1_gnn_w_01_1", "L1_gnn_w_10_1", "L1_gnn_fc_w1", "L1_gnn_fc_w2",
          "L1_mix_Wq", "L1_mix_bq", "L1_mix_Wk", "L1_mix_bk", "L1_mix_Wv", "L1_mix_bv", "L1_mix_Wfc", "L1_mix_bfc",
          "L1_ffn_W_gat", "L1_ffn_att_src", "L1_ffn_att_dst", "L1_ffn_b_gat", "L1_ffn_ln_gamma", "L1_ffn_ln_beta",
          "L1_ffn_W1", "L1_ffn_b1", "L1_ffn_W2", "L1_ffn_b2", "L1_ffn_edge_index"]


def kernel(**inputs):
    import numpy as np
    import concourse.bacc as bacc
    from concourse.bass_utils import run_bass_kernel_spmd

    arrays = {n: np.ascontiguousarray(inputs[n]) for n in _PLAIN}
    dst, src = np.asarray(inputs["dst"]), np.asarray(inputs["src"])
    pairs = np.full(((C1 + 1) * P, 2), NONODE, dst.dtype)
    pairs[:, 1] = 0
    pairs[0, 0] = -1
    pairs[1:E1 + 1, 0] = dst
    pairs[1:E1 + 1, 1] = src
    arrays["pairs"] = pairs
    attr = np.zeros((C1 * P, 4), np.float32)
    attr[:E1] = np.asarray(inputs["edge_attr_4"])
    arrays["attr"] = attr
    emb = np.zeros((10, C1 * P), np.float32)
    emb[:, :E1] = np.asarray(inputs["edge_attr_10"]).T
    arrays["emb_t"] = emb

    nc = bacc.Bacc("TRN2", target_bir_lowering=False, num_devices=1)
    a = {n: nc.dram_tensor(f"in_{n}", list(v.shape), mybir.dt.from_np(v.dtype), kind="ExternalInput").ap()
         for n, v in arrays.items()}
    out = nc.dram_tensor("out", [N, D], F32, kind="ExternalOutput").ap()
    program(nc, a, out)
    r = run_bass_kernel_spmd(nc, [{f"in_{n}": v for n, v in arrays.items()}], core_ids=[0])
    return r.results[0]["out"]
```

```python
from contextlib import ExitStack

import concourse.bass as bass
from concourse import mybir
from concourse.bass import ds

F32 = mybir.dt.float32
I32 = mybir.dt.int32
BF = mybir.dt.bfloat16
ALU = mybir.AluOpType
ACT = mybir.ActivationFunctionType
AX = mybir.AxisListType

P = 128
N = 3125
D = 256
NB = (N + P - 1) // P
NPAD = NB * P
LAST = N - (NB - 1) * P
KC = D // P
EPS = 1e-5
LOW = -1.0e30
RESET = -1.0e32
NONODE = NPAD

E1 = 53125
C1 = (E1 + P - 1) // P
U = 8
T1 = C1 + NB - 1
G1 = (T1 + P - 1) // P
H1 = 8
EG = 32768
CG = EG // P
C2 = (CG + NB + U - 1) // U * U
T2 = C2 + NB - 1
G2 = (T2 + P - 1) // P
NH = NB + 1
H2 = 4
assert T1 % U == 0 and T2 % U == 0

B5 = 5
assert NB % B5 == 0
NE = 8
FE = 1024
CAP = -(-5 * N // (4 * NE))
SLOTS = NE * CAP
NX = 4
FX = 512
MH = 16
DH = 64


class Chain:

    def __init__(self, eng, sem, base=0):
        self.eng, self.sem, self.base, self.n = eng, sem, base, 0

    def link(self, ins):
        self.n += 1
        ins.then_inc(self.sem, 1)
        self.eng.wait_ge(self.sem, self.base + self.n)


class Scope:

    def __init__(self, nc):
        self.nc, self.stack = nc, ExitStack()

    def __enter__(self):
        self.stack.__enter__()
        return self

    def __exit__(self, *a):
        return self.stack.__exit__(*a)

    def sb(self, name, shape, dt=F32):
        return self.stack.enter_context(self.nc.sbuf_tensor(name, shape, dt))

    def ps(self, name, shape, dt=F32):
        return self.stack.enter_context(self.nc.psum_tensor(name, shape, dt))

    def sem(self, name):
        sem = self.nc.alloc_semaphore(name)
        Scope.used.append(sem)
        return sem

    used = []


def recycle_semaphores(nc):
    nc.clear_and_free_semaphores(list(Scope.used))
    Scope.used.clear()
    nc.all_engine_barrier()


def wide(ap, shape):
    return ap.to_broadcast(shape)


def make_constants(nc, k):
    with Scope(nc) as s:
        made = s.sem("constants_made")
        with nc.Block() as block:
            @block.gpsimd
            def _(pool):
                nc.gpsimd.memset(k.ident[:, :], 0.0).then_inc(made, 1)
                nc.gpsimd.memset(k.ones[:, :], 1.0).then_inc(made, 1)
                nc.gpsimd.memset(k.ones_h[:, :], 1.0).then_inc(made, 1)
                nc.gpsimd.memset(k.upper[:, :], 1.0).then_inc(made, 1)
                nc.gpsimd.iota(k.count_row[:, :], [[1, 512]], base=0, channel_multiplier=0,
                               allow_small_or_imprecise_dtypes=True).then_inc(made, 1)
                nc.gpsimd.iota(k.count_col[:, :], [[P, 4]], base=0, channel_multiplier=1,
                               allow_small_or_imprecise_dtypes=True).then_inc(made, 1)
                nc.gpsimd.memset(k.armed_dummy[:, :], 0.0).then_inc(k.armed, 1)
                pool.wait_ge(made, 6)
                nc.gpsimd.affine_select(out=k.ident[:, :], in_=k.ident[:, :], compare_op=ALU.not_equal, fill=1.0,
                                        base=0, pattern=[[-1, P]], channel_multiplier=1).then_inc(made, 1)
                nc.gpsimd.affine_select(out=k.upper[:, :], in_=k.upper[:, :], compare_op=ALU.is_gt, fill=0.0,
                                        base=0, pattern=[[1, P]], channel_multiplier=-1).then_inc(made, 1)
                nc.gpsimd.iota(k.node_id[:, :], [[P, NB]], base=0, channel_multiplier=1,
                               allow_small_or_imprecise_dtypes=True).then_inc(made, 1)
                pool.wait_ge(made, 9)

            @block.vector
            def _(dve):
                v = nc.vector
                dve.wait_ge(made, 9)
                v.tensor_scalar(k.node_mask[:, :], k.node_id[:, :], float(N), None, ALU.is_lt).then_inc(made, 1)
                v.tensor_copy(k.ident_h[:, :], k.ident[:, :]).then_inc(made, 1)
                dve.wait_ge(made, 11)


def build_steps(nc, k, name, pairs, chunks, groups, steps, valid, starts, ends, rel, src, rel_rows, block_row, chunk_i):
    flat = pairs.rearrange("a b -> (a b)")
    windows = flat.rearrange("(c w) -> c w", w=2 * P)
    with Scope(nc) as s:
        last_i = s.sb(name + "last_i", [1, chunks], I32)
        last_b = s.sb(name + "last_b", [1, chunks], I32)
        end_step = s.sb(name + "end_step", [1, chunks])
        below = s.sb(name + "below", [P, groups, chunks])
        cut = s.sb(name + "cut", [P, 8, groups])
        block_i = s.sb(name + "block_i", [P, groups], I32)
        edges = [s.sb(name + f"edges{j}", [P, groups, P, 2], I32) for j in range(3)]
        here = s.sb(name + "here", [P, 2, groups, P])
        near = s.sb(name + "near", [P, 2, groups, P])
        rel_t = s.sb(name + "rel_t", [P, groups, P])
        rel_h = s.sb(name + "rel_h", [P, groups, P], BF)
        tmp = s.sb(name + "tmp", [P, groups, P])
        wide_end = s.ps(name + "wide_end", [P, 512])
        turned = [s.ps(name + f"turned{j}", [P, 512]) for j in range(2)]
        block_dram = nc.dram_tensor(name + "block_of_step", [groups * P], I32, kind="Internal").ap()
        loaded, cmp_done, spread, ready, got, chain, flipped, bdone = (
            s.sem(name + x) for x in ("loaded", "cmp_done", "spread", "ready", "got", "chain", "flipped", "bdone"))
        with nc.Block() as block:
            @block.sync
            def _(sp):
                sp.dma_start(last_i[:, :], pairs[P:chunks * P + 1:P, 0:1].rearrange("c b -> b c"),
                             allow_slow_non_contiguous=True).then_inc(loaded, 16)
                sp.wait_ge(ready, 2)
                sp.dma_start(block_dram.rearrange("(g p) -> p g", p=P), block_i[:, :],
                             allow_slow_non_contiguous=True).then_inc(bdone, 16)
                sp.wait_ge(bdone, 16)
                sp.dma_start(block_row[:, 0:groups * P], block_dram.rearrange("(a n) -> a n", a=1)).then_inc(bdone, 16)
                sp.wait_ge(ready, 3)
                sp.dma_start(rel_rows.rearrange("(g p) e -> p g e", p=P), rel_h[:, :, :]).then_inc(bdone, 16)
                sp.wait_ge(bdone, 48)

            @block.tensor
            def _(pe):
                pe.wait_ge(cmp_done, 1)
                nc.tensor.matmul(wide_end[:, 0:chunks], k.ones[0:1, :], end_step[:, :], start=True, stop=True).then_inc(spread, 1)
                pe.wait_ge(cmp_done, 2)
                for j, x in enumerate((rel_t, here[:, 1])):
                    for g in range(groups):
                        ins = nc.tensor.transpose(turned[j][:, g * P:(g + 1) * P], x[:, g, :], k.ident[:, :])
                    ins.then_inc(flipped, 1)

            @block.gpsimd
            def _(pool):
                pool.wait_ge(ready, 1)
                for g in range(groups):
                    for j in range(3):
                        nc.gpsimd.indirect_dma_start(
                            out=edges[j][:, g].rearrange("p e b -> p (e b)"), out_offset=None, in_=windows,
                            in_offset=bass.IndirectOffsetOnAxis(ap=chunk_i[:, g:g + 1], axis=0),
                            element_offset=2 * j).then_inc(got, 16)

            @block.vector
            def _(dve):
                c = Chain(dve, chain)
                v = nc.vector
                dve.wait_ge(loaded, 16)
                c.link(v.tensor_scalar(last_b[:, :], last_i[:, :], 7, None, ALU.arith_shift_right))
                c.link(v.tensor_copy(end_step[:, :], last_b[:, :]))
                c.link(v.tensor_scalar(end_step[:, :], end_step[:, :], float(NB - 1), None, ALU.min))
                v.tensor_tensor(end_step[:, :], end_step[:, :], k.count_row[0:1, 0:chunks], ALU.add).then_inc(cmp_done, 1)
                dve.wait_ge(spread, 1)
                c.link(v.tensor_tensor(below[:, :, :], wide(wide_end[:, 0:chunks].unsqueeze(1), [P, groups, chunks]),
                                       wide(k.count_col[:, 0:groups].unsqueeze(2), [P, groups, chunks]), ALU.is_lt))
                c.link(v.tensor_reduce(cut[:, 0], below[:, :, :], AX.X, ALU.add))
                c.link(v.tensor_scalar(cut[:, 1], cut[:, 0], float(chunks - 1), None, ALU.min))
                v.tensor_copy(chunk_i[:, :], cut[:, 1]).then_inc(ready, 1)
                c.link(v.tensor_tensor(cut[:, 2], k.count_col[:, 0:groups], cut[:, 0], ALU.subtract))
                c.link(v.tensor_scalar(cut[:, 3], cut[:, 2], float(NB - 1), None, ALU.min))
                v.tensor_copy(block_i[:, :], cut[:, 3]).then_inc(ready, 1)
                c.link(v.tensor_scalar(cut[:, 4], cut[:, 0], float(chunks), 1.0e6, ALU.is_ge, ALU.mult))
                c.link(v.scalar_tensor_tensor(out=cut[:, 5], in0=cut[:, 2], scalar=float(P), in1=cut[:, 4],
                                              op0=ALU.mult, op1=ALU.add))
                dve.wait_ge(got, 48 * groups)
                v.tensor_copy(near[:, 0], edges[0][:, :, :, 0])
                v.tensor_copy(near[:, 1], edges[2][:, :, :, 0])
                v.tensor_copy(here[:, 1], edges[1][:, :, :, 1])
                c.link(v.tensor_copy(here[:, 0], edges[1][:, :, :, 0]))
                c.link(v.tensor_tensor(rel_t[:, :, :], here[:, 0], wide(cut[:, 5].unsqueeze(2), [P, groups, P]), ALU.subtract))
                v.tensor_copy(rel_h[:, :, :], rel_t[:, :, :]).then_inc(ready, 1)
                c.link(v.tensor_scalar(valid[:, :, :], rel_t[:, :, :], 0.0, None, ALU.is_ge))
                c.link(v.tensor_scalar(tmp[:, :, :], rel_t[:, :, :], float(P), None, ALU.is_lt))
                c.link(v.tensor_tensor(valid[:, :, :], valid[:, :, :], tmp[:, :, :], ALU.mult))
                for flags, j in ((starts, 0), (ends, 1)):
                    c.link(v.tensor_tensor(tmp[:, :, :], here[:, 0], near[:, j], ALU.not_equal))
                    c.link(v.scalar_tensor_tensor(out=flags[:, :, :], in0=tmp[:, :, :], scalar=RESET, in1=valid[:, :, :],
                                                  op0=ALU.mult, op1=ALU.mult))
                dve.sem_inc(cmp_done, 1)
                dve.wait_ge(flipped, 2)
                for j, x in enumerate((rel, src)):
                    c.link(v.tensor_copy(x[:, 0:groups * P], turned[j][:, 0:groups * P]))


def segment_softmax(nc, k, name, groups, heads, score, valid, starts, ends, scale, acc=None):
    J = groups * heads // 4
    with Scope(nc) as s:
        x = s.sb(name + "x", [P, groups, heads, P])
        f = s.sb(name + "f", [P, groups, heads, P])
        b = s.sb(name + "b", [P, groups, heads, P])
        hole = s.sb(name + "hole", [P, groups, P])
        edge_val = s.sb(name + "edge_val", [P, groups, heads])
        edge_rst = s.sb(name + "edge_rst", [P, groups, heads])
        rst1 = s.sb(name + "rst1", [P, groups])
        carry = s.sb(name + "carry", [P, groups, heads])
        val_t = s.sb(name + "val_t", [heads, groups * P])
        rst_t = s.sb(name + "rst_t", [heads, groups * P])
        scan_t = s.sb(name + "scan_t", [heads, groups * P + 1])
        bank = [s.ps(name + f"bank{j}", [P, 4, P]) for j in range(min(J, 8))]
        assert J <= 8
        chain, turned, masked, summed, across, carried, back, final, expd, gone = (
            s.sem(name + q) for q in ("chain", "turned", "masked", "summed", "across", "carried", "back", "final", "expd", "gone"))
        cleared = s.sem(name + "cleared")
        with nc.Block() as block:
            @block.gpsimd
            def _(pool):
                if acc is not None:
                    nc.gpsimd.memset(acc[:, :, :], 0.0).then_inc(cleared, 1)
                    pool.wait_ge(cleared, 1)

            @block.tensor
            def _(pe):
                for g in range(groups):
                    for h in range(heads):
                        q = g * heads + h
                        nc.tensor.transpose(bank[q // 4][:, q % 4, :], score[:, g * P:(g + 1) * P, h],
                                            k.ident[:, :]).then_inc(turned, 1)
                for way in range(2):
                    pe.wait_ge(summed, way + 1)
                    for g in range(groups):
                        nc.tensor.transpose(bank[0][0:heads, g, :], edge_val[:, g, :], k.ident[:, :])
                    for g in range(groups):
                        ins = nc.tensor.transpose(bank[1][0:heads, g, :], edge_rst[:, g, :], k.ident[:, :])
                    ins.then_inc(across, 1)
                    pe.wait_ge(carried, way + 1)
                    off = 0 if way == 0 else 1
                    for g in range(groups):
                        ins = nc.tensor.transpose(bank[2][:, 0, g * heads:(g + 1) * heads],
                                                  scan_t[:, off + g * P:off + (g + 1) * P],
                                                  k.ident[0:heads, 0:heads])
                    ins.then_inc(back, 1)
                pe.wait_ge(final, 1)
                for g in range(groups):
                    for h in range(heads):
                        q = g * heads + h
                        nc.tensor.transpose(bank[q // 4][:, q % 4, :], x[:, g, h, :], k.ident[:, :]).then_inc(turned, 1)

            @block.scalar
            def _(act):
                act.wait_ge(expd, 1)
                nc.scalar.activation(x[:, :, :, :], x[:, :, :, :], ACT.Exp, scale=scale).then_inc(gone, 1)

            @block.vector
            def _(dve):
                v = nc.vector
                c = Chain(dve, chain)
                c.link(v.tensor_scalar(hole[:, :, :], valid[:, :, :], 1.0, -LOW, ALU.subtract, ALU.mult))
                for q in range(J):
                    g, h0 = q * 4 // heads, q * 4 % heads
                    dve.wait_ge(turned, 4 * q + 4)
                    v.tensor_tensor(x[:, g, h0:h0 + 4, :], bank[q][:, :, :],
                                    wide(valid[:, g, :].unsqueeze(1), [P, 4, P]), ALU.mult).then_inc(masked, 1)
                for g in range(groups):
                    dve.wait_ge(masked, (g + 1) * heads // 4)
                    c.link(v.tensor_tensor(x[:, g], x[:, g], wide(hole[:, g, :].unsqueeze(1), [P, heads, P]), ALU.add))

                def scans(out, flags, data, way, initial):
                    for g in range(groups):
                        for h in range(heads):
                            o, r, a = out[:, g, h, :], flags[:, g, :], data[:, g, h, :]
                            if way:
                                o, r, a = o[:, ::-1], r[:, ::-1], a[:, ::-1]
                            ins = v.tensor_tensor_scan(o, r, a, LOW if initial is None else initial[:, g, h:h + 1],
                                                       ALU.add, ALU.max)
                    c.link(ins)

                for way, (out, flags, data) in enumerate(((f, starts, x), (b, ends, f))):
                    scans(out, flags, data, way, None)
                    at = P - 1 if way == 0 else 0
                    v.tensor_copy(edge_val[:, :, :], out[:, :, :, at])
                    c.link(v.tensor_reduce(rst1[:, :], flags[:, :, :], AX.X, ALU.min))
                    v.tensor_copy(edge_rst[:, :, :], wide(rst1[:, :].unsqueeze(2), [P, groups, heads])).then_inc(summed, 1)
                    dve.wait_ge(across, way + 1)
                    v.tensor_copy(val_t[:, :], bank[0][0:heads, 0:groups, :].rearrange("p a b -> p (a b)"))
                    c.link(v.tensor_copy(rst_t[:, :], bank[1][0:heads, 0:groups, :].rearrange("p a b -> p (a b)")))
                    n = groups * P
                    if way == 0:
                        v.memset(scan_t[:, 0:1], LOW)
                        v.tensor_tensor_scan(scan_t[:, 1:n + 1], rst_t[:, :], val_t[:, :], LOW, ALU.add, ALU.max).then_inc(carried, 1)
                    else:
                        v.memset(scan_t[:, n:n + 1], LOW)
                        v.tensor_tensor_scan(scan_t[:, 0:n][:, ::-1], rst_t[:, ::-1], val_t[:, ::-1], LOW,
                                             ALU.add, ALU.max).then_inc(carried, 1)
                    dve.wait_ge(back, way + 1)
                    c.link(v.tensor_copy(carry[:, :, :], bank[2][:, 0, 0:groups * heads].rearrange("p (g h) -> p g h", g=groups)))
                    scans(out, flags, data, way, carry)
                v.tensor_tensor(x[:, :, :, :], x[:, :, :, :], b[:, :, :, :], ALU.subtract).then_inc(expd, 1)
                dve.wait_ge(gone, 1)
                for g in range(groups):
                    ins = v.tensor_tensor(x[:, g], x[:, g], wide(valid[:, g, :].unsqueeze(1), [P, heads, P]), ALU.mult)
                ins.then_inc(final, 1)
                for q in range(J):
                    g, h0 = q * 4 // heads, q * 4 % heads
                    dve.wait_ge(turned, groups * heads + 4 * q + 4)
                    ins = v.tensor_copy(score[:, g * P:(g + 1) * P, h0:h0 + 4].rearrange("p t h -> p h t"), bank[q][:, :, :])
                c.link(ins)


def layer_stats(nc, k, name, loads=None):
    with Scope(nc) as s:
        parts = s.sb(name + "parts", [P, NB, 6])
        t = s.sb(name + "t", [P, 4, NB])
        chain, inverse, rooted = s.sem(name + "chain"), s.sem(name + "inverse"), s.sem(name + "rooted")
        with nc.Block() as block:
            if loads is not None:
                @block.sync
                def _(sp):
                    loads(sp)

            @block.scalar
            def _(act):
                act.wait_ge(inverse, 1)
                nc.scalar.activation(k.rstd[:, :], t[:, 1], ACT.Sqrt).then_inc(rooted, 1)

            @block.vector
            def _(dve):
                v = nc.vector
                with dve.Fori(0, NB // B5) as i:
                    for j in range(B5):
                        v.bn_stats(parts[:, ds(i * B5 + j, 1), :], k.X[:, ds(i * B5 + j, 1), :]).then_inc(chain, 1)
                dve.wait_ge(chain, NB)
                c = Chain(dve, chain, NB)
                c.link(v.tensor_tensor(t[:, 0], parts[:, :, 1], parts[:, :, 4], ALU.subtract))
                c.link(v.tensor_tensor(t[:, 0], t[:, 0], t[:, 0], ALU.mult))
                v.tensor_tensor(t[:, 3], parts[:, :, 1], parts[:, :, 4], ALU.add)
                c.link(v.tensor_tensor(t[:, 1], parts[:, :, 2], parts[:, :, 5], ALU.add))
                c.link(v.scalar_tensor_tensor(out=t[:, 2], in0=t[:, 0], scalar=D / 4.0, in1=t[:, 1], op0=ALU.mult, op1=ALU.add))
                c.link(v.tensor_scalar(t[:, 2], t[:, 2], 1.0 / D, EPS, ALU.mult, ALU.add))
                v.reciprocal(t[:, 1], t[:, 2]).then_inc(inverse, 1)
                dve.wait_ge(rooted, 1)
                c.link(v.tensor_tensor(k.rstd[:, :], k.rstd[:, :], k.node_mask[:, :], ALU.mult))
                c.link(v.scalar_tensor_tensor(out=k.shift[:, :], in0=t[:, 3], scalar=-0.5, in1=k.rstd[:, :],
                                              op0=ALU.mult, op1=ALU.mult))


class Loads:

    def __init__(self, nc, s, k, a):
        self.mix_kv = s.sb("mix_kv", [P, 8, D])
        self.mix_out = s.sb("mix_out", [P, KC, 512])
        self.fc = [s.sb(f"fc{j}", [P, KC, D]) for j in range(3)]
        self.got_x, self.got_w, cleared = (s.sem(q) for q in ("got_x", "got_w", "cleared"))
        got_x, got_w = self.got_x, self.got_w
        loads = [(k.W0[:, :, j * D:(j + 1) * D], a["L0_gnn_" + w].rearrange("(c p) f -> p c f", p=P))
                 for j, w in enumerate(("Wq", "Wk", "Wv", "Ws"))]
        loads += [(k.bias0[:, j * D:(j + 1) * D], a["L0_gnn_" + w].rearrange("(a f) -> a f", a=1))
                  for j, w in enumerate(("bq", "bk", "bv", "bs"))]
        loads += [(k.bias0[:, 4 * D:5 * D], a["L0_mix_bout"].rearrange("(a f) -> a f", a=1)),
                  (k.mix_q[:, :, :], a["L0_mix_Wqkv"][0:512, :].rearrange("(j p) c -> p j c", p=P)),
                  (self.mix_kv[:, :, :], a["L0_mix_Wqkv"][512:1536, :].rearrange("(j p) c -> p j c", p=P)),
                  (self.mix_out[:, :, :], a["L0_mix_Wout"].rearrange("(j p) f -> p j f", p=P)),
                  (k.gate[:, :, :], a["L0_ffn_gate_w"].rearrange("(c p) e -> p c e", p=P)),
                  (k.gate_b[:, :], a["L0_ffn_gate_b"].rearrange("(a f) -> a f", a=1)),
                  (k.fc_q[:, :, :], a["L1_mix_Wq"].rearrange("(j p) c -> p j c", p=P))]
        loads += [(self.fc[t][:, :, :], a["L1_mix_" + w].rearrange("(j p) c -> p j c", p=P)) for t, w in enumerate(("Wk", "Wv", "Wfc"))]
        loads += [(k.bias1[:, j * D:(j + 1) * D], a["L1_mix_" + w].rearrange("(a f) -> a f", a=1))
                  for j, w in enumerate(("bk", "bv", "bfc"))]
        loads += [(k.bq_col[:, :], a["L1_mix_bq"].rearrange("(c p) -> p c", p=P))]
        loads += [(k.gat_w[:, :, :], a["L1_ffn_W_gat"].rearrange("(c p) e -> p c e", p=P))]
        self.count = 16 * (len(loads) + 5)
        with nc.Block() as block:
            @block.scalar
            def _(act):
                act.wait_ge(cleared, 1)
                act.dma_start(k.X[:, 0:NB - 1, :], a["x"][0:(NB - 1) * P, :].rearrange("(b p) d -> p b d", p=P)).then_inc(got_x, 16)
                act.dma_start(k.X[0:LAST, NB - 1, :], a["x"][(NB - 1) * P:N, :]).then_inc(got_x, 16)
                for to, of in loads:
                    act.dma_start(to, of, allow_slow_non_contiguous=True).then_inc(got_w, 16)
                for j, w in enumerate(("att_src", "att_dst")):
                    act.dma_start(k.gat_rows[:, j * 16:(j + 1) * 16],
                                 a["L1_ffn_" + w].rearrange("h e -> (h e)").rearrange("(a f) -> a f", a=1)).then_inc(got_w, 16)
                for j, w in enumerate(("b_gat", "ln_gamma", "ln_beta")):
                    act.dma_start(k.gat_rows[:, (j + 2) * 16:(j + 3) * 16],
                                 a["L1_ffn_" + w].rearrange("(a f) -> a f", a=1)).then_inc(got_w, 16)

            @block.vector
            def _(dve):
                nc.vector.memset(k.X[:, NB - 1, :], 0.0).then_inc(cleared, 1)


def turn_weights(nc, k, ld):
    with Scope(nc) as s:
        bank = [s.ps(f"turn_bank{j}", [P, 512]) for j in range(8)]
        turned, kept = s.sem("turned"), s.sem("kept")
        jobs = [(ld.mix_kv[:, j, c * P:(c + 1) * P], k.mix_kvT[:, c, j * P:(j + 1) * P]) for c in range(KC) for j in range(8)]
        jobs += [(ld.mix_out[:, j, c * P:(c + 1) * P], k.mix_outT[:, c, j * P:(j + 1) * P]) for c in range(4) for j in range(KC)]
        for t in range(3):
            jobs += [(ld.fc[t][:, j, c * P:(c + 1) * P], k.fcT[t][:, c, j * P:(j + 1) * P]) for c in range(KC) for j in range(KC)]
        with nc.Block() as block:
            @block.sync
            def _(sp):
                sp.wait_ge(ld.got_x, 32)

            @block.tensor
            def _(pe):
                pe.wait_ge(ld.got_w, ld.count)
                for j, (x, _y) in enumerate(jobs):
                    if j >= 8:
                        pe.wait_ge(kept, j - 7)
                    nc.tensor.transpose(bank[j % 8][:, 0:P], x, k.ident[:, :]).then_inc(turned, 1)

            @block.vector
            def _(dve):
                for j, (_x, y) in enumerate(jobs):
                    dve.wait_ge(turned, j + 1)
                    nc.vector.tensor_copy(y, bank[j % 8][:, 0:P]).then_inc(kept, 1)
                dve.wait_ge(kept, len(jobs))


def normed_block(nc, k, act, b, slot, sem):
    nc.scalar.activation(slot, k.X[:, ds(b, 1), :].rearrange("p b d -> p (b d)"), ACT.Identity,
                         bias=k.shift[:, ds(b, 1)], scale=k.rstd[:, ds(b, 1)]).then_inc(sem, 1)


def project0(nc, k, q_parts, k_tab, v_tab):
    PER = 5
    LASTT = NB // B5 - 1
    with Scope(nc) as s:
        xn = s.sb("p0_xn", [P, B5, D])
        xT = s.sb("p0_xT", [P, B5, KC, P])
        qkv = s.sb("p0_qkv", [P, B5, 3 * D])
        kv = s.sb("p0_kv", [P, B5, MH, DH])
        sq = s.sb("p0_sq", [P, MH, DH])
        st = s.sb("p0_st", [P, 3, MH])
        mean = s.sb("p0_mean", [P, KC, MH])
        zero = s.sb("p0_zero", [P, 512])
        rest = s.sb("p0_rest", [P, D])
        part = s.sb("p0_part", [P, 3, D], BF)
        ps_t = s.ps("p0_t", [P, KC, P])
        ps_a = s.ps("p0_a", [P, 512])
        ps_b = s.ps("p0_b", [P, 512])
        ps_m = s.ps("p0_m", [P, MH, DH])
        dots = s.ps("p0_dots", [P, 4, P])
        normed, turned, kept, ab_done, ab_used, m_done, squared, k_kept, heads, chain, zeroed, centred, dotted = (
            s.sem("p0_" + q) for q in ("normed", "turned", "kept", "ab_done", "ab_used", "m_done", "squared", "k_kept", "heads",
                                       "chain", "zeroed", "centred", "dotted"))
        inverse, rooted = s.sem("p0_inverse"), s.sem("p0_rooted")
        split, parted = s.sem("p0_split"), s.sem("p0_parted")
        out = [s.sem(f"p0_out{j}") for j in range(B5)]
        K8 = MH // 2
        with nc.Block() as block:
            @block.scalar
            def _(act):
                act.sem_inc(ab_used, 1)
                act.sem_inc(k_kept, 1)

                def norm(b, j):
                    act.wait_ge(turned, b + 1)
                    act.wait_ge(k.armed, 1)
                    normed_block(nc, k, act, b, xn[:, j, :], normed)

                def turn(i, first=False, last=False):
                    for j in range(B5):
                        b = i * B5 + j
                        if not (last and j == B5 - 1):
                            norm(b + 1, (j + 1) % B5)
                        if not first:
                            act.wait_ge(out[j], i * 32)
                        act.wait_ge(parted, b + 1)
                        act.wait_ge(ab_done, b + 1)
                        nc.scalar.activation(qkv[:, j, 0:512], ps_a[:, :], ACT.Copy)
                        nc.scalar.activation(qkv[:, j, 512:768], ps_b[:, 0:D], ACT.Copy).then_inc(ab_used, 1)
                        act.wait_ge(m_done, b + 1)
                        nc.scalar.activation(sq[:, :, :], ps_m[:, :, :], ACT.Square).then_inc(squared, 1)
                        nc.scalar.activation(kv[:, j, 0:K8, :], ps_m[:, 0:K8, :], ACT.Copy).then_inc(k_kept, 1)
                        act.wait_ge(inverse, b + 1)
                        nc.scalar.activation(st[:, 2, 0:K8], st[:, 1, 0:K8], ACT.Sqrt).then_inc(rooted, 1)
                norm(0, 0)
                turn(0, first=True)
                with act.Fori(1, LASTT) as i:
                    turn(i)
                turn(LASTT, last=True)

            @block.sync
            def _(sp):
                with sp.Fori(0, NB // B5) as i:
                    for j in range(B5):
                        b = i * B5 + j
                        sp.wait_ge(ab_used, b + 2)
                        for n, tab in enumerate((k_tab, v_tab)):
                            sp.dma_start(tab[ds(b * P, P), :], qkv[:, j, (n + 1) * D:(n + 2) * D]).then_inc(out[j], 16)
                for j in range(B5):
                    sp.wait_ge(out[j], 32 * (NB // B5))

            @block.gpsimd
            def _(pool):
                pool.sem_inc(parted, B5)
                pool.wait_ge(zeroed, 2)
                with pool.Fori(0, NB // B5) as i:
                    def link(n, ins):
                        ins.then_inc(split, 1)
                        pool.wait_ge(k.armed, 1)
                        pool.wait_ge(split, i * (5 * B5) + (n + 1))

                    for j in range(B5):
                        b = i * B5 + j
                        pool.wait_ge(k.armed, 1)
                        pool.wait_ge(ab_used, b + 2)
                        link(5 * j + 0, nc.gpsimd.tensor_tensor(part[:, 0, :], qkv[:, j, 0:D], zero[:, 0:D], ALU.subtract))
                        link(5 * j + 1, nc.gpsimd.tensor_tensor(rest[:, :], qkv[:, j, 0:D], part[:, 0, :], ALU.subtract))
                        link(5 * j + 2, nc.gpsimd.tensor_tensor(part[:, 1, :], rest[:, :], zero[:, 0:D], ALU.subtract))
                        link(5 * j + 3, nc.gpsimd.tensor_tensor(part[:, 2, :], rest[:, :], part[:, 1, :], ALU.subtract))
                        link(5 * j + 4, nc.gpsimd.tensor_copy(q_parts[:, ds(b, 1)].rearrange("p a n d -> p (a n) d"), part[:, :, :]))
                        pool.sem_inc(parted, 1)

            @block.tensor
            def _(pe):
                def turned_block(b, j):
                    pe.wait_ge(normed, b + 1)
                    pe.wait_ge(kept, b + 1)
                    for c in range(KC):
                        ins = nc.tensor.transpose(ps_t[:, c, :], xn[:, j, c * P:(c + 1) * P], k.ident[:, :])
                    ins.then_inc(turned, 1)

                def product(j):
                    for q in range(4):
                        ins = nc.tensor.matmul(dots[:, q, :], kv[:, j, 8 + 2 * q:10 + 2 * q, :].rearrange("p h d -> p (h d)"),
                                               kv[:, j, 2 * q:2 * q + 2, :].rearrange("p h d -> p (h d)"),
                                               start=False, stop=False, skip_group_check=True)
                    return ins

                def turn(i, last=False):
                    for j in range(B5):
                        b = i * B5 + j
                        pe.wait_ge(kept, b + 2)
                        pe.wait_ge(ab_used, b + 1)
                        for ps, lo, n in ((ps_a, 0, 512), (ps_b, 512, 256)):
                            nc.tensor.matmul(ps[:, 0:n], k.ones[0:1, :], k.bias0[:, lo:lo + n], start=True, stop=False)
                            for c in range(KC):
                                ins = nc.tensor.matmul(ps[:, 0:n], xT[:, j, c, :], k.W0[:, c, lo:lo + n],
                                                       start=False, stop=(c == KC - 1))
                        ins.then_inc(ab_done, 1)
                        if not (last and j == B5 - 1):
                            turned_block(b + 1, (j + 1) % B5)
                        pe.wait_ge(k_kept, b + 1)
                        pe.wait_ge(heads, b + 1)
                        for n in range(2):
                            for c in range(KC):
                                ins = nc.tensor.matmul(ps_m[:, 8 * n:8 * n + 8, :].rearrange("p h d -> p (h d)"), xT[:, j, c, :],
                                                       k.mix_kvT[:, c, n * 512:(n + 1) * 512], start=(c == 0), stop=(c == KC - 1))
                        ins.then_inc(m_done, 1)
                        product((j - 1) % B5)
                pe.sem_inc(turned, B5)
                pe.wait_ge(zeroed, 2)
                pe.wait_ge(centred, 3)
                nc.tensor.matmul(dots[:, :, :].rearrange("p a b -> p (a b)"), zero[:, 0:P], zero[:, :], start=True, stop=False,
                                 skip_group_check=True)
                turned_block(0, 0)
                with pe.Fori(0, LASTT) as i:
                    turn(i)
                turn(LASTT, last=True)
                pe.wait_ge(heads, NB + 1)
                pe.wait_ge(k_kept, NB + 1)
                product(B5 - 1).then_inc(dotted, 1)

            @block.vector
            def _(dve):
                v = nc.vector
                v.memset(zero[:, :], 0.0).then_inc(zeroed, 1)
                v.memset(kv[:, B5 - 1], 0.0).then_inc(zeroed, 1)
                dve.sem_inc(kept, 1)
                dve.sem_inc(heads, 1)
                heads_of = k.mix_kvT[:, :, :].rearrange("p c (h d) -> p c h d", d=DH)
                c = Chain(dve, centred)
                c.link(v.tensor_reduce(mean[:, :, :], heads_of, AX.X, ALU.add))
                c.link(v.tensor_scalar(mean[:, :, :], mean[:, :, :], 1.0 / DH, None, ALU.mult))
                c.link(v.tensor_tensor(heads_of, heads_of, wide(mean[:, :, :].unsqueeze(3), [P, KC, MH, DH]), ALU.subtract))
                dve.wait_ge(zeroed, 2)

                def keep(b, j):
                    dve.wait_ge(turned, b + B5 + 1)
                    v.tensor_copy(xT[:, j], ps_t[:, :, :]).then_inc(kept, 1)

                def turn(i, last=False):
                    c = Chain(dve, chain, i * (PER * B5))
                    for j in range(B5):
                        b = i * B5 + j
                        if not (last and j == B5 - 1):
                            keep(b + 1, (j + 1) % B5)
                        dve.wait_ge(squared, b + 1)
                        c.link(v.tensor_reduce(st[:, 0], sq[:, :, :], AX.X, ALU.add))
                        c.link(v.tensor_scalar(st[:, 0], st[:, 0], 1.0 / DH, EPS, ALU.mult, ALU.add))
                        c.link(v.reciprocal(st[:, 1], st[:, 0]))
                        c.link(v.tensor_tensor(st[:, 1, 0:K8], st[:, 1, 0:K8], st[:, 1, K8:MH], ALU.mult))
                        dve.sem_inc(inverse, 1)
                        dve.wait_ge(rooted, b + 1)
                        c.link(v.tensor_tensor(kv[:, j, K8:MH, :], ps_m[:, K8:MH, :], wide(st[:, 2, 0:K8].unsqueeze(2), [P, K8, DH]), ALU.mult))
                        dve.sem_inc(heads, 1)
                    assert c.n == PER * B5
                keep(0, 0)
                with dve.Fori(0, LASTT) as i:
                    turn(i)
                turn(LASTT, last=True)
                dve.wait_ge(dotted, 1)
                v.memset(k.dotsT[:, :, :], 0.0).then_inc(zeroed, 1)
                dve.wait_ge(zeroed, 3)
                for h in range(2):
                    ins = v.tensor_scalar(k.dotsT[h * DH:(h + 1) * DH, :, h * DH:(h + 1) * DH],
                                          dots[h * DH:(h + 1) * DH, :, h * DH:(h + 1) * DH], 1.0 / N, None, ALU.mult)
                ins.then_inc(zeroed, 1)
                dve.wait_ge(zeroed, 4)


def mixer_matrix0(nc, k):
    with Scope(nc) as s:
        ps = [s.ps(f"g0_{q}", [P, 512]) for q in range(6)]
        t = s.sb("g0_t", [P, 4, D])
        ready, done = s.sem("g0_ready"), s.sem("g0_done")
        with nc.Block() as block:
            @block.tensor
            def _(pe):
                for q in range(4):
                    nc.tensor.matmul(ps[q][:, 0:D], k.dotsT[:, q, :], k.mix_outT[:, q, :], start=True, stop=True).then_inc(ready, 1)
                pe.wait_ge(done, 4)
                for c in range(KC):
                    for q in range(4):
                        ins = nc.tensor.matmul(ps[4 + c][:, 0:D], k.mix_q[:, q, c * P:(c + 1) * P], t[:, q, :],
                                               start=(q == 0), stop=(q == 3))
                    ins.then_inc(ready, 1)

            @block.vector
            def _(dve):
                v = nc.vector
                for q in range(4):
                    dve.wait_ge(ready, q + 1)
                    v.tensor_copy(t[:, q, :], ps[q][:, 0:D]).then_inc(done, 1)
                for c in range(KC):
                    dve.wait_ge(ready, 5 + c)
                    v.tensor_tensor(k.W0[:, c, 3 * D:4 * D], k.W0[:, c, 3 * D:4 * D], ps[4 + c][:, 0:D], ALU.add).then_inc(done, 1)
                v.tensor_tensor(k.bias0[:, 3 * D:4 * D], k.bias0[:, 3 * D:4 * D], k.bias0[:, 4 * D:5 * D], ALU.add).then_inc(done, 1)
                dve.wait_ge(done, 7)


def edge_scores(nc, k, e, q_parts, k_tab, score):
    HD = D // H1
    HU = U // 2
    with Scope(nc) as s:
        ix = s.sb("es_ix", [P, 2, U], I32)
        kg = s.sb("es_k", [P, 2, U, D])
        rel_row = s.sb("es_rel_row", [1, 2, U * P], BF)
        hot = s.sb("es_hot", [P, 2, U * P], BF)
        ps_b = s.ps("es_b", [P, U * P])
        ps_q = s.ps("es_q", [P, U, D])
        listed, freed, spread, hotted, asked, multiplied, took = (
            s.sem("es_" + q) for q in ("listed", "freed", "spread", "hotted", "asked", "multiplied", "took"))
        got = [s.sem(f"es_got{h}") for h in range(2)]
        row = [s.sem(f"es_row{h}") for h in range(2)]
        turns = T1 // U
        assert turns % 2 == 1
        with nc.Block() as block:
            @block.gpsimd
            def _(pool):
                def turn(i, h):
                    pool.wait_ge(freed, i + 1)
                    pool.wait_ge(k.armed, 1)
                    nc.gpsimd.tensor_copy(ix[:, h, :], e.src[:, ds(i * U, U)]).then_inc(listed, 1)
                    pool.wait_ge(k.armed, 1)
                    pool.wait_ge(listed, i + 1)
                    for u in range(U):
                        nc.gpsimd.indirect_dma_start(
                            out=kg[:, h, u, :], out_offset=None, in_=k_tab,
                            in_offset=bass.IndirectOffsetOnAxis(ap=ix[:, h, u:u + 1], axis=0)).then_inc(got[h], 16)
                with pool.Fori(0, turns // 2) as w:
                    turn(w * 2, 0)
                    turn(w * 2 + 1, 1)
                turn(turns - 1, 0)

            @block.sync
            def _(sp):
                def turn(i, h):
                    sp.wait_ge(spread, i + 1)
                    sp.dma_start(rel_row[:, h, :], e.rel_rows[ds(i * U, U), :].rearrange("t e -> (t e)").rearrange("(a n) -> a n", a=1)).then_inc(row[h], 16)
                with sp.Fori(0, turns // 2) as w:
                    turn(w * 2, 0)
                    turn(w * 2 + 1, 1)
                turn(turns - 1, 0)

            @block.tensor
            def _(pe):
                pe.sem_inc(spread, 2)

                def spread_row(i, w, h):
                    pe.wait_ge(row[h], w * 16 + 16)
                    pe.wait_ge(hotted, i + 1)
                    for n in range(0, U * P, 512):
                        ins = nc.tensor.matmul(ps_b[:, n:n + 512], k.ones_h[:, :], rel_row[:, h, n:n + 512], start=True, stop=True)
                    ins.then_inc(spread, 1)

                def fetch(i, h):
                    pe.wait_ge(hotted, i + 2)
                    for u, b in enumerate(blocks_of(nc, mybir.EngineType.PE, e, i)):
                        if u % HU == 0:
                            pe.wait_ge(multiplied, i * 2 + (u // HU + 1))
                            pe.wait_ge(k.armed, 1)
                        for n in range(3):
                            ins = nc.tensor.matmul(ps_q[:, u, :], hot[:, h, u * P:(u + 1) * P],
                                                   q_parts[:, ds(b, 1), n, :].rearrange("p a d -> p (a d)"), start=(n == 0), stop=(n == 2))
                        if u % HU == HU - 1:
                            ins.then_inc(asked, 1)
                spread_row(0, 0, 0)
                with pe.Fori(0, turns // 2) as w:
                    spread_row(w * 2 + 1, w, 1)
                    fetch(w * 2, 0)
                    spread_row(w * 2 + 2, w + 1, 0)
                    fetch(w * 2 + 1, 1)
                fetch(turns - 1, 0)

            @block.vector
            def _(dve):
                v = nc.vector
                dve.sem_inc(freed, 2)
                dve.sem_inc(hotted, 1)
                dve.sem_inc(multiplied, 2)

                def mark(i, h):
                    dve.wait_ge(spread, i + 3)
                    v.tensor_scalar(hot[:, h, :], ps_b[:, :], k.count_col[:, 0:1], None, ALU.is_equal).then_inc(hotted, 1)

                def reduce(i, w, h):
                    dve.wait_ge(got[h], w * (16 * U) + 16 * U)
                    for n in range(2):
                        dve.wait_ge(asked, i * 2 + (n + 1))
                        rows = kg[:, h, n * HU:(n + 1) * HU, :]
                        v.tensor_tensor(rows, rows, ps_q[:, n * HU:(n + 1) * HU, :], ALU.mult).then_inc(multiplied, 1)
                    dve.wait_ge(multiplied, i * 2 + 4)
                    v.tensor_reduce(score[:, ds(i * U, U), :].rearrange("p t h -> p (t h)"),
                                    kg[:, h].rearrange("p u (h d) -> p (u h) d", d=HD), AX.X, ALU.add).then_inc(freed, 1)
                mark(0, 0)
                with dve.Fori(0, turns // 2) as w:
                    mark(w * 2 + 1, 1)
                    reduce(w * 2, w, 0)
                    mark(w * 2 + 2, 0)
                    reduce(w * 2 + 1, w, 1)
                reduce(turns - 1, turns // 2, 0)
                v.memset(score[:, T1:G1 * P, :], 0.0).then_inc(took, 1)
                dve.wait_ge(took, 1)
                dve.wait_ge(freed, turns + 2)


def blocks_of(nc, engine, e, i):
    return nc.values_load_multi_w_load_instructions(e.block_row[0:1, ds(i * U, U)], engines=(engine,), min_val=0, max_val=NB - 1)[1]


def attend(nc, k, e, v_tab, weight, acc):
    HD = D // H1
    W = D + H1
    turns = T1 // U
    with Scope(nc) as s:
        ix = s.sb("at_ix", [P, 2, U], I32)
        vg = s.sb("at_v", [P, 2, U, D])
        msg = s.sb("at_msg", [P, 2, U, W])
        hot = s.sb("at_hot", [P, 2, U, P])
        ps = [s.ps(f"at_ps{u}", [P, 512]) for u in range(U)]
        listed, built, summed, added = (s.sem("at_" + q) for q in ("listed", "built", "summed", "added"))
        got = [s.sem(f"at_got{h}") for h in range(2)]
        with nc.Block() as block:
            @block.gpsimd
            def _(pool):
                def turn(i, h):
                    pool.wait_ge(built, i + 1)
                    pool.wait_ge(k.armed, 1)
                    nc.gpsimd.tensor_copy(ix[:, h, :], e.src[:, ds(i * U, U)]).then_inc(listed, 1)
                    pool.wait_ge(k.armed, 1)
                    pool.wait_ge(listed, i + 1)
                    for u in range(U):
                        nc.gpsimd.indirect_dma_start(
                            out=vg[:, h, u, :], out_offset=None, in_=v_tab,
                            in_offset=bass.IndirectOffsetOnAxis(ap=ix[:, h, u:u + 1], axis=0)).then_inc(got[h], 16)
                with pool.Fori(0, turns // 2) as w:
                    turn(w * 2, 0)
                    turn(w * 2 + 1, 1)
                turn(turns - 1, 0)

            @block.tensor
            def _(pe):
                def turn(i, h):
                    pe.wait_ge(built, i + 3)
                    for u in range(U):
                        pe.wait_ge(added, i * U + (u + 1))
                        nc.tensor.matmul(ps[u][:, 0:W], hot[:, h, u, :], msg[:, h, u, :], start=True, stop=True).then_inc(summed, 1)
                with pe.Fori(0, turns // 2) as w:
                    turn(w * 2, 0)
                    turn(w * 2 + 1, 1)
                turn(turns - 1, 0)

            @block.vector
            def _(dve):
                v = nc.vector
                dve.sem_inc(built, 2)
                dve.sem_inc(added, U)

                def build(i, w, h):
                    v.tensor_tensor(hot[:, h], wide(k.count_row[:, 0:P].unsqueeze(1), [P, U, P]),
                                    wide(e.rel[:, ds(i * U, U)].unsqueeze(2), [P, U, P]), ALU.is_equal)
                    v.tensor_copy(msg[:, h, :, D:W], weight[:, ds(i * U, U), :])
                    dve.wait_ge(got[h], w * (16 * U) + 16 * U)
                    v.tensor_tensor(msg[:, h, :, 0:D].rearrange("p u (g d) -> p u g d", d=HD),
                                    vg[:, h].rearrange("p u (g d) -> p u g d", d=HD),
                                    wide(weight[:, ds(i * U, U), :].unsqueeze(3), [P, U, H1, HD]), ALU.mult).then_inc(built, 1)

                def add(i):
                    for u, b in enumerate(blocks_of(nc, mybir.EngineType.DVE, e, i)):
                        dve.wait_ge(summed, i * U + (u + 1))
                        dve.wait_ge(added, i * U + (u + U))
                        dve.wait_ge(k.armed, 1)
                        row = acc[:, ds(b, 1), :].rearrange("p a w -> p (a w)")
                        v.tensor_tensor(row, row, ps[u][:, 0:W], ALU.add).then_inc(added, 1)
                build(0, 0, 0)
                with dve.Fori(0, turns // 2) as w:
                    build(w * 2 + 1, w, 1)
                    add(w * 2)
                    build(w * 2 + 2, w + 1, 0)
                    add(w * 2 + 1)
                add(turns - 1)
                dve.wait_ge(added, T1 + U)


def combine0(nc, k, acc):
    with Scope(nc) as s:
        xn = s.sb("c0_xn", [P, B5, D])
        xT = s.sb("c0_xT", [P, B5, KC, P])
        rd = s.sb("c0_rd", [P, NB, H1])
        ps_t = [s.ps(f"c0_t{j}", [P, 512]) for j in range(2)]
        ps_o = [s.ps(f"c0_o{j}", [P, 512]) for j in range(B5)]
        normed, turned, kept, done, chain = (s.sem("c0_" + q) for q in ("normed", "turned", "kept", "done", "chain"))
        HD = D // H1
        with nc.Block() as block:
            @block.scalar
            def _(act):
                with act.Fori(0, NB // B5) as i:
                    for j in range(B5):
                        act.wait_ge(turned, i * B5 + j + 1)
                        act.wait_ge(k.armed, 1)
                        normed_block(nc, k, act, i * B5 + j, xn[:, j, :], normed)

            @block.tensor
            def _(pe):
                def turned_block(b, j):
                    pe.wait_ge(normed, b + 1)
                    pe.wait_ge(kept, b + (2 if j == 0 else 1))
                    for c in range(KC):
                        ins = nc.tensor.transpose(ps_t[j % 2][:, c * P:(c + 1) * P], xn[:, j, c * P:(c + 1) * P], k.ident[:, :])
                    ins.then_inc(turned, 1)

                def turn(i, last=False):
                    for j in range(B5):
                        b = i * B5 + j
                        if not (last and j == B5 - 1):
                            turned_block(b + 1, (j + 1) % B5)
                        pe.wait_ge(kept, b + 3)
                        nc.tensor.matmul(ps_o[j][:, 0:D], k.ones[0:1, :], k.bias0[:, 3 * D:4 * D], start=True, stop=False)
                        for c in range(KC):
                            ins = nc.tensor.matmul(ps_o[j][:, 0:D], xT[:, j, c, :], k.W0[:, c, 3 * D:4 * D], start=False, stop=(c == KC - 1))
                        ins.then_inc(done, 1)
                pe.sem_inc(turned, B5)
                turned_block(0, 0)
                with pe.Fori(0, NB // B5 - 1) as i:
                    turn(i)
                turn(NB // B5 - 1, last=True)

            @block.vector
            def _(dve):
                v = nc.vector
                dve.sem_inc(kept, 2)
                c = Chain(dve, chain)
                c.link(v.tensor_scalar(rd[:, :, :], acc[:, :, D:D + H1], 1e-30, None, ALU.max))
                c.link(v.reciprocal(rd[:, :, :], rd[:, :, :]))

                def keep(b, j):
                    dve.wait_ge(turned, b + B5 + 1)
                    v.tensor_copy(xT[:, j], ps_t[j % 2][:, 0:D].rearrange("p (c t) -> p c t", t=P)).then_inc(kept, 1)

                def turn(i, last=False):
                    c = Chain(dve, chain, i * (3 * B5) + 2)
                    for j in range(B5):
                        b = i * B5 + j
                        xb = k.X[:, ds(b, 1), :].rearrange("p a d -> p (a d)")
                        ab = acc[:, ds(b, 1), 0:D].rearrange("p a (g d) -> p (a g) d", d=HD)
                        if not (last and j == B5 - 1):
                            keep(b + 1, (j + 1) % B5)
                        c.link(v.tensor_tensor(ab, ab, wide(rd[:, ds(b, 1), :].rearrange("p a g -> p (a g)").unsqueeze(2), [P, H1, HD]), ALU.mult))
                        c.link(v.tensor_tensor(xb, xb, acc[:, ds(b, 1), 0:D].rearrange("p a d -> p (a d)"), ALU.add))
                        dve.wait_ge(done, b + 1)
                        c.link(v.tensor_tensor(xb, xb, ps_o[j][:, 0:D], ALU.add))
                    assert c.n == 3 * B5
                keep(0, 0)
                with dve.Fori(0, NB // B5 - 1) as i:
                    turn(i)
                turn(NB // B5 - 1, last=True)


def gate0(nc, k, XN, logits):
    with Scope(nc) as s:
        xn = s.sb("r0_xn", [P, B5, D])
        xT = s.sb("r0_xT", [P, B5, KC, P])
        ps_t = [s.ps(f"r0_t{j}", [P, 512]) for j in range(2)]
        ps_l = [s.ps(f"r0_l{j}", [P, 512]) for j in range(B5)]
        normed, turned, kept, done, moved = (s.sem("r0_" + q) for q in ("normed", "turned", "kept", "done", "moved"))
        taken = s.sem("r0_taken")
        with nc.Block() as block:
            @block.scalar
            def _(act):
                with act.Fori(0, NB // B5) as i:
                    for j in range(B5):
                        b = i * B5 + j
                        act.wait_ge(turned, b + 1)
                        act.wait_ge(k.armed, 1)
                        normed_block(nc, k, act, b, xn[:, j, :], normed)
                        normed_block(nc, k, act, b, XN[:, ds(b, 1), :].rearrange("p a d -> p (a d)"), moved)
                act.wait_ge(moved, NB)

            @block.tensor
            def _(pe):
                def turned_block(b, j):
                    pe.wait_ge(normed, b + 1)
                    pe.wait_ge(kept, b + (2 if j == 0 else 1))
                    for c in range(KC):
                        ins = nc.tensor.transpose(ps_t[j % 2][:, c * P:(c + 1) * P], xn[:, j, c * P:(c + 1) * P], k.ident[:, :])
                    ins.then_inc(turned, 1)

                def turn(i, last=False):
                    for j in range(B5):
                        b = i * B5 + j
                        if not (last and j == B5 - 1):
                            turned_block(b + 1, (j + 1) % B5)
                        pe.wait_ge(kept, b + 3)
                        pe.wait_ge(taken, b + 1)
                        nc.tensor.matmul(ps_l[j][:, 0:NE], k.ones[0:1, :], k.gate_b[:, :], start=True, stop=False)
                        for c in range(KC):
                            ins = nc.tensor.matmul(ps_l[j][:, 0:NE], xT[:, j, c, :], k.gate[:, c, :], start=False, stop=(c == KC - 1))
                        ins.then_inc(done, 1)
                pe.sem_inc(turned, B5)
                turned_block(0, 0)
                with pe.Fori(0, NB // B5 - 1) as i:
                    turn(i)
                turn(NB // B5 - 1, last=True)

            @block.vector
            def _(dve):
                v = nc.vector
                dve.sem_inc(kept, 2)
                dve.sem_inc(taken, B5)

                def keep(b, j):
                    dve.wait_ge(turned, b + B5 + 1)
                    v.tensor_copy(xT[:, j], ps_t[j % 2][:, 0:D].rearrange("p (c t) -> p c t", t=P)).then_inc(kept, 1)

                def turn(i, last=False):
                    for j in range(B5):
                        b = i * B5 + j
                        if not (last and j == B5 - 1):
                            keep(b + 1, (j + 1) % B5)
                        dve.wait_ge(done, b + 1)
                        dve.wait_ge(k.armed, 1)
                        v.tensor_copy(logits[:, ds(b, 1), :].rearrange("p a e -> p (a e)"), ps_l[j][:, 0:NE]).then_inc(taken, 1)
                keep(0, 0)
                with dve.Fori(0, NB // B5 - 1) as i:
                    turn(i)
                turn(NB // B5 - 1, last=True)
                dve.wait_ge(taken, NB + B5)


def route0(nc, k, XN, logits, buf, slot_i, factor):
    with Scope(nc) as s:
        S = [P, NB, NE]
        t = s.sb("ro_t", [P, 8, NB, NE])
        r = s.sb("ro_r", [P, 10, NB])
        send_i = s.sb("ro_send", [P, NB], I32)
        ps_in = s.ps("ro_in", [P, NB * NE])
        ps_all = s.ps("ro_all", [P, NB * NE])
        zero = s.sb("ro_zero", [P, 512])
        chain, asked, exped, hot, counted, sent, clear, cleared = (
            s.sem("ro_" + q) for q in ("chain", "asked", "exped", "hot", "counted", "sent", "clear", "cleared"))
        per_part = SLOTS * D // P
        run = next(x for x in range(512, 0, -1) if per_part % x == 0)
        with nc.Block() as block:
            @block.sync
            def _(sp):
                sp.wait_ge(clear, 1)
                sp.dma_start(buf[0:SLOTS, :].rearrange("s d -> (s d)").rearrange("(p m r) -> p m r", p=P, r=run),
                             wide(zero[:, 0:run].unsqueeze(1), [P, per_part // run, run])).then_inc(cleared, 16)
                sp.wait_ge(cleared, 16)

            @block.scalar
            def _(act):
                act.wait_ge(asked, 1)
                nc.scalar.activation(t[:, 1], t[:, 0], ACT.Exp).then_inc(exped, 1)

            @block.tensor
            def _(pe):
                pe.wait_ge(hot, 1)
                rhs = t[:, 3].rearrange("p b e -> p (b e)")
                nc.tensor.matmul(ps_in[:, :], k.upper[:, :], rhs, start=True, stop=True)
                nc.tensor.matmul(ps_all[:, :], k.ones[:, :], rhs, start=True, stop=True).then_inc(counted, 1)

            @block.gpsimd
            def _(pool):
                pool.wait_ge(asked, 2)
                pool.wait_ge(cleared, 16)
                for b in range(NB):
                    n = P if b < NB - 1 else LAST
                    nc.gpsimd.indirect_dma_start(
                        out=buf, out_offset=bass.IndirectOffsetOnAxis(ap=send_i[0:n, b:b + 1], axis=0),
                        in_=XN[0:n, b, :], in_offset=None).then_inc(sent, 16)
                pool.wait_ge(sent, 16 * NB)

            @block.vector
            def _(dve):
                v = nc.vector
                c = Chain(dve, chain)
                v.memset(zero[:, :], 0.0).then_inc(clear, 1)
                c.link(v.tensor_reduce(r[:, 0], logits[:, :, :], AX.X, ALU.max))
                v.tensor_tensor(t[:, 0], logits[:, :, :], wide(r[:, 0].unsqueeze(2), S), ALU.subtract).then_inc(asked, 1)
                dve.wait_ge(exped, 1)
                v.tensor_reduce(r[:, 1], t[:, 1], AX.X, ALU.add)
                c.link(v.tensor_reduce(r[:, 2], t[:, 1], AX.X, ALU.max))
                v.reciprocal(r[:, 3], r[:, 1])
                c.link(v.tensor_tensor(t[:, 2], t[:, 1], wide(r[:, 2].unsqueeze(2), S), ALU.is_lt))
                c.link(v.scalar_tensor_tensor(out=t[:, 2], in0=t[:, 2], scalar=100.0, in1=wide(k.count_row[:, 0:NE].unsqueeze(1), S),
                                              op0=ALU.mult, op1=ALU.add))
                c.link(v.tensor_reduce(r[:, 4], t[:, 2], AX.X, ALU.min))
                v.tensor_tensor(t[:, 3], t[:, 2], wide(r[:, 4].unsqueeze(2), S), ALU.is_equal).then_inc(hot, 1)
                dve.wait_ge(counted, 1)
                tot = ps_all[:, :].rearrange("p (b e) -> p b e", e=NE)
                for e in range(NE):
                    ins = v.tensor_tensor_scan(t[:, 4, :, e], wide(k.ones[:, 0:1], [P, NB]), tot[:, :, e], 0.0, ALU.mult, ALU.add)
                c.link(ins)
                c.link(v.tensor_tensor(t[:, 5], t[:, 4], tot, ALU.subtract))
                c.link(v.tensor_tensor(t[:, 5], t[:, 5], ps_in[:, :].rearrange("p (b e) -> p b e", e=NE), ALU.add))
                c.link(v.tensor_tensor(t[:, 5], t[:, 5], t[:, 3], ALU.mult))
                c.link(v.tensor_reduce(r[:, 5], t[:, 5], AX.X, ALU.add))
                v.tensor_scalar(r[:, 6], r[:, 5], float(CAP), None, ALU.is_lt)
                c.link(v.tensor_scalar(r[:, 7], r[:, 5], float(CAP - 1), None, ALU.min))
                v.tensor_tensor(r[:, 3], r[:, 3], r[:, 2], ALU.mult)
                c.link(v.scalar_tensor_tensor(out=r[:, 8], in0=r[:, 4], scalar=float(CAP), in1=r[:, 7], op0=ALU.mult, op1=ALU.add))
                v.tensor_tensor(factor[:, :], r[:, 3], r[:, 6], ALU.mult)
                v.tensor_copy(slot_i[:, :], r[:, 8])
                c.link(v.tensor_scalar(r[:, 7], k.node_id[:, :], float(SLOTS), None, ALU.add))
                c.link(v.tensor_tensor(r[:, 9], r[:, 8], r[:, 7], ALU.subtract))
                c.link(v.tensor_tensor(r[:, 9], r[:, 9], r[:, 6], ALU.mult))
                c.link(v.tensor_tensor(r[:, 9], r[:, 9], r[:, 7], ALU.add))
                c.link(v.tensor_copy(send_i[:, :], r[:, 9]))
                dve.sem_inc(asked, 1)


def experts0(nc, k, a, buf, out_buf, pairs, pair, place_i):
    FC = FE // P
    TC = [(q * P, min(P, CAP - q * P)) for q in range((CAP + P - 1) // P)]
    w1_v = a["L0_ffn_w1"].rearrange("e (c p) f -> e p c f", p=P)
    w2_v = a["L0_ffn_w2"].rearrange("e (c p) f -> e p c f", p=P)
    b1_v = a["L0_ffn_b1"].rearrange("e (c p) -> e p c", p=P)
    with Scope(nc) as s:
        w1 = s.sb("x0_w1", [P, 2, KC, FE])
        w2 = s.sb("x0_w2", [P, 2, FC, D])
        b1 = s.sb("x0_b1", [P, 2, FC])
        b2 = s.sb("x0_b2", [1, 2, D])
        rows = s.sb("x0_rows", [P, 2, len(TC), D])
        xT = s.sb("x0_xT", [P, 2, KC, CAP])
        hid = s.sb("x0_hid", [P, FC, CAP])
        y = s.sb("x0_y", [P, 2, len(TC), D])
        ps_t = [s.ps(f"x0_t{c}", [P, 512]) for c in range(KC)]
        ps_h = [s.ps(f"x0_h{j}", [P, 512]) for j in range(2)]
        ps_y = [s.ps(f"x0_y{j}", [P, 512]) for j in range(2)]
        turned, kept, h_done, h_kept, y_done, y_kept, used = (
            s.sem("x0_" + q) for q in ("turned", "kept", "h_done", "h_kept", "y_done", "y_kept", "used"))
        got = [s.sem(f"x0_got{j}") for j in range(2)]
        out = [s.sem(f"x0_out{j}") for j in range(2)]
        scatter = Scatter(s, "x0_sc_", EARLY_SCATTER, C2 // U)
        NL = 4 + len(TC)

        with nc.Block() as block:
            @block.sync
            def _(sp):
                with sp.Fori(0, NE // 2) as i:
                    for j in range(2):
                        e = i * 2 + j
                        sp.wait_ge(used, e + 1)
                        for c, (o, n) in enumerate(TC):
                            sp.dma_start(rows[0:n, j, c, :], buf[ds(e * CAP + o, n), :]).then_inc(got[j], 16)
                        sp.dma_start(w1[:, j], w1_v[ds(e, 1)].rearrange("a p c f -> p (a c) f")).then_inc(got[j], 16)
                        sp.dma_start(b1[:, j], b1_v[ds(e, 1)].rearrange("a p c -> p (a c)"),
                                     allow_slow_non_contiguous=True).then_inc(got[j], 16)
                        sp.dma_start(w2[:, j], w2_v[ds(e, 1)].rearrange("a p c f -> p (a c) f")).then_inc(got[j], 16)
                        sp.dma_start(b2[:, j, :], a["L0_ffn_b2"][ds(e, 1), :]).then_inc(got[j], 16)

            @block.gpsimd
            def _(pool):
                scatter.run(nc, k, pool, pairs, pair, place_i)

            @block.tensor
            def _(pe):
                pe.sem_inc(used, 2)

                def turn_rows(i, e, j):
                    pe.wait_ge(got[j], i * (16 * NL) + 16 * NL)
                    pe.wait_ge(kept, e + 1)
                    for c in range(KC):
                        for q, (o, n) in enumerate(TC):
                            ins = nc.tensor.transpose(ps_t[c][:, o:o + n], rows[0:n, j, q, c * P:(c + 1) * P], k.ident[0:n, 0:n])
                    ins.then_inc(turned, 1)

                def expert(i, j, last=False):
                    e = i * 2 + j
                    pe.wait_ge(kept, e + 2)
                    for f in range(FC):
                        pe.wait_ge(h_kept, e * FC + (f + 1))
                        for c in range(KC):
                            ins = nc.tensor.matmul(ps_h[f % 2][:, 0:CAP], w1[:, j, c, f * P:(f + 1) * P], xT[:, j, c, :],
                                                   start=(c == 0), stop=(c == KC - 1))
                        ins.then_inc(h_done, 1)
                    if not last:
                        turn_rows(i + j, e + 1, 1 - j)
                    pe.wait_ge(h_kept, e * FC + (FC + 2))
                    for q, (o, n) in enumerate(TC):
                        pe.wait_ge(y_kept, e * len(TC) + (q + 1))
                        nc.tensor.matmul(ps_y[q % 2][0:n, 0:D], k.ones[0:1, 0:n], b2[:, j, :], start=True, stop=False)
                        for f in range(FC):
                            ins = nc.tensor.matmul(ps_y[q % 2][0:n, 0:D], hid[:, f, o:o + n], w2[:, j, f, :],
                                                   start=False, stop=(f == FC - 1))
                        ins.then_inc(y_done, 1)
                    pe.wait_ge(y_done, e * len(TC) + len(TC))
                    pe.sem_inc(used, 1)
                turn_rows(0, 0, 0)
                with pe.Fori(0, NE // 2 - 1) as i:
                    expert(i, 0)
                    expert(i, 1)
                expert(NE // 2 - 1, 0)
                expert(NE // 2 - 1, 1, last=True)

            @block.scalar
            def _(act):
                act.sem_inc(h_kept, 2)
                with act.Fori(0, NE // 2) as i:
                    for j in range(2):
                        e = i * 2 + j
                        for f in range(FC):
                            act.wait_ge(h_done, e * FC + (f + 1))
                            nc.scalar.activation(hid[:, f, :], ps_h[f % 2][:, 0:CAP], ACT.Relu, bias=b1[:, j, f:f + 1]).then_inc(h_kept, 1)
                        act.wait_ge(y_kept, e * len(TC) + (2 + len(TC)))
                        for q, (o, n) in enumerate(TC):
                            act.dma_start(out_buf[ds(e * CAP + o, n), :], y[0:n, j, q, :]).then_inc(out[j], 16)
                for j in range(2):
                    act.wait_ge(out[j], 16 * len(TC) * (NE // 2))

            @block.vector
            def _(dve):
                v = nc.vector
                dve.sem_inc(kept, 1)
                dve.sem_inc(y_kept, 2)

                def keep(e, j):
                    dve.wait_ge(turned, e + 1)
                    v.tensor_copy(xT[:, j, 0, :], ps_t[0][:, 0:CAP])
                    v.tensor_copy(xT[:, j, 1, :], ps_t[1][:, 0:CAP]).then_inc(kept, 1)

                def turn(i, first=False, last=False):
                    for j in range(2):
                        e = i * 2 + j
                        if not (last and j == 1):
                            keep(e + 1, 1 - j)
                        if not first:
                            dve.wait_ge(out[j], i * (16 * len(TC)))
                        for q, (o, n) in enumerate(TC):
                            dve.wait_ge(y_done, e * len(TC) + (q + 1))
                            v.tensor_copy(y[0:n, j, q, :], ps_y[q % 2][0:n, 0:D]).then_inc(y_kept, 1)
                keep(0, 0)
                turn(0, first=True)
                with dve.Fori(1, NE // 2 - 1) as i:
                    turn(i)
                turn(NE // 2 - 1, last=True)


def return0(nc, k, out_buf, slot_i, factor):
    with Scope(nc) as s:
        y = s.sb("re_y", [P, NB, D])
        z = s.sb("re_z", [P, NB, D])
        m = s.sb("re_m", [P, 3, B5, D], I32)
        top = s.sb("re_top", [P, 2])
        chain, cleared, added = s.sem("re_chain"), s.sem("re_cleared"), s.sem("re_added")
        got = [s.sem(f"re_got{g}") for g in range(NB // B5)]
        with nc.Block() as block:
            @block.gpsimd
            def _(pool):
                nc.gpsimd.memset(top[:, 0:1], 1.0e4).then_inc(cleared, 1)
                nc.gpsimd.memset(top[:, 1:2], -1.0e4).then_inc(cleared, 1)
                pool.wait_ge(chain, 2)
                for b in range(NB):
                    nc.gpsimd.indirect_dma_start(
                        out=y[:, b, :], out_offset=None, in_=out_buf,
                        in_offset=bass.IndirectOffsetOnAxis(ap=slot_i[:, b:b + 1], axis=0)).then_inc(got[b // B5], 16)

            @block.vector
            def _(dve):
                v = nc.vector
                c = Chain(dve, chain)
                c.link(v.tensor_scalar(slot_i[:, :], slot_i[:, :], 0, None, ALU.max))
                c.link(v.tensor_scalar(slot_i[:, :], slot_i[:, :], SLOTS - 1, None, ALU.min))
                v.memset(z[:, :, :], 0.0).then_inc(cleared, 1)
                dve.wait_ge(cleared, 3)
                for g in range(NB // B5):
                    yg, zg = y[:, g * B5:(g + 1) * B5, :], z[:, g * B5:(g + 1) * B5, :]
                    xg = k.X[:, g * B5:(g + 1) * B5, :]
                    S = [P, B5, D]
                    dve.wait_ge(got[g], 16 * B5)
                    c.link(v.tensor_tensor(yg, yg, wide(factor[:, g * B5:(g + 1) * B5].unsqueeze(2), S), ALU.mult))
                    v.tensor_tensor(m[:, 0], yg, yg, ALU.is_equal)
                    v.tensor_scalar(m[:, 1], yg, 3.4028234663852886e38, None, ALU.is_gt)
                    c.link(v.tensor_scalar(m[:, 2], yg, -3.4028234663852886e38, None, ALU.is_lt))
                    c.link(v.copy_predicated(zg, m[:, 0], yg))
                    for n in range(2):
                        c.link(v.copy_predicated(zg, m[:, 1 + n], wide(top[:, n:n + 1].unsqueeze(2), S)))
                    c.link(v.tensor_tensor(xg, xg, zg, ALU.add))


EARLY_SCATTER = C2 // U // 2 // 2 * 2


def sort_edges(nc, k, edge_index, pairs, pair, place_i):
    turns = C2 // U
    src_v = edge_index[0:1, :].rearrange("a (p c) -> (a p) c", p=P)
    dst_v = edge_index[1:2, :].rearrange("a (p c) -> (a p) c", p=P)
    with Scope(nc) as s:
        given = s.sb("so_given", [P, 2, CG], I32)
        loop = s.sb("so_loop", [P, 2, NB])
        key = s.sb("so_key", [P, C2])
        digit_i = s.sb("so_digit_i", [P, 2, C2], I32)
        digit = s.sb("so_digit", [P, 2, C2])
        count = s.sb("so_count", [P, C2, NH])
        before = s.sb("so_before", [P, C2, NH])
        lo_h = s.sb("so_lo_h", [P, C2], BF)
        top_h = s.sb("so_top_h", [P, C2], BF)
        lo = s.sb("so_lo", [P, 2, U, P], BF)
        hi = s.sb("so_hi", [P, 2, U, NH], BF)
        low = s.sb("so_low", [P, P])
        tot = s.sb("so_tot", [P, 4, NH])
        same = s.sb("so_same", [P, 2, U, P])
        lo_t = s.sb("so_lo_t", [P, 2, U, P])
        pick = s.sb("so_pick", [P, 2, U, NH])
        place = s.sb("so_place", [P, 2, 3, U])
        edge = s.sb("so_edge", [1, 2, P, 2], I32)
        scatter = Scatter(s, "so_sc_", 0, EARLY_SCATTER)
        ps_c = [s.ps(f"so_c{h}", [P, U, NH]) for h in range(2)]
        ps_r = s.ps("so_r", [P, U, P])
        ps_l = s.ps("so_l", [P, U, P])
        ps_s = s.ps("so_s", [P, 2, NH])
        ps_g = ps_c
        got, iotas, chain, hot, counted, tabled, summed, rowed, ranked, picked, looked, ended, lowered = (
            s.sem("so_" + q) for q in ("got", "iotas", "chain", "hot", "counted", "tabled", "summed", "rowed", "ranked", "picked",
                                       "looked", "ended", "lowered"))
        placed = s.sem("so_placed")
        C_LINKS = 3
        with nc.Block() as block:
            @block.sync
            def _(sp):
                sp.dma_start(given[:, 0, :], dst_v).then_inc(got, 16)
                sp.dma_start(given[:, 1, :], src_v).then_inc(got, 16)
                sp.wait_ge(iotas, 2)
                sp.dma_start(pairs[0:1, :], edge[0:1, 0, 0, :]).then_inc(ended, 16)
                sp.dma_start(pairs[C2 * P + 1:(C2 + 1) * P, :].rearrange("(a r) b -> a r b", a=1), edge[:, 1, 0:P - 1, :]).then_inc(ended, 16)
                sp.wait_ge(ended, 32)

            @block.gpsimd
            def _(pool):
                nc.gpsimd.memset(edge[:, 0], -1).then_inc(iotas, 1)
                nc.gpsimd.memset(edge[:, 1], NONODE).then_inc(iotas, 1)
                pool.wait_ge(iotas, 2)
                scatter.run(nc, k, pool, pairs, pair, place_i, placed)

            @block.tensor
            def _(pe):
                def tally(i, h):
                    pe.wait_ge(hot, i + 1)
                    for u in range(U):
                        ins = nc.tensor.matmul(ps_c[h][:, u, :], lo[:, h, u, :], hi[:, h, u, :], start=True, stop=True)
                    ins.then_inc(counted, 1)
                with pe.Fori(0, turns // 2) as w:
                    tally(w * 2, 0)
                    tally(w * 2 + 1, 1)
                pe.wait_ge(tabled, 1)
                nc.tensor.matmul(ps_s[:, 0, :], k.upper[:, :], tot[:, 0], start=True, stop=True)
                nc.tensor.matmul(ps_s[:, 1, :], k.ones[:, :], tot[:, 0], start=True, stop=True).then_inc(summed, 1)
                def spread_low(i):
                    pe.wait_ge(picked, i + 1)
                    for u in range(U):
                        ins = nc.tensor.matmul(ps_l[:, u, :], wide(lo_h[:, ds(i * U + u, 1)], [P, P]), k.ident_h[:, :], start=True, stop=True)
                    ins.then_inc(lowered, 1)

                def spread_keys(i):
                    pe.wait_ge(ranked, i + 1)
                    for u in range(U):
                        low_col, top_col = (wide(x[:, ds(i * U + u, 1)], [P, P]) for x in (lo_h, top_h))
                        nc.tensor.matmul(ps_r[:, u, :], low_col, k.ident_h[:, :], start=True, stop=False)
                        ins = nc.tensor.matmul(ps_r[:, u, :], top_col, k.ident_h[:, :], start=False, stop=True)
                    ins.then_inc(rowed, 1)

                def look(i, h):
                    pe.wait_ge(placed, i + 1)
                    pe.wait_ge(picked, i + 2)
                    for u in range(U):
                        ins = nc.tensor.matmul(ps_g[h][:, u, :], lo_t[:, h, u, :],
                                               before[:, ds(i * U + u, 1), :].rearrange("p a h -> p (a h)"), start=True, stop=True)
                    ins.then_inc(looked, 1)
                spread_low(0)
                spread_keys(0)
                with pe.Fori(0, turns // 2 - 1) as w:
                    for h in range(2):
                        spread_low(w * 2 + h + 1)
                        look(w * 2 + h, h)
                        spread_keys(w * 2 + h + 1)
                spread_low(turns - 1)
                look(turns - 2, 0)
                spread_keys(turns - 1)
                look(turns - 1, 1)

            @block.vector
            def _(dve):
                v = nc.vector
                c = Chain(dve, chain)
                dve.wait_ge(got, 32)
                v.tensor_copy(pair[:, 0:CG, 0], given[:, 0, :])
                v.tensor_copy(pair[:, 0:CG, 1], given[:, 1, :])
                v.memset(pair[:, CG:C2, 0], NONODE)
                c.link(v.memset(pair[:, CG:C2, 1], 0))
                v.tensor_copy(loop[:, 0, :], k.node_id[:, :])
                c.link(v.tensor_scalar(loop[:, 1, :], k.node_id[:, :], float(NONODE), None, ALU.subtract))
                c.link(v.tensor_tensor(loop[:, 1, :], loop[:, 1, :], k.node_mask[:, :], ALU.mult))
                c.link(v.tensor_scalar(loop[:, 1, :], loop[:, 1, :], float(NONODE), None, ALU.add))
                c.link(v.tensor_tensor(loop[:, 0, :], loop[:, 0, :], k.node_mask[:, :], ALU.mult))
                v.tensor_copy(pair[:, CG:CG + NB, 0], loop[:, 1, :])
                c.link(v.tensor_copy(pair[:, CG:CG + NB, 1], loop[:, 0, :]))
                c.link(v.tensor_scalar(digit_i[:, 0, :], pair[:, :, 0], P - 1, None, ALU.bitwise_and))
                c.link(v.tensor_scalar(digit_i[:, 1, :], pair[:, :, 0], 7, None, ALU.arith_shift_right))
                v.tensor_copy(key[:, :], pair[:, :, 0])
                c.link(v.tensor_copy(digit[:, :, :], digit_i[:, :, :]))
                c.link(v.tensor_tensor(low[:, :], wide(k.count_col[:, 0:1], [P, P]), k.count_row[:, 0:P], ALU.is_gt))
                v.tensor_copy(lo_h[:, :], digit[:, 0, :])
                c.link(v.tensor_scalar(top_h[:, :], digit[:, 1, :], float(P), None, ALU.mult))
                base = c.n

                def mark(i, h):
                    v.tensor_tensor(lo[:, h], wide(k.count_row[:, 0:P].unsqueeze(1), [P, U, P]),
                                    wide(digit[:, 0, ds(i * U, U)].unsqueeze(2), [P, U, P]), ALU.is_equal)
                    v.tensor_tensor(hi[:, h], wide(k.count_row[:, 0:NH].unsqueeze(1), [P, U, NH]),
                                    wide(digit[:, 1, ds(i * U, U)].unsqueeze(2), [P, U, NH]), ALU.is_equal).then_inc(hot, 1)

                def keep(i, h):
                    dve.wait_ge(counted, i + 1)
                    dve.wait_ge(k.armed, 1)
                    v.tensor_copy(count[:, ds(i * U, U), :], ps_c[h][:, :, :]).then_inc(chain, 1)
                assert turns % 2 == 0
                mark(0, 0)
                with dve.Fori(0, turns // 2 - 1) as w:
                    mark(w * 2 + 1, 1)
                    keep(w * 2, 0)
                    mark(w * 2 + 2, 0)
                    keep(w * 2 + 1, 1)
                mark(turns - 1, 1)
                keep(turns - 2, 0)
                keep(turns - 1, 1)
                dve.wait_ge(chain, base + turns)
                c = Chain(dve, chain, base + turns)
                v.tensor_reduce(tot[:, 0], count[:, :, :].rearrange("p c h -> p h c"), AX.X, ALU.add).then_inc(tabled, 1)
                dve.wait_ge(summed, 1)
                c.link(v.tensor_tensor_scan(tot[:, 1], wide(k.ones[:, 0:1], [P, NH]), ps_s[:, 1, :], 0.0, ALU.mult, ALU.add))
                c.link(v.tensor_tensor(tot[:, 1], tot[:, 1], ps_s[:, 1, :], ALU.subtract))
                c.link(v.tensor_tensor(tot[:, 1], tot[:, 1], ps_s[:, 0, :], ALU.add))
                for x in range(NH):
                    ins = v.tensor_tensor_scan(before[:, :, x], wide(k.ones[:, 0:1], [P, C2]), count[:, :, x],
                                               tot[:, 1, x:x + 1], ALU.mult, ALU.add)
                c.link(ins)
                c.link(v.tensor_tensor(before[:, :, :], before[:, :, :], count[:, :, :], ALU.subtract))
                base += turns + c.n
                dve.sem_inc(ranked, 1)
                dve.sem_inc(picked, 1)
                dve.sem_inc(placed, 2)

                def low_hot(i, h):
                    v.tensor_tensor(pick[:, h], wide(k.count_row[:, 0:NH].unsqueeze(1), [P, U, NH]),
                                    wide(digit[:, 1, ds(i * U, U)].unsqueeze(2), [P, U, NH]), ALU.is_equal)
                    dve.wait_ge(lowered, i + 1)
                    v.tensor_scalar(lo_t[:, h], ps_l[:, :, :], k.count_col[:, 0:1], None, ALU.is_equal).then_inc(picked, 1)

                def rank(i, h):
                    dve.wait_ge(rowed, i + 1)
                    dve.wait_ge(k.armed, 1)
                    for u in range(U):
                        ins = v.scalar_tensor_tensor(out=same[:, h, u, :], in0=ps_r[:, u, :], scalar=key[:, ds(i * U + u, 1)], in1=low[:, :],
                                                     op0=ALU.is_equal, op1=ALU.mult, accum_out=place[:, h, 0, u:u + 1])
                    ins.then_inc(ranked, 1)

                def finish(i, h):
                    c = Chain(dve, chain, i * C_LINKS + base)
                    dve.wait_ge(looked, i + 1)
                    dve.wait_ge(ranked, i + 2)
                    c.link(v.tensor_tensor(pick[:, h], pick[:, h], ps_g[h][:, :, :], ALU.mult))
                    c.link(v.tensor_reduce(place[:, h, 1], pick[:, h], AX.X, ALU.add))
                    c.link(v.scalar_tensor_tensor(out=place[:, h, 2], in0=place[:, h, 0], scalar=1.0, in1=place[:, h, 1], op0=ALU.add, op1=ALU.add))
                    v.tensor_copy(place_i[:, ds(i * U, U)], place[:, h, 2]).then_inc(placed, 1)
                    assert c.n == C_LINKS
                low_hot(0, 0)
                with dve.Fori(0, turns // 2 - 1) as w:
                    for h in range(2):
                        rank(w * 2 + h, h)
                        low_hot(w * 2 + h + 1, 1 - h)
                        finish(w * 2 + h, h)
                rank(turns - 2, 0)
                low_hot(turns - 1, 1)
                finish(turns - 2, 0)
                rank(turns - 1, 1)
                finish(turns - 1, 1)
                dve.wait_ge(placed, turns + 2)


class Scatter:

    def __init__(self, s, name, first, last):
        self.first, self.turns = first, last - first
        assert self.turns % 2 == 0
        self.ix = s.sb(name + "ix", [P, 2, U], I32)
        self.pr = s.sb(name + "pr", [P, 2, U, 2], I32)
        self.listed = s.sem(name + "listed")
        self.sent = [s.sem(name + f"sent{h}") for h in range(2)]

    def run(self, nc, k, pool, pairs, pair, place_i, placed=None):
        turns = self.turns

        def turn(i, w, h):
            if placed is not None:
                pool.wait_ge(placed, i + 3)
            if w is not None:
                pool.wait_ge(self.sent[h], w * (16 * U))
            lists = i + 1 if w is None else pool.to_reg(i + 1)
            pool.wait_ge(k.armed, 1)
            nc.gpsimd.tensor_copy(self.ix[:, h, :], place_i[:, ds(i * U + self.first * U, U)])
            nc.gpsimd.tensor_copy(self.pr[:, h], pair[:, ds(i * U + self.first * U, U), :]).then_inc(self.listed, 1)
            pool.wait_ge(k.armed, 1)
            pool.wait_ge(self.listed, lists)
            for u in range(U):
                nc.gpsimd.indirect_dma_start(
                    out=pairs, out_offset=bass.IndirectOffsetOnAxis(ap=self.ix[:, h, u:u + 1], axis=0),
                    in_=self.pr[:, h, u, :], in_offset=None).then_inc(self.sent[h], 16)
        turn(0, None, 0)
        turn(1, None, 1)
        with pool.Fori(1, turns // 2) as w:
            turn(w * 2, w, 0)
            turn(w * 2 + 1, w, 1)
        for h in range(2):
            pool.wait_ge(self.sent[h], 16 * U * (turns // 2))


def edge_factors(nc, k, a, attr, emb_t, e, factor, scale, acc):
    LD = 2048
    Q = 512
    W2 = 2
    R = LD // W2 // Q
    loads = C1 * P // LD
    assert loads % 2 == 0 and C1 * P % LD == 0
    SILU_NORM = 1.679177
    with Scope(nc) as s:
        emb = s.sb("ef_emb", [10 * W2, 2, LD // W2])
        w1 = s.sb("ef_w1", [10 * W2, 64 * W2])
        w2 = s.sb("ef_w2", [64 * W2, W2])
        h = s.sb("ef_h", [64 * W2, 2 * R, Q])
        rad = s.sb("ef_rad", [W2, 2, LD // W2])
        angular = s.sb("ef_angular", [P, G1, P, 4])
        radial_by_step = s.sb("ef_radial_by_step", [P, G1, P])
        rows = s.sb("ef_rows", [P, G1, 4, P])
        bank = [s.ps(f"ef_bank{j}", [P, 4, P]) for j in range(max(G1, 2 * R))]
        ps_h = [x.rearrange("p a b -> p (a b)") for x in bank]
        ps_r = [s.ps(f"ef_r{j}", [W2, Q]) for j in range(2 * R)]
        rad_tab = nc.dram_tensor("edge_radial", [C1, P], F32, kind="Internal").ap()
        rad_loads = rad_tab.rearrange("c e -> (c e)").rearrange("(l a n) -> l a n", a=W2, n=LD // W2)
        emb_loads = emb_t.rearrange("f (l a n) -> l a f n", a=W2, n=LD // W2)
        attr_tab = attr.rearrange("(c e) m -> c (e m)", e=P)
        zeroed, got_w, hid, acted, radial, taken, made, turned, by_step, chain = (
            s.sem("ef_" + q) for q in ("zeroed", "got_w", "hid", "acted", "radial", "taken", "made", "turned", "by_step", "chain"))
        got = [s.sem(f"ef_got{j}") for j in range(2)]
        stored = [s.sem(f"ef_stored{j}") for j in range(2)]
        cleared = s.sem("ef_cleared")
        with nc.Block() as block:
            @block.sync
            def _(sp):
                sp.wait_ge(zeroed, 3)
                for n in range(W2):
                    sp.dma_start(w1[n * 10:(n + 1) * 10, n * 64:(n + 1) * 64], a["L1_gnn_fc_w1"]).then_inc(got_w, 16)
                    sp.dma_start(w2[n * 64:(n + 1) * 64, n:n + 1], a["L1_gnn_fc_w2"]).then_inc(got_w, 16)
                with sp.Fori(0, loads // 2) as i:
                    for j in range(2):
                        sp.wait_ge(hid, i * (2 * R) + (j + 1) * R)
                        for n in range(W2):
                            sp.dma_start(emb[n * 10:(n + 1) * 10, j, :],
                                         emb_loads[ds(i * 2 + j, 1), n].rearrange("l f n -> (l f) n")).then_inc(got[j], 16)

            @block.tensor
            def _(pe):
                pe.sem_inc(hid, 2 * R)
                pe.wait_ge(got_w, 32 * W2)
                with pe.Fori(0, loads // 2) as i:
                    for j in range(2):
                        pe.wait_ge(got[j], i * (16 * W2) + 16 * W2)
                        n = i * (2 * R) + j * R
                        for r in range(R):
                            pe.wait_ge(acted, n + (r + 1))
                            nc.tensor.matmul(ps_h[j * R + r], w1[:, :], emb[:, j, r * Q:(r + 1) * Q], start=True, stop=True).then_inc(hid, 1)
                        for r in range(R):
                            pe.wait_ge(k.armed, 1)
                            pe.wait_ge(acted, n + (r + 1 + R))
                            pe.wait_ge(taken, n + (r + 1))
                            nc.tensor.matmul(ps_r[(1 - j) * R + r][:, :], w2[:, :], h[:, (1 - j) * R + r, :], start=True, stop=True).then_inc(radial, 1)
                for r in range(R):
                    pe.wait_ge(acted, loads * R + (r + 1 + R))
                    pe.wait_ge(taken, loads * R + (r + 1))
                    nc.tensor.matmul(ps_r[R + r][:, :], w2[:, :], h[:, R + r, :], start=True, stop=True).then_inc(radial, 1)
                for g in range(G1):
                    pe.wait_ge(made, g + 1)
                    for m in range(4):
                        ins = nc.tensor.transpose(bank[g][:, m, :], rows[:, g, m, :], k.ident[:, :])
                    ins.then_inc(turned, 1)

            @block.scalar
            def _(act):
                act.sem_inc(acted, 2 * R)
                act.sem_inc(radial, R)
                with act.Fori(0, loads // 2) as i:
                    for r in range(2 * R):
                        act.wait_ge(hid, i * (2 * R) + (r + 1 + 2 * R))
                        act.wait_ge(radial, i * (2 * R) + (r + 1))
                        nc.scalar.activation(h[:, r, :], ps_h[r], ACT.Silu, scale=float(10.0 ** -0.5)).then_inc(acted, 1)

            @block.gpsimd
            def _(pool):
                for g in range(G1):
                    nc.gpsimd.indirect_dma_start(
                        out=angular[:, g].rearrange("p e m -> p (e m)"), out_offset=None, in_=attr_tab,
                        in_offset=bass.IndirectOffsetOnAxis(ap=e.chunk[:, g:g + 1], axis=0)).then_inc(by_step, 16)
                nc.gpsimd.memset(acc[:, :, :], 0.0).then_inc(cleared, 1)
                pool.wait_ge(cleared, 1)
                with pool.Fori(0, loads // 2) as i:
                    for j in range(2):
                        pool.wait_ge(k.armed, 1)
                        pool.wait_ge(taken, i * (2 * R) + (j * R + 4 * R))
                        pool.dma_start(rad_loads[ds(i * 2 + j, 1)].rearrange("l a n -> (l a) n"), rad[:, j, :]).then_inc(stored[j], 16)
                for j in range(2):
                    pool.wait_ge(stored[j], 16 * (loads // 2))
                for g in range(G1):
                    nc.gpsimd.indirect_dma_start(
                        out=radial_by_step[:, g], out_offset=None, in_=rad_tab,
                        in_offset=bass.IndirectOffsetOnAxis(ap=e.chunk[:, g:g + 1], axis=0)).then_inc(by_step, 16)

            @block.vector
            def _(dve):
                v = nc.vector
                v.memset(w1[:, :], 0.0).then_inc(zeroed, 1)
                v.memset(w2[:, :], 0.0).then_inc(zeroed, 1)
                v.memset(h[:, R:2 * R, :], 0.0).then_inc(zeroed, 1)
                dve.sem_inc(taken, 2 * R)
                dve.wait_ge(radial, 2 * R)
                dve.sem_inc(taken, R)

                def turn(i, first=False):
                    for j in range(2):
                        if not first:
                            dve.wait_ge(stored[j], i * 16)
                        for r in range(R):
                            dve.wait_ge(radial, i * (2 * R) + (j * R + r + 1 + 2 * R))
                            v.tensor_scalar(rad[:, j, r * Q:(r + 1) * Q], ps_r[j * R + r][:, :], float(SILU_NORM / 8.0 * scale), None,
                                            ALU.mult).then_inc(taken, 1)
                turn(0, True)
                with dve.Fori(1, loads // 2) as i:
                    turn(i)
                dve.wait_ge(by_step, 32 * G1)
                for g in range(G1):
                    v.tensor_tensor(rows[:, g], angular[:, g].rearrange("p e m -> p m e"),
                                    wide(radial_by_step[:, g].unsqueeze(1), [P, 4, P]), ALU.mult).then_inc(made, 1)
                for g in range(G1):
                    dve.wait_ge(turned, g + 1)
                    ins = v.tensor_copy(factor[:, g * P:(g + 1) * P, :].rearrange("p t m -> p m t"), bank[g][:, :, :])
                ins.then_inc(chain, 1)
                dve.wait_ge(chain, 1)


def gram1(nc, k, x_tab, sums):
    with Scope(nc) as s:
        xn = s.sb("g1_xn", [P, B5, D])
        xp = s.sb("g1_xp", [P, B5, D])
        zero = s.sb("g1_zero", [P, 512])
        ps = [s.ps(f"g1_{c}", [P, 512]) for c in range(KC)]
        ps_row = s.ps("g1_row", [P, 512])
        normed, used, zeroed, done, moved = (s.sem("g1_" + q) for q in ("normed", "used", "zeroed", "done", "moved"))
        out = [s.sem(f"g1_out{j}") for j in range(B5)]
        with nc.Block() as block:
            @block.scalar
            def _(act):
                def turn(i, first=False):
                    for j in range(B5):
                        act.wait_ge(used, i * B5 + j + 1)
                        if not first:
                            act.wait_ge(out[j], i * 16)
                        act.wait_ge(k.armed, 1)
                        b = i * B5 + j
                        for lo, n, m in ((0, 64, 1), (64, 192, 3)):
                            nc.scalar.activation(xp[:, j, lo:lo + n].rearrange("p (m i) -> p m i", m=m),
                                                 k.X[:, ds(b, 1), lo:lo + n].rearrange("p b d -> p (b d)").rearrange("p (i m) -> p m i", m=m),
                                                 ACT.Identity, bias=k.shift[:, ds(b, 1)], scale=k.rstd[:, ds(b, 1)])
                        normed_block(nc, k, act, b, xn[:, j, :], normed)
                turn(0, True)
                with act.Fori(1, NB // B5) as i:
                    turn(i)

            @block.sync
            def _(sp):
                with sp.Fori(0, NB // B5) as i:
                    for j in range(B5):
                        sp.wait_ge(normed, i * B5 + j + 1)
                        sp.dma_start(x_tab[ds((i * B5 + j) * P, P), :], xp[:, j, :]).then_inc(out[j], 16)
                for j in range(B5):
                    sp.wait_ge(out[j], 16 * (NB // B5))

            @block.tensor
            def _(pe):
                pe.sem_inc(used, B5)
                pe.wait_ge(zeroed, 1)
                for x in (*ps, ps_row):
                    nc.tensor.matmul(x[:, :], zero[:, 0:P], zero[:, :], start=True, stop=False, skip_group_check=True)
                with pe.Fori(0, NB // B5) as i:
                    for j in range(B5):
                        pe.wait_ge(normed, i * B5 + j + 1)
                        for c in range(KC):
                            nc.tensor.matmul(ps[c][:, 0:D], xn[:, j, c * P:(c + 1) * P], xn[:, j, :], start=False, stop=False, skip_group_check=True)
                            nc.tensor.matmul(ps[c][:, D:D + 1], xn[:, j, c * P:(c + 1) * P], k.ones[:, 0:1], start=False, stop=False, skip_group_check=True)
                        nc.tensor.matmul(ps_row[0:1, 0:D], k.ones[:, 0:1], xn[:, j, :], start=False, stop=False, skip_group_check=True).then_inc(used, 1)
                pe.wait_ge(used, NB + B5)
                pe.sem_inc(done, 1)

            @block.vector
            def _(dve):
                v = nc.vector
                v.memset(zero[:, :], 0.0).then_inc(zeroed, 1)
                dve.wait_ge(done, 1)
                for c in range(KC):
                    v.tensor_copy(sums[:, c, 0:D + 1], ps[c][:, 0:D + 1])
                v.tensor_copy(sums[0:1, 2, 0:D], ps_row[0:1, 0:D]).then_inc(moved, 1)
                dve.wait_ge(moved, 1)


def mixer_matrix1(nc, k, sums, G, g_bias):
    HD = 32
    with Scope(nc) as s:
        u = s.sb("m1x_u", [P, KC, D])
        vs = s.sb("m1x_vs", [1, D])
        pT = s.sb("m1x_pT", [P, KC, P])
        mask = s.sb("m1x_mask", [P, P])
        t = s.sb("m1x_t", [P, KC, D])
        n_row = s.sb("m1x_n", [1, 1])
        ps = [s.ps(f"m1x_{j}", [P, 512]) for j in range(6)]
        step, ready = s.sem("m1x_step"), s.sem("m1x_ready")
        wkT, wvT, wfcT = k.fcT
        bk, bv, bfc = (k.bias1[:, j * D:(j + 1) * D] for j in range(3))
        with nc.Block() as block:
            @block.tensor
            def _(pe):
                pe.wait_ge(step, 1)
                for c in range(KC):
                    for q in range(KC):
                        nc.tensor.matmul(ps[c][:, 0:D], sums[:, q, c * P:(c + 1) * P], wvT[:, q, :], start=(q == 0), stop=False)
                    nc.tensor.matmul(ps[c][:, 0:D], sums[0:1, 2, c * P:(c + 1) * P], bv, start=False, stop=True)
                for q in range(KC):
                    nc.tensor.matmul(ps[2][0:1, 0:D], sums[:, q, D:D + 1], wvT[:, q, :], start=(q == 0), stop=False)
                nc.tensor.matmul(ps[2][0:1, 0:D], n_row[:, :], bv, start=False, stop=True).then_inc(ready, 1)
                pe.wait_ge(step, 2)
                for c in range(KC):
                    for q in range(KC):
                        nc.tensor.matmul(ps[3][:, c * P:(c + 1) * P], u[:, q, c * P:(c + 1) * P], wkT[:, q, c * P:(c + 1) * P],
                                         start=(q == 0), stop=False, skip_group_check=True)
                    ins = nc.tensor.matmul(ps[3][:, c * P:(c + 1) * P], vs[:, c * P:(c + 1) * P], bk[:, c * P:(c + 1) * P],
                                           start=False, stop=True, skip_group_check=True)
                ins.then_inc(ready, 1)
                pe.wait_ge(step, 3)
                for c in range(KC):
                    ins = nc.tensor.matmul(ps[c][:, 0:D], pT[:, c, :], wfcT[:, c, :], start=True, stop=True)
                ins.then_inc(ready, 1)
                pe.wait_ge(step, 4)
                for c in range(KC):
                    for q in range(KC):
                        nc.tensor.matmul(ps[4 + c][:, 0:D], k.fc_q[:, q, c * P:(c + 1) * P], t[:, q, :], start=(q == 0), stop=(q == KC - 1))
                for q in range(KC):
                    nc.tensor.matmul(ps[2][0:1, 0:D], k.bq_col[:, q:q + 1], t[:, q, :], start=(q == 0), stop=False)
                nc.tensor.matmul(ps[2][0:1, 0:D], k.ones[0:1, 0:1], bfc, start=False, stop=True).then_inc(ready, 1)

            @block.vector
            def _(dve):
                v = nc.vector
                v.memset(n_row[:, :], float(N))
                v.memset(mask[:, :], 0.0).then_inc(step, 1)
                dve.wait_ge(step, 1)
                for h in range(P // HD):
                    v.memset(mask[h * HD:(h + 1) * HD, h * HD:(h + 1) * HD], 1.0 / N)
                dve.wait_ge(ready, 1)
                for c in range(KC):
                    v.tensor_copy(u[:, c, :], ps[c][:, 0:D])
                v.tensor_copy(vs[:, :], ps[2][0:1, 0:D]).then_inc(step, 1)
                dve.wait_ge(ready, 2)
                dve.wait_ge(step, 2)
                v.tensor_tensor(pT[:, :, :], ps[3][:, 0:2 * P].rearrange("p (c d) -> p c d", d=P),
                                wide(mask[:, :].unsqueeze(1), [P, KC, P]), ALU.mult).then_inc(step, 1)
                dve.wait_ge(ready, 3)
                v.tensor_copy(t[:, 0, :], ps[0][:, 0:D])
                v.tensor_copy(t[:, 1, :], ps[1][:, 0:D]).then_inc(step, 1)
                dve.wait_ge(ready, 4)
                for c in range(KC):
                    v.tensor_copy(G[:, c, :], ps[4 + c][:, 0:D])
                v.tensor_copy(g_bias[:, :], ps[2][0:1, 0:D]).then_inc(step, 1)
                dve.wait_ge(step, 5)


def convolve(nc, k, e, x_tab, factor, acc):
    turns = T1 // U
    M = 64
    with Scope(nc) as s:
        ix = s.sb("cv_ix", [P, 2, U], I32)
        xg = s.sb("cv_x", [P, 2, U, D])
        hot = s.sb("cv_hot", [P, 2, U, P])
        msg = s.sb("cv_msg", [P, 2, U, 512])
        s1w = s.sb("cv_s1w", [P, U, 3, M])
        ps = [s.ps(f"cv_ps{u}", [P, 512]) for u in range(U)]
        listed, freed, built, chain, summed, added = (s.sem("cv_" + q) for q in ("listed", "freed", "built", "chain", "summed", "added"))
        scaled = s.sem("cv_scaled")
        got = [s.sem(f"cv_got{h}") for h in range(2)]
        with nc.Block() as block:
            @block.gpsimd
            def _(pool):
                def turn(i, h):
                    pool.wait_ge(freed, i + 1)
                    pool.wait_ge(scaled, i + 1)
                    pool.wait_ge(k.armed, 1)
                    nc.gpsimd.tensor_copy(ix[:, h, :], e.src[:, ds(i * U, U)]).then_inc(listed, 1)
                    pool.wait_ge(k.armed, 1)
                    pool.wait_ge(listed, i + 1)
                    for u in range(U):
                        nc.gpsimd.indirect_dma_start(
                            out=xg[:, h, u, :], out_offset=None, in_=x_tab,
                            in_offset=bass.IndirectOffsetOnAxis(ap=ix[:, h, u:u + 1], axis=0)).then_inc(got[h], 16)
                with pool.Fori(0, turns // 2) as w:
                    turn(w * 2, 0)
                    turn(w * 2 + 1, 1)
                turn(turns - 1, 0)

            @block.tensor
            def _(pe):
                def turn(i, h):
                    pe.wait_ge(built, i + 1)
                    pe.wait_ge(scaled, i + 3)
                    for u in range(U):
                        pe.wait_ge(added, i * (2 * U) + (2 * u + 2))
                        nc.tensor.matmul(ps[u][:, :], hot[:, h, u, :], msg[:, h, u, :], start=True, stop=True).then_inc(summed, 1)
                with pe.Fori(0, turns // 2) as w:
                    turn(w * 2, 0)
                    turn(w * 2 + 1, 1)
                turn(turns - 1, 0)

            @block.scalar
            def _(act):
                act.sem_inc(scaled, 2)
                act.sem_inc(summed, 2 * U)

                def turn(i, w, h):
                    act.wait_ge(got[h], w * (16 * U) + 16 * U)
                    act.wait_ge(summed, i * U + U)
                    act.wait_ge(k.armed, 1)
                    for u in range(U):
                        nc.scalar.activation(msg[:, h, u, 0:D], xg[:, h, u, :], ACT.Copy, scale=factor[:, ds(i * U + u, 1), 0])
                        for m in range(3):
                            ins = nc.scalar.activation(msg[:, h, u, D + m * M:D + (m + 1) * M], xg[:, h, u, 0:M], ACT.Copy,
                                                       scale=factor[:, ds(i * U + u, 1), 1 + m])
                    ins.then_inc(scaled, 1)
                with act.Fori(0, turns // 2) as w:
                    turn(w * 2, w, 0)
                    turn(w * 2 + 1, w, 1)
                turn(turns - 1, turns // 2, 0)

            @block.vector
            def _(dve):
                v = nc.vector
                dve.sem_inc(added, 2 * U)
                dve.sem_inc(freed, 2)
                S = [P, U, 3, M]

                def build(i, w, h):
                    v.tensor_tensor(hot[:, h], wide(k.count_row[:, 0:P].unsqueeze(1), [P, U, P]),
                                    wide(e.rel[:, ds(i * U, U)].unsqueeze(2), [P, U, P]), ALU.is_equal)
                    dve.wait_ge(got[h], (0 if w is None else w) * (16 * U) + 16 * U)
                    if w is not None:
                        dve.wait_ge(built, i)
                    dve.wait_ge(k.armed, 1)
                    weights = wide(factor[:, ds(i * U, U), 1:4].unsqueeze(3), S)
                    v.tensor_tensor(s1w[:, :, :, :], xg[:, h, :, M:D].rearrange("p u (m i) -> p u m i", m=3), weights, ALU.mult).then_inc(freed, 1)
                    blocks = None if w is None else blocks_of(nc, mybir.EngineType.DVE, e, i - 1)
                    last = msg[:, h, :, D + 3 * M:512]
                    dve.wait_ge(freed, i + 3)
                    v.tensor_tensor(last, s1w[:, :, 0, :], s1w[:, :, 1, :], ALU.add).then_inc(chain, 1)
                    dve.wait_ge(chain, i + 1)
                    v.tensor_tensor(last, last, s1w[:, :, 2, :], ALU.add).then_inc(built, 1)
                    return blocks

                def add(i, blocks):
                    for u, b in enumerate(blocks):
                        dve.wait_ge(summed, i * U + (u + 1 + 2 * U))
                        for n in range(2):
                            dve.wait_ge(added, i * (2 * U) + (2 * (u + U) + n - 1))
                            dve.wait_ge(k.armed, 1)
                            row = acc[:, ds(b, 1), n * D:(n + 1) * D].rearrange("p a w -> p (a w)")
                            v.tensor_tensor(row, row, ps[u][:, n * D:(n + 1) * D], ALU.add).then_inc(added, 1)
                build(0, None, 0)
                with dve.Fori(0, turns // 2) as w:
                    blocks = build(w * 2 + 1, w, 1)
                    add(w * 2, blocks)
                    blocks = build(w * 2 + 2, w + 1, 0)
                    add(w * 2 + 1, blocks)
                add(turns - 1, blocks_of(nc, mybir.EngineType.DVE, e, turns - 1))
                dve.wait_ge(added, 2 * (T1 + U))


def combine1(nc, k, a, acc, G, g_bias):
    M = 64
    with Scope(nc) as s:
        xn = s.sb("c1_xn", [P, B5, D])
        ac = s.sb("c1_ac", [P, B5, 512])
        xT = s.sb("c1_xT", [P, B5, KC, P])
        aT = s.sb("c1_aT", [P, B5, 4, P])
        w = s.sb("c1_w", [P, 4, D])
        raw = s.sb("c1_raw", [P, 4, M])
        ps_t, ps_a, ps_o = ([s.ps(f"c1_{q}{j}", [P, 512]) for j in range(2)] for q in "tao")
        got, cleared, wready, normed, turned, kept, done, chain = (
            s.sem("c1_" + q) for q in ("got", "cleared", "wready", "normed", "turned", "kept", "done", "chain"))
        names = ("L1_gnn_w_00_0", "L1_gnn_w_10_1", "L1_gnn_w_01_1", "L1_gnn_w_11_0")
        with nc.Block() as block:
            @block.sync
            def _(sp):
                for j, n in enumerate(names):
                    for half in range(2):
                        sp.dma_start(raw[half * M:(half + 1) * M, j, :], a[n]).then_inc(got, 16)
                sp.wait_ge(got, 128)

            @block.scalar
            def _(act):
                with act.Fori(0, NB // B5) as i:
                    for j in range(B5):
                        b = i * B5 + j
                        act.wait_ge(turned, b + 1)
                        act.wait_ge(k.armed, 1)
                        nc.scalar.activation(ac[:, j, :], acc[:, ds(b, 1), :].rearrange("p a w -> p (a w)"), ACT.Copy)
                        normed_block(nc, k, act, b, xn[:, j, :], normed)

            @block.tensor
            def _(pe):
                def turned_block(b, j):
                    pe.wait_ge(normed, b + 1)
                    pe.wait_ge(kept, b + (2 if j == 0 else 1))
                    for c in range(KC):
                        nc.tensor.transpose(ps_t[j % 2][:, c * P:(c + 1) * P], xn[:, j, c * P:(c + 1) * P], k.ident[:, :])
                    for c in range(4):
                        ins = nc.tensor.transpose(ps_a[j % 2][:, c * P:(c + 1) * P], ac[:, j, c * P:(c + 1) * P], k.ident[:, :])
                    ins.then_inc(turned, 1)

                def turn(i, last=False):
                    for j in range(B5):
                        b = i * B5 + j
                        if not (last and j == B5 - 1):
                            turned_block(b + 1, (j + 1) % B5)
                        pe.wait_ge(kept, b + 3)
                        pe.wait_ge(chain, b + (2 if j == 0 else 1))
                        nc.tensor.matmul(ps_o[j % 2][:, 0:D], k.ones[0:1, :], g_bias[:, :], start=True, stop=False)
                        for c in range(KC):
                            nc.tensor.matmul(ps_o[j % 2][:, 0:D], xT[:, j, c, :], G[:, c, :], start=False, stop=False)
                        for c in range(4):
                            ins = nc.tensor.matmul(ps_o[j % 2][:, 0:D], aT[:, j, c, :], w[:, c, :], start=False, stop=(c == 3))
                        ins.then_inc(done, 1)
                pe.sem_inc(turned, B5)
                pe.wait_ge(wready, 1)
                turned_block(0, 0)
                with pe.Fori(0, NB // B5 - 1) as i:
                    turn(i)
                turn(NB // B5 - 1, last=True)

            @block.vector
            def _(dve):
                v = nc.vector
                v.memset(w[:, :, :], 0.0).then_inc(cleared, 1)
                dve.wait_ge(cleared, 1)
                dve.wait_ge(got, 128)
                for r in range(8):
                    lo, c = (r % 2) * M, r // 2
                    if r == 0:
                        ins = v.tensor_copy(w[lo:lo + M, c, 0:M], raw[lo:lo + M, 0, :])
                    elif r == 7:
                        ins = v.tensor_scalar(w[lo:lo + M, c, 0:M], raw[lo:lo + M, 3, :], float(3.0 ** -0.5), None, ALU.mult)
                    else:
                        m, j = (r - 1, 1) if r < 4 else (r - 4, 2)
                        ins = v.tensor_copy(w[lo:lo + M, c, M + m:D:3], raw[lo:lo + M, j, :])
                ins.then_inc(wready, 1)
                dve.sem_inc(kept, 2)
                dve.sem_inc(chain, 2)

                def keep(b, j):
                    dve.wait_ge(turned, b + B5 + 1)
                    v.tensor_copy(xT[:, j], ps_t[j % 2][:, 0:D].rearrange("p (c t) -> p c t", t=P))
                    v.tensor_copy(aT[:, j], ps_a[j % 2][:, :].rearrange("p (c t) -> p c t", t=P)).then_inc(kept, 1)

                def turn(i, last=False):
                    for j in range(B5):
                        b = i * B5 + j
                        xb = k.X[:, ds(b, 1), :].rearrange("p a d -> p (a d)")
                        if not (last and j == B5 - 1):
                            keep(b + 1, (j + 1) % B5)
                        dve.wait_ge(done, b + 1)
                        dve.wait_ge(k.armed, 1)
                        v.tensor_tensor(xb, xb, ps_o[j % 2][:, 0:D], ALU.add).then_inc(chain, 1)
                keep(0, 0)
                with dve.Fori(0, NB // B5 - 1) as i:
                    turn(i)
                turn(NB // B5 - 1, last=True)
                dve.wait_ge(chain, NB + 2)


GW = 16 + H2


def gate_rows(nc, k, h_tab, d_parts, xnT, row_cols):
    with Scope(nc) as s:
        xn = s.sb("gr_xn", [P, B5, D])
        xT = s.sb("gr_xT", [P, B5, KC, P])
        h = s.sb("gr_h", [P, B5, GW + H2])
        as_dst = s.sb("gr_as_dst", [P, NB, H2])
        pr = s.sb("gr_pr", [P, 2, 16])
        ps_t = [s.ps(f"gr_t{j}", [P, 512]) for j in range(2)]
        ps_h = [s.ps(f"gr_ps_h{j}", [P, 512]) for j in range(B5)]
        ps_c = s.ps("gr_c", [P, 80])
        normed, turned, kept, done, ready, chain, spread = (
            s.sem("gr_" + q) for q in ("normed", "turned", "kept", "done", "ready", "chain", "spread"))
        out = [s.sem(f"gr_out{j}") for j in range(B5)]
        PER = 4
        with nc.Block() as block:
            @block.scalar
            def _(act):
                with act.Fori(0, NB // B5) as i:
                    for j in range(B5):
                        act.wait_ge(turned, i * B5 + j + 1)
                        act.wait_ge(k.armed, 1)
                        normed_block(nc, k, act, i * B5 + j, xn[:, j, :], normed)

            @block.sync
            def _(sp):
                with sp.Fori(0, NB // B5) as i:
                    for j in range(B5):
                        sp.wait_ge(ready, i * B5 + j + 1)
                        sp.dma_start(h_tab[ds((i * B5 + j) * P, P), :], h[:, j, 0:GW]).then_inc(out[j], 16)
                for j in range(B5):
                    sp.wait_ge(out[j], 16 * (NB // B5))

            @block.tensor
            def _(pe):
                nc.tensor.matmul(ps_c[:, :], k.ones[0:1, :], k.gat_rows[:, :], start=True, stop=True).then_inc(spread, 1)
                def turned_block(b, j):
                    pe.wait_ge(normed, b + 1)
                    pe.wait_ge(kept, 2 * b + (4 if j == 0 else 2))
                    for c in range(KC):
                        ins = nc.tensor.transpose(ps_t[j % 2][:, c * P:(c + 1) * P], xn[:, j, c * P:(c + 1) * P], k.ident[:, :])
                    ins.then_inc(turned, 1)

                def turn(i, last=False):
                    for j in range(B5):
                        b = i * B5 + j
                        if not (last and j == B5 - 1):
                            turned_block(b + 1, (j + 1) % B5)
                        pe.wait_ge(kept, 2 * b + 5)
                        for c in range(KC):
                            ins = nc.tensor.matmul(ps_h[j][:, 0:16], xT[:, j, c, :], k.gat_w[:, c, :], start=(c == 0), stop=(c == KC - 1))
                        ins.then_inc(done, 1)
                pe.sem_inc(turned, B5)
                turned_block(0, 0)
                with pe.Fori(0, NB // B5 - 1) as i:
                    turn(i)
                turn(NB // B5 - 1, last=True)

            @block.vector
            def _(dve):
                v = nc.vector
                dve.sem_inc(kept, 4)
                dve.wait_ge(spread, 1)
                v.tensor_copy(row_cols[:, :], ps_c[:, :]).then_inc(chain, 1)
                dve.wait_ge(chain, 1)

                def keep(b, j):
                    dve.wait_ge(turned, b + B5 + 1)
                    v.tensor_copy(xT[:, j], ps_t[j % 2][:, 0:D].rearrange("p (c t) -> p c t", t=P)).then_inc(kept, 1)
                    v.tensor_copy(xnT[:, :, ds(b * P, P)], ps_t[j % 2][:, 0:D].rearrange("p (c t) -> p c t", t=P)).then_inc(kept, 1)

                def turn(i, first=False, last=False):
                    c = Chain(dve, chain, i * (PER * B5) + 1)
                    for j in range(B5):
                        b = i * B5 + j
                        if not (last and j == B5 - 1):
                            keep(b + 1, (j + 1) % B5)
                        if not first:
                            dve.wait_ge(out[j], i * 16)
                        dve.wait_ge(done, b + 1)
                        c.link(v.tensor_copy(h[:, j, 0:16], ps_h[j][:, 0:16]))
                        v.tensor_tensor(pr[:, 0], h[:, j, 0:16], row_cols[:, 0:16], ALU.mult)
                        c.link(v.tensor_tensor(pr[:, 1], h[:, j, 0:16], row_cols[:, 16:32], ALU.mult))
                        c.link(v.tensor_reduce(h[:, j, 16:24], pr[:, :, :].rearrange("p a (h e) -> p (a h) e", e=NX), AX.X, ALU.add))
                        dve.sem_inc(ready, 1)
                        c.link(v.tensor_copy(as_dst[:, ds(b, 1), :].rearrange("p a h -> p (a h)"), h[:, j, GW:GW + H2]))
                    assert c.n == PER * B5
                keep(0, 0)
                turn(0, first=True)
                with dve.Fori(1, NB // B5 - 1) as i:
                    turn(i)
                turn(NB // B5 - 1, last=True)
                c = Chain(dve, chain, NB * PER + 1)
                c.link(v.tensor_copy(d_parts[:, :, 0, :], as_dst[:, :, :]))
                for n in range(2):
                    c.link(v.tensor_tensor(as_dst[:, :, :], as_dst[:, :, :], d_parts[:, :, n, :], ALU.subtract))
                    c.link(v.tensor_copy(d_parts[:, :, n + 1, :], as_dst[:, :, :]))


EARLY = T2 // U // 2
assert EARLY < NB


class Experts1:

    def __init__(self, nc, s, a):
        self.nc, self.a = nc, a
        self.w1 = s.sb("x1_w1", [P, NX, KC, FX])
        self.w2 = s.sb("x1_w2", [P, NX, FX // P, D])
        self.b1 = s.sb("x1_b1", [P, NX, FX // P])
        self.b2 = s.sb("x1_b2", [1, NX, D])
        self.got = s.sem("x1_got")
        self.loads = 16 * (2 * NX + 2)

    def load(self, sp):
        a = self.a
        for e in range(NX):
            sp.dma_start(self.w1[:, e], a["L1_ffn_W1"][e].rearrange("(c p) f -> p c f", p=P)).then_inc(self.got, 16)
            sp.dma_start(self.w2[:, e], a["L1_ffn_W2"][e].rearrange("(c p) f -> p c f", p=P)).then_inc(self.got, 16)
        sp.dma_start(self.b1[:, :, :], a["L1_ffn_b1"].rearrange("e (c p) -> p e c", p=P), allow_slow_non_contiguous=True).then_inc(self.got, 16)
        sp.dma_start(self.b2[:, :, :], a["L1_ffn_b2"].rearrange("(a e) d -> a e d", a=1)).then_inc(self.got, 16)


class ExpertPass:

    def __init__(self, nc, k, s, name, x1, xnT):
        self.nc, self.k, self.x1, self.xnT = nc, k, x1, xnT
        self.hid = s.sb(name + "hid", [P, 2, FX // P, P])
        self.ps_h = [s.ps(name + f"h{j}", [P, 512]) for j in range(2)]
        self.ps_y = [s.ps(name + f"y{j}", [P, 512]) for j in range(2)]
        self.h_done, self.h_kept, self.y_done, self.y_taken = (
            s.sem(name + q) for q in ("h_done", "h_kept", "y_done", "y_taken"))

    def hidden(self, pe, b, n, e):
        pe.wait_ge(self.h_kept, n * NX + (e + 1))
        pe.wait_ge(self.k.armed, 1)
        for f in range(FX // P):
            for c in range(KC):
                ins = self.nc.tensor.matmul(self.ps_h[e % 2][:, f * P:(f + 1) * P], self.x1.w1[:, e, c, f * P:(f + 1) * P],
                                            self.xnT[:, c:c + 1, ds(b * P, P)].rearrange("p a t -> p (a t)"),
                                            start=(c == 0), stop=(c == KC - 1))
        ins.then_inc(self.h_done, 1)

    def output(self, pe, n, e):
        pe.wait_ge(self.h_kept, n * NX + (e + 3))
        pe.wait_ge(self.y_taken, n * NX + (e + 1))
        self.nc.tensor.matmul(self.ps_y[e % 2][:, 0:D], self.k.ones[0:1, :], self.x1.b2[:, e, :], start=True, stop=False)
        for f in range(FX // P):
            ins = self.nc.tensor.matmul(self.ps_y[e % 2][:, 0:D], self.hid[:, e % 2, f, :], self.x1.w2[:, e, f, :],
                                        start=False, stop=(f == FX // P - 1))
        ins.then_inc(self.y_done, 1)

    def first_half(self, pe, b, n):
        self.hidden(pe, b, n, 0)
        self.hidden(pe, b, n, 1)
        self.output(pe, n, 0)
        self.hidden(pe, b, n, 2)

    def second_half(self, pe, b, n):
        self.output(pe, n, 1)
        self.hidden(pe, b, n, 3)
        self.output(pe, n, 2)
        self.output(pe, n, 3)

    def activate(self, act, n, e):
        act.wait_ge(self.h_done, n * NX + (e + 1))
        for f in range(FX // P):
            ins = self.nc.scalar.activation(self.hid[:, e % 2, f, :], self.ps_h[e % 2][:, f * P:(f + 1) * P], ACT.Gelu,
                                            bias=self.x1.b1[:, e, f:f + 1])
        ins.then_inc(self.h_kept, 1)


def gate_scores(nc, k, e, h_tab, d_parts, rows, score, x1, xnT, y_tab):
    turns = T2 // U
    with Scope(nc) as s:
        ix = s.sb("gs_ix", [P, 2, U], I32)
        hg = s.sb("gs_h", [P, 2, U, GW])
        rel_row = s.sb("gs_rel_row", [1, 2, U * P], BF)
        hot = s.sb("gs_hot", [P, 2, U * P], BF)
        t = s.sb("gs_t", [P, U, H2])
        as_dst = s.sb("gs_as_dst", [P, U, H2])
        ps_b = s.ps("gs_b", [P, U * P])
        ps_d = [s.ps(f"gs_d{h}", [P, 512]) for h in range(2)]
        y = s.sb("gs_y", [P, NX, D])
        run = ExpertPass(nc, k, s, "gs_x_", x1, xnT)
        stored = s.sem("gs_stored")
        listed, freed, spread, hotted, asked, chain, took = (
            s.sem("gs_" + q) for q in ("listed", "freed", "spread", "hotted", "asked", "chain", "took"))
        got = [s.sem(f"gs_got{h}") for h in range(2)]
        row = [s.sem(f"gs_row{h}") for h in range(2)]
        assert turns % 2 == 1
        with nc.Block() as block:
            @block.gpsimd
            def _(pool):
                def turn(i, h):
                    pool.wait_ge(freed, i + 1)
                    pool.wait_ge(k.armed, 1)
                    nc.gpsimd.tensor_copy(ix[:, h, :], e.src[:, ds(i * U, U)]).then_inc(listed, 1)
                    pool.wait_ge(k.armed, 1)
                    pool.wait_ge(listed, i + 1)
                    for u in range(U):
                        nc.gpsimd.indirect_dma_start(
                            out=hg[:, h, u, :], out_offset=None, in_=h_tab,
                            in_offset=bass.IndirectOffsetOnAxis(ap=ix[:, h, u:u + 1], axis=0)).then_inc(got[h], 16)
                with pool.Fori(0, turns // 2) as w:
                    turn(w * 2, 0)
                    turn(w * 2 + 1, 1)
                turn(turns - 1, 0)

            @block.scalar
            def _(act):
                act.sem_inc(run.h_kept, 2)
                act.sem_inc(run.y_taken, 2)

                def keep(n, e, first):
                    if e == 0 and not first:
                        act.wait_ge(stored, n * 16)
                    act.wait_ge(run.y_done, n * NX + (e + 1))
                    nc.scalar.activation(y[:, e, :], run.ps_y[e % 2][:, 0:D], ACT.Copy).then_inc(run.y_taken, 1)

                def one(n, first=False):
                    run.activate(act, n, 0)
                    run.activate(act, n, 1)
                    keep(n, 0, first)
                    run.activate(act, n, 2)
                    keep(n, 1, first)
                    run.activate(act, n, 3)
                    keep(n, 2, first)
                    keep(n, 3, first)
                    act.wait_ge(run.y_taken, n * NX + (NX + 2))
                    act.dma_start(y_tab[ds(n * P, P), :], y[:, :, :].rearrange("p e d -> p (e d)")).then_inc(stored, 16)
                one(0, first=True)
                with act.Fori(1, EARLY) as n:
                    one(n)
                act.wait_ge(stored, 16 * EARLY)

            @block.sync
            def _(sp):
                def turn(i, h):
                    sp.wait_ge(spread, i + 1)
                    sp.dma_start(rel_row[:, h, :], e.rel_rows[ds(i * U, U), :].rearrange("t e -> (t e)").rearrange("(a n) -> a n", a=1)).then_inc(row[h], 16)
                with sp.Fori(0, turns // 2) as w:
                    turn(w * 2, 0)
                    turn(w * 2 + 1, 1)
                turn(turns - 1, 0)

            @block.tensor
            def _(pe):
                pe.sem_inc(spread, 2)
                pe.wait_ge(x1.got, x1.loads)

                def spread_row(i, w, h):
                    pe.wait_ge(row[h], w * 16 + 16)
                    pe.wait_ge(hotted, i + 1)
                    for n in range(0, U * P, 512):
                        ins = nc.tensor.matmul(ps_b[:, n:n + 512], k.ones_h[:, :], rel_row[:, h, n:n + 512], start=True, stop=True)
                    ins.then_inc(spread, 1)

                def fetch(i, h):
                    pe.wait_ge(hotted, i + 2)
                    pe.wait_ge(freed, i + 1)
                    pe.wait_ge(k.armed, 1)
                    for u, b in enumerate(blocks_of(nc, mybir.EngineType.PE, e, i)):
                        ins = nc.tensor.matmul(ps_d[h][:, u * 3 * H2:(u + 1) * 3 * H2], hot[:, h, u * P:(u + 1) * P],
                                               d_parts[:, ds(b, 1)].rearrange("p a n h -> p (a n h)"), start=True, stop=True)
                    ins.then_inc(asked, 1)
                spread_row(0, 0, 0)
                with pe.Fori(0, turns // 2) as w:
                    spread_row(w * 2 + 1, w, 1)
                    fetch(w * 2, 0)
                    run.first_half(pe, w, w)
                    spread_row(w * 2 + 2, w + 1, 0)
                    fetch(w * 2 + 1, 1)
                    run.second_half(pe, w, w)
                fetch(turns - 1, 0)

            @block.vector
            def _(dve):
                v = nc.vector
                dve.sem_inc(freed, 2)
                dve.sem_inc(hotted, 1)

                def mark(i, h):
                    dve.wait_ge(spread, i + 3)
                    v.tensor_scalar(hot[:, h, :], ps_b[:, :], k.count_col[:, 0:1], None, ALU.is_equal).then_inc(hotted, 1)

                def add(i, w, h):
                    dve.wait_ge(got[h], w * (16 * U) + 16 * U)
                    dve.wait_ge(asked, i + 1)
                    v.tensor_reduce(as_dst[:, :, :], ps_d[h][:, 0:U * 3 * H2].rearrange("p (u n h) -> p u h n", n=3, h=H2), AX.X, ALU.add).then_inc(chain, 1)
                    dve.wait_ge(chain, i * 3 + 1)
                    v.tensor_tensor(t[:, :, :], hg[:, h, :, 16:GW], as_dst[:, :, :], ALU.add).then_inc(chain, 1)
                    dve.wait_ge(k.armed, 1)
                    v.tensor_copy(rows[:, ds(i * U, U), :], hg[:, h, :, 0:16]).then_inc(freed, 1)
                    dve.wait_ge(chain, i * 3 + 2)
                    v.scalar_tensor_tensor(out=score[:, ds(i * U, U), :], in0=t[:, :, :], scalar=0.2, in1=t[:, :, :],
                                           op0=ALU.mult, op1=ALU.max).then_inc(chain, 1)
                    dve.wait_ge(chain, i * 3 + 3)
                mark(0, 0)
                with dve.Fori(0, turns // 2) as w:
                    mark(w * 2 + 1, 1)
                    add(w * 2, w, 0)
                    mark(w * 2 + 2, 0)
                    add(w * 2 + 1, w, 1)
                add(turns - 1, turns // 2, 0)
                v.memset(score[:, T2:G2 * P, :], 0.0).then_inc(took, 1)
                dve.wait_ge(took, 1)
                dve.wait_ge(freed, turns + 2)


def gate_sums(nc, k, e, rows, weight, acc):
    W = 16 + H2
    turns = T2 // U
    assert NB * W <= 512
    with Scope(nc) as s:
        msg = s.sb("gu_msg", [P, 2, U, W])
        hot = s.sb("gu_hot", [P, 2, U, P])
        zero = s.sb("gu_zero", [P, 512])
        ps = s.ps("gu_ps", [P, 512])
        zeroed, built, summed, kept = (s.sem("gu_" + q) for q in ("zeroed", "built", "summed", "kept"))
        with nc.Block() as block:
            @block.tensor
            def _(pe):
                pe.sem_inc(summed, 2)
                pe.wait_ge(zeroed, 1)
                nc.tensor.matmul(ps[:, :], zero[:, 0:P], zero[:, :], start=True, stop=False, skip_group_check=True)

                def turn(i, h):
                    blocks = blocks_of(nc, mybir.EngineType.PE, e, i)
                    pe.wait_ge(built, i + 1)
                    pe.wait_ge(k.armed, 1)
                    for u, b in enumerate(blocks):
                        ins = nc.tensor.matmul(ps[:, ds(b * W, W)], hot[:, h, u, :], msg[:, h, u, :], start=False, stop=False,
                                               skip_group_check=True)
                    ins.then_inc(summed, 1)
                with pe.Fori(0, turns // 2) as w:
                    turn(w * 2, 0)
                    turn(w * 2 + 1, 1)
                turn(turns - 1, 0)

            @block.vector
            def _(dve):
                v = nc.vector
                v.memset(zero[:, :], 0.0).then_inc(zeroed, 1)

                def build(i, h):
                    dve.wait_ge(summed, i + 1)
                    v.tensor_tensor(hot[:, h], wide(k.count_row[:, 0:P].unsqueeze(1), [P, U, P]),
                                    wide(e.rel[:, ds(i * U, U)].unsqueeze(2), [P, U, P]), ALU.is_equal)
                    v.tensor_copy(msg[:, h, :, 16:W], weight[:, ds(i * U, U), :])
                    v.tensor_tensor(msg[:, h, :, 0:16].rearrange("p u (g d) -> p u g d", d=NX),
                                    rows[:, ds(i * U, U), :].rearrange("p u (g d) -> p u g d", d=NX),
                                    wide(weight[:, ds(i * U, U), :].unsqueeze(3), [P, U, H2, NX]), ALU.mult).then_inc(built, 1)
                with dve.Fori(0, turns // 2) as w:
                    build(w * 2, 0)
                    build(w * 2 + 1, 1)
                build(turns - 1, 0)
                dve.wait_ge(summed, turns + 2)
                v.tensor_copy(acc[:, :, :].rearrange("p b w -> p (b w)"), ps[:, 0:NB * W]).then_inc(kept, 1)
                dve.wait_ge(kept, 1)


def top_two(nc, k, acc, row_cols, gates):
    with Scope(nc) as s:
        S16, S4 = [P, NB, 16], [P, NB, NX]
        t = s.sb("tt_t", [P, 3, NB, 16])
        q = s.sb("tt_q", [P, 8, NB, NX])
        r = s.sb("tt_r", [P, 10, NB])
        chain, ask, ans = s.sem("tt_chain"), s.sem("tt_ask"), s.sem("tt_ans")
        with nc.Block() as block:
            @block.scalar
            def _(act):
                act.wait_ge(ask, 1)
                nc.scalar.activation(r[:, 3], r[:, 2], ACT.Sqrt).then_inc(ans, 1)
                act.wait_ge(ask, 2)
                nc.scalar.activation(r[:, 7], r[:, 6], ACT.Exp).then_inc(ans, 1)

            @block.vector
            def _(dve):
                v = nc.vector
                c = Chain(dve, chain)
                row = lambda j: wide(row_cols[:, 16 * j:16 * j + 16].unsqueeze(1), S16)
                c.link(v.tensor_scalar(q[:, 0], acc[:, :, 16:20], 1e-16, None, ALU.add))
                c.link(v.reciprocal(q[:, 1], q[:, 0]))
                c.link(v.tensor_tensor(t[:, 0].rearrange("p b (h e) -> p b h e", e=NX),
                                       acc[:, :, 0:16].rearrange("p b (h e) -> p b h e", e=NX),
                                       wide(q[:, 1].unsqueeze(3), [P, NB, H2, NX]), ALU.mult))
                c.link(v.tensor_tensor(t[:, 0], t[:, 0], row(2), ALU.add))
                c.link(v.tensor_reduce(r[:, 0], t[:, 0], AX.X, ALU.add))
                c.link(v.tensor_scalar(r[:, 0], r[:, 0], 1.0 / 16, None, ALU.mult))
                c.link(v.tensor_tensor(t[:, 0], t[:, 0], wide(r[:, 0].unsqueeze(2), S16), ALU.subtract))
                c.link(v.tensor_tensor(t[:, 1], t[:, 0], t[:, 0], ALU.mult))
                c.link(v.tensor_reduce(r[:, 1], t[:, 1], AX.X, ALU.add))
                c.link(v.tensor_scalar(r[:, 1], r[:, 1], 1.0 / 16, EPS, ALU.mult, ALU.add))
                v.reciprocal(r[:, 2], r[:, 1]).then_inc(ask, 1)
                dve.wait_ge(ans, 1)
                c.link(v.tensor_tensor(t[:, 0], t[:, 0], wide(r[:, 3].unsqueeze(2), S16), ALU.mult))
                c.link(v.tensor_tensor(t[:, 0], t[:, 0], row(3), ALU.mult))
                c.link(v.tensor_tensor(t[:, 0], t[:, 0], row(4), ALU.add))
                c.link(v.tensor_reduce(q[:, 2], t[:, 0].rearrange("p b (h e) -> p b e h", e=NX), AX.X, ALU.add))
                c.link(v.tensor_scalar(q[:, 2], q[:, 2], 1.0 / H2, None, ALU.mult))
                count = wide(k.count_row[:, 0:NX].unsqueeze(1), S4)

                def first_best(score, best, hot, tmp):
                    c.link(v.tensor_reduce(best, score, AX.X, ALU.max))
                    c.link(v.tensor_tensor(tmp, score, wide(best.unsqueeze(2), S4), ALU.is_lt))
                    c.link(v.scalar_tensor_tensor(out=tmp, in0=tmp, scalar=100.0, in1=count, op0=ALU.mult, op1=ALU.add))
                    c.link(v.tensor_reduce(r[:, 8], tmp, AX.X, ALU.min))
                    c.link(v.tensor_tensor(hot, tmp, wide(r[:, 8].unsqueeze(2), S4), ALU.is_equal))
                first_best(q[:, 2], r[:, 4], q[:, 3], q[:, 5])
                c.link(v.scalar_tensor_tensor(out=q[:, 6], in0=q[:, 3], scalar=LOW, in1=q[:, 2], op0=ALU.mult, op1=ALU.add))
                first_best(q[:, 6], r[:, 5], q[:, 4], q[:, 5])
                v.tensor_tensor(r[:, 6], r[:, 5], r[:, 4], ALU.subtract).then_inc(ask, 1)
                dve.wait_ge(ans, 2)
                c.link(v.tensor_scalar(r[:, 8], r[:, 7], 1.0, None, ALU.add))
                c.link(v.reciprocal(r[:, 9], r[:, 8]))
                c.link(v.tensor_tensor(r[:, 7], r[:, 7], r[:, 9], ALU.mult))
                v.tensor_tensor(q[:, 3], q[:, 3], wide(r[:, 9].unsqueeze(2), S4), ALU.mult)
                c.link(v.tensor_tensor(q[:, 4], q[:, 4], wide(r[:, 7].unsqueeze(2), S4), ALU.mult))
                c.link(v.tensor_tensor(gates[:, :, :], q[:, 3], q[:, 4], ALU.add))


def experts1(nc, k, x1, xnT, y_tab, gates):
    LATE = NB - EARLY
    R = EARLY // LATE
    REST = EARLY - R * LATE
    assert R >= 1 and REST <= R
    with Scope(nc) as s:
        y = s.sb("x1_y", [P, R, NX, D])
        run = ExpertPass(nc, k, s, "x1_", x1, xnT)
        added, taken = s.sem("x1_added"), s.sem("x1_taken")
        back = [s.sem(f"x1_back{r}") for r in range(R)]
        with nc.Block() as block:
            def fetched(sp, i, count):
                for r in range(count):
                    sp.wait_ge(taken, i + 1)
                    sp.dma_start(y[:, r].rearrange("p e d -> p (e d)"), y_tab[ds((i * R + r) * P, P), :]).then_inc(back[r], 16)

            @block.sync
            def _(sp):
                with sp.Fori(0, LATE) as i:
                    fetched(sp, i, R)
                fetched(sp, LATE, REST)

            @block.tensor
            def _(pe):
                with pe.Fori(0, LATE) as i:
                    run.first_half(pe, i + EARLY, i)
                    run.second_half(pe, i + EARLY, i)

            @block.scalar
            def _(act):
                act.sem_inc(run.h_kept, 2)
                with act.Fori(0, LATE) as i:
                    for e in range(NX):
                        run.activate(act, i, e)

            @block.vector
            def _(dve):
                v = nc.vector
                dve.sem_inc(run.y_taken, 2)
                dve.sem_inc(taken, 1)

                def gate(b, e):
                    return gates[:, ds(b, 1), e:e + 1].rearrange("p a b -> p (a b)")

                def add(b, e, of, sem):
                    xb = k.X[:, ds(b, 1), :].rearrange("p a d -> p (a d)")
                    v.scalar_tensor_tensor(out=xb, in0=of, scalar=gate(b, e), in1=xb, op0=ALU.mult, op1=ALU.add).then_inc(sem, 1)

                def stored(i, count, done):
                    for r in range(count):
                        dve.wait_ge(back[r], i * 16 + 16)
                    for e in range(NX):
                        for r in range(count):
                            if e:
                                dve.wait_ge(added, done + ((e - 1) * count + r + 1))
                            dve.wait_ge(k.armed, 1)
                            add(i * R + r, e, y[:, r, e, :], added)
                    dve.wait_ge(added, done + NX * count)
                    dve.sem_inc(taken, 1)
                with dve.Fori(0, LATE) as i:
                    stored(i, R, i * (NX * R))
                    for e in range(NX):
                        dve.wait_ge(run.y_done, i * NX + (e + 1))
                        dve.wait_ge(run.y_taken, i * NX + (e + 2))
                        dve.wait_ge(k.armed, 1)
                        add(i + EARLY, e, run.ps_y[e % 2][:, 0:D], run.y_taken)
                if REST:
                    stored(LATE, REST, NX * R * LATE)
                dve.wait_ge(run.y_taken, LATE * NX + 2)


def store(nc, k, out):
    with Scope(nc) as s:
        stored = s.sem("stored")
        with nc.Block() as block:
            @block.sync
            def _(sp):
                sp.dma_start(out[0:(NB - 1) * P, :].rearrange("(b p) d -> p b d", p=P), k.X[:, 0:NB - 1, :]).then_inc(stored, 16)
                sp.dma_start(out[(NB - 1) * P:N, :], k.X[0:LAST, NB - 1, :]).then_inc(stored, 16)
                sp.wait_ge(stored, 32)


class Kept:

    def __init__(self, s):
        self.ident = s.sb("ident", [P, P])
        self.ident_h = s.sb("ident_h", [P, P], BF)
        self.ones = s.sb("ones", [P, P])
        self.ones_h = s.sb("ones_h", [1, P], BF)
        self.upper = s.sb("upper", [P, P])
        self.count_row = s.sb("count_row", [P, 512])
        self.count_col = s.sb("count_col", [P, 4])
        self.armed_dummy = s.sb("armed_dummy", [P, 1])
        self.node_id = s.sb("node_id", [P, NB])
        self.node_mask = s.sb("node_mask", [P, NB])
        self.X = s.sb("X", [P, NB, D])
        self.rstd = s.sb("rstd", [P, NB])
        self.shift = s.sb("shift", [P, NB])
        self.W0 = s.sb("W0", [P, KC, 4 * D])
        self.bias0 = s.sb("bias0", [1, 5 * D])
        self.mix_q = s.sb("mix_q", [P, 4, D])
        self.mix_kvT = s.sb("mix_kvT", [P, KC, 1024])
        self.mix_outT = s.sb("mix_outT", [P, 4, D])
        self.dotsT = s.sb("dotsT", [P, 4, P])
        self.gate = s.sb("gate", [P, KC, NE])
        self.gate_b = s.sb("gate_b", [1, NE])
        self.fc_q = s.sb("fc_q", [P, KC, D])
        self.bias1 = s.sb("bias1", [1, 3 * D])
        self.bq_col = s.sb("bq_col", [P, KC])
        self.gat_w = s.sb("gat_w", [P, KC, 16])
        self.gat_rows = s.sb("gat_rows", [1, 80])
        self.fcT = [s.sb(f"fcT{j}", [P, KC, D]) for j in range(3)]


class Graph:

    def __init__(self, s, name, groups):
        self.valid, self.starts, self.ends = (s.sb(name + x, [P, groups, P]) for x in ("valid", "starts", "ends"))
        self.rel = s.sb(name + "rel", [P, groups * P])
        self.src = s.sb(name + "src", [P, groups * P], I32)
        self.rel_rows = s.nc.dram_tensor(name + "rel_rows", [groups * P, P], BF, kind="Internal").ap()
        self.block_row = s.sb(name + "block_row", [1, groups * P], I32)
        self.chunk = s.sb(name + "chunk", [P, groups], I32)


def program(nc, a, out):
    with Scope(nc) as s:
        k = Kept(s)
        k.armed = nc.alloc_semaphore("armed")
        Scope.used.clear()

        def dram(name, shape, dt=F32):
            return nc.dram_tensor(name, shape, dt, kind="Internal").ap()

        def steps(e, name, pairs, chunks, groups, n):
            build_steps(nc, k, name, pairs, chunks, groups, n, e.valid, e.starts, e.ends, e.rel, e.src, e.rel_rows,
                        e.block_row, e.chunk)

        k_tab, v_tab, x_tab = (dram(n + "_tab", [NPAD, D]) for n in "kvx")
        h_tab = dram("h_tab", [NPAD, GW])
        slots, slots_out = dram("expert_rows", [SLOTS + NPAD, D]), dram("expert_out", [SLOTS, D])
        make_constants(nc, k)
        with Scope(nc) as g:
            e1 = Graph(g, "e1_", G1)
            with Scope(nc) as t:
                ld = Loads(nc, t, k, a)
                steps(e1, "s1_", a["pairs"], C1, G1, T1)
                turn_weights(nc, k, ld)

            layer_stats(nc, k, "n0_")
            with Scope(nc) as t:
                score = t.sb("score1", [P, G1 * P, H1])
                with Scope(nc) as t2:
                    q_parts = t2.sb("q_parts", [P, NB, 3, D], BF)
                    project0(nc, k, q_parts, k_tab, v_tab)
                    mixer_matrix0(nc, k)
                    edge_scores(nc, k, e1, q_parts, k_tab, score)
                acc = t.sb("acc0", [P, NB, D + H1])
                segment_softmax(nc, k, "m1_", G1, H1, score, e1.valid, e1.starts, e1.ends, float((D // H1) ** -0.5), acc)
                attend(nc, k, e1, v_tab, score, acc)
                combine0(nc, k, acc)
            with Scope(nc) as t:
                pairs2 = dram("pairs2", [(C2 + 1) * P, 2], I32)
                pair = t.sb("gating_pair", [P, C2, 2], I32)
                place_i = t.sb("gating_place", [P, C2], I32)
                sort_edges(nc, k, a["L1_ffn_edge_index"], pairs2, pair, place_i)
                layer_stats(nc, k, "n1_")
                XN = t.sb("XN", [P, NB, D])
                logits = t.sb("logits", [P, NB, NE])
                slot_i = t.sb("slot_i", [P, NB], I32)
                factor = t.sb("factor", [P, NB])
                gate0(nc, k, XN, logits)
                route0(nc, k, XN, logits, slots, slot_i, factor)
                experts0(nc, k, a, slots, slots_out, pairs2, pair, place_i)
                return0(nc, k, slots_out, slot_i, factor)

            recycle_semaphores(nc)

            layer_stats(nc, k, "n2_")
            with Scope(nc) as t:
                G = t.sb("G", [P, KC, D])
                g_bias = t.sb("g_bias", [1, D])
                acc = t.sb("acc1", [P, NB, 512])
                with Scope(nc) as t2:
                    factors = t2.sb("factors", [P, G1 * P, 4])
                    with Scope(nc) as t3:
                        sums = t3.sb("sums", [P, 3, D + 1])
                        gram1(nc, k, x_tab, sums)
                        edge_factors(nc, k, a, a["attr"], a["emb_t"], e1, factors, 128.0 ** -0.5 * 16.0 ** -0.5, acc)
                        mixer_matrix1(nc, k, sums, G, g_bias)
                    convolve(nc, k, e1, x_tab, factors, acc)
                combine1(nc, k, a, acc, G, g_bias)

        e2 = Graph(s, "e2_", G2)
        steps(e2, "s2_", pairs2, C2, G2, T2)
        x1 = Experts1(nc, s, a)
        layer_stats(nc, k, "n3_", x1.load)
        xnT = s.sb("xnT", [P, KC, NPAD])
        row_cols = s.sb("row_cols", [P, 80])
        gates = s.sb("gates", [P, NB, NX])
        y_tab = dram("experts1_out", [EARLY * P, NX * D])
        d_parts = s.sb("d_parts", [P, NB, 3, H2], BF)
        gate_rows(nc, k, h_tab, d_parts, xnT, row_cols)
        with Scope(nc) as t:
            acc = t.sb("acc2", [P, NB, 16 + H2])
            rows = t.sb("gate_edge_rows", [P, G2 * P, 16])
            score = t.sb("score2", [P, G2 * P, H2])
            gate_scores(nc, k, e2, h_tab, d_parts, rows, score, x1, xnT, y_tab)
            segment_softmax(nc, k, "m2_", G2, H2, score, e2.valid, e2.starts, e2.ends, 1.0)
            gate_sums(nc, k, e2, rows, score, acc)
            top_two(nc, k, acc, row_cols, gates)
        experts1(nc, k, x1, xnT, y_tab, gates)
        store(nc, k, out)


_PLAIN = ["x", "L0_gnn_Wq", "L0_gnn_bq", "L0_gnn_Wk", "L0_gnn_bk", "L0_gnn_Wv", "L0_gnn_bv", "L0_gnn_Ws", "L0_gnn_bs",
          "L0_mix_Wqkv", "L0_mix_Wout", "L0_mix_bout", "L0_ffn_gate_w", "L0_ffn_gate_b", "L0_ffn_w1", "L0_ffn_b1", "L0_ffn_w2",
          "L0_ffn_b2", "L1_gnn_w_00_0", "L1_gnn_w_11_0", "L1_gnn_w_01_1", "L1_gnn_w_10_1", "L1_gnn_fc_w1", "L1_gnn_fc_w2",
          "L1_mix_Wq", "L1_mix_bq", "L1_mix_Wk", "L1_mix_bk", "L1_mix_Wv", "L1_mix_bv", "L1_mix_Wfc", "L1_mix_bfc",
          "L1_ffn_W_gat", "L1_ffn_att_src", "L1_ffn_att_dst", "L1_ffn_b_gat", "L1_ffn_ln_gamma", "L1_ffn_ln_beta",
          "L1_ffn_W1", "L1_ffn_b1", "L1_ffn_W2", "L1_ffn_b2", "L1_ffn_edge_index"]


def kernel(**inputs):
    import numpy as np
    import concourse.bacc as bacc
    from concourse.bass_utils import run_bass_kernel_spmd

    arrays = {n: np.ascontiguousarray(inputs[n]) for n in _PLAIN}
    dst, src = np.asarray(inputs["dst"]), np.asarray(inputs["src"])
    pairs = np.full(((C1 + 1) * P, 2), NONODE, dst.dtype)
    pairs[:, 1] = 0
    pairs[0, 0] = -1
    pairs[1:E1 + 1, 0] = dst
    pairs[1:E1 + 1, 1] = src
    arrays["pairs"] = pairs
    attr = np.zeros((C1 * P, 4), np.float32)
    attr[:E1] = np.asarray(inputs["edge_attr_4"])
    arrays["attr"] = attr
    emb = np.zeros((10, C1 * P), np.float32)
    emb[:, :E1] = np.asarray(inputs["edge_attr_10"]).T
    arrays["emb_t"] = emb

    nc = bacc.Bacc("TRN2", target_bir_lowering=False, num_devices=1)
    a = {n: nc.dram_tensor(f"in_{n}", list(v.shape), mybir.dt.from_np(v.dtype), kind="ExternalInput").ap()
         for n, v in arrays.items()}
    out = nc.dram_tensor("out", [N, D], F32, kind="ExternalOutput").ap()
    program(nc, a, out)
    r = run_bass_kernel_spmd(nc, [{f"in_{n}": v for n, v in arrays.items()}], core_ids=[0])
    return r.results[0]["out"]
```
